# Optimizing a Trainium2 kernel written in Bass

```python
import numpy as np
import jax
import jax.numpy as jnp

def _softmax(x, axis=-1):
    return jax.nn.softmax(x, axis=axis)

def _gelu(x):
    return jax.nn.gelu(x, approximate=True)

def _silu(x):
    return jax.nn.silu(x)

def _sigmoid(x):
    return jax.nn.sigmoid(x)

def _layernorm(x, axis=-1, eps=1e-05):
    m = jnp.mean(x, axis=axis, keepdims=True)
    v = jnp.var(x, axis=axis, keepdims=True)
    return (x - m) / jnp.sqrt(v + eps)

def _scatter_add(tgt, idx, src, axis=0):
    return tgt.at[idx].add(src)

def _segment_sum(src, seg, n):
    return jax.ops.segment_sum(src, seg, n)
kernel_name = 'mk_flamingo_gated_d4_seqx_r8_9ae807'

def setup_inputs(seed: int=0):
    np.random.seed(seed)
    _w = jnp.asarray

    def _rec_inputs():
        import jax
        import jax.numpy as jnp
        _rk = jax.random.key(seed)
        x = -0.0002928 + 1 * jax.random.normal(jax.random.fold_in(_rk, 1), (64, 64, 128), jnp.float32)
        _lenS = 64 - jax.random.randint(jax.random.fold_in(_rk, 7), (64,), 0, max(1, 64 // 4) + 1, jnp.int32)
        _lenS2 = 64 - jax.random.randint(jax.random.fold_in(_rk, 8), (64,), 0, max(1, 64 // 4) + 1, jnp.int32)
        _ctx_768P = jax.random.normal(jax.random.fold_in(_rk, 11), (64, 16, 96), jnp.float32)
        _ctx_768c = jax.random.dirichlet(jax.random.fold_in(_rk, 511), 0.3 * jnp.ones((16,), jnp.float32), (64, 64))
        _ctx_768t = jnp.einsum('bsk,bkd->bsd', _ctx_768c, _ctx_768P)
        _ctx_768t = _ctx_768t * jax.lax.rsqrt(jnp.mean(jnp.square(_ctx_768t)) + 1e-12) * 0.953939
        ctx_768 = -0.00055796 + 0.999787 * (_ctx_768t + 0.3 * jax.random.normal(jax.random.fold_in(_rk, 611), (64, 64, 96), jnp.float32))
        _validS = jnp.arange(64)[None, :] < _lenS[:, None]
        _validS2 = jnp.arange(64)[None, :] < _lenS2[:, None]
        _causal = jnp.tril(jnp.ones((64, 64), dtype=bool))
        mask_BxS_bf1 = jnp.ones((64, 64), dtype=bool)
        mask_BxS2_bf1 = jnp.ones((64, 64), dtype=bool)
        _g = jax.random.normal(jax.random.fold_in(_rk, 9001), (2, 4), jnp.float32)
        _g = jnp.sign(_g) * jnp.maximum(jnp.abs(_g), 1.0) + (_g == 0) * 1.0
        g_xattn = _g[0]
        g_ffn = _g[1]
        return (x, ctx_768, mask_BxS_bf1, mask_BxS2_bf1, g_xattn, g_ffn)
    x, ctx_768, mask_BxS_bf1, mask_BxS2_bf1, g_xattn, g_ffn = _rec_inputs()

    def _L0_xattn_setup():
        import jax, jax.numpy as jnp
        import numpy as np
        HEADS = 16
        DIM_HEAD = 64
        key = jax.random.key(seed)
        ks = jax.random.split(key, 7)
        b, n, m = (2, 256, 128)
        query_dim, context_dim = (128, 96)
        inner = HEADS * DIM_HEAD
        s_q = 1.0 / np.sqrt(query_dim)
        s_c = 1.0 / np.sqrt(context_dim)
        s_i = 1.0 / np.sqrt(inner)
        return {'x': jax.random.normal(ks[0], (b, n, query_dim), jnp.float32), 'context': jax.random.normal(ks[1], (b, m, context_dim), jnp.float32), 'Wq': jax.random.normal(ks[2], (query_dim, inner), jnp.float32) * s_q, 'Wk': jax.random.normal(ks[3], (context_dim, inner), jnp.float32) * s_c, 'Wv': jax.random.normal(ks[4], (context_dim, inner), jnp.float32) * s_c, 'Wo': jax.random.normal(ks[5], (inner, query_dim), jnp.float32) * s_i, 'bo': jax.random.normal(ks[6], (query_dim,), jnp.float32) * 0.01}
    _L0_xattn_all = _L0_xattn_setup()
    _L0_xattn_in = {k: v for k, v in _L0_xattn_all.items() if k in ('Wq', 'Wk', 'Wv', 'Wo', 'bo')}
    del _L0_xattn_all

    def _L0_ffn_setup():
        import jax, jax.numpy as jnp
        import numpy as np
        D = 128
        E = 8
        key = jax.random.key(seed)
        ks = jax.random.split(key, 7)
        s = 1.0 / np.sqrt(D)
        x = jax.random.normal(ks[0], (4, 256, D), dtype=jnp.float32)
        Wg = jax.random.uniform(ks[1], (D, E), minval=-s, maxval=s, dtype=jnp.float32)
        bg = jax.random.uniform(ks[2], (E,), minval=-s, maxval=s, dtype=jnp.float32)
        W1 = jax.random.uniform(ks[3], (E, D, D), minval=-s, maxval=s, dtype=jnp.float32)
        b1 = jax.random.uniform(ks[4], (E, D), minval=-s, maxval=s, dtype=jnp.float32)
        W2 = jax.random.uniform(ks[5], (E, D, D), minval=-s, maxval=s, dtype=jnp.float32)
        b2 = jax.random.uniform(ks[6], (E, D), minval=-s, maxval=s, dtype=jnp.float32)
        return {'x': x, 'Wg': Wg, 'bg': bg, 'W1': W1, 'b1': b1, 'W2': W2, 'b2': b2}
    _L0_ffn_all = _L0_ffn_setup()
    _L0_ffn_in = {k: v for k, v in _L0_ffn_all.items() if k in ('Wg', 'bg', 'W1', 'b1', 'W2', 'b2')}
    del _L0_ffn_all

    def _L1_xattn_setup():
        import jax, jax.numpy as jnp
        import numpy as np
        B, T, DT, G, DV = (16, 64, 128, 72, 96)
        H, DH = (4, 32)
        INNER = H * DH
        HID = 4 * DT
        N_STATE = 64
        K_TOP = 32

        def layernorm(x, g, b, eps=1e-05):
            m = x.mean(-1, keepdims=True)
            v = x.var(-1, keepdims=True)
            return (x - m) * jax.lax.rsqrt(v + eps) * g + b

        def s4d(x, log_dt, A_re, A_im, C_re, C_im, D_skip):
            Bb, L, D = x.shape
            dt = jnp.exp(log_dt)
            A = A_re + 1j * A_im
            C = C_re + 1j * C_im
            dtA = dt[:, None] * A
            dC = C * (jnp.exp(dtA) - 1.0) / A
            powers = jnp.exp(dtA[:, :, None] * jnp.arange(L))
            K = 2.0 * jnp.einsum('dn,dnl->dl', dC, powers).real
            n = 2 * L
            Kf = jnp.fft.rfft(K, n=n, axis=-1)
            xf = jnp.fft.rfft(x, n=n, axis=1)
            y = jnp.fft.irfft(xf * Kf.T[None], n=n, axis=1)[:, :L]
            return y + x * D_skip
        key = jax.random.key(seed)
        ks = jax.random.split(key, 16)
        s = 0.02
        inp = {'x_text': jax.random.normal(ks[0], (B, T, DT), jnp.float32), 'x_vision': jax.random.normal(ks[1], (B, G, DV), jnp.float32), 'text_mask': jnp.ones((B, T), bool), 'vision_mask': jnp.ones((B, G), bool), 'Wq': jax.random.normal(ks[2], (DT, INNER), jnp.float32) * s, 'Wk': jax.random.normal(ks[3], (DV, INNER), jnp.float32) * s, 'Wv': jax.random.normal(ks[4], (DV, DT), jnp.float32) * s, 'W_film_in': jax.random.normal(ks[5], (DT, 2 * DT), jnp.float32) * s, 'b_film_in': jnp.zeros((2 * DT,), jnp.float32), 'W_film_out': jax.random.normal(ks[6], (DT, 2 * DT), jnp.float32) * s, 'b_film_out': jnp.zeros((2 * DT,), jnp.float32), 'g_norm_in': jnp.ones((DT,), jnp.float32), 'b_norm_in': jnp.zeros((DT,), jnp.float32), 'g_norm_out': jnp.ones((DT,), jnp.float32), 'b_norm_out': jnp.zeros((DT,), jnp.float32), 'g_ffn': jnp.ones((DT,), jnp.float32), 'b_ffn': jnp.zeros((DT,), jnp.float32), 'W1': jax.random.normal(ks[7], (DT, HID), jnp.float32) * s, 'b1': jnp.zeros((HID,), jnp.float32), 'W2': jax.random.normal(ks[8], (HID, DT), jnp.float32) * s, 'b2': jnp.zeros((DT,), jnp.float32), 'log_dt': jnp.log(0.001) + jax.random.uniform(ks[9], (DT,), jnp.float32) * (jnp.log(0.1) - jnp.log(0.001)), 'A_re': -0.5 * jnp.ones((DT, N_STATE), jnp.float32), 'A_im': jnp.tile(jnp.pi * jnp.arange(N_STATE, dtype=jnp.float32), (DT, 1)), 'C_re': jax.random.normal(ks[10], (DT, N_STATE), jnp.float32) * 0.5 ** 0.5, 'C_im': jax.random.normal(ks[11], (DT, N_STATE), jnp.float32) * 0.5 ** 0.5, 'D_skip': jax.random.normal(ks[12], (DT,), jnp.float32), 'mod_gate': jnp.array(0.5, jnp.float32)}
        return inp
    _L1_xattn_all = _L1_xattn_setup()
    _L1_xattn_in = {k: v for k, v in _L1_xattn_all.items() if k in ('Wq', 'Wk', 'Wv', 'W_film_in', 'b_film_in', 'W_film_out', 'b_film_out', 'g_norm_in', 'b_norm_in', 'g_norm_out', 'b_norm_out', 'g_ffn', 'b_ffn', 'W1', 'b1', 'W2', 'b2', 'log_dt', 'A_re', 'A_im', 'C_re', 'C_im', 'D_skip', 'mod_gate')}
    del _L1_xattn_all

    def _L1_ffn_setup():
        import jax, jax.numpy as jnp
        import numpy as np
        NUM_EXPERTS = 8
        HIDDEN = 128
        D_FF = 512
        SCALE = 0.8
        SPARSITY = 0.1

        def _perturb_attractive(w, scale=SCALE, sparsity=SPARSITY):
            a = jnp.abs(w)
            flat = a.ravel()
            n = flat.shape[0]
            k = max(1, int(n * sparsity / 2))
            s = jnp.sort(flat)
            thr_bot = s[k - 1]
            thr_top = s[n - k]
            tier = jnp.where(a >= thr_top, -1.0, jnp.where(a <= thr_bot, 1.0, 0.0))
            return w + scale * w * tier

        def _stack_expert_params(w):
            pw = _perturb_attractive(w)
            return jnp.concatenate([w[None], jnp.broadcast_to(pw, (NUM_EXPERTS - 1,) + w.shape)], axis=0)
        key = jax.random.key(seed)
        ks = jax.random.split(key, 6)
        B, S, H, F, E = (2, 256, HIDDEN, D_FF, NUM_EXPERTS)
        return {'x': jax.random.normal(ks[0], (B, S, H), dtype=jnp.float32), 'W1': jax.random.normal(ks[1], (H, F), dtype=jnp.float32) * (1.0 / np.sqrt(H)), 'b1': jax.random.normal(ks[2], (F,), dtype=jnp.float32) * 0.02, 'W2': jax.random.normal(ks[3], (F, H), dtype=jnp.float32) * (1.0 / np.sqrt(F)), 'b2': jax.random.normal(ks[4], (H,), dtype=jnp.float32) * 0.02, 'ln_gamma': jnp.ones((H,), dtype=jnp.float32), 'ln_beta': jnp.zeros((H,), dtype=jnp.float32), 'Wr': jax.random.normal(ks[5], (H, E), dtype=jnp.float32) * (1.0 / np.sqrt(H)), 'br': jnp.zeros((E,), dtype=jnp.float32)}
    _L1_ffn_all = _L1_ffn_setup()
    _L1_ffn_in = {k: v for k, v in _L1_ffn_all.items() if k in ('W1', 'b1', 'W2', 'b2', 'ln_gamma', 'ln_beta', 'Wr', 'br')}
    del _L1_ffn_all

    def _L2_xattn_setup():
        import jax, jax.numpy as jnp
        import numpy as np
        HEADS = 8
        DIM_HEAD = 64
        SCALE = DIM_HEAD ** (-0.5)
        key = jax.random.key(seed)
        ks = jax.random.split(key, 7)
        b, n, m = (4, 256, 128)
        qd, cd, inner = (128, 96, HEADS * DIM_HEAD)
        s = lambda fan_in: 1.0 / np.sqrt(fan_in)
        return {'x': jax.random.normal(ks[0], (b, n, qd), jnp.float32), 'context': jax.random.normal(ks[1], (b, m, cd), jnp.float32), 'Wq': jax.random.normal(ks[2], (qd, inner), jnp.float32) * s(qd), 'Wk': jax.random.normal(ks[3], (cd, inner), jnp.float32) * s(cd), 'Wv': jax.random.normal(ks[4], (cd, inner), jnp.float32) * s(cd), 'Wout': jax.random.normal(ks[5], (inner, qd), jnp.float32) * s(inner), 'bout': jax.random.normal(ks[6], (qd,), jnp.float32) * 0.01}
    _L2_xattn_all = _L2_xattn_setup()
    _L2_xattn_in = {k: v for k, v in _L2_xattn_all.items() if k in ('Wq', 'Wk', 'Wv', 'Wout', 'bout')}
    del _L2_xattn_all

    def _L2_ffn_setup():
        import jax, jax.numpy as jnp
        import numpy as np
        EPS = 1e-05

        def act_quant(x):
            scale = 127.0 / jnp.clip(jnp.max(jnp.abs(x), axis=-1, keepdims=True), EPS, None)
            q = jnp.clip(jnp.round(x * scale), -128.0, 127.0) / scale
            return x + jax.lax.stop_gradient(q - x)

        def weight_quant(w):
            scale = 1.0 / jnp.clip(jnp.mean(jnp.abs(w)), EPS, None)
            q = jnp.clip(jnp.round(w * scale), -1.0, 1.0) / scale
            return w + jax.lax.stop_gradient(q - w)

        def bitlinear(x, w):
            return act_quant(x) @ weight_quant(w).T
        key = jax.random.key(seed)
        k1, k2, k3, k4 = jax.random.split(key, 4)
        H, I = (128, 512)
        B, S = (4, 512)
        init = 0.02
        x = jax.random.normal(k1, (B, S, H), dtype=jnp.float32)
        w_gate = jax.random.normal(k2, (I, H), dtype=jnp.float32) * init
        w_up = jax.random.normal(k3, (I, H), dtype=jnp.float32) * init
        w_down = jax.random.normal(k4, (H, I), dtype=jnp.float32) * init
        return {'x': x, 'w_gate': w_gate, 'w_up': w_up, 'w_down': w_down}
    _L2_ffn_all = _L2_ffn_setup()
    _L2_ffn_in = {k: v for k, v in _L2_ffn_all.items() if k in ('w_gate', 'w_up', 'w_down')}
    del _L2_ffn_all

    def _L3_xattn_setup():
        import jax, jax.numpy as jnp
        import numpy as np
        HEADS = 8
        DIM_HEAD = 64
        QUERY_DIM = 128
        CONTEXT_DIM = 96
        INNER = HEADS * DIM_HEAD
        key = jax.random.key(seed)
        ks = jax.random.split(key, 7)
        B, Sq, Skv = (4, 512, 128)
        x = jax.random.normal(ks[0], (B, Sq, QUERY_DIM), dtype=jnp.float32)
        context = jax.random.normal(ks[1], (B, Skv, CONTEXT_DIM), dtype=jnp.float32)
        Wq = jax.random.normal(ks[2], (QUERY_DIM, INNER), dtype=jnp.float32) * QUERY_DIM ** (-0.5)
        Wk = jax.random.normal(ks[3], (CONTEXT_DIM, INNER), dtype=jnp.float32) * CONTEXT_DIM ** (-0.5)
        Wv = jax.random.normal(ks[4], (CONTEXT_DIM, INNER), dtype=jnp.float32) * CONTEXT_DIM ** (-0.5)
        Wo = jax.random.normal(ks[5], (INNER, QUERY_DIM), dtype=jnp.float32) * INNER ** (-0.5)
        bo = jax.random.normal(ks[6], (QUERY_DIM,), dtype=jnp.float32) * 0.01
        return {'x': x, 'context': context, 'Wq': Wq, 'Wk': Wk, 'Wv': Wv, 'Wo': Wo, 'bo': bo}
    _L3_xattn_all = _L3_xattn_setup()
    _L3_xattn_in = {k: v for k, v in _L3_xattn_all.items() if k in ('Wq', 'Wk', 'Wv', 'Wo', 'bo')}
    del _L3_xattn_all

    def _L3_ffn_setup():
        import jax, jax.numpy as jnp
        import numpy as np

        def _bitlinear(x, w_latent):
            scale = jax.lax.stop_gradient(jnp.clip(jnp.mean(jnp.abs(w_latent), axis=1, keepdims=True), 1e-05, None))
            tern = jnp.clip(jnp.round(w_latent / scale), -1.0, 1.0)
            w = w_latent + jax.lax.stop_gradient(tern - w_latent)
            return x @ (w * scale).T
        key = jax.random.key(seed)
        ks = jax.random.split(key, 6)
        dim, hidden, rank = (128, 512, 16)
        B, S = (4, 512)
        x = jax.random.normal(ks[0], (B, S, dim), dtype=jnp.float32)
        w_fc = 0.02 * jax.random.normal(ks[1], (hidden, dim), dtype=jnp.float32)
        w_proj = 0.02 * jax.random.normal(ks[2], (dim, hidden), dtype=jnp.float32)
        u = 0.02 * jax.random.normal(ks[3], (hidden, rank), dtype=jnp.float32)
        v = 0.02 * jax.random.normal(ks[4], (rank, dim), dtype=jnp.float32)
        fast_b = jax.random.normal(ks[5], (rank, rank), dtype=jnp.float32)
        gate = jnp.float32(0.05)
        return {'x': x, 'fast_b': fast_b, 'w_fc': w_fc, 'w_proj': w_proj, 'u': u, 'v': v, 'gate': gate}
    _L3_ffn_all = _L3_ffn_setup()
    _L3_ffn_in = {k: v for k, v in _L3_ffn_all.items() if k in ('fast_b', 'w_fc', 'w_proj', 'u', 'v', 'gate')}
    del _L3_ffn_all
    return {'x': x, 'ctx_768': ctx_768, 'mask_BxS_bf1': mask_BxS_bf1, 'mask_BxS2_bf1': mask_BxS2_bf1, 'g_xattn': g_xattn, 'g_ffn': g_ffn, 'L0_xattn_Wq': _L0_xattn_in['Wq'], 'L0_xattn_Wk': _L0_xattn_in['Wk'], 'L0_xattn_Wv': _L0_xattn_in['Wv'], 'L0_xattn_Wo': _L0_xattn_in['Wo'], 'L0_xattn_bo': _L0_xattn_in['bo'], 'L0_ffn_Wg': _L0_ffn_in['Wg'], 'L0_ffn_bg': _L0_ffn_in['bg'], 'L0_ffn_W1': _L0_ffn_in['W1'], 'L0_ffn_b1': _L0_ffn_in['b1'], 'L0_ffn_W2': _L0_ffn_in['W2'], 'L0_ffn_b2': _L0_ffn_in['b2'], 'L1_xattn_Wq': _L1_xattn_in['Wq'], 'L1_xattn_Wk': _L1_xattn_in['Wk'], 'L1_xattn_Wv': _L1_xattn_in['Wv'], 'L1_xattn_W_film_in': _L1_xattn_in['W_film_in'], 'L1_xattn_b_film_in': _L1_xattn_in['b_film_in'], 'L1_xattn_W_film_out': _L1_xattn_in['W_film_out'], 'L1_xattn_b_film_out': _L1_xattn_in['b_film_out'], 'L1_xattn_g_norm_in': _L1_xattn_in['g_norm_in'], 'L1_xattn_b_norm_in': _L1_xattn_in['b_norm_in'], 'L1_xattn_g_norm_out': _L1_xattn_in['g_norm_out'], 'L1_xattn_b_norm_out': _L1_xattn_in['b_norm_out'], 'L1_xattn_g_ffn': _L1_xattn_in['g_ffn'], 'L1_xattn_b_ffn': _L1_xattn_in['b_ffn'], 'L1_xattn_W1': _L1_xattn_in['W1'], 'L1_xattn_b1': _L1_xattn_in['b1'], 'L1_xattn_W2': _L1_xattn_in['W2'], 'L1_xattn_b2': _L1_xattn_in['b2'], 'L1_xattn_log_dt': _L1_xattn_in['log_dt'], 'L1_xattn_A_re': _L1_xattn_in['A_re'], 'L1_xattn_A_im': _L1_xattn_in['A_im'], 'L1_xattn_C_re': _L1_xattn_in['C_re'], 'L1_xattn_C_im': _L1_xattn_in['C_im'], 'L1_xattn_D_skip': _L1_xattn_in['D_skip'], 'L1_xattn_mod_gate': _L1_xattn_in['mod_gate'], 'L1_ffn_W1': _L1_ffn_in['W1'], 'L1_ffn_b1': _L1_ffn_in['b1'], 'L1_ffn_W2': _L1_ffn_in['W2'], 'L1_ffn_b2': _L1_ffn_in['b2'], 'L1_ffn_ln_gamma': _L1_ffn_in['ln_gamma'], 'L1_ffn_ln_beta': _L1_ffn_in['ln_beta'], 'L1_ffn_Wr': _L1_ffn_in['Wr'], 'L1_ffn_br': _L1_ffn_in['br'], 'L2_xattn_Wq': _L2_xattn_in['Wq'], 'L2_xattn_Wk': _L2_xattn_in['Wk'], 'L2_xattn_Wv': _L2_xattn_in['Wv'], 'L2_xattn_Wout': _L2_xattn_in['Wout'], 'L2_xattn_bout': _L2_xattn_in['bout'], 'L2_ffn_w_gate': _L2_ffn_in['w_gate'], 'L2_ffn_w_up': _L2_ffn_in['w_up'], 'L2_ffn_w_down': _L2_ffn_in['w_down'], 'L3_xattn_Wq': _L3_xattn_in['Wq'], 'L3_xattn_Wk': _L3_xattn_in['Wk'], 'L3_xattn_Wv': _L3_xattn_in['Wv'], 'L3_xattn_Wo': _L3_xattn_in['Wo'], 'L3_xattn_bo': _L3_xattn_in['bo'], 'L3_ffn_fast_b': _L3_ffn_in['fast_b'], 'L3_ffn_w_fc': _L3_ffn_in['w_fc'], 'L3_ffn_w_proj': _L3_ffn_in['w_proj'], 'L3_ffn_u': _L3_ffn_in['u'], 'L3_ffn_v': _L3_ffn_in['v'], 'L3_ffn_gate': _L3_ffn_in['gate']}

def reference(x, ctx_768, mask_BxS_bf1, mask_BxS2_bf1, g_xattn, g_ffn, L0_xattn_Wq, L0_xattn_Wk, L0_xattn_Wv, L0_xattn_Wo, L0_xattn_bo, L0_ffn_Wg, L0_ffn_bg, L0_ffn_W1, L0_ffn_b1, L0_ffn_W2, L0_ffn_b2, L1_xattn_Wq, L1_xattn_Wk, L1_xattn_Wv, L1_xattn_W_film_in, L1_xattn_b_film_in, L1_xattn_W_film_out, L1_xattn_b_film_out, L1_xattn_g_norm_in, L1_xattn_b_norm_in, L1_xattn_g_norm_out, L1_xattn_b_norm_out, L1_xattn_g_ffn, L1_xattn_b_ffn, L1_xattn_W1, L1_xattn_b1, L1_xattn_W2, L1_xattn_b2, L1_xattn_log_dt, L1_xattn_A_re, L1_xattn_A_im, L1_xattn_C_re, L1_xattn_C_im, L1_xattn_D_skip, L1_xattn_mod_gate, L1_ffn_W1, L1_ffn_b1, L1_ffn_W2, L1_ffn_b2, L1_ffn_ln_gamma, L1_ffn_ln_beta, L1_ffn_Wr, L1_ffn_br, L2_xattn_Wq, L2_xattn_Wk, L2_xattn_Wv, L2_xattn_Wout, L2_xattn_bout, L2_ffn_w_gate, L2_ffn_w_up, L2_ffn_w_down, L3_xattn_Wq, L3_xattn_Wk, L3_xattn_Wv, L3_xattn_Wo, L3_xattn_bo, L3_ffn_fast_b, L3_ffn_w_fc, L3_ffn_w_proj, L3_ffn_u, L3_ffn_v, L3_ffn_gate):
    import jax
    import jax.numpy as jnp

    def _L0_xattn_ref(x, context, Wq, Wk, Wv, Wo, bo):
        import jax, jax.numpy as jnp
        import numpy as np
        HEADS = 16
        DIM_HEAD = 64
        b, n, _ = x.shape
        h, d = (HEADS, DIM_HEAD)
        scale = d ** (-0.5)
        q = (x @ Wq).reshape(b, n, h, d).transpose(0, 2, 1, 3)
        k = (context @ Wk).reshape(b, -1, h, d).transpose(0, 2, 1, 3)
        v = (context @ Wv).reshape(b, -1, h, d).transpose(0, 2, 1, 3)
        sim = jnp.einsum('bhid,bhjd->bhij', q, k) * scale
        attn = jax.nn.softmax(sim, axis=-1)
        out = jnp.einsum('bhij,bhjd->bhid', attn, v)
        out = out.transpose(0, 2, 1, 3).reshape(b, n, h * d)
        return out @ Wo + bo

    def _L0_ffn_ref(x, Wg, bg, W1, b1, W2, b2):
        import jax, jax.numpy as jnp
        import numpy as np
        D = 128
        E = 8
        N, T, d = x.shape
        x_flat = x.reshape(N * T, d)
        logits = x_flat @ Wg + bg
        probs = jax.nn.softmax(logits, axis=-1)
        assignments = jnp.argmax(probs, axis=-1)
        h = jnp.einsum('nd,edh->neh', x_flat, W1) + b1[None]
        h = jax.nn.gelu(h, approximate=False)
        eo = jnp.einsum('neh,ehd->ned', h, W2) + b2[None]
        selected = jnp.take_along_axis(eo, assignments[:, None, None], axis=1)[:, 0, :]
        w = jnp.take_along_axis(probs, assignments[:, None], axis=1)
        out = (w * selected).reshape(N, T, d)
        return out

    def _L1_xattn_ref(x_text, x_vision, text_mask, vision_mask, Wq, Wk, Wv, W_film_in, b_film_in, W_film_out, b_film_out, g_norm_in, b_norm_in, g_norm_out, b_norm_out, g_ffn, b_ffn, W1, b1, W2, b2, log_dt, A_re, A_im, C_re, C_im, D_skip, mod_gate):
        import jax, jax.numpy as jnp
        import numpy as np
        B, T, DT, G, DV = (16, 64, 128, 72, 96)
        H, DH = (4, 32)
        INNER = H * DH
        HID = 4 * DT
        N_STATE = 64
        K_TOP = 32

        def layernorm(x, g, b, eps=1e-05):
            m = x.mean(-1, keepdims=True)
            v = x.var(-1, keepdims=True)
            return (x - m) * jax.lax.rsqrt(v + eps) * g + b

        def s4d(x, log_dt, A_re, A_im, C_re, C_im, D_skip):
            Bb, L, D = x.shape
            dt = jnp.exp(log_dt)
            A = A_re + 1j * A_im
            C = C_re + 1j * C_im
            dtA = dt[:, None] * A
            dC = C * (jnp.exp(dtA) - 1.0) / A
            powers = jnp.exp(dtA[:, :, None] * jnp.arange(L))
            K = 2.0 * jnp.einsum('dn,dnl->dl', dC, powers).real
            n = 2 * L
            Kf = jnp.fft.rfft(K, n=n, axis=-1)
            xf = jnp.fft.rfft(x, n=n, axis=1)
            y = jnp.fft.irfft(xf * Kf.T[None], n=n, axis=1)[:, :L]
            return y + x * D_skip
        Bb, Tt, D = x_text.shape
        Gg = x_vision.shape[1]
        Q = (x_text @ Wq).reshape(Bb, Tt, H, DH)
        K = (x_vision @ Wk).reshape(Bb, Gg, H, DH)
        scores = jnp.einsum('bthd,bghd->bhtg', Q, K) / np.sqrt(DH).astype(np.float32)
        scores = jnp.where(vision_mask[:, None, None, :], scores, -jnp.inf)
        topv, topi = jax.lax.top_k(scores, K_TOP)
        probs = jax.nn.softmax(topv, axis=-1)
        bi = jnp.arange(Bb)[:, None, None, None]
        hi = jnp.arange(H)[None, :, None, None]
        ti = jnp.arange(Tt)[None, None, :, None]
        attn = jnp.zeros_like(scores).at[bi, hi, ti, topi].set(probs)
        attn_mean = attn.mean(axis=1)
        V = x_vision @ Wv
        c_t = jnp.einsum('btg,bgd->btd', attn_mean, V)
        c_t = c_t * text_mask[..., None]
        x = layernorm(x_text, g_norm_in, b_norm_in)
        scale_in, shift_in = jnp.split(c_t @ W_film_in + b_film_in, 2, axis=-1)
        x = x * (1.0 + mod_gate * scale_in) + mod_gate * shift_in
        y = s4d(x, log_dt, A_re, A_im, C_re, C_im, D_skip)
        scale_out, shift_out = jnp.split(c_t @ W_film_out + b_film_out, 2, axis=-1)
        y = y * (1.0 + mod_gate * scale_out) + mod_gate * shift_out
        xt = x_text + y
        h = layernorm(xt, g_ffn, b_ffn)
        h = jax.nn.gelu(h @ W1 + b1, approximate=False) @ W2 + b2
        xt = xt + h
        return layernorm(xt, g_norm_out, b_norm_out)

    def _L1_ffn_ref(x, W1, b1, W2, b2, ln_gamma, ln_beta, Wr, br):
        import jax, jax.numpy as jnp
        import numpy as np
        NUM_EXPERTS = 8
        HIDDEN = 128
        D_FF = 512
        SCALE = 0.8
        SPARSITY = 0.1

        def _perturb_attractive(w, scale=SCALE, sparsity=SPARSITY):
            a = jnp.abs(w)
            flat = a.ravel()
            n = flat.shape[0]
            k = max(1, int(n * sparsity / 2))
            s = jnp.sort(flat)
            thr_bot = s[k - 1]
            thr_top = s[n - k]
            tier = jnp.where(a >= thr_top, -1.0, jnp.where(a <= thr_bot, 1.0, 0.0))
            return w + scale * w * tier

        def _stack_expert_params(w):
            pw = _perturb_attractive(w)
            return jnp.concatenate([w[None], jnp.broadcast_to(pw, (NUM_EXPERTS - 1,) + w.shape)], axis=0)
        mu = jnp.mean(x, axis=-1, keepdims=True)
        var = jnp.mean(jnp.square(x - mu), axis=-1, keepdims=True)
        h = (x - mu) * jax.lax.rsqrt(var + 1e-05) * ln_gamma + ln_beta
        logits = jnp.einsum('bsh,he->bse', h, Wr) + br
        probs = jax.nn.softmax(logits, axis=-1)
        W1s = _stack_expert_params(W1)
        b1s = _stack_expert_params(b1)
        W2s = _stack_expert_params(W2)
        b2s = _stack_expert_params(b2)
        pre = jnp.einsum('bsh,ehf->besf', x, W1s) + b1s[None, :, None, :]
        act = jax.nn.gelu(pre)
        y = jnp.einsum('besf,efh->besh', act, W2s) + b2s[None, :, None, :]
        out = jnp.einsum('bse,besh->bsh', probs, y)
        return out

    def _L2_xattn_ref(x, context, Wq, Wk, Wv, Wout, bout):
        import jax, jax.numpy as jnp
        import numpy as np
        HEADS = 8
        DIM_HEAD = 64
        SCALE = DIM_HEAD ** (-0.5)
        b, n, _ = x.shape
        m = context.shape[1]
        q = (x @ Wq).reshape(b, n, HEADS, DIM_HEAD)
        k = (context @ Wk).reshape(b, m, HEADS, DIM_HEAD)
        v = (context @ Wv).reshape(b, m, HEADS, DIM_HEAD)
        sim = jnp.einsum('bihd,bjhd->bhij', q, k) * SCALE
        attn = jax.nn.softmax(sim, axis=-1)
        out = jnp.einsum('bhij,bjhd->bihd', attn, v).reshape(b, n, HEADS * DIM_HEAD)
        return out @ Wout + bout

    def _L2_ffn_ref(x, w_gate, w_up, w_down):
        import jax, jax.numpy as jnp
        import numpy as np
        EPS = 1e-05

        def act_quant(x):
            scale = 127.0 / jnp.clip(jnp.max(jnp.abs(x), axis=-1, keepdims=True), EPS, None)
            q = jnp.clip(jnp.round(x * scale), -128.0, 127.0) / scale
            return x + jax.lax.stop_gradient(q - x)

        def weight_quant(w):
            scale = 1.0 / jnp.clip(jnp.mean(jnp.abs(w)), EPS, None)
            q = jnp.clip(jnp.round(w * scale), -1.0, 1.0) / scale
            return w + jax.lax.stop_gradient(q - w)

        def bitlinear(x, w):
            return act_quant(x) @ weight_quant(w).T
        g = bitlinear(x, w_gate)
        u = bitlinear(x, w_up)
        h = jnp.square(jax.nn.relu(g)) * u
        return bitlinear(h, w_down)

    def _L3_xattn_ref(x, context, Wq, Wk, Wv, Wo, bo):
        import jax, jax.numpy as jnp
        import numpy as np
        HEADS = 8
        DIM_HEAD = 64
        QUERY_DIM = 128
        CONTEXT_DIM = 96
        INNER = HEADS * DIM_HEAD
        B, Sq, _ = x.shape
        h, d = (HEADS, DIM_HEAD)
        scale = d ** (-0.5)
        q = (x @ Wq).reshape(B, Sq, h, d).transpose(0, 2, 1, 3)
        k = (context @ Wk).reshape(B, -1, h, d).transpose(0, 2, 1, 3)
        v = (context @ Wv).reshape(B, -1, h, d).transpose(0, 2, 1, 3)
        scores = jnp.einsum('bhid,bhjd->bhij', q, k) * scale
        attn = jax.nn.softmax(scores, axis=-1)
        out = jnp.einsum('bhij,bhjd->bhid', attn, v)
        out = out.transpose(0, 2, 1, 3).reshape(B, Sq, h * d)
        return out @ Wo + bo

    def _L3_ffn_ref(x, fast_b, w_fc, w_proj, u, v, gate):
        import jax, jax.numpy as jnp
        import numpy as np

        def _bitlinear(x, w_latent):
            scale = jax.lax.stop_gradient(jnp.clip(jnp.mean(jnp.abs(w_latent), axis=1, keepdims=True), 1e-05, None))
            tern = jnp.clip(jnp.round(w_latent / scale), -1.0, 1.0)
            w = w_latent + jax.lax.stop_gradient(tern - w_latent)
            return x @ (w * scale).T
        h = _bitlinear(x, w_fc) + gate * (x @ v.T @ fast_b.T @ u.T)
        r = jnp.maximum(h, 0.0)
        return _bitlinear(r * r, w_proj)
    x = x + jnp.tanh(g_xattn[0]) * _L0_xattn_ref(_layernorm(x, axis=-1), ctx_768, L0_xattn_Wq, L0_xattn_Wk, L0_xattn_Wv, L0_xattn_Wo, L0_xattn_bo)
    x = x + jnp.tanh(g_ffn[0]) * _L0_ffn_ref(_layernorm(x, axis=-1), L0_ffn_Wg, L0_ffn_bg, L0_ffn_W1, L0_ffn_b1, L0_ffn_W2, L0_ffn_b2)
    x = x + jnp.tanh(g_xattn[1]) * _L1_xattn_ref(_layernorm(x, axis=-1), ctx_768, mask_BxS_bf1, mask_BxS2_bf1, L1_xattn_Wq, L1_xattn_Wk, L1_xattn_Wv, L1_xattn_W_film_in, L1_xattn_b_film_in, L1_xattn_W_film_out, L1_xattn_b_film_out, L1_xattn_g_norm_in, L1_xattn_b_norm_in, L1_xattn_g_norm_out, L1_xattn_b_norm_out, L1_xattn_g_ffn, L1_xattn_b_ffn, L1_xattn_W1, L1_xattn_b1, L1_xattn_W2, L1_xattn_b2, L1_xattn_log_dt, L1_xattn_A_re, L1_xattn_A_im, L1_xattn_C_re, L1_xattn_C_im, L1_xattn_D_skip, L1_xattn_mod_gate)
    x = x + jnp.tanh(g_ffn[1]) * _L1_ffn_ref(_layernorm(x, axis=-1), L1_ffn_W1, L1_ffn_b1, L1_ffn_W2, L1_ffn_b2, L1_ffn_ln_gamma, L1_ffn_ln_beta, L1_ffn_Wr, L1_ffn_br)
    x = x + jnp.tanh(g_xattn[2]) * _L2_xattn_ref(_layernorm(x, axis=-1), ctx_768, L2_xattn_Wq, L2_xattn_Wk, L2_xattn_Wv, L2_xattn_Wout, L2_xattn_bout)
    x = x + jnp.tanh(g_ffn[2]) * _L2_ffn_ref(_layernorm(x, axis=-1), L2_ffn_w_gate, L2_ffn_w_up, L2_ffn_w_down)
    x = x + jnp.tanh(g_xattn[3]) * _L3_xattn_ref(_layernorm(x, axis=-1), ctx_768, L3_xattn_Wq, L3_xattn_Wk, L3_xattn_Wv, L3_xattn_Wo, L3_xattn_bo)
    x = x + jnp.tanh(g_ffn[3]) * _L3_ffn_ref(_layernorm(x, axis=-1), L3_ffn_fast_b, L3_ffn_w_fc, L3_ffn_w_proj, L3_ffn_u, L3_ffn_v, L3_ffn_gate)
    return x

_drawn_inputs = setup_inputs


def setup_inputs(seed=0):
    import zlib

    import numpy as np

    out = dict(_drawn_inputs(seed))
    spreads = {'L1_xattn_b_film_in': (0.0, 0.1),
     'L1_xattn_b_film_out': (0.0, 0.1),
     'L1_xattn_g_norm_in': (1.0, 0.2),
     'L1_xattn_b_norm_in': (0.0, 0.1),
     'L1_xattn_g_norm_out': (1.0, 0.2),
     'L1_xattn_b_norm_out': (0.0, 0.1),
     'L1_xattn_g_ffn': (1.0, 0.6),
     'L1_xattn_b_ffn': (0.0, 0.8),
     'L1_xattn_b1': (0.0, 0.646),
     'L1_xattn_b2': (0.0, 0.1),
     'L1_xattn_A_re': (-0.5, 0.548),
     'L1_ffn_ln_gamma': (1.0, 0.6),
     'L1_ffn_ln_beta': (0.0, 0.8),
     'L1_ffn_br': (0.0, 0.8)}
    factors = {'g_ffn': 31.976,
     'L0_xattn_bo': 8.0,
     'L0_ffn_bg': 7.284,
     'L0_ffn_b1': 8.0,
     'L0_ffn_b2': 7.154,
     'L1_xattn_Wq': 8.0,
     'L1_xattn_Wk': 8.0,
     'L1_xattn_Wv': 3.898,
     'L1_xattn_W_film_in': 4.833,
     'L1_xattn_W_film_out': 5.88,
     'L1_ffn_b1': 7.797,
     'L1_ffn_b2': 4.369,
     'L2_xattn_bout': 8.0,
     'L2_ffn_w_gate': 8.0,
     'L2_ffn_w_up': 8.0,
     'L2_ffn_w_down': 8.0,
     'L3_xattn_bo': 33.186,
     'L3_ffn_fast_b': 8.0,
     'L3_ffn_w_fc': 8.0,
     'L3_ffn_w_proj': 8.0,
     'L3_ffn_u': 8.0,
     'L3_ffn_v': 8.0}
    for name, (base, spread) in spreads.items():
        noise = np.random.default_rng([zlib.crc32(name.encode()), seed]).standard_normal(out[name].shape)
        drawn = base * np.exp(spread * noise) if base else spread * noise
        out[name] = jnp.asarray(drawn.astype(out[name].dtype))
    for name, factor in factors.items():
        out[name] = (out[name] * factor).astype(out[name].dtype)
    return out
```

```python
from contextlib import ExitStack

import concourse.bass as bass
from concourse import mybir

ALU = mybir.AluOpType
ACT = mybir.ActivationFunctionType
AX = mybir.AxisListType
F32 = mybir.dt.float32
BF16 = mybir.dt.bfloat16
I32 = mybir.dt.int32
U8 = mybir.dt.uint8

P = 128
B, SEQ, D = 64, 64, 128
CTX, DC = 64, 96
TOK = B * SEQ
TILES = TOK // P
GT = 4
GROUPS = TILES // GT
BANK = 512
EPS = 1e-5
EPSQ = 1e-5
ROUND = 12582912.0


class Signal:

    def __init__(self, sem, base, total):
        self.sem, self.base, self.end = sem, base, base + (total or 0)

    def at(self, count):
        return self.base + (max(count, 0) if isinstance(count, int) else count)


class Semaphores:

    def __init__(self, new):
        self.new, self.spare, self.used = new, [], [[]]

    def next_sublayer(self):
        if len(self.used) > 1:
            self.spare += self.used[-2]
        self.used.append([])

    def take(self, name, total=None):
        sem, base = self.spare.pop(0) if total and self.spare else (self.new(name), 0)
        if total:
            self.used[-1].append((sem, base + total))
        return Signal(sem, base, total)


def pipelined_tiles(eng, step):
    for t in (0, 1):
        step(t, t % 2)
    with eng.Fori(1, TILES // 2 - 1) as it:
        step(2 * it, 0)
        step(2 * it + 1, 1)
    for t in (TILES - 2, TILES - 1):
        step(t, t % 2)


def pipelined_groups(eng, body):
    body(0, True)
    with eng.Fori(1, GROUPS - 1) as g:
        body(g, True)
    body(GROUPS - 1, False)


def allocate(nc, ctx):
    k = Parts()
    k.nc = nc
    k.sb = lambda name, shape, dt=F32: ctx.enter_context(nc.sbuf_tensor(name, shape, dt))
    k.semaphores = Semaphores(lambda name: ctx.enter_context(nc.semaphore(name)))
    k.sem = k.semaphores.take
    k.ps = ctx.enter_context(nc.psum_tensor("ps", [P, 8, BANK], F32))
    k.x = k.sb("x_res", [P, TILES, D])
    k.ctxT = k.sb("ctxT", [P, TOK])
    k.ident = k.sb("ident", [P, P])
    k.onesq = k.sb("ones_square", [P, P])
    k.ones = k.onesq[0:1, :]
    k.gates = k.sb("gates", [P, 8])
    k.toep = k.sb("toeplitz", [P, D, SEQ])
    k.arena = k.sb("arena", [P, 30720])
    k.stat = k.sb("ln_stat", [P, 2, GT, 6])
    k.mv = k.sb("ln_mv", [P, 2, GT, 2])
    k.rstd = k.sb("ln_rstd", [P, 2, GT])
    k.veps = k.sb("ln_veps", [P, 2, GT])
    k.half = k.sb("minus_half", [P, GT])
    k.eps = k.sb("eps", [P, GT])
    k.xn = k.sb("xn", [P, 2, GT, D])
    k.xnT = k.sb("xnT", [P, 2, GT * P])
    return k


class Parts:
    pass


class Carve:

    def __init__(self, k, start=0):
        self.k, self.at = k, start

    def f32(self, *shape):
        n = 1
        for s in shape:
            n *= s
        v = self.k.arena[:, self.at:self.at + n]
        self.at += n
        assert self.at <= 30720, self.at
        if len(shape) == 1:
            return v
        names = " ".join(f"a{i}" for i in range(len(shape)))
        return v.rearrange(f"p ({names}) -> p {names}", **{f"a{i}": s for i, s in enumerate(shape[:-1])})

    def bf16(self, *shape):
        n = 1
        for s in shape:
            n *= s
        v = self.k.arena[:, self.at:self.at + n // 2].bitcast(BF16)
        self.at += n // 2
        assert self.at <= 30720, self.at
        if len(shape) == 1:
            return v
        names = " ".join(f"a{i}" for i in range(len(shape)))
        return v.rearrange(f"p ({names}) -> p {names}", **{f"a{i}": s for i, s in enumerate(shape[:-1])})


def setup(k, io):
    nc = k.nc
    c_in, g_in, zero, made, turned, laid, tanh = (k.sem("setup_" + n) for n in (
        "ctx_loaded", "gates_loaded", "zeroed", "constants", "ctx_turned", "ctx_laid", "gates_ready"))
    x_in, ready = k.sem("setup_x_loaded"), k.sem("setup_done", 1)
    carve = Carve(k)
    ctx_tok = carve.f32(TILES, DC)
    graw = carve.f32(8)

    def sp(e):
        e.dma_start(ctx_tok[:], io["ctx_768"].rearrange("b s c -> (b s) c").rearrange("(t p) c -> p t c", p=P)).then_inc(c_in.sem, 16)
        k.thresholds.sp(e)
        e.dma_start(k.x[:], io["x"].rearrange("b s c -> (b s) c").rearrange("(t p) c -> p t c", p=P)).then_inc(x_in.sem, 16)
        e.dma_start(graw[:, 0:4], io["g_xattn"].rearrange("(a n) -> a n", a=1).partition_broadcast(P)).then_inc(g_in.sem, 16)
        e.dma_start(graw[:, 4:8], io["g_ffn"].rearrange("(a n) -> a n", a=1).partition_broadcast(P)).then_inc(g_in.sem, 16)

    def pool(e):
        nc.gpsimd.memset(k.ident[:], 0.0).then_inc(zero.sem, 1)
        e.wait_ge(zero.sem, zero.at(1))
        nc.gpsimd.memset(k.onesq[:], 1.0).then_inc(zero.sem, 1)
        e.wait_ge(zero.sem, zero.at(2))
        nc.gpsimd.memset(k.half[:], -0.5).then_inc(zero.sem, 1)
        e.wait_ge(zero.sem, zero.at(3))
        nc.gpsimd.memset(k.eps[:], EPS).then_inc(zero.sem, 1)
        e.wait_ge(zero.sem, zero.at(4))
        nc.gpsimd.memset(k.ctxT[DC:P, :], 0.0).then_inc(zero.sem, 1)
        e.wait_ge(zero.sem, zero.at(5))
        nc.gpsimd.memset(k.ctxT[DC:DC + 1, :], 1.0).then_inc(zero.sem, 1)
        e.wait_ge(zero.sem, zero.at(6))
        nc.gpsimd.affine_select(out=k.ident[:], in_=k.ident[:], compare_op=ALU.not_equal, fill=1.0, base=0,
                                pattern=[[-1, P]], channel_multiplier=1).then_inc(made.sem, 1)

    def pe(e):
        e.wait_ge(made.sem, made.at(1))
        e.wait_ge(c_in.sem, c_in.at(16))
        for n in range(TILES // 4):
            e.wait_ge(laid.sem, laid.at(n - 7))
            for j in range(4):
                last = nc.tensor.transpose(k.ps[0:DC, n % 8, j * P:(j + 1) * P], ctx_tok[:, 4 * n + j, :], k.ident[:])
            last.then_inc(turned.sem, 1)

    def dve(e):
        for n in range(TILES // 4):
            e.wait_ge(turned.sem, turned.at(n + 1))
            nc.vector.tensor_copy(k.ctxT[0:DC, n * BANK:(n + 1) * BANK], k.ps[0:DC, n % 8, :]).then_inc(laid.sem, 1)

    def act(e):
        e.wait_ge(g_in.sem, g_in.at(32))
        nc.scalar.activation(k.gates[:], graw[:], ACT.Tanh).then_inc(tanh.sem, 1)
        e.wait_ge(x_in.sem, x_in.at(16))
        e.wait_ge(laid.sem, laid.at(TILES // 4))
        e.wait_ge(made.sem, made.at(1))
        e.wait_ge(tanh.sem, tanh.at(1))
        e.sem_inc(ready.sem, 1)

    k.x_ready = ready
    return dict(sp=sp, pool=pool, pe=pe, dve=dve, act=act)


def attention(k, io, name, heads, wq, wk, wv, wo, bo, gate, rounds=None):
    nc = k.nc
    DH = 64
    SCALE = DH ** -0.5
    C = heads // 2
    INNER = heads * DH
    NG = heads // 4
    SB = heads * CTX // BANK
    sem = lambda n, total=TILES: k.sem(f"{name}_{n}", total)
    w_in, w_turned, w_laid = sem("w_loaded", None), sem("w_turned", 3 * C // 4), sem("w_laid", 3 * C // 4)
    w_made, w_copied, bias_made = sem("w_folded", 2 * (heads // 4) + 1), sem("w_fold_copied", heads // 4), sem("bias_made", 1)
    st_done, mv_done, ve_done, rs_done, xn_done = (sem("ln_" + n) for n in ("stats", "mv", "veps", "rstd", "xn"))
    xt_full, xt_laid = sem("xnT_full"), sem("xnT_laid")
    g_full, g_laid = sem("g_full", NG * TILES), sem("g_laid", NG * TILES)
    s_full, s_max, s_sub, s_exp = sem("scores"), sem("max"), sem("shifted"), sem("exp")
    s_sum, s_rec, s_prob = sem("sum"), sem("recip"), sem("probs")
    p_full, p_laid = sem("probsT_full"), sem("probsT_laid")
    v_full, v0_laid, v1_laid = sem("v_full", 2 * TILES), sem("v0_laid"), sem("v1_laid")
    y_full, x_done = sem("y_full"), sem("x_done")
    c_laid = sem("ctx_tile")

    cv = Carve(k)
    w_qk = cv.f32(2, INNER)
    w_v = cv.f32(INNER)
    w_o = cv.f32(C, D)
    bo_row = cv.f32(D)
    w_T = cv.f32(3, C, P)
    mT = cv.f32(heads, D)
    mT_pair = mT.rearrange("p (c m) d -> p c m d", m=2)
    wvo = cv.f32(2, C, D)
    G = cv.f32(2, heads, P)
    VW = cv.f32(2, 2, C, D)
    PR = cv.f32(2, heads, CTX)
    PT = cv.f32(2, C, P)
    cg = cv.f32(2, P)
    mx = cv.f32(2, heads)
    sm = cv.f32(2, heads)
    rc = cv.f32(2, heads)
    ps = k.ps
    before = k.x_ready
    k.x_ready = x_done
    pairs = 3 * C

    def sp(e):
        e.wait_ge(before.sem, before.end)
        e.dma_start(w_qk[:, 0, :], io[wq]).then_inc(w_in.sem, 16)
        e.dma_start(w_qk[0:DC, 1, :], io[wk]).then_inc(w_in.sem, 16)
        e.dma_start(w_v[0:DC, :], io[wv]).then_inc(w_in.sem, 16)
        e.dma_start(w_o[:], io[wo].rearrange("(c p) d -> p c d", p=P)).then_inc(w_in.sem, 16)
        e.dma_start(bo_row[DC:DC + 1, :], io[bo].rearrange("(a d) -> a d", a=1)).then_inc(w_in.sem, 16)

    def fold_pe(e):
        e.wait_ge(w_in.sem, w_in.at(80))
        for n in range(pairs):
            which, c = divmod(n, C)
            if n % 4 == 0:
                e.wait_ge(w_laid.sem, w_laid.at(n // 4 - 3))
            if which == 0:
                last = nc.tensor.transpose(ps[:, n // 4 % 4, (n % 4) * P:(n % 4 + 1) * P], w_qk[:, 0, c * P:(c + 1) * P], k.ident[:])
            else:
                src = w_qk[0:DC, 1, c * P:(c + 1) * P] if which == 1 else w_v[0:DC, c * P:(c + 1) * P]
                last = nc.tensor.transpose(ps[:, n // 4 % 4, (n % 4) * P:(n % 4) * P + DC], src, k.ident[0:DC, 0:DC])
            if n % 4 == 3:
                last.then_inc(w_turned.sem, 1)
        e.wait_ge(w_laid.sem, w_laid.at(pairs // 4))
        for q in range(heads // 4):
            fold_v, q0 = divmod(q, C // 4)
            e.wait_ge(w_made.sem, w_made.at(2 * q - 2))
            for j in range(4):
                for m in range(2):
                    c, rows = 4 * q0 + j, slice(64 * m, 64 * m + 64)
                    last = nc.tensor.matmul(ps[0:DC, 4 + (2 * q + m) % 4, j * P:(j + 1) * P],
                                            w_T[rows, 2 if fold_v else 1, c, 0:DC],
                                            w_o[rows, c, :] if fold_v else w_T[rows, 0, c, :], start=True, stop=True)
            last.then_inc(w_copied.sem, 1)

    def fold_dve(e):
        e.wait_ge(before.sem, before.end)
        nc.vector.memset(mT[DC:P, :, :], 0.0)
        nc.vector.memset(wvo[DC:P, :, :, :], 0.0).then_inc(bias_made.sem, 1)
        for n in range(pairs // 4):
            e.wait_ge(w_turned.sem, w_turned.at(n + 1))
            c0 = 4 * n % C
            src = ps[:, n % 4, :].rearrange("p (c d) -> p c d", c=4)
            if 4 * n < C:
                nc.vector.tensor_copy(w_T[:, 0, c0:c0 + 4, :], src).then_inc(w_laid.sem, 1)
            else:
                nc.vector.tensor_copy(w_T[:, 4 * n // C, c0:c0 + 4, 0:DC], src[:, :, 0:DC]).then_inc(w_laid.sem, 1)
        for q in range(heads // 4):
            fold_v, q0 = divmod(q, C // 4)
            e.wait_ge(w_copied.sem, w_copied.at(q + 1))
            for m in range(2):
                src = ps[0:DC, 4 + (2 * q + m) % 4, :].rearrange("p (c d) -> p c d", c=4)
                if fold_v:
                    nc.vector.tensor_scalar(wvo[0:DC, m, 4 * q0:4 * q0 + 4, :], src, k.gates[0:DC, gate:gate + 1], None,
                                            ALU.mult).then_inc(w_made.sem, 1)
                else:
                    nc.vector.tensor_copy(mT_pair[0:DC, 4 * q0:4 * q0 + 4, m, :], src).then_inc(w_made.sem, 1)
        e.wait_ge(w_in.sem, w_in.at(80))
        e.wait_ge(bias_made.sem, bias_made.at(1))
        nc.vector.tensor_scalar(wvo[DC:DC + 1, 0, 0, :], bo_row[DC:DC + 1, :], k.gates[DC:DC + 1, gate:gate + 1], None,
                                ALU.mult).then_inc(w_made.sem, 1)

    FOLDED = 2 * (heads // 4) + 1

    def ln_stats(e, t, s):
        nc.vector.bn_stats(k.stat[:, s, 0, :], k.x[:, t, :]).then_inc(st_done.sem, 1)

    def ln_aggr(e, t, s):
        nc.vector.bn_aggr(k.mv[:, s, 0, :], k.stat[:, s, 0, :]).then_inc(mv_done.sem, 1)

    def ln_apply(e, t, s):
        e.wait_ge(rs_done.sem, rs_done.at(t + 1))
        nc.vector.tensor_scalar(k.xn[:, s, 0, :], k.x[:, t, :], k.mv[:, s, 0, 0:1], k.rstd[:, s, 0:1],
                                ALU.subtract, ALU.mult).then_inc(xn_done.sem, 1)

    def ln_pool(e, t, s):
        e.wait_ge(mv_done.sem, mv_done.at(t + 1))
        nc.gpsimd.tensor_tensor(k.veps[:, s, 0:1], k.mv[:, s, 0, 1:2], k.eps[:, 0:1], ALU.add).then_inc(ve_done.sem, 1)
        e.wait_ge(ve_done.sem, ve_done.at(t + 1))
        nc.gpsimd.tensor_tensor(k.rstd[:, s, 0:1], k.veps[:, s, 0:1], k.half[:, 0:1], ALU.pow).then_inc(rs_done.sem, 1)

    def more(t, ahead):
        return not isinstance(t, int) or t + ahead < TILES

    def g_product(e, t, s, n):
        if n == 0:
            e.wait_ge(c_laid.sem, c_laid.at(t + 1))
        e.wait_ge(g_laid.sem, g_laid.at(NG * t + n - 1))
        for j in range(4):
            last = nc.tensor.matmul(ps[:, n % 2, j * P:(j + 1) * P], mT[:, 4 * n + j, :], cg[:, s, :], start=True, stop=True)
        last.then_inc(g_full.sem, 1)

    def xn_turn(e, t, s):
        e.wait_ge(xn_done.sem, xn_done.at(t + 1))
        nc.tensor.transpose(ps[:, 3, 0:P], k.xn[:, s, 0, :], k.ident[:]).then_inc(xt_full.sem, 1)

    def v_product(e, t, s, b):
        if SB == 2:
            laid, count = (v1_laid, t) if b == 0 else (v0_laid, t + 1)
        else:
            laid, count = (v0_laid, t) if b == 0 else (v1_laid, t)
        e.wait_ge(laid.sem, laid.at(count))
        for n in range(C * D // BANK):
            for m in range(2):
                bank = 6 + n if SB == 2 else 6 + b
                last = nc.tensor.matmul(ps[64 * m:64 * m + 64, bank, :], cg[:, s, b * CTX:(b + 1) * CTX],
                                        wvo[:, m, 4 * n:4 * n + 4, :], start=True, stop=True)
        last.then_inc(v_full.sem, 1)

    def pe_y(e, t, s):
        e.wait_ge(p_laid.sem, p_laid.at(t + 1))
        e.wait_ge(v0_laid.sem, v0_laid.at(t + 1))
        e.wait_ge(v1_laid.sem, v1_laid.at(t + 1))
        if rounds and more(t, 1):
            rounds.pe_total(e, t)
        for c in range(C):
            for b in range(2):
                last = nc.tensor.matmul(ps[64 * b:64 * b + 64, 2, 0:D], PT[:, s, c, 64 * b:64 * b + 64], VW[:, s, b, c, :],
                                        start=(c == 0), stop=(c == C - 1))
        last.then_inc(y_full.sem, 1)

    def pe_step(e, t, s):
        o = 1 - s
        e.wait_ge(g_laid.sem, g_laid.at(NG * (t + 1)))
        e.wait_ge(xt_laid.sem, xt_laid.at(t + 1))
        e.wait_ge(s_sub.sem, s_sub.at(t))
        for n in range(SB):
            for b in range(2):
                last = nc.tensor.matmul(ps[64 * b:64 * b + 64, 4 + n, :], k.xnT[:, s, 64 * b:64 * b + 64],
                                        G[:, s, 8 * n:8 * n + 8, b * CTX:(b + 1) * CTX], start=True, stop=True)
        last.then_inc(s_full.sem, 1)
        v_product(e, t, s, 0)
        if more(t, 1):
            for n in range(NG // 2):
                g_product(e, t + 1, o, n)
        v_product(e, t, s, 1)
        if not (isinstance(t, int) and t == 0):
            pe_y(e, t - 1, o)
        if more(t, 1):
            xn_turn(e, t + 1, o)
        if more(t, 1):
            for n in range(NG // 2, NG):
                g_product(e, t + 1, o, n)
        e.wait_ge(s_prob.sem, s_prob.at(t + 1))
        e.wait_ge(x_done.sem, x_done.at(t))
        if rounds:
            e.wait_ge(rounds.read.sem, rounds.read.at(t))
        if more(t, 1):
            e.wait_ge(xt_laid.sem, xt_laid.at(t + 2))
        for c in range(C):
            last = nc.tensor.transpose(ps[:, 2 + c // 4, c % 4 * P:(c % 4 + 1) * P], PR[:, s, 2 * c:2 * c + 2, :], k.ident[:])
        last.then_inc(p_full.sem, 1)

    def pe(e):
        fold_pe(e)
        e.wait_ge(w_made.sem, w_made.at(FOLDED))
        for n in range(NG):
            g_product(e, 0, 0, n)
        xn_turn(e, 0, 0)
        pipelined_tiles(e, lambda t, s: pe_step(e, t, s))
        pe_y(e, TILES - 1, 1)

    def g_copy(e, t, s, n):
        e.wait_ge(g_full.sem, g_full.at(NG * t + n + 1))
        nc.scalar.copy(G[:, s, 4 * n:4 * n + 4, :], ps[:, n % 2, :].rearrange("p (h j) -> p h j", h=4)).then_inc(g_laid.sem, 1)

    def xn_copy(e, t, s):
        e.wait_ge(xt_full.sem, xt_full.at(t + 1))
        nc.scalar.copy(k.xnT[:, s, 0:P], ps[:, 3, 0:P]).then_inc(xt_laid.sem, 1)

    def act_step(e, t, s):
        o = 1 - s
        e.wait_ge(s_sub.sem, s_sub.at(t + 1))
        nc.scalar.activation(PR[:, s, :, :], PR[:, s, :, :], ACT.Exp, scale=SCALE).then_inc(s_exp.sem, 1)
        if more(t, 1):
            for n in range(NG // 2):
                g_copy(e, t + 1, o, n)
        e.wait_ge(v_full.sem, v_full.at(2 * t + 2))
        src = ps[:, 6:8, :] if SB == 2 else ps[:, 7, :]
        dst = VW[:, s, 1, :, :].rearrange("p c d -> p (c d)")
        if SB == 2:
            dst = dst.rearrange("p (n w) -> p n w", n=2)
        nc.scalar.copy(dst, src).then_inc(v1_laid.sem, 1)
        if more(t, 1):
            xn_copy(e, t + 1, o)
            for n in range(NG // 2, NG):
                g_copy(e, t + 1, o, n)
        e.wait_ge(p_full.sem, p_full.at(t + 1))
        dst = PT[:, s, :, :].rearrange("p c q -> p (c q)")
        if SB == 2:
            nc.scalar.copy(dst.rearrange("p (n w) -> p n w", n=2), ps[:, 2:4, :]).then_inc(p_laid.sem, 1)
        else:
            nc.scalar.copy(dst, ps[:, 2, :]).then_inc(p_laid.sem, 1)

    def act(e):
        for n in range(NG):
            g_copy(e, 0, 0, n)
        xn_copy(e, 0, 0)
        pipelined_tiles(e, lambda t, s: act_step(e, t, s))

    def dve_add(e, t):
        e.wait_ge(y_full.sem, y_full.at(t + 1))
        nc.vector.tensor_tensor(k.x[:, t, :], ps[:, 2, 0:D], k.x[:, t, :], ALU.add).then_inc(x_done.sem, 1)

    def dve_step(e, t, s):
        S = ps[:, 4:4 + SB, :].rearrange("p n (h j) -> p (n h) j", j=CTX)
        if more(t, 2):
            ln_stats(e, t + 2, s)
        e.wait_ge(s_full.sem, s_full.at(t + 1))
        nc.vector.tensor_reduce(mx[:, s, :], S, AX.X, ALU.max).then_inc(s_max.sem, 1)
        e.wait_ge(s_max.sem, s_max.at(t + 1))
        nc.vector.tensor_tensor(PR[:, s, :, :], S, mx[:, s, :].unsqueeze(2).to_broadcast([P, heads, CTX]), ALU.subtract).then_inc(s_sub.sem, 1)
        if more(t, 2):
            ln_aggr(e, t + 2, s)
        e.wait_ge(v_full.sem, v_full.at(2 * t + 1))
        src = ps[:, 6:8, :] if SB == 2 else ps[:, 6, :]
        dst = VW[:, s, 0, :, :].rearrange("p c d -> p (c d)")
        if SB == 2:
            dst = dst.rearrange("p (n w) -> p n w", n=2)
        nc.vector.tensor_copy(dst, src).then_inc(v0_laid.sem, 1)
        e.wait_ge(s_exp.sem, s_exp.at(t + 1))
        nc.vector.tensor_reduce(sm[:, s, :], PR[:, s, :, :], AX.X, ALU.add).then_inc(s_sum.sem, 1)
        if more(t, 2):
            ln_apply(e, t + 2, s)
        e.wait_ge(s_sum.sem, s_sum.at(t + 1))
        nc.vector.reciprocal(rc[:, s, :], sm[:, s, :]).then_inc(s_rec.sem, 1)
        if not (isinstance(t, int) and t == 0):
            dve_add(e, t - 1)
        if rounds:
            rounds.dve_round(e, t)

    def dve(e):
        fold_dve(e)
        if rounds:
            rounds.dve_start(e)
        for t in range(2):
            ln_stats(e, t, t)
        e.wait_ge(st_done.sem, st_done.at(2))
        for t in range(2):
            ln_aggr(e, t, t)
        for t in range(2):
            ln_apply(e, t, t)
        pipelined_tiles(e, lambda t, s: dve_step(e, t, s))
        dve_add(e, TILES - 1)

    def ctx_copy(e, t, s):
        nc.gpsimd.tensor_copy(cg[:, s, :], k.ctxT[:, bass.ts(t, P)]).then_inc(c_laid.sem, 1)

    def pool_step(e, t, s):
        if more(t, 2):
            ln_pool(e, t + 2, s)
        e.wait_ge(s_rec.sem, s_rec.at(t + 1))
        nc.gpsimd.tensor_tensor(PR[:, s, :, :], PR[:, s, :, :], rc[:, s, :].unsqueeze(2).to_broadcast([P, heads, CTX]),
                                ALU.mult).then_inc(s_prob.sem, 1)
        if more(t, 2):
            e.wait_ge(v_full.sem, v_full.at(2 * t + 2))
            ctx_copy(e, t + 2, s)

    def pool(e):
        e.wait_ge(before.sem, before.end)
        for t in range(2):
            ctx_copy(e, t, t)
        for t in range(2):
            ln_pool(e, t, t)
        pipelined_tiles(e, lambda t, s: pool_step(e, t, s))

    return dict(sp=sp, pe=pe, act=act, dve=dve, pool=pool)


class GroupNorm:

    def __init__(self, k, name, slot, src, dst):
        self.k, self.s, self.src, self.dst = k, slot, src, dst
        self.stats, self.mv, self.ve, self.rs, self.out = (k.sem(f"{name}_{n}", GROUPS) for n in ("stats", "mv", "veps", "rstd", "normed"))

    def dve_stats(self, g):
        k = self.k
        for j in range(GT):
            last = k.nc.vector.bn_stats(k.stat[:, self.s, j, :], self.src(g, j))
        last.then_inc(self.stats.sem, 1)

    def dve_aggregate(self, e, n, covered):
        k = self.k
        if not covered:
            e.wait_ge(self.stats.sem, self.stats.at(n + 1))
        for j in range(GT):
            last = k.nc.vector.bn_aggr(k.mv[:, self.s, j, :], k.stat[:, self.s, j, :])
        last.then_inc(self.mv.sem, 1)

    def pool_rstd(self, e, n):
        k = self.k
        e.wait_ge(self.mv.sem, self.mv.at(n + 1))
        k.nc.gpsimd.tensor_tensor(k.veps[:, self.s, :], k.mv[:, self.s, :, 1], k.eps[:], ALU.add).then_inc(self.ve.sem, 1)
        e.wait_ge(self.ve.sem, self.ve.at(n + 1))
        k.nc.gpsimd.tensor_tensor(k.rstd[:, self.s, :], k.veps[:, self.s, :], k.half[:], ALU.pow).then_inc(self.rs.sem, 1)

    def dve_apply(self, e, g, n):
        k = self.k
        e.wait_ge(self.rs.sem, self.rs.at(n + 1))
        for j in range(GT):
            last = k.nc.vector.tensor_scalar(self.dst(g, j), self.src(g, j), k.mv[:, self.s, j, 0:1], k.rstd[:, self.s, j:j + 1],
                                             ALU.subtract, ALU.mult)
        last.then_inc(self.out.sem, 1)


def experts(k, io, name, top1, gate, loads, prepare=None):
    nc = k.nc
    E, C = (8, 1) if top1 else (2, 4)
    U = E * C
    NR = 8
    GELU = ACT.Gelu if top1 else ACT.Gelu_apprx_tanh
    sem = lambda n, total=GROUPS: k.sem(f"{name}_{n}", total)
    w_in, made, xt_full, xt_laid = sem("w_loaded", None), sem("constants", 1), sem("xT_full"), sem("xT_laid")
    h_full, h_laid = sem("h_full", U * GROUPS), sem("h_laid", U * GROUPS)
    o_full, o_used = sem("o_full", E * GROUPS), sem("o_used", E * GROUPS)
    l_full, l_laid, lt_full = sem("logits"), sem("logits_laid"), sem("logitsT")
    r_max, r_shift, r_exp, r_sum, r_w = (sem(n) for n in ("r_max", "r_shift", "r_exp", "r_sum", "r_weights"))
    r_step = sem("r_step", (5 if top1 else 3) * GROUPS)
    wt_full, wt_laid, b_full, x_done = sem("weightsT"), sem("weightsT_laid"), sem("bias_full"), sem("x_done")
    if not top1:
        r2_full, r2_laid = sem("router_in_full"), sem("router_in_laid")

    cv = Carve(k)
    w1 = cv.f32(E, C * P)
    w2 = cv.f32(E, C, D)
    b1 = cv.f32(E, C)
    b2 = cv.f32(D)
    wr = cv.f32(NR)
    br = cv.f32(1)
    hT = cv.f32(2, GT * P)
    lT = cv.f32(GT * P)
    wT = cv.f32(GT * P)
    rank = cv.f32(NR)
    m4, s4, r4 = cv.f32(GT), cv.f32(GT), cv.f32(GT)
    ex, eq, rk, oh = (cv.f32(GT, NR) for _ in range(4))
    rm = cv.f32(GT)
    wgt = cv.f32(GT, E)
    gam, bet = cv.f32(1), cv.f32(1)
    ln2T = cv.f32(GT * P)
    xnT = k.xnT[:, 0, :]
    ps = k.ps
    before = k.x_ready
    k.x_ready = x_done
    ln = GroupNorm(k, name + "_ln", 0, lambda g, j: k.x[:, 4 * g + j, :], lambda g, j: k.xn[:, 0, j, :])
    ln2 = None if top1 else GroupNorm(k, name + "_ln2", 1, lambda g, j: k.xn[:, 0, j, :], lambda g, j: k.xn[:, 1, j, :])
    v = Parts()
    v.w1, v.w2, v.b1, v.b2, v.wr, v.br, v.gam, v.bet, v.cv, v.w_in, v.before = w1, w2, b1, b2, wr, br, gam, bet, cv, w_in, before
    n_loads = v.loads = loads(k, io, v)
    prep = prepare(k, io, v) if prepare else {}

    def sp(e):
        e.wait_ge(before.sem, before.end)
        for dst, src in n_loads:
            with nc.allow_non_contiguous_dma(reason="biases are small"):
                e.dma_start(dst, src).then_inc(w_in.sem, 16)

    READY = 16 * len(n_loads)

    def turn_x(e, n):
        e.wait_ge(ln.out.sem, ln.out.at(n + 1))
        e.wait_ge(xt_laid.sem, xt_laid.at(n))
        for j in range(GT):
            last = nc.tensor.transpose(ps[:, 5, j * P:(j + 1) * P], k.xn[:, 0, j, :], k.ident[:])
        last.then_inc(xt_full.sem, 1)

    def turn_router_in(e, n):
        e.wait_ge(ln2.out.sem, ln2.out.at(n + 1))
        e.wait_ge(r2_laid.sem, r2_laid.at(n))
        for j in range(GT):
            last = nc.tensor.transpose(ps[:, 2, j * P:(j + 1) * P], k.xn[:, 1, j, :], k.ident[:])
        last.then_inc(r2_full.sem, 1)

    def logits(e, n):
        if top1:
            e.wait_ge(xt_laid.sem, xt_laid.at(n + 1))
        else:
            e.wait_ge(r2_laid.sem, r2_laid.at(n + 1))
        e.wait_ge(r_sum.sem, r_sum.at(n))
        nc.tensor.matmul(ps[0:NR, 6, :], wr[:], xnT if top1 else ln2T[:], start=True, stop=True).then_inc(l_full.sem, 1)

    def turn_logits(e, n):
        for j in range(GT):
            last = nc.tensor.transpose(ps[:, 6, j * NR:(j + 1) * NR], lT[0:NR, j * P:(j + 1) * P], k.ident[0:NR, 0:NR])
        last.then_inc(lt_full.sem, 1)

    def hidden(e, g, u):
        if u == 0:
            e.wait_ge(xt_laid.sem, xt_laid.at(g + 1))
        x, c = divmod(u, C)
        nc.tensor.matmul(ps[:, u % 2, :], w1[:, x, c * P:(c + 1) * P], xnT, start=True, stop=True).then_inc(h_full.sem, 1)

    def outputs(e, g, u):
        x, c = divmod(u, C)
        e.wait_ge(h_laid.sem, h_laid.at(U * g + u + 1))
        if c == 0:
            e.wait_ge(o_used.sem, o_used.at(E * g + max(x - 1, 0)))
        for j in range(GT):
            last = nc.tensor.matmul(ps[:, 3 + x % 2, j * P:(j + 1) * P], hT[:, u % 2, j * P:(j + 1) * P], w2[:, x, c, :],
                                    start=(c == 0 and j == 0), stop=(c == C - 1 and j == GT - 1), skip_group_check=True)
        if c == C - 1:
            last.then_inc(o_full.sem, 1)

    def bias_term(e, g):
        e.wait_ge(r_w.sem, r_w.at(g + 1))
        e.wait_ge(x_done.sem, x_done.at(g))
        for j in range(GT):
            last = nc.tensor.transpose(ps[0:E, 7, j * P:(j + 1) * P], wgt[:, j, :], k.ident[:])
        last.then_inc(wt_full.sem, 1)

    def bias_term2(e, g):
        e.wait_ge(wt_laid.sem, wt_laid.at(g + 1))
        for j in range(GT):
            last = nc.tensor.matmul(ps[:, 7, j * P:(j + 1) * P], wT[0:E, j * P:(j + 1) * P], b2[0:E, :], start=True, stop=True)
        last.then_inc(b_full.sem, 1)

    def pe(e):
        if "pe" in prep:
            prep["pe"](e)
        e.wait_ge(w_in.sem, w_in.at(READY))
        turn_x(e, 0)
        if not top1:
            turn_router_in(e, 0)
        logits(e, 0)

        def body(g, more):
            hidden(e, g, 0)
            e.wait_ge(l_laid.sem, l_laid.at(g + 1))
            hidden(e, g, 1)
            turn_logits(e, g)
            for u in range(1, U):
                if u > 1:
                    hidden(e, g, u)
                if u == U - 1 and more:
                    turn_x(e, g + 1)
                if u == 4:
                    bias_term(e, g)
                outputs(e, g, u - 1)
                if u == 5:
                    bias_term2(e, g)
            if more and top1:
                logits(e, g + 1)
            outputs(e, g, U - 1)
            if more and not top1:
                turn_router_in(e, g + 1)
                logits(e, g + 1)

        pipelined_groups(e, body)

    def act(e):
        if "act" in prep:
            prep["act"](e)
        e.wait_ge(w_in.sem, w_in.at(READY))

        def copy_x(n):
            e.wait_ge(xt_full.sem, xt_full.at(n + 1))
            nc.scalar.copy(xnT, ps[:, 5, :]).then_inc(xt_laid.sem, 1)

        def copy_router_in(n):
            e.wait_ge(r2_full.sem, r2_full.at(n + 1))
            nc.scalar.activation(ln2T[:], ps[:, 2, :], ACT.Identity, bias=bet[:], scale=gam[:]).then_inc(r2_laid.sem, 1)

        def copy_logits(n):
            e.wait_ge(l_full.sem, l_full.at(n + 1))
            nc.scalar.activation(lT[0:NR, :], ps[0:NR, 6, :], ACT.Identity, bias=br[0:NR, :]).then_inc(l_laid.sem, 1)

        copy_x(0)
        if not top1:
            copy_router_in(0)
        copy_logits(0)

        def body(g, more):
            for u in range(U):
                if u == 2:
                    e.wait_ge(r_shift.sem, r_shift.at(g + 1))
                    nc.scalar.activation(ex[:], ex[:], ACT.Exp).then_inc(r_exp.sem, 1)
                if u == 5:
                    e.wait_ge(wt_full.sem, wt_full.at(g + 1))
                    nc.scalar.copy(wT[0:E, :], ps[0:E, 7, :]).then_inc(wt_laid.sem, 1)
                x, c = divmod(u, C)
                e.wait_ge(h_full.sem, h_full.at(U * g + u + 1))
                nc.scalar.activation(hT[:, u % 2, :], ps[:, u % 2, :], GELU, bias=b1[:, x, c:c + 1]).then_inc(h_laid.sem, 1)
            if more:
                copy_x(g + 1)
                if not top1:
                    copy_router_in(g + 1)
                copy_logits(g + 1)

        pipelined_groups(e, body)

    def dve(e):
        if "dve" in prep:
            prep["dve"](e)
        e.wait_ge(before.sem, before.end)
        e.wait_ge(w_in.sem, w_in.at(READY))
        e.wait_ge(made.sem, made.at(1))
        steps = 5 if top1 else 3

        def spread(v):
            return v.unsqueeze(2).to_broadcast([P, GT, NR])

        def router(g):
            L = ps[:, 6, 0:GT * NR].rearrange("p (j r) -> p j r", r=NR)
            e.wait_ge(lt_full.sem, lt_full.at(g + 1))
            nc.vector.tensor_reduce(m4[:], L, AX.X, ALU.max).then_inc(r_max.sem, 1)
            e.wait_ge(r_max.sem, r_max.at(g + 1))
            nc.vector.tensor_tensor(ex[:], L, spread(m4), ALU.subtract).then_inc(r_shift.sem, 1)
            if top1:
                nc.vector.tensor_tensor(eq[:], L, spread(m4), ALU.is_equal).then_inc(r_step.sem, 1)
                e.wait_ge(r_step.sem, r_step.at(steps * g + 1))
                nc.vector.tensor_tensor(rk[:], eq[:], rank.unsqueeze(1).to_broadcast([P, GT, NR]), ALU.mult).then_inc(r_step.sem, 1)
                e.wait_ge(r_step.sem, r_step.at(steps * g + 2))
                nc.vector.tensor_reduce(rm[:], rk[:], AX.X, ALU.max).then_inc(r_step.sem, 1)
                e.wait_ge(r_step.sem, r_step.at(steps * g + 3))
                nc.vector.tensor_tensor(oh[:], rk[:], spread(rm), ALU.is_equal)
            e.wait_ge(r_exp.sem, r_exp.at(g + 1))
            nc.vector.tensor_reduce(s4[:], ex[:], AX.X, ALU.add).then_inc(r_sum.sem, 1)
            if not top1:
                nc.vector.tensor_reduce(m4[:], ex[:, :, 1:NR], AX.X, ALU.add)
            e.wait_ge(r_sum.sem, r_sum.at(g + 1))
            nc.vector.reciprocal(r4[:], s4[:]).then_inc(r_step.sem, 1)
            e.wait_ge(r_step.sem, r_step.at(steps * g + steps - 1 if top1 else steps * g + 1))
            nc.vector.tensor_scalar(s4[:], r4[:], k.gates[:, gate:gate + 1], None, ALU.mult).then_inc(r_step.sem, 1)
            e.wait_ge(r_step.sem, r_step.at(steps * g + steps if top1 else steps * g + 2))
            if top1:
                nc.vector.tensor_tensor(wgt[:], oh[:], spread(s4), ALU.mult).then_inc(r_w.sem, 1)
            else:
                nc.vector.tensor_tensor(wgt[:, :, 0], ex[:, :, 0], s4[:], ALU.mult).then_inc(r_step.sem, 1)
                nc.vector.tensor_tensor(wgt[:, :, 1], m4[:], s4[:], ALU.mult).then_inc(r_w.sem, 1)

        def add_expert(g, x):
            e.wait_ge(o_full.sem, o_full.at(E * g + x + 1))
            if x:
                e.wait_ge(o_used.sem, o_used.at(E * g + x))
            else:
                e.wait_ge(r_w.sem, r_w.at(g + 1))
            for j in range(GT):
                last = nc.vector.scalar_tensor_tensor(k.x[:, 4 * g + j, :], ps[:, 3 + x % 2, j * P:(j + 1) * P], wgt[:, j, x:x + 1],
                                                      k.x[:, 4 * g + j, :], ALU.mult, ALU.add)
            last.then_inc(o_used.sem, 1)

        ln.dve_stats(0)
        ln.dve_aggregate(e, 0, False)
        ln.dve_apply(e, 0, 0)
        if not top1:
            e.wait_ge(ln.out.sem, ln.out.at(1))
            ln2.dve_stats(0)
            ln2.dve_aggregate(e, 0, False)
            ln2.dve_apply(e, 0, 0)

        def body(g, more):
            if more:
                ln.dve_stats(g + 1)
            router(g)
            if more:
                ln.dve_aggregate(e, g + 1, True)
                if not top1:
                    ln.dve_apply(e, g + 1, g + 1)
                    e.wait_ge(ln.out.sem, ln.out.at(g + 2))
                    ln2.dve_stats(g + 1)
                    e.wait_ge(ln2.stats.sem, ln2.stats.at(g + 2))
            for x in range(E):
                add_expert(g, x)
                if more and x == 0:
                    if top1:
                        ln.dve_apply(e, g + 1, g + 1)
                    else:
                        ln2.dve_aggregate(e, g + 1, True)
                        ln2.dve_apply(e, g + 1, g + 1)
            e.wait_ge(b_full.sem, b_full.at(g + 1))
            e.wait_ge(o_used.sem, o_used.at(E * (g + 1)))
            nc.vector.tensor_tensor(k.x[:, bass.ts(g, GT), :], ps[:, 7, :].rearrange("p (j d) -> p j d", j=GT),
                                    k.x[:, bass.ts(g, GT), :], ALU.add).then_inc(x_done.sem, 1)

        pipelined_groups(e, body)

    def pool(e):
        if "pool" in prep:
            prep["pool"](e)
        e.wait_ge(before.sem, before.end)
        for r in range(NR):
            ins = nc.gpsimd.memset(rank[:, r:r + 1], float(NR - r))
        ins.then_inc(made.sem, 1)
        e.wait_ge(made.sem, made.at(1))
        ln.pool_rstd(e, 0)
        if not top1:
            ln2.pool_rstd(e, 0)

        def body(g, more):
            if more:
                ln.pool_rstd(e, g + 1)
                if not top1:
                    ln2.pool_rstd(e, g + 1)

        pipelined_groups(e, body)

    return dict(sp=sp, pe=pe, act=act, dve=dve, pool=pool)


def ffn0(k, io):
    def loads(k, io, v):
        return [
            (v.w1, io["L0_ffn_W1"].rearrange("e d f -> d e f")),
            (v.w2[:, :, 0, :], io["L0_ffn_W2"].rearrange("e f d -> f e d")),
            (v.b1[:, :, 0], io["L0_ffn_b1"].rearrange("e f -> f e")),
            (v.b2[0:8, :], io["L0_ffn_b2"]),
            (v.wr, io["L0_ffn_Wg"]),
            (v.br[0:8, :], io["L0_ffn_bg"].rearrange("(n a) -> n a", a=1)),
        ]
    return experts(k, io, "f0", True, 4, loads)


def state_space_kernel(k, io, cv, carve_done):
    nc = k.nc
    N, L = 64, SEQ
    sem = lambda n: k.sem("ssm_" + n)
    w_in, step_v, step_a, stored, t_in = (sem(n) for n in ("loaded", "vector_step", "scalar_step", "stored", "toeplitz_in"))
    a_re, a_im, c_re, c_im = (cv.f32(N) for _ in range(4))
    ldt, dt, dsk = cv.f32(1), cv.f32(1), cv.f32(1)
    zr, ang, turns, red, half = (cv.f32(N) for _ in range(5))
    er, sn, sh, u, v, p, q, den = (cv.f32(N) for _ in range(8))
    pr = cv.f32(2, N)
    pi = cv.f32(2, N)
    zre, zim = cv.f32(N, L), cv.f32(N, L)
    t1, t2 = cv.f32(N, L // 2), cv.f32(N, L // 2)
    kpad = cv.f32(2 * L)
    scratch = nc.dram_tensor("ssm_toeplitz_scratch", (SEQ, D, SEQ), F32).ap()
    TWO_PI = 6.283185307179586
    C1 = 6.28125
    C2 = 0.0019350051879882812
    C3 = TWO_PI - C1 - C2
    PI_IN = 3.1415925

    def sp(e):
        for dst, name in ((a_re, "A_re"), (a_im, "A_im"), (c_re, "C_re"), (c_im, "C_im")):
            e.dma_start(dst, io["L1_xattn_" + name]).then_inc(w_in.sem, 16)
        for dst, name in ((ldt, "log_dt"), (dsk, "D_skip")):
            e.dma_start(dst, io["L1_xattn_" + name].rearrange("(p a) -> p a", a=1)).then_inc(w_in.sem, 16)

    def act(e):
        e.wait_ge(w_in.sem, w_in.at(96))
        nc.scalar.activation(dt, ldt, ACT.Exp).then_inc(step_a.sem, 1)
        e.wait_ge(step_a.sem, step_a.at(1))
        nc.scalar.activation(er, a_re, ACT.Exp, scale=dt).then_inc(step_a.sem, 1)
        e.wait_ge(step_v.sem, step_v.at(5))
        nc.scalar.activation(sn, red, ACT.Sin)
        nc.scalar.activation(sh, red, ACT.Sin, scale=0.5).then_inc(step_a.sem, 1)

    def dve(e):
        n = [0]

        def go(ins):
            n[0] += 1
            ins.then_inc(step_v.sem, 1)
            e.wait_ge(step_v.sem, step_v.at(n[0]))

        V = nc.vector
        e.wait_ge(step_a.sem, step_a.at(2))
        go(V.tensor_scalar(ang, a_im, dt, None, ALU.mult))
        go(V.tensor_scalar(turns, ang, 1.0 / TWO_PI, ROUND, ALU.mult, ALU.add))
        go(V.tensor_scalar(turns, turns, -ROUND, None, ALU.add))
        go(V.scalar_tensor_tensor(red, turns, -C1, ang, ALU.mult, ALU.add))
        V.scalar_tensor_tensor(ang, turns, -C2, red, ALU.mult, ALU.add).then_inc(k_fix.sem, 1)
        e.wait_ge(k_fix.sem, k_fix.at(1))
        V.scalar_tensor_tensor(half, turns, -C3, ang, ALU.mult, ALU.add).then_inc(k_fix.sem, 1)
        e.wait_ge(k_fix.sem, k_fix.at(2))
        go(V.tensor_scalar(red, half, PI_IN, -PI_IN, ALU.min, ALU.max))
        e.wait_ge(step_a.sem, step_a.at(3))
        go(V.tensor_tensor(pi[:, 0, :], er, sn, ALU.mult))
        go(V.tensor_tensor(u, sh, sh, ALU.mult))
        go(V.tensor_scalar(u, u, -2.0, 1.0, ALU.mult, ALU.add))
        go(V.tensor_tensor(pr[:, 0, :], er, u, ALU.mult))
        go(V.tensor_scalar(v, pr[:, 0, :], -1.0, None, ALU.add))
        go(V.tensor_tensor(p, c_re, v, ALU.mult))
        go(V.tensor_tensor(u, c_im, pi[:, 0, :], ALU.mult))
        go(V.tensor_tensor(p, p, u, ALU.subtract))
        go(V.tensor_tensor(q, c_re, pi[:, 0, :], ALU.mult))
        go(V.tensor_tensor(u, c_im, v, ALU.mult))
        go(V.tensor_tensor(q, q, u, ALU.add))
        go(V.tensor_tensor(den, a_re, a_re, ALU.mult))
        go(V.tensor_tensor(u, a_im, a_im, ALU.mult))
        go(V.tensor_tensor(den, den, u, ALU.add))
        go(V.reciprocal(u, den))
        go(V.tensor_scalar(den, u, 2.0, None, ALU.mult))
        go(V.tensor_tensor(u, p, a_re, ALU.mult))
        go(V.tensor_tensor(v, q, a_im, ALU.mult))
        go(V.tensor_tensor(u, u, v, ALU.add))
        go(V.tensor_tensor(zre[:, :, 0], u, den, ALU.mult))
        go(V.tensor_tensor(u, q, a_re, ALU.mult))
        go(V.tensor_tensor(v, p, a_im, ALU.mult))
        go(V.tensor_tensor(u, u, v, ALU.subtract))
        go(V.tensor_tensor(zim[:, :, 0], u, den, ALU.mult))
        w, s = 1, 0
        while w < L:
            cr = pr[:, s, :].unsqueeze(2).to_broadcast([P, N, w])
            ci = pi[:, s, :].unsqueeze(2).to_broadcast([P, N, w])
            a, b = t1[:, :, 0:w], t2[:, :, 0:w]
            go(V.tensor_tensor(a, zre[:, :, 0:w], cr, ALU.mult))
            go(V.tensor_tensor(b, zim[:, :, 0:w], ci, ALU.mult))
            go(V.tensor_tensor(zre[:, :, w:2 * w], a, b, ALU.subtract))
            if 2 * w < L:
                go(V.tensor_tensor(a, zre[:, :, 0:w], ci, ALU.mult))
                go(V.tensor_tensor(b, zim[:, :, 0:w], cr, ALU.mult))
                go(V.tensor_tensor(zim[:, :, w:2 * w], a, b, ALU.add))
                o = 1 - s
                go(V.tensor_tensor(u, pr[:, s, :], pr[:, s, :], ALU.mult))
                go(V.tensor_tensor(v, pi[:, s, :], pi[:, s, :], ALU.mult))
                go(V.tensor_tensor(pr[:, o, :], u, v, ALU.subtract))
                go(V.tensor_tensor(u, pr[:, s, :], pi[:, s, :], ALU.mult))
                go(V.tensor_scalar(pi[:, o, :], u, 2.0, None, ALU.mult))
                s = o
            w *= 2
        go(V.memset(kpad[:, 0:L], 0.0))
        go(V.tensor_reduce(kpad[:, L - 1:2 * L - 1], zre.rearrange("p n l -> p l n"), AX.X, ALU.add))
        go(V.memset(kpad[:, 2 * L - 1:2 * L], 0.0))
        V.tensor_tensor(kpad[:, L - 1:L], kpad[:, L - 1:L], dsk, ALU.add).then_inc(step_last.sem, 1)

    k_fix, step_last = sem("angle"), sem("kernel_made")

    def sp_store(e):
        e.wait_ge(step_last.sem, step_last.at(1))
        windows = kpad[:, L - 1:2 * L - 1]
        windows = bass.AP(windows.tensor, windows.offset, [windows.ap[0], [-1, SEQ], [1, SEQ]])
        e.dma_start(scratch.rearrange("r d t -> d r t"), windows).then_inc(stored.sem, 16)
        e.wait_ge(stored.sem, stored.at(16))
        for b in range(2):
            e.dma_start(k.toep[b * SEQ:(b + 1) * SEQ, :, :], scratch).then_inc(t_in.sem, 16)

    return sp, act, dve, sp_store, t_in


def attention_ssm(k, io):
    nc = k.nc
    H, DH, KTOP, GATE, HID = 4, 32, 32, 1, 4
    SCALE = float(DH) ** -0.5
    MASKED, TAKEN = -1e38, -3e38
    sem = lambda n, total=TILES: k.sem("a1_" + n, total)
    io1 = {n[len("L1_xattn_"):]: v for n, v in io.items() if n.startswith("L1_xattn_")}
    before = k.x_ready
    ps = k.ps

    cv = Carve(k)
    U = cv.f32(TILES, D)
    XS = cv.f32(TILES, D)
    FO = cv.f32(TILES, 2 * D)
    wq, wk, wv = cv.f32(P), cv.f32(P), cv.f32(P)
    wf = cv.f32(4 * D)
    wfraw = cv.f32(4 * D)
    bf = cv.f32(4 * D)
    w1 = cv.f32(HID * P)
    w2 = cv.f32(HID, D)
    rows = cv.f32(5, D)
    cols = cv.f32(2 + HID)
    mg = cv.f32(1)
    head_of = cv.f32(H)
    mb = cv.f32(TILES, CTX)
    tmask = cv.f32(TILES)
    start_rings = cv.at
    mask8 = cv.f32(TILES * CTX // 4).bitcast(U8)
    tm8 = cv.f32(P // 4).bitcast(U8)
    tmf = cv.f32(P)
    stage_end = cv.at
    cv.at = start_rings
    qT = cv.f32(2, P)
    kbd = cv.f32(2, 2, H, CTX)
    W = cv.f32(2, H, CTX)
    W2 = cv.f32(2, H, CTX)
    PEN = cv.f32(2, H, CTX)
    m8 = cv.f32(4, H, 8)
    nm, sums, rec = cv.f32(2, H), cv.f32(2, H), cv.f32(2, H)
    vs = cv.f32(2, 2, D)
    aT = cv.f32(2, P)
    cT = cv.f32(2, P)
    F = cv.f32(2, 4 * D)
    L2 = cv.f32(2, D)
    cg = cv.f32(2, P)
    cv2 = Carve(k, start_rings)
    hin = cv2.f32(GT * P)
    hT = cv2.f32(2, GT * P)
    gb = cv2.f32(1)
    cv3 = Carve(k)

    w_in, w2_in, prep = sem("w_loaded", None), sem("masks_loaded", None), sem("prepared", 6)
    prep_p, prep_t, prep_tt = sem("prepared_pool", 1), sem("text_mask_turned", 1), sem("text_mask_laid", 1)
    lnA = [sem("ln_" + n) for n in ("stats", "mv", "veps", "rstd", "out")]
    lnB = [sem("ln2_" + n) for n in ("stats", "mv", "veps", "rstd", "out")]
    u_kept, c_laid = sem("u_kept"), sem("ctx_tile")
    xt_full, xt_laid, q_full, q_laid, k_full, k_laid = (sem(n) for n in ("xT_full", "xT_laid", "q_full", "q_laid", "k_full", "k_laid"))
    s_full, s_laid, s_masked, v_full, v_laid = (sem(n) for n in ("scores", "scores_laid", "masked", "v_full", "v_laid"))
    tk = sem("top", 7 * TILES)
    tk_done, pen1, pen2, e_done, r_done, r_step, a_done = (sem(n) for n in ("top_done", "penalty", "selected", "exp", "recip", "recip_step", "attn"))
    a_full, a_laid, c_full, cT_laid, f_full, f_laid, fo_kept = (sem(n) for n in ("attnT_full", "attnT_laid", "cT_full", "cT_laid", "film_full", "film_laid", "film_kept"))
    xs_step, xs_done = sem("xs_step"), sem("xs_done")

    ssm_sp, ssm_act, ssm_dve, ssm_store, toep_in = state_space_kernel(k, io, cv3, None)
    b_full, b_laid = sem("conv_full", 8), sem("conv_laid", 8)
    y_step, y_done = sem("y_step", 2 * GROUPS), sem("y_done", GROUPS)
    hid_full, hid_laid = sem("hid_full", HID * GROUPS), sem("hid_laid", HID * GROUPS)
    ht_full, ht_laid, o_full, o_added = (sem(n, GROUPS) for n in ("hinT_full", "hinT_laid", "ffn_full", "ffn_added"))
    z_step, x_done = sem("z_step", 2 * GROUPS), sem("x_done", GROUPS)
    k.x_ready = x_done
    lnC = GroupNorm(k, "a1_lnC", 0, lambda g, j: XS[:, 4 * g + j, :], lambda g, j: k.xn[:, 0, j, :])
    lnD = GroupNorm(k, "a1_lnD", 1, lambda g, j: XS[:, 4 * g + j, :], lambda g, j: XS[:, 4 * g + j, :])

    def flat(v):
        return v.rearrange("p h j -> p (h j)")

    def more(t, ahead):
        return not isinstance(t, int) or t + ahead < TILES

    loads = [
        (wq, io1["Wq"]), (wk[0:DC, :], io1["Wk"]), (wv[0:DC, :], io1["Wv"]),
        (wfraw[:, 0:2 * D], io1["W_film_in"]), (wfraw[:, 2 * D:], io1["W_film_out"]),
        (bf[0:1, 0:2 * D], io1["b_film_in"].rearrange("(a n) -> a n", a=1)),
        (bf[0:1, 2 * D:], io1["b_film_out"].rearrange("(a n) -> a n", a=1)),
        (w1, io1["W1"]), (w2, io1["W2"].rearrange("(c p) d -> p c d", p=P)),
        (rows[:, 0, :], io1["g_norm_in"].rearrange("(a n) -> a n", a=1).partition_broadcast(P)),
        (rows[:, 1, :], io1["b_norm_in"].rearrange("(a n) -> a n", a=1).partition_broadcast(P)),
        (rows[:, 2, :], io1["g_norm_out"].rearrange("(a n) -> a n", a=1).partition_broadcast(P)),
        (rows[:, 3, :], io1["b_norm_out"].rearrange("(a n) -> a n", a=1).partition_broadcast(P)),
        (rows[0:1, 4, :], io1["b2"].rearrange("(a n) -> a n", a=1)),
        (cols[:, 0:1], io1["g_ffn"].rearrange("(p a) -> p a", a=1)),
        (cols[:, 1:2], io1["b_ffn"].rearrange("(p a) -> p a", a=1)),
        (cols[:, 2:2 + HID], io1["b1"].rearrange("(c p) -> p c", p=P)),
        (mg, io1["mod_gate"].rearrange("(a n) -> a n", a=1).partition_broadcast(P)),
    ]
    READY = 16 * len(loads)
    ctx_mask = io["mask_BxS2_bf1"].rearrange("(t b) j -> b t j", b=2)
    masks = [(mask8[b * SEQ:(b + 1) * SEQ, :].rearrange("p (t j) -> p t j", j=CTX), ctx_mask[b:b + 1].partition_broadcast(SEQ)) for b in range(2)]
    masks.append((tm8[0:TILES, :], io["mask_BxS_bf1"].rearrange("b s -> (b s)").rearrange("(t p) -> t p", p=P)))

    def sp(e):
        e.wait_ge(before.sem, before.end)
        ssm_sp(e)
        ssm_store(e)
        with nc.allow_non_contiguous_dma(reason="per-channel columns are small"):
            for dst, src in loads:
                e.dma_start(dst, src).then_inc(w_in.sem, 16)
            for dst, src in masks:
                if len(src.shape) == 4:
                    src = src.rearrange("p a t j -> p (a t) j")
                e.dma_start(dst, src).then_inc(w2_in.sem, 16)

    def ctx_copy(t, s):
        nc.gpsimd.tensor_copy(cg[:, s, :], k.ctxT[:, bass.ts(t, P)]).then_inc(c_laid.sem, 1)

    def rstd(e, ln, t, s, slot):
        e.wait_ge(ln[1].sem, ln[1].at(t + 1))
        nc.gpsimd.tensor_tensor(k.veps[:, slot, s:s + 1], k.mv[:, slot, s, 1:2], k.eps[:, 0:1], ALU.add).then_inc(ln[2].sem, 1)
        e.wait_ge(ln[2].sem, ln[2].at(t + 1))
        nc.gpsimd.tensor_tensor(k.rstd[:, slot, s:s + 1], k.veps[:, slot, s:s + 1], k.half[:, 0:1], ALU.pow).then_inc(ln[3].sem, 1)

    def modulate(e, t, s):
        e.wait_ge(f_laid.sem, f_laid.at(t + 1))
        nc.gpsimd.tensor_tensor(L2[:, s, :], L2[:, s, :], F[:, s, 0:D], ALU.mult).then_inc(xs_step.sem, 1)
        e.wait_ge(xs_step.sem, xs_step.at(t + 1))
        e.nop(nofuse=True)
        nc.gpsimd.tensor_tensor(XS[:, t, :], L2[:, s, :], F[:, s, D:2 * D], ALU.add).then_inc(xs_done.sem, 1)
        nc.gpsimd.tensor_copy(FO[:, t, :], F[:, s, 2 * D:4 * D]).then_inc(fo_kept.sem, 1)

    def norm_in(e, t, s):
        e.wait_ge(lnB[4].sem, lnB[4].at(t + 1))
        e.nop(nofuse=True)
        nc.gpsimd.tensor_copy(U[:, t, :], k.xn[:, s, 0, :]).then_inc(u_kept.sem, 1)
        nc.gpsimd.tensor_tensor(L2[:, s, :], L2[:, s, :], rows[:, 0, :], ALU.mult).then_inc(l2_step.sem, 1)
        e.wait_ge(l2_step.sem, l2_step.at(2 * t + 1))
        nc.gpsimd.tensor_tensor(L2[:, s, :], L2[:, s, :], rows[:, 1, :], ALU.add).then_inc(l2_step.sem, 1)

    l2_step = sem("l2_step", 2 * TILES)

    def pool_step(e, t, s):
        o = 1 - s
        e.wait_ge(s_laid.sem, s_laid.at(t + 1))
        e.nop(nofuse=True)
        nc.gpsimd.tensor_tensor(W[:, s, :, :], W[:, s, :, :], mb[:, t, :].unsqueeze(1).to_broadcast([P, H, CTX]), ALU.add).then_inc(s_masked.sem, 1)
        if more(t, 2):
            rstd(e, lnA, t + 2, s, 0)
            rstd(e, lnB, t + 2, s, 1)
        if not (isinstance(t, int) and t == 0):
            modulate(e, t - 1, o)
        e.wait_ge(tk_done.sem, tk_done.at(t + 1))
        e.nop(nofuse=True)
        nc.gpsimd.tensor_scalar(PEN[:, s, :, :], W2[:, s, :, :], TAKEN, MASKED, ALU.is_gt, ALU.mult).then_inc(pen1.sem, 1)
        e.wait_ge(pen1.sem, pen1.at(t + 1))
        nc.gpsimd.tensor_tensor(W[:, s, :, :], W[:, s, :, :], PEN[:, s, :, :], ALU.add).then_inc(pen2.sem, 1)
        e.wait_ge(r_done.sem, r_done.at(t + 1))
        nc.gpsimd.tensor_tensor(W[:, s, :, :], W[:, s, :, :], rec[:, s, :].unsqueeze(2).to_broadcast([P, H, CTX]), ALU.mult).then_inc(a_done.sem, 1)
        if more(t, 2):
            e.wait_ge(v_full.sem, v_full.at(t + 1))
            e.nop(nofuse=True)
            ctx_copy(t + 2, s)
        if more(t, 1):
            norm_in(e, t + 1, o)

    def pool(e):
        e.wait_ge(before.sem, before.end)
        e.wait_ge(ssm_done.sem, ssm_done.at(1))
        e.wait_ge(toep_in.sem, toep_in.at(32))
        e.wait_ge(w2_in.sem, w2_in.at(48))
        nc.gpsimd.tensor_scalar(mb.rearrange("p t j -> p (t j)"), mask8, -1.0, -MASKED, ALU.add, ALU.mult).then_inc(prep_p.sem, 1)
        e.wait_ge(prep_p.sem, prep_p.at(1))
        e.wait_ge(prep_tt.sem, prep_tt.at(1))
        e.wait_ge(w_in.sem, w_in.at(READY))
        for t in range(2):
            ctx_copy(t, t)
        for t in range(2):
            rstd(e, lnA, t, t, 0)
            rstd(e, lnB, t, t, 1)
        norm_in(e, 0, 0)
        pipelined_tiles(e, lambda t, s: pool_step(e, t, s))
        modulate(e, TILES - 1, 1)
        def tail_sum(g):
            yg = XS[:, bass.ts(g, GT), :]
            fo = FO[:, bass.ts(g, GT), :]
            nc.gpsimd.tensor_tensor(yg, yg, fo[:, :, 0:D], ALU.mult).then_inc(y_step.sem, 1)
            e.wait_ge(y_step.sem, y_step.at(2 * g + 1))
            e.nop(nofuse=True)
            nc.gpsimd.tensor_tensor(yg, yg, fo[:, :, D:2 * D], ALU.add).then_inc(y_step.sem, 1)
            e.wait_ge(y_step.sem, y_step.at(2 * g + 2))
            e.nop(nofuse=True)
            nc.gpsimd.tensor_tensor(yg, yg, U[:, bass.ts(g, GT), :], ALU.add).then_inc(y_done.sem, 1)

        e.wait_ge(b_laid.sem, b_laid.at(8))
        e.wait_ge(fo_kept.sem, fo_kept.at(TILES))
        e.wait_ge(u_kept.sem, u_kept.at(TILES))
        tail_sum(0)
        lnC.pool_rstd(e, 0)

        def body(g, more_):
            if more_:
                tail_sum(g + 1)
                lnC.pool_rstd(e, g + 1)
            lnD.pool_rstd(e, g)
            yg = XS[:, bass.ts(g, GT), :]
            e.wait_ge(lnD.out.sem, lnD.out.at(g + 1))
            e.nop(nofuse=True)
            nc.gpsimd.tensor_tensor(yg, yg, rows[:, 2, :].unsqueeze(1).to_broadcast([P, GT, D]), ALU.mult).then_inc(z_step.sem, 1)
            e.wait_ge(z_step.sem, z_step.at(2 * g + 1))
            e.nop(nofuse=True)
            nc.gpsimd.tensor_tensor(yg, yg, rows[:, 3, :].unsqueeze(1).to_broadcast([P, GT, D]), ALU.add).then_inc(z_step.sem, 1)
            e.wait_ge(z_step.sem, z_step.at(2 * g + 2))
            e.nop(nofuse=True)
            nc.gpsimd.tensor_tensor(k.x[:, bass.ts(g, GT), :], k.x[:, bass.ts(g, GT), :], yg, ALU.add).then_inc(x_done.sem, 1)

        pipelined_groups(e, body)

    ssm_done = sem("ssm_read", 1)

    def dve_prep(e):
        e.wait_ge(before.sem, before.end)
        ssm_dve(e)
        nc.vector.drain().then_inc(ssm_done.sem, 1)
        e.wait_ge(toep_in.sem, toep_in.at(32))
        e.wait_ge(w_in.sem, w_in.at(READY))
        e.wait_ge(w2_in.sem, w2_in.at(48))
        V = nc.vector
        V.memset(wk[DC:P, :], 0.0)
        V.memset(wv[DC:P, :], 0.0)
        V.memset(head_of[:], 0.0).then_inc(prep.sem, 1)
        e.wait_ge(prep.sem, prep.at(1))
        for h in range(H):
            V.memset(head_of[h * DH:(h + 1) * DH, h:h + 1], 1.0)
        V.tensor_scalar(wf, wfraw, mg, None, ALU.mult).then_inc(prep.sem, 1)
        V.tensor_scalar(bf[0:1, :], bf[0:1, :], mg[0:1, :], None, ALU.mult).then_inc(prep.sem, 1)
        V.tensor_scalar(rows[:, 2:4, :], rows[:, 2:4, :], k.gates[:, GATE:GATE + 1], None, ALU.mult).then_inc(prep.sem, 1)
        V.tensor_scalar(tmf[0:TILES, :], tm8[0:TILES, :], 1.0 / H, None, ALU.mult).then_inc(prep.sem, 1)
        e.wait_ge(prep.sem, prep.at(5))
        bfv = bf[0:1, :].rearrange("p (a b d) -> p a b d", a=2, b=2)
        V.tensor_scalar(bfv[:, :, 0, :], bfv[:, :, 0, :], 1.0, None, ALU.add).then_inc(prep.sem, 1)
        e.wait_ge(prep_t.sem, prep_t.at(1))
        V.tensor_copy(tmask, ps[:, 0, 0:TILES]).then_inc(prep_tt.sem, 1)
        e.wait_ge(prep.sem, prep.at(6))
        e.wait_ge(prep_p.sem, prep_p.at(1))

    def topk_round(e, t, s, r):
        V = nc.vector
        src = W if r == 0 else W2
        for h in range(H):
            ins = V.max(m8[:, r, h, :], src[:, s, h, :])
        ins.then_inc(tk.sem, 1)
        e.wait_ge(tk.sem, tk.at(7 * t + 2 * r + 1))
        e.nop(nofuse=True)
        if r == 0:
            V.tensor_scalar(nm[:, s, :], m8[:, 0, :, 0], -SCALE, None, ALU.mult)
        for h in range(H):
            ins = V.match_replace(W2[:, s, h, :], m8[:, r, h, :], src[:, s, h, :], TAKEN)
        if r == KTOP // 8 - 1:
            ins.then_inc(tk_done.sem, 1)
        else:
            ins.then_inc(tk.sem, 1)
            e.wait_ge(tk.sem, tk.at(7 * t + 2 * r + 2))
            e.nop(nofuse=True)

    def dve_step(e, t, s):
        V = nc.vector
        n = more(t, 2)
        if n:
            V.bn_stats(k.stat[:, 0, s, :], k.x[:, t + 2, :]).then_inc(lnA[0].sem, 1)
        e.wait_ge(s_masked.sem, s_masked.at(t + 1))
        e.nop(nofuse=True)
        topk_round(e, t, s, 0)
        if n:
            V.bn_aggr(k.mv[:, 0, s, :], k.stat[:, 0, s, :]).then_inc(lnA[1].sem, 1)
        topk_round(e, t, s, 1)
        if n:
            e.wait_ge(lnA[3].sem, lnA[3].at(t + 3))
            e.wait_ge(u_kept.sem, u_kept.at(t + 1))
            e.nop(nofuse=True)
            V.tensor_scalar(k.xn[:, s, 0, :], k.x[:, t + 2, :], k.mv[:, 0, s, 0:1], k.rstd[:, 0, s:s + 1],
                            ALU.subtract, ALU.mult).then_inc(lnA[4].sem, 1)
            e.wait_ge(lnA[4].sem, lnA[4].at(t + 3))
            V.bn_stats(k.stat[:, 1, s, :], k.xn[:, s, 0, :]).then_inc(lnB[0].sem, 1)
        topk_round(e, t, s, 2)
        if n:
            V.bn_aggr(k.mv[:, 1, s, :], k.stat[:, 1, s, :]).then_inc(lnB[1].sem, 1)
        topk_round(e, t, s, 3)
        e.wait_ge(e_done.sem, e_done.at(t + 1))
        V.reciprocal(rec[:, s, :], sums[:, s, :]).then_inc(r_step.sem, 1)
        e.wait_ge(r_step.sem, r_step.at(t + 1))
        V.tensor_scalar(rec[:, s, :], rec[:, s, :], tmask[:, t:t + 1] if isinstance(t, int) else tmask[:, bass.ts(t, 1)], None, ALU.mult).then_inc(r_done.sem, 1)
        if more(t, 1):
            o = 1 - s
            e.wait_ge(lnB[3].sem, lnB[3].at(t + 2))
            e.wait_ge(xs_done.sem, xs_done.at(t))
            e.nop(nofuse=True)
            V.tensor_scalar(L2[:, o, :], k.xn[:, o, 0, :], k.mv[:, 1, o, 0:1], k.rstd[:, 1, o:o + 1],
                            ALU.subtract, ALU.mult).then_inc(lnB[4].sem, 1)

    def dve(e):
        V = nc.vector
        dve_prep(e)
        for t in range(2):
            V.bn_stats(k.stat[:, 0, t, :], k.x[:, t, :]).then_inc(lnA[0].sem, 1)
        e.wait_ge(lnA[0].sem, lnA[0].at(2))
        for t in range(2):
            V.bn_aggr(k.mv[:, 0, t, :], k.stat[:, 0, t, :]).then_inc(lnA[1].sem, 1)
        for t in range(2):
            e.wait_ge(lnA[3].sem, lnA[3].at(t + 1))
            V.tensor_scalar(k.xn[:, t, 0, :], k.x[:, t, :], k.mv[:, 0, t, 0:1], k.rstd[:, 0, t:t + 1],
                            ALU.subtract, ALU.mult).then_inc(lnA[4].sem, 1)
            e.wait_ge(lnA[4].sem, lnA[4].at(t + 1))
            V.bn_stats(k.stat[:, 1, t, :], k.xn[:, t, 0, :]).then_inc(lnB[0].sem, 1)
            e.wait_ge(lnB[0].sem, lnB[0].at(t + 1))
            V.bn_aggr(k.mv[:, 1, t, :], k.stat[:, 1, t, :]).then_inc(lnB[1].sem, 1)
        e.wait_ge(lnB[3].sem, lnB[3].at(1))
        V.tensor_scalar(L2[:, 0, :], k.xn[:, 0, 0, :], k.mv[:, 1, 0, 0:1], k.rstd[:, 1, 0:1],
                        ALU.subtract, ALU.mult).then_inc(lnB[4].sem, 1)
        pipelined_tiles(e, lambda t, s: dve_step(e, t, s))
        for q in range(8):
            e.wait_ge(b_full.sem, b_full.at(q // 2 * 2 + 2))
            V.tensor_copy(XS[:, :, 16 * q:16 * q + 16], ps[:, q, :].rearrange("p (d t) -> p t d", t=TILES)).then_inc(b_laid.sem, 1)
        e.wait_ge(y_done.sem, y_done.at(1))
        lnC.dve_stats(0)
        lnC.dve_aggregate(e, 0, False)
        lnC.dve_apply(e, 0, 0)

        def body(g, more_):
            if more_:
                e.wait_ge(y_done.sem, y_done.at(g + 2))
                e.nop(nofuse=True)
                lnC.dve_stats(g + 1)
            e.wait_ge(o_full.sem, o_full.at(g + 1))
            yg = XS[:, bass.ts(g, GT), :]
            V.tensor_tensor(yg, ps[:, 3, :].rearrange("p (j d) -> p j d", j=GT), yg, ALU.add).then_inc(o_added.sem, 1)
            e.wait_ge(o_added.sem, o_added.at(g + 1))
            e.nop(nofuse=True)
            lnD.dve_stats(g)
            e.wait_ge(lnD.stats.sem, lnD.stats.at(g + 1))
            e.nop(nofuse=True)
            if more_:
                lnC.dve_aggregate(e, g + 1, True)
            lnD.dve_aggregate(e, g, True)
            if more_:
                lnC.dve_apply(e, g + 1, g + 1)
            lnD.dve_apply(e, g, g)

        pipelined_groups(e, body)

    def act_front(e, t, s):
        e.wait_ge(xt_full.sem, xt_full.at(t + 1))
        nc.scalar.copy(k.xnT[:, s, 0:P], ps[:, 0, 0:P]).then_inc(xt_laid.sem, 1)
        e.wait_ge(k_full.sem, k_full.at(t + 1))
        for h in range(H):
            last = nc.scalar.activation(kbd[:, s, :, h, :], ps[:, 2, 0:P].rearrange("p (b j) -> p b j", b=2), ACT.Copy,
                                        scale=head_of[:, h:h + 1])
        last.then_inc(k_laid.sem, 1)
        e.wait_ge(q_full.sem, q_full.at(t + 1))
        nc.scalar.copy(qT[:, s, :], ps[:, 1, 0:P]).then_inc(q_laid.sem, 1)

    def act_film(e, t, s):
        e.wait_ge(a_full.sem, a_full.at(t + 1))
        nc.scalar.copy(aT[0:CTX, s, :], ps[0:CTX, 5, 0:P]).then_inc(a_laid.sem, 1)
        e.wait_ge(c_full.sem, c_full.at(t + 1))
        nc.scalar.copy(cT[:, s, :], ps[:, 6, 0:P]).then_inc(cT_laid.sem, 1)
        e.wait_ge(f_full.sem, f_full.at(t + 1))
        nc.scalar.copy(F[:, s, :], ps[:, 7, :]).then_inc(f_laid.sem, 1)

    def act_step(e, t, s):
        o = 1 - s
        e.wait_ge(s_full.sem, s_full.at(t + 1))
        nc.scalar.copy(flat(W[:, s, :, :]), ps[:, 3, 0:H * CTX]).then_inc(s_laid.sem, 1)
        e.wait_ge(v_full.sem, v_full.at(t + 1))
        nc.scalar.copy(vs[0:CTX, s, :, :].rearrange("p b d -> p (b d)"), ps[0:CTX, 4, 0:2 * D]).then_inc(v_laid.sem, 1)
        if more(t, 1):
            act_front(e, t + 1, o)
        if not (isinstance(t, int) and t == 0):
            act_film(e, t - 1, o)
        e.wait_ge(pen2.sem, pen2.at(t + 1))
        for h in range(H):
            last = nc.scalar.activation(W[:, s, h, :], W[:, s, h, :], ACT.Exp, bias=nm[:, s, h:h + 1], scale=SCALE,
                                        accum_out=sums[:, s, h:h + 1])
        last.then_inc(e_done.sem, 1)

    def act(e):
        e.wait_ge(before.sem, before.end)
        ssm_act(e)
        e.wait_ge(w_in.sem, w_in.at(READY))
        e.wait_ge(prep_p.sem, prep_p.at(1))
        e.wait_ge(prep_tt.sem, prep_tt.at(1))
        act_front(e, 0, 0)
        pipelined_tiles(e, lambda t, s: act_step(e, t, s))
        act_film(e, TILES - 1, 1)
        e.wait_ge(b_laid.sem, b_laid.at(8))

        def turn_copy(n):
            e.wait_ge(ht_full.sem, ht_full.at(n + 1))
            nc.scalar.activation(hin, ps[:, 0, :], ACT.Identity, bias=cols[:, 1:2], scale=cols[:, 0:1]).then_inc(ht_laid.sem, 1)

        turn_copy(0)

        def body(g, more_):
            for c in range(HID):
                e.wait_ge(hid_full.sem, hid_full.at(HID * g + c + 1))
                nc.scalar.activation(hT[:, c % 2, :], ps[:, 1 + c % 2, :], ACT.Gelu, bias=cols[:, 2 + c:3 + c]).then_inc(hid_laid.sem, 1)
            if more_:
                turn_copy(g + 1)

        pipelined_groups(e, body)

    T = nc.tensor

    def pe_front(e, t, s):
        e.wait_ge(lnA[4].sem, lnA[4].at(t + 1))
        T.transpose(ps[:, 0, 0:P], k.xn[:, s, 0, :], k.ident[:]).then_inc(xt_full.sem, 1)
        e.wait_ge(c_laid.sem, c_laid.at(t + 1))
        e.wait_ge(k_laid.sem, k_laid.at(t))
        T.matmul(ps[:, 2, 0:P], wk, cg[:, s, :], start=True, stop=True).then_inc(k_full.sem, 1)
        e.wait_ge(xt_laid.sem, xt_laid.at(t + 1))
        T.matmul(ps[:, 1, 0:P], wq, k.xnT[:, s, 0:P], start=True, stop=True).then_inc(q_full.sem, 1)

    def pe_film(e, t, s):
        e.wait_ge(a_done.sem, a_done.at(t + 1))
        for h in range(H):
            last = T.matmul(ps[0:CTX, 5, 0:P], W[:, s, h, :], k.ident[:], start=(h == 0), stop=(h == H - 1))
        last.then_inc(a_full.sem, 1)
        e.wait_ge(a_laid.sem, a_laid.at(t + 1))
        e.nop(nofuse=True)
        for b in range(2):
            last = T.matmul(ps[:, 6, b * SEQ:(b + 1) * SEQ], vs[0:CTX, s, b, :], aT[0:CTX, s, b * SEQ:(b + 1) * SEQ], start=True, stop=True)
        last.then_inc(c_full.sem, 1)
        e.wait_ge(cT_laid.sem, cT_laid.at(t + 1))
        T.matmul(ps[:, 7, :], cT[:, s, :], wf, start=True, stop=False)
        T.matmul(ps[:, 7, :], k.ones, bf[0:1, :], start=False, stop=True).then_inc(f_full.sem, 1)

    def pe_step(e, t, s):
        o = 1 - s
        e.wait_ge(q_laid.sem, q_laid.at(t + 1))
        e.wait_ge(k_laid.sem, k_laid.at(t + 1))
        e.wait_ge(s_laid.sem, s_laid.at(t))
        e.nop(nofuse=True)
        for b in range(2):
            last = T.matmul(ps[64 * b:64 * b + 64, 3, 0:H * CTX], qT[:, s, 64 * b:64 * b + 64], flat(kbd[:, s, b, :, :]), start=True, stop=True)
        last.then_inc(s_full.sem, 1)
        e.wait_ge(v_laid.sem, v_laid.at(t))
        e.nop(nofuse=True)
        for b in range(2):
            last = T.matmul(ps[0:CTX, 4, b * D:(b + 1) * D], cg[:, s, b * CTX:(b + 1) * CTX], wv, start=True, stop=True)
        last.then_inc(v_full.sem, 1)
        if more(t, 1):
            pe_front(e, t + 1, o)
        if not (isinstance(t, int) and t == 0):
            pe_film(e, t - 1, o)

    def pe(e):
        e.wait_ge(w2_in.sem, w2_in.at(48))
        e.wait_ge(prep.sem, prep.at(5))
        T.transpose(ps[:, 0, 0:TILES], tmf[0:TILES, :], k.ident[0:TILES, 0:TILES]).then_inc(prep_t.sem, 1)
        e.wait_ge(prep.sem, prep.at(6))
        e.wait_ge(prep_p.sem, prep_p.at(1))
        e.wait_ge(prep_tt.sem, prep_tt.at(1))
        e.wait_ge(w_in.sem, w_in.at(READY))
        pe_front(e, 0, 0)
        pipelined_tiles(e, lambda t, s: pe_step(e, t, s))
        pe_film(e, TILES - 1, 1)
        e.wait_ge(f_laid.sem, f_laid.at(TILES))
        e.wait_ge(xs_done.sem, xs_done.at(TILES))
        for q in range(0, 8, 2):
            for flip in range(2):
                for i in range(16):
                    for b in range(2):
                        bank = q + (b ^ flip)
                        d = 16 * bank + i
                        half = slice(b * SEQ, (b + 1) * SEQ)
                        last = T.matmul(ps[half, bank, i * TILES:(i + 1) * TILES], k.toep[half, d, :], XS[half, :, d], start=True, stop=True)
            last.then_inc(b_full.sem, 2)
        e.wait_ge(b_laid.sem, b_laid.at(8))

        def turn(n):
            e.wait_ge(lnC.out.sem, lnC.out.at(n + 1))
            for j in range(GT):
                last = T.transpose(ps[:, 0, j * P:(j + 1) * P], k.xn[:, 0, j, :], k.ident[:])
            last.then_inc(ht_full.sem, 1)

        turn(0)

        def hidden(g, c):
            if c == 0:
                e.wait_ge(ht_laid.sem, ht_laid.at(g + 1))
            T.matmul(ps[:, 1 + c % 2, :], w1[:, c * P:(c + 1) * P], hin, start=True, stop=True).then_inc(hid_full.sem, 1)

        def outputs(g, c):
            e.wait_ge(hid_laid.sem, hid_laid.at(HID * g + c + 1))
            if c == 0:
                e.wait_ge(o_added.sem, o_added.at(g))
            for j in range(GT):
                T.matmul(ps[:, 3, j * P:(j + 1) * P], hT[:, c % 2, j * P:(j + 1) * P], w2[:, c, :],
                         start=(c == 0 and j == 0), stop=False, skip_group_check=True)

        def body(g, more_):
            hidden(g, 0)
            hidden(g, 1)
            outputs(g, 0)
            hidden(g, 2)
            outputs(g, 1)
            hidden(g, 3)
            outputs(g, 2)
            outputs(g, 3)
            for j in range(GT):
                last = T.matmul(ps[:, 3, j * P:(j + 1) * P], k.ones, rows[0:1, 4, :], start=False, stop=(j == GT - 1), skip_group_check=True)
            last.then_inc(o_full.sem, 1)
            if more_:
                turn(g + 1)

        pipelined_groups(e, body)

    return dict(sp=sp, pe=pe, act=act, dve=dve, pool=pool)


class Thresholds:

    BITS = 31

    def __init__(self, k, io):
        self.k, self.io = k, io
        sem = lambda n: k.sem("thr_" + n)
        self.w_in, self.ready, self.counted, self.total, self.read, self.step = (sem(n) for n in ("loaded", "ready", "counted", "totals", "totals_read", "step"))
        self.abs = k.sb("thr_abs", [P, 1024 + 8])
        self.hits = k.sb("thr_hits", [P, 2, 1024 + 8], BF16)
        self.need = k.sb("thr_need", [P, 8])
        self.count = k.sb("thr_count", [P, 8])
        self.cur = k.sb("thr_found", [P, 8], I32)
        self.cand = k.sb("thr_candidate", [P, 8], I32)
        self.bit = k.sb("thr_bit", [P, 8], I32)
        self.enough = k.sb("thr_enough", [P, 8], I32)
        self.sets = [(0, 512, P * 512), (512, 512, P * 512), (1024, 4, P * 4), (1028, 1, P)]

    def sp(self, e):
        io, a = self.io, self.abs
        with self.k.nc.allow_non_contiguous_dma(reason="biases are small"):
            e.dma_start(a[:, 0:512], io["L1_ffn_W1"]).then_inc(self.w_in.sem, 16)
            e.dma_start(a[:, 512:1024].rearrange("p (c d) -> p c d", c=4), io["L1_ffn_W2"].rearrange("(c p) d -> p c d", p=P)).then_inc(self.w_in.sem, 16)
            e.dma_start(a[:, 1024:1028], io["L1_ffn_b1"].rearrange("(c p) -> p c", p=P)).then_inc(self.w_in.sem, 16)
            e.dma_start(a[:, 1028:1029], io["L1_ffn_b2"].rearrange("(p a) -> p a", a=1)).then_inc(self.w_in.sem, 16)

    def dve_start(self, e):
        V = self.k.nc.vector
        V.memset(self.cur[:], 0)
        V.memset(self.cand[:], 1 << (self.BITS - 1))
        V.memset(self.bit[:], 1 << (self.BITS - 1))
        for i, (_, _, n) in enumerate(self.sets):
            kth = max(1, int(n * 0.1 / 2))
            V.memset(self.need[:, 2 * i:2 * i + 1], float(kth))
            V.memset(self.need[:, 2 * i + 1:2 * i + 2], float(n - kth + 1))
        e.wait_ge(self.w_in.sem, self.w_in.at(64))
        bits = self.abs[:, 0:1029].bitcast(I32)
        V.tensor_scalar(bits, bits, 0x7FFFFFFF, None, ALU.bitwise_and).then_inc(self.ready.sem, 1)
        e.wait_ge(self.ready.sem, self.ready.at(1))

    def dve_round(self, e, t):
        V = self.k.nc.vector
        first, last = isinstance(t, int) and t == 0, isinstance(t, int) and t == self.BITS
        if not first:
            e.wait_ge(self.total.sem, self.total.at(t))
            V.tensor_tensor(self.enough[:], self.k.ps[:, 2, D:D + 8], self.need[:], ALU.is_ge).then_inc(self.read.sem, 1)
            e.wait_ge(self.read.sem, self.read.at(t))
            e.nop(nofuse=True)
            V.copy_predicated(self.cur[:], self.enough[:], self.cand[:])
            V.tensor_scalar(self.bit[:], self.bit[:], 1, None, ALU.logical_shift_right).then_inc(self.step.sem, 1)
            if last:
                return
            e.wait_ge(self.step.sem, self.step.at(2 * t - 1))
            e.nop(nofuse=True)
            V.tensor_tensor(self.cand[:], self.cur[:], self.bit[:], ALU.bitwise_or).then_inc(self.step.sem, 1)
            e.wait_ge(self.step.sem, self.step.at(2 * t))
            e.nop(nofuse=True)
        for i, (at, n, _) in enumerate(self.sets):
            for j in range(2):
                c = 2 * i + j
                ins = V.tensor_scalar(self.hits[:, j, at:at + n], self.abs[:, at:at + n], self.cand[:, c:c + 1].bitcast(F32), 0.0,
                                      ALU.is_ge, ALU.add, accum_out=self.count[:, c:c + 1])
        ins.then_inc(self.counted.sem, 1)

    def pe_total(self, e, t):
        e.wait_ge(self.counted.sem, self.counted.at(t + 1))
        self.k.nc.tensor.matmul(self.k.ps[:, 2, D:D + 8], self.k.onesq[:], self.count[:], start=True, stop=True).then_inc(self.total.sem, 1)

    @property
    def value(self):
        return self.cur[:].bitcast(F32)


def ffn1(k, io):
    th = k.thresholds

    def loads(k, io, v):
        row = lambda n: io[n].rearrange("(a n) -> a n", a=1)
        col = lambda n: io[n].rearrange("(p a) -> p a", a=1)
        return [
            (v.w1[:, 0, :], io["L1_ffn_W1"]),
            (v.w2[:, 0, :, :], io["L1_ffn_W2"].rearrange("(c p) d -> p c d", p=P)),
            (v.b1[:, 0, :], io["L1_ffn_b1"].rearrange("(c p) -> p c", p=P)),
            (v.b2[0:2, :], row("L1_ffn_b2").partition_broadcast(2)),
            (v.wr, io["L1_ffn_Wr"]),
            (v.br[0:8, :], col("L1_ffn_br")),
            (v.gam, col("L1_ffn_ln_gamma")),
            (v.bet, col("L1_ffn_ln_beta")),
        ]

    def prepare(k, io, v):
        V = k.nc.vector
        step, ready = k.sem("f1_perturb_step"), k.sem("f1_perturbed")
        m1, m2, q, a2 = (v.cv.f32(512) for _ in range(4))

        def dve(e):
            e.wait_ge(v.before.sem, v.before.end)
            e.wait_ge(v.w_in.sem, v.w_in.at(16 * len(v.loads)))
            n = 0

            def go(ins):
                nonlocal n
                n += 1
                ins.then_inc(step.sem, 1)
                e.wait_ge(step.sem, step.at(n))

            def perturb(dst, w, a, i, rows=slice(0, P), only=None):
                width = w.shape[-1]
                x1, x2, xq = m1[rows, 0:width], m2[rows, 0:width], q[rows, 0:width]
                top, bot = th.value[rows, 2 * i:2 * i + 1], th.value[rows, 2 * i + 1:2 * i + 2]
                go(V.tensor_scalar(x1, a, top, None, ALU.is_ge))
                go(V.tensor_scalar(x2, a, bot, None, ALU.is_le))
                go(V.tensor_tensor(xq, x1, x2, ALU.mult))
                go(V.tensor_tensor(x2, x2, xq, ALU.subtract))
                go(V.tensor_tensor(x2, x2, x1, ALU.subtract))
                go(V.scalar_tensor_tensor(xq, w, 0.8, x2, ALU.mult, ALU.mult))
                if only is not None:
                    go(V.tensor_scalar(xq, xq, only, None, ALU.mult))
                go(V.tensor_tensor(dst, w, xq, ALU.add))

            perturb(v.w1[:, 1, :], v.w1[:, 0, :], th.abs[:, 0:512], 0)
            w2 = v.w2.rearrange("p x c d -> p x (c d)")
            perturb(w2[:, 1, :], w2[:, 0, :], th.abs[:, 512:1024], 1)
            perturb(v.b1[:, 1, :], v.b1[:, 0, :], th.abs[:, 1024:1028], 2)
            go(V.tensor_scalar(a2[0:2, 0:D].bitcast(I32), v.b2[0:2, :].bitcast(I32), 0x7FFFFFFF, None, ALU.bitwise_and))
            perturb(v.b2[0:2, :], v.b2[0:2, :], a2[0:2, 0:D], 3, slice(0, 2), k.ident[0:2, 1:2])
            V.drain().then_inc(ready.sem, 1)

        def pe(e):
            e.wait_ge(ready.sem, ready.at(1))

        return dict(dve=dve, pe=pe, act=pe)

    return experts(k, io, "f1", False, 5, loads, prepare)


def ffn2(k, io):
    nc, ps = k.nc, k.ps
    GATE, IC = 6, 4
    HID = IC * P
    sem = lambda n, total=TILES: k.sem("f2_" + n, total)
    w_in, w_sum, w_tot, w_tern = sem("w_loaded", None), sem("w_sums", 1), sem("w_totals", 1), sem("w_ternary", 1)
    w_step, w_turned, w_laid = sem("w_step", 7), sem("w_turned", 3), sem("w_laid", 3)
    q_step, q_done, qt_full, qt_laid = sem("q_step", 5 * GROUPS), sem("q_done", GROUPS), sem("qT_full", GROUPS), sem("qT_laid", GROUPS)
    s_done = sem("h_scale", 3 * TILES)
    g_full, r_done, r2_done, h_done, a_done, hr_done, hq_done = (sem(n) for n in ("gate_up", "relu", "relu_squared", "h", "h_max", "h_rounded", "h_quantized"))
    ht_full, ht_laid, y_full, x_step, x_done = sem("hT_full"), sem("hT_laid"), sem("y_full"), sem("x_added"), sem("x_done", GROUPS)
    before = k.x_ready
    k.x_ready = x_done
    ln = GroupNorm(k, "f2_ln", 0, lambda g, j: k.x[:, 4 * g + j, :], lambda g, j: k.xn[:, 0, j, :])

    cv = Carve(k)
    wraw = cv.f32(3, HID)
    wt = cv.f32(3, HID)
    wb = cv.bf16(3, HID)
    wT = cv.bf16(3, HID)
    identb = cv.bf16(P)
    sums, mean, inv = cv.f32(4), cv.f32(4), cv.f32(4)
    am, sc, cgt, cut = cv.f32(GT), cv.f32(GT), cv.f32(2, GT), cv.f32(2, GT)
    qf = cv.f32(GT, D)
    qb = cv.bf16(GT, D)
    qT = cv.bf16(GT * P)
    r, r2, h, hq = (cv.f32(2, HID) for _ in range(4))
    hb = cv.bf16(2, HID)
    hT = cv.bf16(2, HID)
    ah, sh, yc = cv.f32(2), cv.f32(2), cv.f32(2)
    junk = cv.f32(HID)
    onesq = k.onesq
    bank16 = lambda b: ps[:, b, :].bitcast(BF16)

    def sp(e):
        e.wait_ge(before.sem, before.end)
        e.dma_start(wraw[:, 0, :].rearrange("p (c d) -> p c d", c=IC), io["L2_ffn_w_gate"].rearrange("(c p) d -> p c d", p=P)).then_inc(w_in.sem, 16)
        e.dma_start(wraw[:, 1, :].rearrange("p (c d) -> p c d", c=IC), io["L2_ffn_w_up"].rearrange("(c p) d -> p c d", p=P)).then_inc(w_in.sem, 16)
        e.dma_start(wraw[:, 2, :], io["L2_ffn_w_down"]).then_inc(w_in.sem, 16)

    T, V, S = nc.tensor, nc.vector, nc.scalar

    def quantize(e, g):
        n = 5 * g
        e.wait_ge(ln.out.sem, ln.out.at(g + 1))
        V.tensor_reduce(am[:], k.xn[:, 0, :, :], AX.X, ALU.max, apply_absolute_value=True).then_inc(q_step.sem, 1)
        e.wait_ge(q_step.sem, q_step.at(n + 1))
        V.tensor_scalar(am[:], am[:], EPSQ, 1.0 / 127.0, ALU.max, ALU.mult).then_inc(q_step.sem, 1)
        e.wait_ge(q_step.sem, q_step.at(n + 2))
        V.reciprocal(sc[:], am[:]).then_inc(q_step.sem, 1)
        e.wait_ge(q_step.sem, q_step.at(n + 3))
        for j in range(GT):
            last = V.tensor_scalar(qf[:, j, :], k.xn[:, 0, j, :], sc[:, j:j + 1], ROUND, ALU.mult, ALU.add)
        last.then_inc(q_step.sem, 1)
        e.wait_ge(q_step.sem, q_step.at(n + 4))
        V.tensor_scalar(qb[:], qf[:], -ROUND, 127.0, ALU.add, ALU.min).then_inc(q_done.sem, 1)

    def scales(e, g):
        V.tensor_scalar(cgt[:, 0, :], am[:], mean[:, 0:1], None, ALU.mult)
        V.tensor_scalar(cut[:, 0, :], am[:], mean[:, 1:2], None, ALU.mult).then_inc(q_step.sem, 1)

    def dve(e):
        e.wait_ge(before.sem, before.end)
        e.wait_ge(w_in.sem, w_in.at(48))
        for i in range(3):
            ins = V.tensor_reduce(sums[:, i:i + 1], wraw[:, i, :], AX.X, ALU.add, apply_absolute_value=True)
        V.tensor_copy(identb[:], k.ident[:]).then_inc(w_sum.sem, 1)
        ln.dve_stats(0)
        e.wait_ge(w_tot.sem, w_tot.at(1))
        V.tensor_scalar(mean[:, 0:3], ps[:, 0, 0:3], 1.0 / (P * HID), EPSQ, ALU.mult, ALU.max).then_inc(w_step.sem, 1)
        e.wait_ge(w_step.sem, w_step.at(1))
        ln.dve_aggregate(e, 0, True)
        V.reciprocal(inv[:, 0:3], mean[:, 0:3]).then_inc(w_step.sem, 1)
        e.wait_ge(w_step.sem, w_step.at(2))
        for i in range(3):
            V.tensor_scalar(wt[:, i, :], wraw[:, i, :], inv[:, i:i + 1], ROUND, ALU.mult, ALU.add).then_inc(w_step.sem, 1)
        V.tensor_scalar(mean[:, 2:3], mean[:, 2:3], k.gates[:, GATE:GATE + 1], None, ALU.mult).then_inc(w_step.sem, 1)
        e.wait_ge(w_step.sem, w_step.at(6))
        V.tensor_scalar(wt[:], wt[:], -ROUND, 1.0, ALU.add, ALU.min).then_inc(w_step.sem, 1)
        e.wait_ge(w_step.sem, w_step.at(7))
        V.tensor_scalar(wb[:], wt[:], -1.0, None, ALU.max).then_inc(w_tern.sem, 1)
        ln.dve_apply(e, 0, 0)
        quantize(e, 0)

        def body(g, more):
            scales(e, g)
            if more:
                ln.dve_stats(g + 1)
            for j in range(GT):
                t, s = GT * g + j, j % 2
                if j == 0:
                    e.wait_ge(q_step.sem, q_step.at(5 * g + 5))
                e.wait_ge(r2_done.sem, r2_done.at(t + 1))
                V.scalar_tensor_tensor(h[:, s, :], ps[:, 2 + s, :], cut[:, 0, j:j + 1], r2[:, s, :], ALU.mult, ALU.mult).then_inc(h_done.sem, 1)
                e.wait_ge(h_done.sem, h_done.at(t + 1))
                V.tensor_reduce(ah[:, s:s + 1], h[:, s, :], AX.X, ALU.max, apply_absolute_value=True).then_inc(a_done.sem, 1)
                if j == 0 and more:
                    e.wait_ge(a_done.sem, a_done.at(t + 1))
                    e.nop(nofuse=True)
                    ln.dve_aggregate(e, g + 1, True)
                e.wait_ge(a_done.sem, a_done.at(t + 1))
                V.tensor_scalar(ah[:, s:s + 1], ah[:, s:s + 1], EPSQ, 1.0 / 127.0, ALU.max, ALU.mult).then_inc(s_done.sem, 1)
                e.wait_ge(s_done.sem, s_done.at(3 * t + 1))
                V.reciprocal(sh[:, s:s + 1], ah[:, s:s + 1]).then_inc(s_done.sem, 1)
                e.wait_ge(s_done.sem, s_done.at(3 * t + 2))
                V.tensor_scalar(hq[:, s, :], h[:, s, :], sh[:, s:s + 1], ROUND, ALU.mult, ALU.add).then_inc(hr_done.sem, 1)
                V.tensor_scalar(yc[:, s:s + 1], ah[:, s:s + 1], mean[:, 2:3], None, ALU.mult).then_inc(s_done.sem, 1)
                e.wait_ge(hr_done.sem, hr_done.at(t + 1))
                V.tensor_scalar(hb[:, s, :], hq[:, s, :], -ROUND, 127.0, ALU.add, ALU.min).then_inc(hq_done.sem, 1)
                if j == 1 and more:
                    ln.dve_apply(e, g + 1, g + 1)
                if j == 2 and more:
                    quantize(e, g + 1)
                if j > 0:
                    add(g, j - 1)
            add(g, GT - 1, True)

        def add(g, j, end=False):
            t, s = GT * g + j, j % 2
            e.wait_ge(s_done.sem, s_done.at(3 * t + 3))
            e.wait_ge(y_full.sem, y_full.at(t + 1))
            V.scalar_tensor_tensor(k.x[:, t, :], ps[:, 7, 0:D], yc[:, s:s + 1], k.x[:, t, :], ALU.mult, ALU.add).then_inc(x_step.sem, 1)
            if end:
                e.wait_ge(x_step.sem, x_step.at(t + 1))
                e.nop(nofuse=True)
                e.sem_inc(x_done.sem, 1)

        pipelined_groups(e, body)

    def pe(e):
        e.wait_ge(w_sum.sem, w_sum.at(1))
        T.matmul(ps[:, 0, 0:3], onesq[:], sums[:, 0:3], start=True, stop=True).then_inc(w_tot.sem, 1)
        e.wait_ge(w_tern.sem, w_tern.at(1))
        for i in range(3):
            for c in range(IC):
                last = T.transpose(bank16(4 + i)[:, c * P:(c + 1) * P], wb[:, i, c * P:(c + 1) * P], identb[:])
            last.then_inc(w_turned.sem, 1)
        e.wait_ge(w_laid.sem, w_laid.at(3))

        def turn(n):
            e.wait_ge(q_done.sem, q_done.at(n + 1))
            for j in range(GT):
                last = T.transpose(bank16(4)[:, j * P:(j + 1) * P], qb[:, j, :], identb[:])
            last.then_inc(qt_full.sem, 1)

        def gate_up(g, j):
            t, s = GT * g + j, j % 2
            if j == 0:
                e.wait_ge(qt_laid.sem, qt_laid.at(g + 1))
            e.wait_ge(h_done.sem, h_done.at(t - 1))
            T.matmul(ps[:, s, :], qT[:, j * P:(j + 1) * P], wT[:, 0, :], start=True, stop=True)
            T.matmul(ps[:, 2 + s, :], qT[:, j * P:(j + 1) * P], wT[:, 1, :], start=True, stop=True).then_inc(g_full.sem, 1)

        def turn_h(g, j):
            t, s = GT * g + j, j % 2
            e.wait_ge(hq_done.sem, hq_done.at(t + 1))
            for c in range(IC):
                last = T.transpose(bank16(5 + s)[:, c * P:(c + 1) * P], hb[:, s, c * P:(c + 1) * P], identb[:])
            last.then_inc(ht_full.sem, 1)

        def down(g, j):
            t, s = GT * g + j, j % 2
            e.wait_ge(ht_laid.sem, ht_laid.at(t + 1))
            e.wait_ge(x_step.sem, x_step.at(t))
            for c in range(IC):
                last = T.matmul(ps[:, 7, 0:D], hT[:, s, c * P:(c + 1) * P], wT[:, 2, c * P:(c + 1) * P], start=(c == 0), stop=(c == IC - 1))
            last.then_inc(y_full.sem, 1)

        turn(0)

        def body(g, more):
            gate_up(g, 0)
            for j in range(GT):
                if j + 1 < GT:
                    gate_up(g, j + 1)
                turn_h(g, j)
                if j == GT - 1 and more:
                    turn(g + 1)
                down(g, j)

        pipelined_groups(e, body)

    def act(e):
        for i in range(3):
            e.wait_ge(w_turned.sem, w_turned.at(i + 1))
            S.copy(wT[:, i, :], bank16(4 + i)[:, 0:HID]).then_inc(w_laid.sem, 1)

        def turn_copy(n):
            e.wait_ge(qt_full.sem, qt_full.at(n + 1))
            S.copy(qT[:], bank16(4)[:, 0:GT * P]).then_inc(qt_laid.sem, 1)

        turn_copy(0)

        def relu(g, j):
            t, s = GT * g + j, j % 2
            e.wait_ge(g_full.sem, g_full.at(t + 1))
            if j == 0:
                e.wait_ge(q_step.sem, q_step.at(5 * g + 5))
            S.activation(r[:, s, :], ps[:, s, :], ACT.Relu, scale=cgt[:, 0, j:j + 1]).then_inc(r_done.sem, 1)

        def body(g, more):
            relu(g, 0)
            for j in range(GT):
                if j + 1 < GT:
                    relu(g, j + 1)
                t, s = GT * g + j, j % 2
                e.wait_ge(ht_full.sem, ht_full.at(t + 1))
                S.copy(hT[:, s, :], bank16(5 + s)[:, 0:HID]).then_inc(ht_laid.sem, 1)
            if more:
                turn_copy(g + 1)

        pipelined_groups(e, body)

    def pool(e):
        e.wait_ge(before.sem, before.end)
        ln.pool_rstd(e, 0)

        def body(g, more):
            for j in range(GT):
                t, s = GT * g + j, j % 2
                e.wait_ge(r_done.sem, r_done.at(t + 1))
                nc.gpsimd.tensor_tensor(r2[:, s, :], r[:, s, :], r[:, s, :], ALU.mult).then_inc(r2_done.sem, 1)
                if j == 0 and more:
                    ln.pool_rstd(e, g + 1)

        pipelined_groups(e, body)

    return dict(sp=sp, pe=pe, act=act, dve=dve, pool=pool)


def ffn3(k, io):
    nc, ps = k.nc, k.ps
    GATE, IC, R = 7, 4, 16
    HID = IC * P
    sem = lambda n, total=GROUPS: k.sem("f3_" + n, total)
    w_in, w_step, w_low, w_ready = sem("w_loaded", None), sem("w_step", 6), sem("low_rank", 1), sem("w_ready", 1)
    w_turned, w_laid = sem("w_turned", 2), sem("w_laid", 2)
    u_full, u_laid, t_full, t_laid = (sem(n, 1) for n in ("uT_full", "uT_laid", "fv_full", "fv_laid"))
    xt_full, xt_laid, o_full, x_done = (sem(n) for n in ("xT_full", "xT_laid", "o_full", "x_done"))
    h_full, r_done, h_laid = (sem(n, IC * GROUPS) for n in ("h_full", "relu", "squared"))
    before = k.x_ready
    k.x_ready = x_done
    ln = GroupNorm(k, "f3_ln", 0, lambda g, j: k.x[:, 4 * g + j, :], lambda g, j: k.xn[:, 0, j, :])
    cv = Carve(k)
    wf, wp = cv.f32(IC, D), cv.f32(HID)
    tf, tp = cv.f32(IC, D), cv.f32(HID)
    wfT, wpT = cv.f32(HID), cv.f32(IC, D)
    un, uT = cv.f32(IC, R), cv.f32(IC, P)
    fbT, vn, fv = cv.f32(R), cv.f32(D), cv.f32(D)
    gate = cv.f32(1)
    s5, i5 = cv.f32(IC + 1), cv.f32(IC + 1)
    r, hT = cv.f32(2, GT * P), cv.f32(2, GT * P)
    xnT = k.xnT[:, 0, :]
    T, V, S = nc.tensor, nc.vector, nc.scalar

    def sp(e):
        e.wait_ge(before.sem, before.end)
        with nc.allow_non_contiguous_dma(reason="a 16 by 16 matrix, transposed"):
            for dst, src in (
                (wf, io["L3_ffn_w_fc"].rearrange("(c p) d -> p c d", p=P)), (wp, io["L3_ffn_w_proj"]),
                (un, io["L3_ffn_u"].rearrange("(c p) r -> p c r", p=P)), (fbT[0:R, :], io["L3_ffn_fast_b"].rearrange("i j -> j i")),
                (vn[0:R, :], io["L3_ffn_v"]), (gate, io["L3_ffn_gate"].rearrange("(a n) -> a n", a=1).partition_broadcast(P)),
            ):
                e.dma_start(dst, src).then_inc(w_in.sem, 16)

    def dve(e):
        e.wait_ge(before.sem, before.end)
        e.wait_ge(w_in.sem, w_in.at(96))
        n = 0

        def go(ins):
            nonlocal n
            n += 1
            ins.then_inc(w_step.sem, 1)
            e.wait_ge(w_step.sem, w_step.at(n))

        ln.dve_stats(0)
        V.tensor_reduce(s5[:, 0:IC], wf[:], AX.X, ALU.add, apply_absolute_value=True)
        go(V.tensor_reduce(s5[:, IC:IC + 1], wp[:], AX.X, ALU.add, apply_absolute_value=True))
        ln.dve_aggregate(e, 0, True)
        V.tensor_scalar(s5[:, 0:IC], s5[:, 0:IC], 1.0 / D, EPSQ, ALU.mult, ALU.max)
        go(V.tensor_scalar(s5[:, IC:IC + 1], s5[:, IC:IC + 1], 1.0 / HID, EPSQ, ALU.mult, ALU.max))
        go(V.reciprocal(i5[:], s5[:]))
        for c in range(IC):
            V.tensor_scalar(tf[:, c, :], wf[:, c, :], i5[:, c:c + 1], ROUND, ALU.mult, ALU.add)
        go(V.tensor_scalar(tp[:], wp[:], i5[:, IC:IC + 1], ROUND, ALU.mult, ALU.add))
        V.tensor_scalar(tf[:], tf[:], -ROUND, 1.0, ALU.add, ALU.min)
        go(V.tensor_scalar(tp[:], tp[:], -ROUND, 1.0, ALU.add, ALU.min))
        for c in range(IC):
            V.tensor_scalar(tf[:, c, :], tf[:, c, :], -1.0, s5[:, c:c + 1], ALU.max, ALU.mult)
        go(V.tensor_scalar(tp[:], tp[:], -1.0, s5[:, IC:IC + 1], ALU.max, ALU.mult))
        e.wait_ge(u_full.sem, u_full.at(1))
        V.tensor_copy(uT[0:R, :, :], ps[0:R, 0, :].rearrange("p (c f) -> p c f", c=IC)).then_inc(u_laid.sem, 1)
        e.wait_ge(t_full.sem, t_full.at(1))
        V.tensor_copy(fv[0:R, :], ps[0:R, 1, 0:D]).then_inc(t_laid.sem, 1)
        e.wait_ge(w_low.sem, w_low.at(1))
        V.scalar_tensor_tensor(tf[:], ps[:, 2, :].rearrange("p (c d) -> p c d", c=IC), gate[:], tf[:], ALU.mult, ALU.add).then_inc(w_ready.sem, 1)
        for i, dst in enumerate((wfT[:], wpT.rearrange("p c d -> p (c d)"))):
            e.wait_ge(w_turned.sem, w_turned.at(i + 1))
            V.tensor_scalar(dst, ps[:, 3 + i, :], 1.0 if i == 0 else k.gates[:, GATE:GATE + 1], None, ALU.mult).then_inc(w_laid.sem, 1)
        ln.dve_apply(e, 0, 0)

        def body(g, more):
            if more:
                ln.dve_stats(g + 1)
                e.wait_ge(ln.stats.sem, ln.stats.at(g + 2))
                e.nop(nofuse=True)
                ln.dve_aggregate(e, g + 1, True)
                e.wait_ge(xt_full.sem, xt_full.at(g + 1))
                e.nop(nofuse=True)
                ln.dve_apply(e, g + 1, g + 1)
            e.wait_ge(o_full.sem, o_full.at(g + 1))
            e.nop(nofuse=True)
            xg = k.x[:, bass.ts(g, GT), :]
            V.tensor_tensor(xg, ps[:, 3, :].rearrange("p (j d) -> p j d", j=GT), xg, ALU.add).then_inc(x_done.sem, 1)

        pipelined_groups(e, body)

    def pe(e):
        e.wait_ge(w_in.sem, w_in.at(96))
        e.wait_ge(before.sem, before.end)
        for c in range(IC):
            last = T.transpose(ps[0:R, 0, c * P:(c + 1) * P], un[:, c, :], k.ident[:])
        last.then_inc(u_full.sem, 1)
        T.matmul(ps[0:R, 1, 0:D], fbT[0:R, :], vn[0:R, :], start=True, stop=True).then_inc(t_full.sem, 1)
        e.wait_ge(u_laid.sem, u_laid.at(1))
        e.wait_ge(t_laid.sem, t_laid.at(1))
        for c in range(IC):
            last = T.matmul(ps[:, 2, c * P:(c + 1) * P], uT[0:R, c, :], fv[0:R, :], start=True, stop=True)
        last.then_inc(w_low.sem, 1)
        e.wait_ge(w_ready.sem, w_ready.at(1))
        for i in range(2):
            for c in range(IC):
                last = T.transpose(ps[:, 3 + i, c * P:(c + 1) * P], tf[:, c, :] if i == 0 else tp[:, c * P:(c + 1) * P], k.ident[:])
            last.then_inc(w_turned.sem, 1)
        e.wait_ge(w_laid.sem, w_laid.at(2))

        def turn(n):
            e.wait_ge(ln.out.sem, ln.out.at(n + 1))
            for j in range(GT):
                last = T.transpose(ps[:, 0, j * P:(j + 1) * P], k.xn[:, 0, j, :], k.ident[:])
            last.then_inc(xt_full.sem, 1)

        def hidden(g, c):
            if c == 0:
                e.wait_ge(xt_laid.sem, xt_laid.at(g + 1))
            T.matmul(ps[:, 1 + c % 2, :], wfT[:, c * P:(c + 1) * P], xnT, start=True, stop=True).then_inc(h_full.sem, 1)

        def outputs(g, c):
            e.wait_ge(h_laid.sem, h_laid.at(IC * g + c + 1))
            if c == 0:
                e.wait_ge(x_done.sem, x_done.at(g))
            for j in range(GT):
                last = T.matmul(ps[:, 3, j * P:(j + 1) * P], hT[:, c % 2, j * P:(j + 1) * P], wpT[:, c, :],
                                start=(c == 0 and j == 0), stop=(c == IC - 1 and j == GT - 1), skip_group_check=True)
            if c == IC - 1:
                last.then_inc(o_full.sem, 1)

        turn(0)

        def body(g, more):
            hidden(g, 0)
            hidden(g, 1)
            outputs(g, 0)
            hidden(g, 2)
            outputs(g, 1)
            hidden(g, 3)
            if more:
                turn(g + 1)
            outputs(g, 2)
            outputs(g, 3)

        pipelined_groups(e, body)

    def act(e):
        def turn_copy(n):
            e.wait_ge(xt_full.sem, xt_full.at(n + 1))
            S.copy(xnT, ps[:, 0, :]).then_inc(xt_laid.sem, 1)

        turn_copy(0)

        def body(g, more):
            for c in range(IC):
                e.wait_ge(h_full.sem, h_full.at(IC * g + c + 1))
                S.activation(r[:, c % 2, :], ps[:, 1 + c % 2, :], ACT.Relu).then_inc(r_done.sem, 1)
            if more:
                turn_copy(g + 1)

        pipelined_groups(e, body)

    def pool(e):
        e.wait_ge(before.sem, before.end)
        ln.pool_rstd(e, 0)

        def body(g, more):
            for c in range(IC):
                e.wait_ge(r_done.sem, r_done.at(IC * g + c + 1))
                nc.gpsimd.tensor_tensor(hT[:, c % 2, :], r[:, c % 2, :], r[:, c % 2, :], ALU.mult).then_inc(h_laid.sem, 1)
                if c == 0 and more:
                    ln.pool_rstd(e, g + 1)

        pipelined_groups(e, body)

    return dict(sp=sp, pe=pe, act=act, dve=dve, pool=pool)


def store(k, io):
    nc = k.nc
    out_done = k.sem("out_stored")
    before = k.x_ready

    def sp(e):
        e.wait_ge(before.sem, before.end)
        e.dma_start(io["out"].rearrange("b s c -> (b s) c").rearrange("(t p) c -> p t c", p=P), k.x[:]).then_inc(out_done.sem, 16)
        e.wait_ge(out_done.sem, out_done.at(16))

    return dict(sp=sp)


def build_program(nc, io, upto=99, start=0):
    with ExitStack() as ctx:
        k = allocate(nc, ctx)
        k.thresholds = Thresholds(k, io)
        parts = [setup(k, io)]
        sublayers = [
            lambda: attention(k, io, "a0", 16, "L0_xattn_Wq", "L0_xattn_Wk", "L0_xattn_Wv", "L0_xattn_Wo", "L0_xattn_bo", 0, k.thresholds),
            lambda: ffn0(k, io),
            lambda: attention_ssm(k, io),
            lambda: ffn1(k, io),
            lambda: attention(k, io, "a2", 8, "L2_xattn_Wq", "L2_xattn_Wk", "L2_xattn_Wv", "L2_xattn_Wout", "L2_xattn_bout", 2),
            lambda: ffn2(k, io),
            lambda: attention(k, io, "a3", 8, "L3_xattn_Wq", "L3_xattn_Wk", "L3_xattn_Wv", "L3_xattn_Wo", "L3_xattn_bo", 3),
            lambda: ffn3(k, io),
        ]
        for make in sublayers[start:upto]:
            k.semaphores.next_sublayer()
            parts.append(make())
        parts.append(store(k, io))
        block = ctx.enter_context(nc.Block())

        @block.sync
        def _(e):
            for part in parts:
                if "sp" in part:
                    part["sp"](e)

        @block.tensor
        def _(e):
            for part in parts:
                if "pe" in part:
                    part["pe"](e)

        @block.scalar
        def _(e):
            for part in parts:
                if "act" in part:
                    part["act"](e)

        @block.vector
        def _(e):
            for part in parts:
                if "dve" in part:
                    part["dve"](e)

        @block.gpsimd
        def _(e):
            for part in parts:
                if "pool" in part:
                    part["pool"](e)


def kernel(**inputs):
    import numpy as np
    import concourse.bacc as bacc
    from concourse.bass_utils import run_bass_kernel_spmd

    nc = bacc.Bacc("TRN2", target_bir_lowering=False, num_devices=1)
    arrays, io = {}, {}
    for name, value in inputs.items():
        a = np.ascontiguousarray(value)
        if a.dtype == np.bool_:
            a = a.view(np.uint8)
        if a.ndim == 0:
            a = a.reshape(1)
        arrays[name] = a
        io[name] = nc.dram_tensor(name, a.shape, mybir.dt.from_np(a.dtype), kind="ExternalInput").ap()
    io["out"] = nc.dram_tensor("out", inputs["x"].shape, F32, kind="ExternalOutput").ap()
    build_program(nc, io)
    return run_bass_kernel_spmd(nc, [arrays], core_ids=[0]).results[0]["out"]
```

```python
from contextlib import ExitStack

import concourse.bass as bass
from concourse import mybir

ALU = mybir.AluOpType
ACT = mybir.ActivationFunctionType
AX = mybir.AxisListType
F32 = mybir.dt.float32
BF16 = mybir.dt.bfloat16
I32 = mybir.dt.int32
U8 = mybir.dt.uint8

P = 128
B, SEQ, D = 64, 64, 128
CTX, DC = 64, 96
TOK = B * SEQ
TILES = TOK // P
GT = 4
GROUPS = TILES // GT
BANK = 512
EPS = 1e-5
EPSQ = 1e-5
ROUND = 12582912.0


class Signal:

    def __init__(self, sem, base, total):
        self.sem, self.base, self.end = sem, base, base + (total or 1)

    def at(self, count):
        return self.base + (max(count, 0) if isinstance(count, int) else count)


class Semaphores:

    def __init__(self, new):
        self.new, self.spare, self.used = new, [], [[]]

    def next_sublayer(self):
        if len(self.used) > 1:
            self.spare += self.used[-2]
        self.used.append([])

    def take(self, name, total=None):
        sem, base = self.spare.pop(0) if total and self.spare else (self.new(name), 0)
        if total:
            self.used[-1].append((sem, base + total))
        return Signal(sem, base, total)


def pipelined_tiles(eng, step, tail=2):
    for t in (0, 1):
        step(t, t % 2)
    with eng.Fori(1, (TILES - tail) // 2) as it:
        step(2 * it, 0)
        step(2 * it + 1, 1)
    for t in range(TILES - tail, TILES):
        step(t, t % 2)


def pipelined_groups(eng, body):
    body(0, True)
    with eng.Fori(1, GROUPS - 1) as g:
        body(g, True)
    body(GROUPS - 1, False)


def allocate(nc, ctx):
    k = Parts()
    k.nc = nc
    k.sb = lambda name, shape, dt=F32: ctx.enter_context(nc.sbuf_tensor(name, shape, dt))
    k.semaphores = Semaphores(lambda name: ctx.enter_context(nc.semaphore(name)))
    k.sem = k.semaphores.take
    k.ps = ctx.enter_context(nc.psum_tensor("ps", [P, 8, BANK], F32))
    k.x = k.sb("x_res", [P, TILES, D])
    k.ctxT = k.sb("ctxT", [P, TOK])
    k.ident = k.sb("ident", [P, P])
    k.onesq = k.sb("ones_square", [P, P])
    k.ones = k.onesq[0:1, :]
    k.gates = k.sb("gates", [P, 8])
    k.toep = k.sb("toeplitz", [P, D, SEQ])
    k.arena = k.sb("arena", [P, 30720])
    k.stat = k.sb("ln_stat", [P, 2, GT, 6])
    k.mv = k.sb("ln_mv", [P, 2, GT, 2])
    k.rstd = k.sb("ln_rstd", [P, 2, GT])
    k.veps = k.sb("ln_veps", [P, 2, GT])
    k.half = k.sb("minus_half", [P, GT])
    k.eps = k.sb("eps", [P, GT])
    k.xn = k.sb("xn", [P, 2, GT, D])
    k.xnT = k.sb("xnT", [P, 2, GT * P])
    return k


class Parts:
    pass


class Carve:

    def __init__(self, space, start=0):
        self.space, self.at, self.size = space, start, space.shape[1]

    def cut(self, shape, dtype, per_word):
        n = 1
        for s in shape:
            n *= s
        v = self.space[:, self.at:self.at + n // per_word]
        self.at += n // per_word
        assert self.at <= self.size, self.at
        if dtype != F32:
            v = v.bitcast(dtype)
        if len(shape) == 1:
            return v
        names = " ".join(f"a{i}" for i in range(len(shape)))
        return v.rearrange(f"p ({names}) -> p {names}", **{f"a{i}": s for i, s in enumerate(shape[:-1])})

    def f32(self, *shape):
        return self.cut(shape, F32, 1)

    def bf16(self, *shape):
        return self.cut(shape, BF16, 2)


def setup(k, io):
    nc = k.nc
    c_in, g_in, zero, made, turned, laid, tanh = (k.sem("setup_" + n) for n in (
        "ctx_loaded", "gates_loaded", "zeroed", "constants", "ctx_turned", "ctx_laid", "gates_ready"))
    x_in, ready = k.sem("setup_x_loaded"), k.sem("setup_done", 1)
    carve = Carve(k.arena, 24032)
    ctx_tok = carve.f32(TILES, DC)
    graw = carve.f32(8)

    def sp(e):
        e.dma_start(ctx_tok[:], io["ctx_768"].rearrange("b s c -> (b s) c").rearrange("(t p) c -> p t c", p=P)).then_inc(c_in.sem, 16)
        e.dma_start(graw[:, 0:4], io["g_xattn"].rearrange("(a n) -> a n", a=1).partition_broadcast(P)).then_inc(g_in.sem, 16)
        e.dma_start(graw[:, 4:8], io["g_ffn"].rearrange("(a n) -> a n", a=1).partition_broadcast(P)).then_inc(g_in.sem, 16)
        k.ssm.sp_load(e)
        e.dma_start(k.x[:], io["x"].rearrange("b s c -> (b s) c").rearrange("(t p) c -> p t c", p=P)).then_inc(x_in.sem, 16)

    def pool(e):
        nc.gpsimd.memset(k.ident[:], 0.0).then_inc(zero.sem, 1)
        e.wait_ge(zero.sem, zero.at(1))
        nc.gpsimd.memset(k.onesq[:], 1.0).then_inc(zero.sem, 1)
        e.wait_ge(zero.sem, zero.at(2))
        nc.gpsimd.memset(k.half[:], -0.5).then_inc(zero.sem, 1)
        e.wait_ge(zero.sem, zero.at(3))
        nc.gpsimd.memset(k.eps[:], EPS).then_inc(zero.sem, 1)
        e.wait_ge(zero.sem, zero.at(4))
        nc.gpsimd.memset(k.ctxT[DC:P, :], 0.0).then_inc(zero.sem, 1)
        e.wait_ge(zero.sem, zero.at(5))
        nc.gpsimd.memset(k.ctxT[DC:DC + 1, :], 1.0).then_inc(zero.sem, 1)
        e.wait_ge(zero.sem, zero.at(6))
        nc.gpsimd.affine_select(out=k.ident[:], in_=k.ident[:], compare_op=ALU.not_equal, fill=1.0, base=0,
                                pattern=[[-1, P]], channel_multiplier=1).then_inc(made.sem, 1)

    def pool_ready(e):
        e.wait_ge(x_in.sem, x_in.at(16))
        e.wait_ge(laid.sem, laid.at(TILES // 4))
        e.wait_ge(made.sem, made.at(1))
        e.wait_ge(tanh.sem, tanh.at(1))
        e.sem_inc(ready.sem, 1)

    def pe(e):
        e.wait_ge(made.sem, made.at(1))
        e.wait_ge(c_in.sem, c_in.at(16))
        for n in range(TILES // 4):
            e.wait_ge(laid.sem, laid.at(n - 7))
            for j in range(4):
                last = nc.tensor.transpose(k.ps[0:DC, n % 8, j * P:(j + 1) * P], ctx_tok[:, 4 * n + j, :], k.ident[:])
            last.then_inc(turned.sem, 1)

    def dve(e):
        k.ssm.dve_start(e)
        for n in range(TILES // 4):
            e.wait_ge(turned.sem, turned.at(n + 1))
            nc.vector.tensor_copy(k.ctxT[0:DC, n * BANK:(n + 1) * BANK], k.ps[0:DC, n % 8, :]).then_inc(laid.sem, 1)

    def act(e):
        k.ssm.act_start(e)
        e.wait_ge(g_in.sem, g_in.at(32))
        nc.scalar.activation(k.gates[:], graw[:], ACT.Tanh).then_inc(tanh.sem, 1)

    k.gates_ready = tanh
    k.x_ready = ready
    k.context_laid, k.context_tiles = laid, TILES // 4
    return dict(sp=sp, pool=pool, pe=pe, dve=dve, act=act), dict(pool=pool_ready)


def attention(k, io, name, heads, wq, wk, wv, wo, bo, gate, freed, start, rounds=None, ssm=None):
    nc, gates_ready = k.nc, k.gates_ready
    DH = 64
    SCALE = DH ** -0.5
    C = heads // 2
    INNER = heads * DH
    NG = heads // 4
    SB = heads * CTX // BANK
    sem = lambda n, total=TILES: k.sem(f"{name}_{n}", total)
    w_in, w_turned, w_laid = sem("w_loaded", None), sem("w_turned", 3 * C // 4), sem("w_laid", 3 * C // 4)
    w_made, w_copied, rows_zeroed = sem("w_folded", 2 * (heads // 4) + 1), sem("w_fold_copied", heads // 4), sem("rows_zeroed", 2)
    st_done, mv_done, ve_done, rs_done, xn_done = (sem("ln_" + n) for n in ("stats", "mv", "veps", "rstd", "xn"))
    xt_full, xt_laid = sem("xnT_full"), sem("xnT_laid")
    g_full, g_laid = sem("g_full", NG * TILES), sem("g_laid", NG * TILES)
    s_full, s_max, s_sub, s_exp = sem("scores"), sem("max"), sem("shifted"), sem("exp")
    s_sum, s_rec, s_prob = sem("sum"), sem("recip"), sem("probs")
    p_full, p_laid = sem("probsT_full"), sem("probsT_laid")
    v_full, v0_laid, v1_laid = sem("v_full", 2 * TILES), sem("v0_laid"), sem("v1_laid")
    y_full, x_done = sem("y_full"), sem("x_done")
    c_laid = sem("ctx_tile")

    cv = Carve(k.arena, start)
    w_qk = cv.f32(2, INNER)
    w_v = cv.f32(INNER)
    w_o = cv.f32(C, D)
    bo_row = cv.f32(D)
    w_T = cv.f32(3, C, P)
    mT = cv.f32(heads, D)
    mT_pair = mT.rearrange("p (c m) d -> p c m d", m=2)
    wvo = cv.f32(2, C, D)
    G = cv.f32(2, heads, P)
    VW = cv.f32(2, 2, C, D)
    PR = cv.f32(2, heads, CTX)
    PT = cv.f32(2, C, P)
    cg = cv.f32(2, P)
    mx = cv.f32(2, heads)
    sm = cv.f32(2, heads)
    rc = cv.f32(2, heads)
    ps = k.ps
    before = k.x_ready
    k.x_ready = x_done
    pairs = 3 * C

    def sp(e):
        if freed:
            e.wait_ge(freed.sem, freed.end)
        e.dma_start(w_qk[:, 0, :], io[wq]).then_inc(w_in.sem, 16)
        e.dma_start(w_qk[0:DC, 1, :], io[wk]).then_inc(w_in.sem, 16)
        e.dma_start(w_v[0:DC, :], io[wv]).then_inc(w_in.sem, 16)
        e.dma_start(w_o[:], io[wo].rearrange("(c p) d -> p c d", p=P)).then_inc(w_in.sem, 16)
        e.dma_start(bo_row[DC:DC + 1, :], io[bo].rearrange("(a d) -> a d", a=1)).then_inc(w_in.sem, 16)

    def fold_pe(e):
        e.wait_ge(k.context_laid.sem, k.context_laid.at(k.context_tiles))
        if freed:
            e.wait_ge(freed.sem, freed.end)
        e.wait_ge(w_in.sem, w_in.at(80))
        for n in range(pairs):
            which, c = divmod(n, C)
            if n % 4 == 0:
                e.wait_ge(w_laid.sem, w_laid.at(n // 4 - 3))
            if which == 0:
                last = nc.tensor.transpose(ps[:, n // 4 % 4, (n % 4) * P:(n % 4 + 1) * P], w_qk[:, 0, c * P:(c + 1) * P], k.ident[:])
            else:
                src = w_qk[0:DC, 1, c * P:(c + 1) * P] if which == 1 else w_v[0:DC, c * P:(c + 1) * P]
                last = nc.tensor.transpose(ps[:, n // 4 % 4, (n % 4) * P:(n % 4) * P + DC], src, k.ident[0:DC, 0:DC])
            if n % 4 == 3:
                last.then_inc(w_turned.sem, 1)
        e.wait_ge(w_laid.sem, w_laid.at(pairs // 4))
        for q in range(heads // 4):
            fold_v, q0 = divmod(q, C // 4)
            e.wait_ge(w_made.sem, w_made.at(2 * q - 2))
            for j in range(4):
                for m in range(2):
                    c, rows = 4 * q0 + j, slice(64 * m, 64 * m + 64)
                    last = nc.tensor.matmul(ps[0:DC, 4 + (2 * q + m) % 4, j * P:(j + 1) * P],
                                            w_T[rows, 2 if fold_v else 1, c, 0:DC],
                                            w_o[rows, c, :] if fold_v else w_T[rows, 0, c, :], start=True, stop=True)
            last.then_inc(w_copied.sem, 1)
        e.wait_ge(w_made.sem, w_made.at(2 * (heads // 4)))

    def fold_pool(e):
        if freed:
            e.wait_ge(freed.sem, freed.end)
        nc.gpsimd.memset(mT[DC:P, :, :], 0.0).then_inc(rows_zeroed.sem, 1)
        e.wait_ge(rows_zeroed.sem, rows_zeroed.at(1))
        nc.gpsimd.memset(wvo[DC:P, :, :, :], 0.0).then_inc(rows_zeroed.sem, 1)
        e.wait_ge(rows_zeroed.sem, rows_zeroed.at(2))

    def fold_act(e):
        for n in range(pairs // 4):
            e.wait_ge(w_turned.sem, w_turned.at(n + 1))
            c0 = 4 * n % C
            src = ps[:, n % 4, :].rearrange("p (c d) -> p c d", c=4)
            if 4 * n < C:
                nc.scalar.copy(w_T[:, 0, c0:c0 + 4, :], src).then_inc(w_laid.sem, 1)
            else:
                nc.scalar.copy(w_T[:, 4 * n // C, c0:c0 + 4, 0:DC], src[:, :, 0:DC]).then_inc(w_laid.sem, 1)
        e.wait_ge(gates_ready.sem, gates_ready.end)
        for q in range(heads // 4):
            fold_v, q0 = divmod(q, C // 4)
            e.wait_ge(w_copied.sem, w_copied.at(q + 1))
            for m in range(2):
                src = ps[0:DC, 4 + (2 * q + m) % 4, :].rearrange("p (c d) -> p c d", c=4)
                if fold_v:
                    nc.scalar.activation(wvo[0:DC, m, 4 * q0:4 * q0 + 4, :], src, ACT.Copy,
                                         scale=k.gates[0:DC, gate:gate + 1]).then_inc(w_made.sem, 1)
                else:
                    nc.scalar.copy(mT_pair[0:DC, 4 * q0:4 * q0 + 4, m, :], src).then_inc(w_made.sem, 1)
        e.wait_ge(rows_zeroed.sem, rows_zeroed.at(2))
        nc.scalar.activation(wvo[DC:DC + 1, 0, 0, :], bo_row[DC:DC + 1, :], ACT.Copy,
                             scale=k.gates[DC:DC + 1, gate:gate + 1]).then_inc(w_made.sem, 1)

    FOLDED = 2 * (heads // 4) + 1

    def ln_stats(e, t, s):
        nc.vector.bn_stats(k.stat[:, s, 0, :], k.x[:, t, :]).then_inc(st_done.sem, 1)

    def ln_aggr(e, t, s):
        nc.vector.bn_aggr(k.mv[:, s, 0, :], k.stat[:, s, 0, :]).then_inc(mv_done.sem, 1)

    def ln_apply(e, t, s):
        e.wait_ge(rs_done.sem, rs_done.at(t + 1))
        nc.vector.tensor_scalar(k.xn[:, s, 0, :], k.x[:, t, :], k.mv[:, s, 0, 0:1], k.rstd[:, s, 0:1],
                                ALU.subtract, ALU.mult).then_inc(xn_done.sem, 1)

    def ln_pool(e, t, s):
        e.wait_ge(mv_done.sem, mv_done.at(t + 1))
        nc.gpsimd.tensor_tensor(k.veps[:, s, 0:1], k.mv[:, s, 0, 1:2], k.eps[:, 0:1], ALU.add).then_inc(ve_done.sem, 1)
        e.wait_ge(ve_done.sem, ve_done.at(t + 1))
        nc.gpsimd.tensor_tensor(k.rstd[:, s, 0:1], k.veps[:, s, 0:1], k.half[:, 0:1], ALU.pow).then_inc(rs_done.sem, 1)

    def more(t, ahead):
        return not isinstance(t, int) or t + ahead < TILES

    def g_product(e, t, s, n):
        if n == 0:
            e.wait_ge(c_laid.sem, c_laid.at(t + 1))
        e.wait_ge(g_laid.sem, g_laid.at(NG * t + n - 1))
        for j in range(4):
            last = nc.tensor.matmul(ps[:, n % 2, j * P:(j + 1) * P], mT[:, 4 * n + j, :], cg[:, s, :], start=True, stop=True)
        last.then_inc(g_full.sem, 1)

    def xn_turn(e, t, s):
        e.wait_ge(xn_done.sem, xn_done.at(t + 1))
        nc.tensor.transpose(ps[:, 3, 0:P], k.xn[:, s, 0, :], k.ident[:]).then_inc(xt_full.sem, 1)

    def v_product(e, t, s, b):
        if SB == 2:
            laid, count = (v1_laid, t) if b == 0 else (v0_laid, t + 1)
        else:
            laid, count = (v0_laid, t) if b == 0 else (v1_laid, t)
        e.wait_ge(laid.sem, laid.at(count))
        for n in range(C * D // BANK):
            for m in range(2):
                bank = 6 + n if SB == 2 else 6 + b
                last = nc.tensor.matmul(ps[64 * m:64 * m + 64, bank, :], cg[:, s, b * CTX:(b + 1) * CTX],
                                        wvo[:, m, 4 * n:4 * n + 4, :], start=True, stop=True)
        last.then_inc(v_full.sem, 1)

    def pe_y(e, t, s):
        e.wait_ge(p_laid.sem, p_laid.at(t + 1))
        e.wait_ge(v0_laid.sem, v0_laid.at(t + 1))
        e.wait_ge(v1_laid.sem, v1_laid.at(t + 1))
        if rounds and more(t, 1):
            rounds.pe_total(e, t)
        for c in range(C):
            for b in range(2):
                last = nc.tensor.matmul(ps[64 * b:64 * b + 64, 2, 0:D], PT[:, s, c, 64 * b:64 * b + 64], VW[:, s, b, c, :],
                                        start=(c == 0), stop=(c == C - 1))
        last.then_inc(y_full.sem, 1)

    def pe_step(e, t, s):
        o = 1 - s
        e.wait_ge(g_laid.sem, g_laid.at(NG * (t + 1)))
        e.wait_ge(xt_laid.sem, xt_laid.at(t + 1))
        e.wait_ge(s_sub.sem, s_sub.at(t))
        for n in range(SB):
            for b in range(2):
                last = nc.tensor.matmul(ps[64 * b:64 * b + 64, 4 + n, :], k.xnT[:, s, 64 * b:64 * b + 64],
                                        G[:, s, 8 * n:8 * n + 8, b * CTX:(b + 1) * CTX], start=True, stop=True)
        last.then_inc(s_full.sem, 1)
        v_product(e, t, s, 0)
        if more(t, 1):
            for n in range(NG // 2):
                g_product(e, t + 1, o, n)
        v_product(e, t, s, 1)
        if not (isinstance(t, int) and t == 0):
            pe_y(e, t - 1, o)
        if more(t, 1):
            xn_turn(e, t + 1, o)
        if more(t, 1):
            for n in range(NG // 2, NG):
                g_product(e, t + 1, o, n)
        e.wait_ge(s_prob.sem, s_prob.at(t + 1))
        e.wait_ge(x_done.sem, x_done.at(t))
        if rounds:
            e.wait_ge(rounds.read.sem, rounds.read.at(t))
        if more(t, 1):
            e.wait_ge(xt_laid.sem, xt_laid.at(t + 2))
        for c in range(C):
            last = nc.tensor.transpose(ps[:, 2 + c // 4, c % 4 * P:(c % 4 + 1) * P], PR[:, s, 2 * c:2 * c + 2, :], k.ident[:])
        last.then_inc(p_full.sem, 1)

    def pe(e):
        e.wait_ge(before.sem, before.end)
        e.wait_ge(w_made.sem, w_made.at(FOLDED))
        for n in range(NG):
            g_product(e, 0, 0, n)
        xn_turn(e, 0, 0)
        pipelined_tiles(e, lambda t, s: pe_step(e, t, s))
        pe_y(e, TILES - 1, 1)

    def g_copy(e, t, s, n):
        e.wait_ge(g_full.sem, g_full.at(NG * t + n + 1))
        nc.scalar.copy(G[:, s, 4 * n:4 * n + 4, :], ps[:, n % 2, :].rearrange("p (h j) -> p h j", h=4)).then_inc(g_laid.sem, 1)

    def xn_copy(e, t, s):
        e.wait_ge(xt_full.sem, xt_full.at(t + 1))
        nc.scalar.copy(k.xnT[:, s, 0:P], ps[:, 3, 0:P]).then_inc(xt_laid.sem, 1)

    def act_step(e, t, s):
        o = 1 - s
        e.wait_ge(s_sub.sem, s_sub.at(t + 1))
        nc.scalar.activation(PR[:, s, :, :], PR[:, s, :, :], ACT.Exp, scale=SCALE).then_inc(s_exp.sem, 1)
        if more(t, 1):
            for n in range(NG // 2):
                g_copy(e, t + 1, o, n)
        e.wait_ge(v_full.sem, v_full.at(2 * t + 2))
        src = ps[:, 6:8, :] if SB == 2 else ps[:, 7, :]
        dst = VW[:, s, 1, :, :].rearrange("p c d -> p (c d)")
        if SB == 2:
            dst = dst.rearrange("p (n w) -> p n w", n=2)
        nc.scalar.copy(dst, src).then_inc(v1_laid.sem, 1)
        if more(t, 1):
            xn_copy(e, t + 1, o)
            for n in range(NG // 2, NG):
                g_copy(e, t + 1, o, n)
        e.wait_ge(p_full.sem, p_full.at(t + 1))
        dst = PT[:, s, :, :].rearrange("p c q -> p (c q)")
        if SB == 2:
            nc.scalar.copy(dst.rearrange("p (n w) -> p n w", n=2), ps[:, 2:4, :]).then_inc(p_laid.sem, 1)
        else:
            nc.scalar.copy(dst, ps[:, 2, :]).then_inc(p_laid.sem, 1)

    def act(e):
        e.wait_ge(before.sem, before.end)
        for n in range(NG):
            g_copy(e, 0, 0, n)
        xn_copy(e, 0, 0)
        pipelined_tiles(e, lambda t, s: act_step(e, t, s))

    def dve_add(e, t):
        e.wait_ge(y_full.sem, y_full.at(t + 1))
        nc.vector.tensor_tensor(k.x[:, t, :], ps[:, 2, 0:D], k.x[:, t, :], ALU.add).then_inc(x_done.sem, 1)

    def dve_step(e, t, s):
        S = ps[:, 4:4 + SB, :].rearrange("p n (h j) -> p (n h) j", j=CTX)
        if more(t, 2):
            ln_stats(e, t + 2, s)
        e.wait_ge(s_full.sem, s_full.at(t + 1))
        nc.vector.tensor_reduce(mx[:, s, :], S, AX.X, ALU.max).then_inc(s_max.sem, 1)
        e.wait_ge(s_max.sem, s_max.at(t + 1))
        nc.vector.tensor_tensor(PR[:, s, :, :], S, mx[:, s, :].unsqueeze(2).to_broadcast([P, heads, CTX]), ALU.subtract).then_inc(s_sub.sem, 1)
        if more(t, 2):
            ln_aggr(e, t + 2, s)
        e.wait_ge(v_full.sem, v_full.at(2 * t + 1))
        src = ps[:, 6:8, :] if SB == 2 else ps[:, 6, :]
        dst = VW[:, s, 0, :, :].rearrange("p c d -> p (c d)")
        if SB == 2:
            dst = dst.rearrange("p (n w) -> p n w", n=2)
        nc.vector.tensor_copy(dst, src).then_inc(v0_laid.sem, 1)
        e.wait_ge(s_exp.sem, s_exp.at(t + 1))
        nc.vector.tensor_reduce(sm[:, s, :], PR[:, s, :, :], AX.X, ALU.add).then_inc(s_sum.sem, 1)
        if more(t, 2):
            ln_apply(e, t + 2, s)
        e.wait_ge(s_sum.sem, s_sum.at(t + 1))
        nc.vector.reciprocal(rc[:, s, :], sm[:, s, :]).then_inc(s_rec.sem, 1)
        if not (isinstance(t, int) and t == 0):
            dve_add(e, t - 1)
        if rounds:
            rounds.dve_round(e, t)

    def dve(e):
        if rounds:
            rounds.dve_start(e)
        e.wait_ge(before.sem, before.end)
        for t in range(2):
            ln_stats(e, t, t)
        e.wait_ge(st_done.sem, st_done.at(2))
        for t in range(2):
            ln_aggr(e, t, t)
        for t in range(2):
            ln_apply(e, t, t)
        pipelined_tiles(e, lambda t, s: dve_step(e, t, s))
        dve_add(e, TILES - 1)

    def ctx_copy(e, t, s):
        nc.gpsimd.tensor_copy(cg[:, s, :], k.ctxT[:, bass.ts(t, P)]).then_inc(c_laid.sem, 1)

    def pool_step(e, t, s):
        if more(t, 2):
            ln_pool(e, t + 2, s)
        e.wait_ge(s_rec.sem, s_rec.at(t + 1))
        nc.gpsimd.tensor_tensor(PR[:, s, :, :], PR[:, s, :, :], rc[:, s, :].unsqueeze(2).to_broadcast([P, heads, CTX]),
                                ALU.mult).then_inc(s_prob.sem, 1)
        if more(t, 2):
            e.wait_ge(v_full.sem, v_full.at(2 * t + 2))
            ctx_copy(e, t + 2, s)
        if ssm:
            ssm.pool_pair(e, t)

    def pool(e):
        e.wait_ge(before.sem, before.end)
        for t in range(2):
            ctx_copy(e, t, t)
        for t in range(2):
            ln_pool(e, t, t)
        pipelined_tiles(e, lambda t, s: pool_step(e, t, s))

    return dict(pe=pe, act=act, dve=dve, pool=pool), dict(sp=sp, pe=fold_pe, act=fold_act, pool=fold_pool)


class GroupNorm:

    def __init__(self, k, name, slot, src, dst):
        self.k, self.s, self.src, self.dst = k, slot, src, dst
        self.stats, self.mv, self.ve, self.rs, self.out = (k.sem(f"{name}_{n}", GROUPS) for n in ("stats", "mv", "veps", "rstd", "normed"))

    def dve_stats(self, g):
        k = self.k
        for j in range(GT):
            last = k.nc.vector.bn_stats(k.stat[:, self.s, j, :], self.src(g, j))
        last.then_inc(self.stats.sem, 1)

    def dve_aggregate(self, e, n, covered):
        k = self.k
        if not covered:
            e.wait_ge(self.stats.sem, self.stats.at(n + 1))
        for j in range(GT):
            last = k.nc.vector.bn_aggr(k.mv[:, self.s, j, :], k.stat[:, self.s, j, :])
        last.then_inc(self.mv.sem, 1)

    def pool_rstd(self, e, n):
        k = self.k
        e.wait_ge(self.mv.sem, self.mv.at(n + 1))
        k.nc.gpsimd.tensor_tensor(k.veps[:, self.s, :], k.mv[:, self.s, :, 1], k.eps[:], ALU.add).then_inc(self.ve.sem, 1)
        e.wait_ge(self.ve.sem, self.ve.at(n + 1))
        k.nc.gpsimd.tensor_tensor(k.rstd[:, self.s, :], k.veps[:, self.s, :], k.half[:], ALU.pow).then_inc(self.rs.sem, 1)

    def dve_apply(self, e, g, n):
        k = self.k
        e.wait_ge(self.rs.sem, self.rs.at(n + 1))
        for j in range(GT):
            last = k.nc.vector.tensor_scalar(self.dst(g, j), self.src(g, j), k.mv[:, self.s, j, 0:1], k.rstd[:, self.s, j:j + 1],
                                             ALU.subtract, ALU.mult)
        last.then_inc(self.out.sem, 1)


def experts(k, io, name, top1, gate, loads, freed, space, start=0, prepare=None):
    nc = k.nc
    E, C = (8, 1) if top1 else (2, 4)
    U = E * C
    NR = 8
    GELU = ACT.Gelu if top1 else ACT.Gelu_apprx_tanh
    sem = lambda n, total=GROUPS: k.sem(f"{name}_{n}", total)
    w_in, made, xt_full, xt_laid = sem("w_loaded", None), sem("constants", 1), sem("xT_full"), sem("xT_laid")
    h_full, h_laid = sem("h_full", U * GROUPS), sem("h_laid", U * GROUPS)
    o_full, o_used = sem("o_full", E * GROUPS), sem("o_used", E * GROUPS)
    l_full, l_laid, lt_full = sem("logits"), sem("logits_laid"), sem("logitsT")
    r_max, r_shift, r_exp, r_sum, r_w = (sem(n) for n in ("r_max", "r_shift", "r_exp", "r_sum", "r_weights"))
    r_step = sem("r_step", (5 if top1 else 3) * GROUPS)
    wt_full, wt_laid, b_full, x_done = sem("weightsT"), sem("weightsT_laid"), sem("bias_full"), sem("x_done")
    if not top1:
        r2_full, r2_laid = sem("router_in_full"), sem("router_in_laid")

    cv = Carve(space, start)
    w1 = cv.f32(E, C * P)
    w2 = cv.f32(E, C, D)
    b1 = cv.f32(E, C)
    b2 = cv.f32(D)
    wr = cv.f32(NR)
    br = cv.f32(1)
    hT = cv.f32(2, GT * P)
    lT = cv.f32(GT * P)
    wT = cv.f32(GT * P)
    rank = cv.f32(NR)
    m4, s4, r4 = cv.f32(GT), cv.f32(GT), cv.f32(GT)
    ex, eq, rk, oh = (cv.f32(GT, NR) for _ in range(4))
    rm = cv.f32(GT)
    wgt = cv.f32(GT, E)
    gam, bet = cv.f32(1), cv.f32(1)
    ln2T = cv.f32(GT * P)
    xnT = k.xnT[:, 0, :]
    ps = k.ps
    before = k.x_ready
    k.x_ready = x_done
    ln = GroupNorm(k, name + "_ln", 0, lambda g, j: k.x[:, 4 * g + j, :], lambda g, j: k.xn[:, 0, j, :])
    ln2 = None if top1 else GroupNorm(k, name + "_ln2", 1, lambda g, j: k.xn[:, 0, j, :], lambda g, j: k.xn[:, 1, j, :])
    v = Parts()
    v.w1, v.w2, v.b1, v.b2, v.wr, v.br, v.gam, v.bet, v.cv, v.w_in, v.before = w1, w2, b1, b2, wr, br, gam, bet, cv, w_in, before
    n_loads = v.loads = loads(k, io, v)
    prep = prepare(k, io, v) if prepare else {}

    def sp(e):
        e.wait_ge(freed.sem, freed.end)
        for dst, src in n_loads:
            with nc.allow_non_contiguous_dma(reason="biases are small"):
                e.dma_start(dst, src).then_inc(w_in.sem, 16)

    READY = 16 * len(n_loads)

    def turn_x(e, n):
        e.wait_ge(ln.out.sem, ln.out.at(n + 1))
        e.wait_ge(xt_laid.sem, xt_laid.at(n))
        for j in range(GT):
            last = nc.tensor.transpose(ps[:, 5, j * P:(j + 1) * P], k.xn[:, 0, j, :], k.ident[:])
        last.then_inc(xt_full.sem, 1)

    def turn_router_in(e, n):
        e.wait_ge(ln2.out.sem, ln2.out.at(n + 1))
        e.wait_ge(r2_laid.sem, r2_laid.at(n))
        for j in range(GT):
            last = nc.tensor.transpose(ps[:, 2, j * P:(j + 1) * P], k.xn[:, 1, j, :], k.ident[:])
        last.then_inc(r2_full.sem, 1)

    def logits(e, n):
        if top1:
            e.wait_ge(xt_laid.sem, xt_laid.at(n + 1))
        else:
            e.wait_ge(r2_laid.sem, r2_laid.at(n + 1))
        e.wait_ge(r_sum.sem, r_sum.at(n))
        nc.tensor.matmul(ps[0:NR, 6, :], wr[:], xnT if top1 else ln2T[:], start=True, stop=True).then_inc(l_full.sem, 1)

    def turn_logits(e, n):
        for j in range(GT):
            last = nc.tensor.transpose(ps[:, 6, j * NR:(j + 1) * NR], lT[0:NR, j * P:(j + 1) * P], k.ident[0:NR, 0:NR])
        last.then_inc(lt_full.sem, 1)

    def hidden(e, g, u):
        if u == 0:
            e.wait_ge(xt_laid.sem, xt_laid.at(g + 1))
        x, c = divmod(u, C)
        nc.tensor.matmul(ps[:, u % 2, :], w1[:, x, c * P:(c + 1) * P], xnT, start=True, stop=True).then_inc(h_full.sem, 1)

    def outputs(e, g, u):
        x, c = divmod(u, C)
        e.wait_ge(h_laid.sem, h_laid.at(U * g + u + 1))
        if c == 0:
            e.wait_ge(o_used.sem, o_used.at(E * g + max(x - 1, 0)))
        for j in range(GT):
            last = nc.tensor.matmul(ps[:, 3 + x % 2, j * P:(j + 1) * P], hT[:, u % 2, j * P:(j + 1) * P], w2[:, x, c, :],
                                    start=(c == 0 and j == 0), stop=(c == C - 1 and j == GT - 1), skip_group_check=True)
        if c == C - 1:
            last.then_inc(o_full.sem, 1)

    def bias_term(e, g):
        e.wait_ge(r_w.sem, r_w.at(g + 1))
        e.wait_ge(x_done.sem, x_done.at(g))
        for j in range(GT):
            last = nc.tensor.transpose(ps[0:E, 7, j * P:(j + 1) * P], wgt[:, j, :], k.ident[:])
        last.then_inc(wt_full.sem, 1)

    def bias_term2(e, g):
        e.wait_ge(wt_laid.sem, wt_laid.at(g + 1))
        for j in range(GT):
            last = nc.tensor.matmul(ps[:, 7, j * P:(j + 1) * P], wT[0:E, j * P:(j + 1) * P], b2[0:E, :], start=True, stop=True)
        last.then_inc(b_full.sem, 1)

    def pe(e):
        if "pe" in prep:
            prep["pe"](e)
        e.wait_ge(w_in.sem, w_in.at(READY))
        turn_x(e, 0)
        if not top1:
            turn_router_in(e, 0)
        logits(e, 0)

        def body(g, more):
            hidden(e, g, 0)
            e.wait_ge(l_laid.sem, l_laid.at(g + 1))
            hidden(e, g, 1)
            turn_logits(e, g)
            for u in range(1, U):
                if u > 1:
                    hidden(e, g, u)
                if u == U - 1 and more:
                    turn_x(e, g + 1)
                if u == 4:
                    bias_term(e, g)
                outputs(e, g, u - 1)
                if u == 5:
                    bias_term2(e, g)
            if more and top1:
                logits(e, g + 1)
            outputs(e, g, U - 1)
            if more and not top1:
                turn_router_in(e, g + 1)
                logits(e, g + 1)

        pipelined_groups(e, body)

    def act(e):
        if "act" in prep:
            prep["act"](e)
        e.wait_ge(w_in.sem, w_in.at(READY))

        def copy_x(n):
            e.wait_ge(xt_full.sem, xt_full.at(n + 1))
            nc.scalar.copy(xnT, ps[:, 5, :]).then_inc(xt_laid.sem, 1)

        def copy_router_in(n):
            e.wait_ge(r2_full.sem, r2_full.at(n + 1))
            nc.scalar.activation(ln2T[:], ps[:, 2, :], ACT.Identity, bias=bet[:], scale=gam[:]).then_inc(r2_laid.sem, 1)

        def copy_logits(n):
            e.wait_ge(l_full.sem, l_full.at(n + 1))
            nc.scalar.activation(lT[0:NR, :], ps[0:NR, 6, :], ACT.Identity, bias=br[0:NR, :]).then_inc(l_laid.sem, 1)

        copy_x(0)
        if not top1:
            copy_router_in(0)
        copy_logits(0)

        def body(g, more):
            for u in range(U):
                if u == 2:
                    e.wait_ge(r_shift.sem, r_shift.at(g + 1))
                    nc.scalar.activation(ex[:], ex[:], ACT.Exp).then_inc(r_exp.sem, 1)
                if u == 5:
                    e.wait_ge(wt_full.sem, wt_full.at(g + 1))
                    nc.scalar.copy(wT[0:E, :], ps[0:E, 7, :]).then_inc(wt_laid.sem, 1)
                x, c = divmod(u, C)
                e.wait_ge(h_full.sem, h_full.at(U * g + u + 1))
                nc.scalar.activation(hT[:, u % 2, :], ps[:, u % 2, :], GELU, bias=b1[:, x, c:c + 1]).then_inc(h_laid.sem, 1)
            if more:
                copy_x(g + 1)
                if not top1:
                    copy_router_in(g + 1)
                copy_logits(g + 1)

        pipelined_groups(e, body)

    def dve(e):
        if "dve" in prep:
            prep["dve"](e)
        e.wait_ge(before.sem, before.end)
        e.wait_ge(w_in.sem, w_in.at(READY))
        e.wait_ge(made.sem, made.at(1))
        steps = 5 if top1 else 3

        def spread(v):
            return v.unsqueeze(2).to_broadcast([P, GT, NR])

        def router(g):
            L = ps[:, 6, 0:GT * NR].rearrange("p (j r) -> p j r", r=NR)
            e.wait_ge(lt_full.sem, lt_full.at(g + 1))
            nc.vector.tensor_reduce(m4[:], L, AX.X, ALU.max).then_inc(r_max.sem, 1)
            e.wait_ge(r_max.sem, r_max.at(g + 1))
            nc.vector.tensor_tensor(ex[:], L, spread(m4), ALU.subtract).then_inc(r_shift.sem, 1)
            if top1:
                nc.vector.tensor_tensor(eq[:], L, spread(m4), ALU.is_equal).then_inc(r_step.sem, 1)
                e.wait_ge(r_step.sem, r_step.at(steps * g + 1))
                nc.vector.tensor_tensor(rk[:], eq[:], rank.unsqueeze(1).to_broadcast([P, GT, NR]), ALU.mult).then_inc(r_step.sem, 1)
                e.wait_ge(r_step.sem, r_step.at(steps * g + 2))
                nc.vector.tensor_reduce(rm[:], rk[:], AX.X, ALU.max).then_inc(r_step.sem, 1)
                e.wait_ge(r_step.sem, r_step.at(steps * g + 3))
                nc.vector.tensor_tensor(oh[:], rk[:], spread(rm), ALU.is_equal)
            e.wait_ge(r_exp.sem, r_exp.at(g + 1))
            nc.vector.tensor_reduce(s4[:], ex[:], AX.X, ALU.add).then_inc(r_sum.sem, 1)
            if not top1:
                nc.vector.tensor_reduce(m4[:], ex[:, :, 1:NR], AX.X, ALU.add)
            e.wait_ge(r_sum.sem, r_sum.at(g + 1))
            nc.vector.reciprocal(r4[:], s4[:]).then_inc(r_step.sem, 1)
            e.wait_ge(r_step.sem, r_step.at(steps * g + steps - 1 if top1 else steps * g + 1))
            nc.vector.tensor_scalar(s4[:], r4[:], k.gates[:, gate:gate + 1], None, ALU.mult).then_inc(r_step.sem, 1)
            e.wait_ge(r_step.sem, r_step.at(steps * g + steps if top1 else steps * g + 2))
            if top1:
                nc.vector.tensor_tensor(wgt[:], oh[:], spread(s4), ALU.mult).then_inc(r_w.sem, 1)
            else:
                nc.vector.tensor_tensor(wgt[:, :, 0], ex[:, :, 0], s4[:], ALU.mult).then_inc(r_step.sem, 1)
                nc.vector.tensor_tensor(wgt[:, :, 1], m4[:], s4[:], ALU.mult).then_inc(r_w.sem, 1)

        def add_expert(g, x):
            e.wait_ge(o_full.sem, o_full.at(E * g + x + 1))
            if x:
                e.wait_ge(o_used.sem, o_used.at(E * g + x))
            else:
                e.wait_ge(r_w.sem, r_w.at(g + 1))
            for j in range(GT):
                last = nc.vector.scalar_tensor_tensor(k.x[:, 4 * g + j, :], ps[:, 3 + x % 2, j * P:(j + 1) * P], wgt[:, j, x:x + 1],
                                                      k.x[:, 4 * g + j, :], ALU.mult, ALU.add)
            last.then_inc(o_used.sem, 1)

        ln.dve_stats(0)
        ln.dve_aggregate(e, 0, False)
        ln.dve_apply(e, 0, 0)
        if not top1:
            e.wait_ge(ln.out.sem, ln.out.at(1))
            ln2.dve_stats(0)
            ln2.dve_aggregate(e, 0, False)
            ln2.dve_apply(e, 0, 0)

        def body(g, more):
            if more:
                ln.dve_stats(g + 1)
            router(g)
            if more:
                ln.dve_aggregate(e, g + 1, True)
                if not top1:
                    ln.dve_apply(e, g + 1, g + 1)
                    e.wait_ge(ln.out.sem, ln.out.at(g + 2))
                    ln2.dve_stats(g + 1)
                    e.wait_ge(ln2.stats.sem, ln2.stats.at(g + 2))
            for x in range(E):
                add_expert(g, x)
                if more and x == 0:
                    if top1:
                        ln.dve_apply(e, g + 1, g + 1)
                    else:
                        ln2.dve_aggregate(e, g + 1, True)
                        ln2.dve_apply(e, g + 1, g + 1)
            e.wait_ge(b_full.sem, b_full.at(g + 1))
            e.wait_ge(o_used.sem, o_used.at(E * (g + 1)))
            nc.vector.tensor_tensor(k.x[:, bass.ts(g, GT), :], ps[:, 7, :].rearrange("p (j d) -> p j d", j=GT),
                                    k.x[:, bass.ts(g, GT), :], ALU.add).then_inc(x_done.sem, 1)

        pipelined_groups(e, body)

    def pool(e):
        if "pool" in prep:
            prep["pool"](e)
        e.wait_ge(before.sem, before.end)
        for r in range(NR):
            ins = nc.gpsimd.memset(rank[:, r:r + 1], float(NR - r))
        ins.then_inc(made.sem, 1)
        e.wait_ge(made.sem, made.at(1))
        ln.pool_rstd(e, 0)
        if not top1:
            ln2.pool_rstd(e, 0)

        def body(g, more):
            if more:
                ln.pool_rstd(e, g + 1)
                if not top1:
                    ln2.pool_rstd(e, g + 1)

        pipelined_groups(e, body)

    return dict(sp=sp, pe=pe, act=act, dve=dve, pool=pool)


def ffn0(k, io, freed):
    def loads(k, io, v):
        return [
            (v.w1, io["L0_ffn_W1"].rearrange("e d f -> d e f")),
            (v.w2[:, :, 0, :], io["L0_ffn_W2"].rearrange("e f d -> f e d")),
            (v.b1[:, :, 0], io["L0_ffn_b1"].rearrange("e f -> f e")),
            (v.b2[0:8, :], io["L0_ffn_b2"]),
            (v.wr, io["L0_ffn_Wg"]),
            (v.br[0:8, :], io["L0_ffn_bg"].rearrange("(n a) -> n a", a=1)),
        ]
    return experts(k, io, "f0", True, 4, loads, freed, k.arena, 25000)


class StateSpaceKernel:

    N, L = 64, SEQ
    PAIRS = L // 2

    def __init__(self, k, io):
        self.k, self.io = k, io
        sem = lambda n: k.sem("ssm_" + n)
        self.w_in, self.scalar_step, self.step, self.started, self.paired, self.summed = (
            sem(n) for n in ("loaded", "scalar_step", "vector_step", "started", "pairs", "kernel_made"))
        self.stored, self.toep_in = sem("stored"), sem("toeplitz_in")
        self.Z = k.toep[:].rearrange("p a b -> p (a b)").rearrange("p (l c n) -> p l c n", l=self.L, c=2)
        self.padded = k.sb("ssm_padded_kernel", [P, 2 * self.L])
        self.z2 = k.sb("ssm_z_squared", [P, 3, self.N])
        self.t1 = k.sb("ssm_product", [P, 2, 2, self.N])
        self.t2 = k.sb("ssm_cross_product", [P, 2, 2, self.N])
        self.scratch = k.nc.dram_tensor("ssm_toeplitz_scratch", (SEQ, D, SEQ), F32).ap()
        cv = Carve(k.arena, 27200)
        self.a_re, self.a_im, self.c_re, self.c_im = (cv.f32(self.N) for _ in range(4))
        self.ldt, self.dt, self.skip = cv.f32(1), cv.f32(1), cv.f32(1)
        self.ang, self.turns, self.red, self.half, self.er, self.sn, self.sh = (cv.f32(self.N) for _ in range(7))
        self.u, self.v, self.p, self.q, self.den, self.zr, self.zi = (cv.f32(self.N) for _ in range(7))

    def sp_load(self, e):
        io = self.io
        for dst, name in ((self.a_re, "A_re"), (self.a_im, "A_im"), (self.c_re, "C_re"), (self.c_im, "C_im")):
            e.dma_start(dst, io["L1_xattn_" + name]).then_inc(self.w_in.sem, 16)
        for dst, name in ((self.ldt, "log_dt"), (self.skip, "D_skip")):
            e.dma_start(dst, io["L1_xattn_" + name].rearrange("(p a) -> p a", a=1)).then_inc(self.w_in.sem, 16)

    def act_start(self, e):
        S = self.k.nc.scalar
        e.wait_ge(self.w_in.sem, 96)
        S.activation(self.dt, self.ldt, ACT.Exp).then_inc(self.scalar_step.sem, 1)
        e.wait_ge(self.scalar_step.sem, 1)
        S.activation(self.er, self.a_re, ACT.Exp, scale=self.dt).then_inc(self.scalar_step.sem, 1)
        e.wait_ge(self.step.sem, 7)
        S.activation(self.sn, self.red, ACT.Sin)
        S.activation(self.sh, self.red, ACT.Sin, scale=0.5).then_inc(self.scalar_step.sem, 1)

    def dve_start(self, e):
        V = self.k.nc.vector
        TWO_PI = 6.283185307179586
        C1 = 6.28125
        C2 = 0.0019350051879882812
        C3 = TWO_PI - C1 - C2
        PI_IN = 3.1415925
        n = 0

        def then(ins):
            nonlocal n
            n += 1
            ins.then_inc(self.step.sem, 1)
            e.wait_ge(self.step.sem, n)

        a_re, a_im, c_re, c_im, zr, zi = self.a_re, self.a_im, self.c_re, self.c_im, self.zr, self.zi
        u, v, p, q, den, Z, z2 = self.u, self.v, self.p, self.q, self.den, self.Z, self.z2
        e.wait_ge(self.scalar_step.sem, 2)
        then(V.tensor_scalar(self.ang, a_im, self.dt, None, ALU.mult))
        then(V.tensor_scalar(self.turns, self.ang, 1.0 / TWO_PI, ROUND, ALU.mult, ALU.add))
        then(V.tensor_scalar(self.turns, self.turns, -ROUND, None, ALU.add))
        then(V.scalar_tensor_tensor(self.red, self.turns, -C1, self.ang, ALU.mult, ALU.add))
        then(V.scalar_tensor_tensor(self.ang, self.turns, -C2, self.red, ALU.mult, ALU.add))
        then(V.scalar_tensor_tensor(self.half, self.turns, -C3, self.ang, ALU.mult, ALU.add))
        then(V.tensor_scalar(self.red, self.half, PI_IN, -PI_IN, ALU.min, ALU.max))
        V.tensor_tensor(den, a_re, a_re, ALU.mult)
        then(V.tensor_tensor(u, a_im, a_im, ALU.mult))
        then(V.tensor_tensor(den, den, u, ALU.add))
        then(V.reciprocal(u, den))
        then(V.tensor_scalar(den, u, 2.0, None, ALU.mult))
        e.wait_ge(self.scalar_step.sem, 3)
        V.tensor_tensor(zi, self.er, self.sn, ALU.mult)
        then(V.tensor_tensor(u, self.sh, self.sh, ALU.mult))
        then(V.tensor_scalar(u, u, -2.0, 1.0, ALU.mult, ALU.add))
        then(V.tensor_tensor(zr, self.er, u, ALU.mult))
        then(V.tensor_scalar(v, zr, -1.0, None, ALU.add))
        V.tensor_tensor(p, c_re, v, ALU.mult)
        V.tensor_tensor(u, c_im, zi, ALU.mult)
        V.tensor_tensor(q, c_re, zi, ALU.mult)
        then(V.tensor_tensor(self.half, c_im, v, ALU.mult))
        V.tensor_tensor(p, p, u, ALU.subtract)
        then(V.tensor_tensor(q, q, self.half, ALU.add))
        then(V.tensor_tensor(u, p, a_re, ALU.mult))
        then(V.tensor_tensor(v, q, a_im, ALU.mult))
        then(V.tensor_tensor(u, u, v, ALU.add))
        then(V.tensor_tensor(Z[:, 0, 0, :], u, den, ALU.mult))
        then(V.tensor_tensor(u, q, a_re, ALU.mult))
        then(V.tensor_tensor(v, p, a_im, ALU.mult))
        then(V.tensor_tensor(u, u, v, ALU.subtract))
        then(V.tensor_tensor(Z[:, 0, 1, :], u, den, ALU.mult))
        then(V.tensor_tensor(u, Z[:, 0, 0, :], zr, ALU.mult))
        then(V.tensor_tensor(v, Z[:, 0, 1, :], zi, ALU.mult))
        then(V.tensor_tensor(Z[:, 1, 0, :], u, v, ALU.subtract))
        then(V.tensor_tensor(u, Z[:, 0, 0, :], zi, ALU.mult))
        then(V.tensor_tensor(v, Z[:, 0, 1, :], zr, ALU.mult))
        then(V.tensor_tensor(Z[:, 1, 1, :], u, v, ALU.add))
        then(V.tensor_tensor(u, zr, zr, ALU.mult))
        then(V.tensor_tensor(v, zi, zi, ALU.mult))
        then(V.tensor_tensor(z2[:, 0, :], u, v, ALU.subtract))
        then(V.tensor_tensor(u, zr, zi, ALU.mult))
        V.tensor_scalar(z2[:, 1, :], u, 2.0, None, ALU.mult)
        V.tensor_scalar(z2[:, 2, :], u, -2.0, None, ALU.mult)
        V.memset(self.padded[:, 0:self.L - 1], 0.0)
        V.memset(self.padded[:, 2 * self.L - 1:2 * self.L], 0.0)
        V.tensor_copy(self.padded[:, self.L - 1:self.L], self.skip).then_inc(self.started.sem, 1)

    def pool_pair(self, e, t):
        if isinstance(t, int) and t == 0:
            return
        G, before, z2 = self.k.nc.gpsimd, self.Z[:, bass.ts(t - 1, 2), :, :], self.z2
        four = lambda v: v.unsqueeze(1).to_broadcast([P, 4, self.N])
        two = lambda v: v.unsqueeze(1).to_broadcast([P, 2, self.N])
        e.wait_ge(self.started.sem, 1)
        if not isinstance(t, int) or t > 1:
            e.wait_ge(self.paired.sem, 2 * (t - 1))
            e.nop(nofuse=True)
        G.tensor_tensor(self.t1[:].rearrange("p a c n -> p (a c) n"), before.rearrange("p a c n -> p (a c) n"), four(z2[:, 0, :]), ALU.mult)
        G.tensor_tensor(self.t2[:, :, 0, :], before[:, :, 1, :], two(z2[:, 2, :]), ALU.mult)
        G.tensor_tensor(self.t2[:, :, 1, :], before[:, :, 0, :], two(z2[:, 1, :]), ALU.mult).then_inc(self.paired.sem, 1)
        e.wait_ge(self.paired.sem, 2 * t - 1)
        e.nop(nofuse=True)
        G.tensor_tensor(self.Z[:, bass.ts(t, 2), :, :], self.t1[:], self.t2[:], ALU.add).then_inc(self.paired.sem, 1)

    def dve_sum(self, e):
        V = self.k.nc.vector
        e.wait_ge(self.paired.sem, 2 * (self.PAIRS - 1))
        V.tensor_copy(self.t1[:, 0, 0, 0:1], self.padded[:, self.L - 1:self.L]).then_inc(self.summed.sem, 1)
        e.wait_ge(self.summed.sem, 1)
        V.tensor_reduce(self.padded[:, self.L - 1:2 * self.L - 1], self.Z[:, :, 0, :], AX.X, ALU.add).then_inc(self.summed.sem, 1)
        e.wait_ge(self.summed.sem, 2)
        V.tensor_tensor(self.padded[:, self.L - 1:self.L], self.padded[:, self.L - 1:self.L], self.t1[:, 0, 0, 0:1], ALU.add).then_inc(self.summed.sem, 1)

    def sp_matrices(self, e):
        e.wait_ge(self.summed.sem, 3)
        windows = self.padded[:, self.L - 1:2 * self.L - 1]
        windows = bass.AP(windows.tensor, windows.offset, [windows.ap[0], [-1, SEQ], [1, SEQ]])
        e.dma_start(self.scratch.rearrange("r d t -> d r t"), windows).then_inc(self.stored.sem, 16)
        e.wait_ge(self.stored.sem, 16)
        for b in range(2):
            e.dma_start(self.k.toep[b * SEQ:(b + 1) * SEQ, :, :], self.scratch).then_inc(self.toep_in.sem, 16)


def attention_ssm(k, io, freed):
    nc = k.nc
    H, DH, KTOP, GATE, HID = 4, 32, 32, 1, 4
    SCALE = float(DH) ** -0.5
    MASKED, TAKEN = -1e38, -3e38
    sem = lambda n, total=TILES: k.sem("a1_" + n, total)
    io1 = {n[len("L1_xattn_"):]: v for n, v in io.items() if n.startswith("L1_xattn_")}
    before = k.x_ready
    ps = k.ps

    cv = Carve(k.arena)
    U = cv.f32(TILES, D)
    XS = cv.f32(TILES, D)
    FO = cv.f32(TILES, 2 * D)
    wq, wk, wv = cv.f32(P), cv.f32(P), cv.f32(P)
    wf = cv.f32(4 * D)
    wfraw = cv.f32(4 * D)
    bf = cv.f32(4 * D)
    w1 = cv.f32(HID * P)
    w2 = cv.f32(HID, D)
    rows = cv.f32(5, D)
    cols = cv.f32(2 + HID)
    mg = cv.f32(1)
    head_of = cv.f32(H)
    mb = cv.f32(TILES, CTX)
    tmask = cv.f32(TILES)
    start_rings = cv.at
    mask8 = cv.f32(TILES * CTX // 4).bitcast(U8)
    tm8 = cv.f32(P // 4).bitcast(U8)
    tmf = cv.f32(P)
    stage_end = cv.at
    cv.at = start_rings
    qT = cv.f32(2, P)
    kbd = cv.f32(2, 2, H, CTX)
    W = cv.f32(2, H, CTX)
    W2 = cv.f32(2, H, CTX)
    EX = cv.f32(2, H, CTX)
    m8 = cv.f32(4, H, 8)
    nm, sums, rec = cv.f32(2, H), cv.f32(2, H), cv.f32(2, H)
    vs = cv.f32(2, 2, D)
    aT = cv.f32(2, P)
    cT = cv.f32(2, P)
    F = cv.f32(2, 2 * D)
    cg = cv.f32(2, P)
    cv2 = Carve(k.arena, start_rings)
    hin = cv2.f32(GT * P)
    hT = cv2.f32(2, GT * P)
    gb = cv2.f32(1)

    w_in, w2_in, prep = sem("w_loaded", None), sem("masks_loaded", None), sem("prepared", 6)
    prep_p, prep_t, prep_tt = sem("prepared_pool", 1), sem("text_mask_turned", 1), sem("text_mask_laid", 1)
    lnA = [sem("ln_" + n) for n in ("stats", "mv", "veps", "rstd", "out")]
    lnB = [sem("ln2_" + n) for n in ("stats", "mv", "veps", "rstd", "out")]
    u_kept, c_laid = sem("u_kept"), sem("ctx_tile")
    xt_full, xt_laid, q_full, q_laid, k_full, k_laid = (sem(n) for n in ("xT_full", "xT_laid", "q_full", "q_laid", "k_full", "k_laid"))
    s_full, s_laid, s_masked, v_full, v_laid = (sem(n) for n in ("scores", "scores_laid", "masked", "v_full", "v_laid"))
    tk = sem("top", 8 * TILES)
    e_done, sel_done, n_step, a_done = sem("exp"), sem("selected"), sem("norm_step", 3 * TILES), sem("attn")
    a_full, a_laid, c_full, cT_laid, f_full, f_laid = (sem(n) for n in ("attnT_full", "attnT_laid", "cT_full", "cT_laid", "film_full", "film_laid"))
    xs_step, xs_done = sem("xs_step"), sem("xs_done")

    b_full, b_laid = sem("conv_full", 8), sem("conv_laid", 8)
    k.conv_done = b_full
    y_step, y_done = sem("y_step", 2 * GROUPS), sem("y_done", GROUPS)
    hid_full, hid_laid = sem("hid_full", HID * GROUPS), sem("hid_laid", HID * GROUPS)
    ht_full, ht_laid, o_full, o_added = (sem(n, GROUPS) for n in ("hinT_full", "hinT_laid", "ffn_full", "ffn_added"))
    z_step, x_done = sem("z_step", 2 * GROUPS), sem("x_done", GROUPS)
    k.x_ready = x_done
    lnC = GroupNorm(k, "a1_lnC", 0, lambda g, j: XS[:, 4 * g + j, :], lambda g, j: k.xn[:, 0, j, :])
    lnD = GroupNorm(k, "a1_lnD", 1, lambda g, j: XS[:, 4 * g + j, :], lambda g, j: XS[:, 4 * g + j, :])

    def flat(v):
        return v.rearrange("p h j -> p (h j)")

    def more(t, ahead):
        return not isinstance(t, int) or t + ahead < TILES

    loads = [
        (wq, io1["Wq"]), (wk[0:DC, :], io1["Wk"]), (wv[0:DC, :], io1["Wv"]),
        (wfraw[:, 0:2 * D], io1["W_film_in"]), (wfraw[:, 2 * D:], io1["W_film_out"]),
        (bf[0:1, 0:2 * D], io1["b_film_in"].rearrange("(a n) -> a n", a=1)),
        (bf[0:1, 2 * D:], io1["b_film_out"].rearrange("(a n) -> a n", a=1)),
        (w1, io1["W1"]), (w2, io1["W2"].rearrange("(c p) d -> p c d", p=P)),
        (rows[:, 0, :], io1["g_norm_in"].rearrange("(a n) -> a n", a=1).partition_broadcast(P)),
        (rows[:, 1, :], io1["b_norm_in"].rearrange("(a n) -> a n", a=1).partition_broadcast(P)),
        (rows[:, 2, :], io1["g_norm_out"].rearrange("(a n) -> a n", a=1).partition_broadcast(P)),
        (rows[:, 3, :], io1["b_norm_out"].rearrange("(a n) -> a n", a=1).partition_broadcast(P)),
        (rows[0:1, 4, :], io1["b2"].rearrange("(a n) -> a n", a=1)),
        (cols[:, 0:1], io1["g_ffn"].rearrange("(p a) -> p a", a=1)),
        (cols[:, 1:2], io1["b_ffn"].rearrange("(p a) -> p a", a=1)),
        (cols[:, 2:2 + HID], io1["b1"].rearrange("(c p) -> p c", p=P)),
        (mg, io1["mod_gate"].rearrange("(a n) -> a n", a=1).partition_broadcast(P)),
    ]
    READY = 16 * len(loads)
    ctx_mask = io["mask_BxS2_bf1"].rearrange("(t b) j -> b t j", b=2)
    masks = [(mask8[b * SEQ:(b + 1) * SEQ, :].rearrange("p (t j) -> p t j", j=CTX), ctx_mask[b:b + 1].partition_broadcast(SEQ)) for b in range(2)]
    masks.append((tm8[0:TILES, :], io["mask_BxS_bf1"].rearrange("b s -> (b s)").rearrange("(t p) -> t p", p=P)))

    def sp(e):
        e.wait_ge(freed.sem, freed.end)
        with nc.allow_non_contiguous_dma(reason="per-channel columns are small"):
            for dst, src in loads:
                e.dma_start(dst, src).then_inc(w_in.sem, 16)
            for dst, src in masks:
                if len(src.shape) == 4:
                    src = src.rearrange("p a t j -> p (a t) j")
                e.dma_start(dst, src).then_inc(w2_in.sem, 16)

    def ctx_copy(t, s):
        nc.gpsimd.tensor_copy(cg[:, s, :], k.ctxT[:, bass.ts(t, P)]).then_inc(c_laid.sem, 1)

    def rstd(e, ln, t, s, slot):
        e.wait_ge(ln[1].sem, ln[1].at(t + 1))
        nc.gpsimd.tensor_tensor(k.veps[:, slot, s:s + 1], k.mv[:, slot, s, 1:2], k.eps[:, 0:1], ALU.add).then_inc(ln[2].sem, 1)
        e.wait_ge(ln[2].sem, ln[2].at(t + 1))
        nc.gpsimd.tensor_tensor(k.rstd[:, slot, s:s + 1], k.veps[:, slot, s:s + 1], k.half[:, 0:1], ALU.pow).then_inc(ln[3].sem, 1)

    def modulate(e, t, s):
        e.wait_ge(f_laid.sem, f_laid.at(t + 1))
        e.nop(nofuse=True)
        nc.gpsimd.tensor_tensor(XS[:, t, :], XS[:, t, :], F[:, s, 0:D], ALU.mult).then_inc(xs_step.sem, 1)
        e.wait_ge(xs_step.sem, xs_step.at(t + 1))
        e.nop(nofuse=True)
        nc.gpsimd.tensor_tensor(XS[:, t, :], XS[:, t, :], F[:, s, D:2 * D], ALU.add).then_inc(xs_done.sem, 1)

    def norm_in(e, t, s):
        e.wait_ge(lnB[4].sem, lnB[4].at(t + 1))
        e.nop(nofuse=True)
        nc.gpsimd.tensor_copy(U[:, t, :], k.xn[:, s, 0, :]).then_inc(u_kept.sem, 1)
        nc.gpsimd.tensor_tensor(XS[:, t, :], XS[:, t, :], rows[:, 0, :], ALU.mult).then_inc(l2_step.sem, 1)
        e.wait_ge(l2_step.sem, l2_step.at(2 * t + 1))
        e.nop(nofuse=True)
        nc.gpsimd.tensor_tensor(XS[:, t, :], XS[:, t, :], rows[:, 1, :], ALU.add).then_inc(l2_step.sem, 1)

    l2_step = sem("l2_step", 2 * TILES)

    def mask_scores(e, t, s):
        e.wait_ge(s_laid.sem, s_laid.at(t + 1))
        e.nop(nofuse=True)
        nc.gpsimd.tensor_tensor(W[:, s, :, :], W[:, s, :, :], mb[:, t, :].unsqueeze(1).to_broadcast([P, H, CTX]), ALU.add).then_inc(s_masked.sem, 1)

    def pool_step(e, t, s):
        o = 1 - s
        if more(t, 1):
            mask_scores(e, t + 1, o)
        if more(t, 3):
            rstd(e, lnA, t + 3, o, 0)
            rstd(e, lnB, t + 3, o, 1)
        if not (isinstance(t, int) and t == 0):
            modulate(e, t - 1, o)
        if more(t, 2):
            e.wait_ge(v_full.sem, v_full.at(t + 1))
            e.nop(nofuse=True)
            ctx_copy(t + 2, s)
        if more(t, 3):
            norm_in(e, t + 3, o)

    def pool(e):
        e.wait_ge(before.sem, before.end)
        e.wait_ge(prep_p.sem, prep_p.at(1))
        e.wait_ge(prep_tt.sem, prep_tt.at(1))
        e.wait_ge(w_in.sem, w_in.at(READY))
        for t in range(2):
            ctx_copy(t, t)
        for t in range(3):
            rstd(e, lnA, t, t % 2, 0)
            rstd(e, lnB, t, t % 2, 1)
            norm_in(e, t, t % 2)
        mask_scores(e, 0, 0)
        pipelined_tiles(e, lambda t, s: pool_step(e, t, s), tail=4)
        modulate(e, TILES - 1, 1)
        def tail_sum(g):
            yg = XS[:, bass.ts(g, GT), :]
            fo = FO[:, bass.ts(g, GT), :]
            nc.gpsimd.tensor_tensor(yg, yg, fo[:, :, 0:D], ALU.mult).then_inc(y_step.sem, 1)
            e.wait_ge(y_step.sem, y_step.at(2 * g + 1))
            e.nop(nofuse=True)
            nc.gpsimd.tensor_tensor(yg, yg, fo[:, :, D:2 * D], ALU.add).then_inc(y_step.sem, 1)
            e.wait_ge(y_step.sem, y_step.at(2 * g + 2))
            e.nop(nofuse=True)
            nc.gpsimd.tensor_tensor(yg, yg, U[:, bass.ts(g, GT), :], ALU.add).then_inc(y_done.sem, 1)

        e.wait_ge(b_laid.sem, b_laid.at(8))
        e.wait_ge(f_laid.sem, f_laid.at(TILES))
        e.wait_ge(u_kept.sem, u_kept.at(TILES))
        tail_sum(0)
        lnC.pool_rstd(e, 0)

        def body(g, more_):
            if more_:
                tail_sum(g + 1)
                lnC.pool_rstd(e, g + 1)
            lnD.pool_rstd(e, g)
            yg = XS[:, bass.ts(g, GT), :]
            e.wait_ge(lnD.out.sem, lnD.out.at(g + 1))
            e.nop(nofuse=True)
            nc.gpsimd.tensor_tensor(yg, yg, rows[:, 2, :].unsqueeze(1).to_broadcast([P, GT, D]), ALU.mult).then_inc(z_step.sem, 1)
            e.wait_ge(z_step.sem, z_step.at(2 * g + 1))
            e.nop(nofuse=True)
            nc.gpsimd.tensor_tensor(yg, yg, rows[:, 3, :].unsqueeze(1).to_broadcast([P, GT, D]), ALU.add).then_inc(z_step.sem, 1)
            e.wait_ge(z_step.sem, z_step.at(2 * g + 2))
            e.nop(nofuse=True)
            nc.gpsimd.tensor_tensor(k.x[:, bass.ts(g, GT), :], k.x[:, bass.ts(g, GT), :], yg, ALU.add).then_inc(x_done.sem, 1)

        pipelined_groups(e, body)


    def dve_prep(e):
        e.wait_ge(before.sem, before.end)
        e.wait_ge(w_in.sem, w_in.at(READY))
        e.wait_ge(w2_in.sem, w2_in.at(48))
        V = nc.vector
        V.tensor_scalar(mb.rearrange("p t j -> p (t j)"), mask8, -1.0, -MASKED, ALU.add, ALU.mult).then_inc(prep_p.sem, 1)
        V.memset(wk[DC:P, :], 0.0)
        V.memset(wv[DC:P, :], 0.0)
        V.memset(head_of[:], 0.0).then_inc(prep.sem, 1)
        e.wait_ge(prep.sem, prep.at(1))
        for h in range(H):
            V.memset(head_of[h * DH:(h + 1) * DH, h:h + 1], 1.0)
        V.tensor_scalar(wf, wfraw, mg, None, ALU.mult).then_inc(prep.sem, 1)
        V.tensor_scalar(bf[0:1, :], bf[0:1, :], mg[0:1, :], None, ALU.mult).then_inc(prep.sem, 1)
        V.tensor_scalar(rows[:, 2:4, :], rows[:, 2:4, :], k.gates[:, GATE:GATE + 1], None, ALU.mult).then_inc(prep.sem, 1)
        V.tensor_scalar(tmf[0:TILES, :], tm8[0:TILES, :], 1.0 / H, None, ALU.mult).then_inc(prep.sem, 1)
        e.wait_ge(prep.sem, prep.at(5))
        bfv = bf[0:1, :].rearrange("p (a b d) -> p a b d", a=2, b=2)
        V.tensor_scalar(bfv[:, :, 0, :], bfv[:, :, 0, :], 1.0, None, ALU.add).then_inc(prep.sem, 1)
        e.wait_ge(prep_t.sem, prep_t.at(1))
        V.tensor_copy(tmask, ps[:, 0, 0:TILES]).then_inc(prep_tt.sem, 1)
        e.wait_ge(prep.sem, prep.at(6))
        e.wait_ge(prep_p.sem, prep_p.at(1))

    def topk_round(e, t, s, r):
        V = nc.vector
        src = W if r == 0 else W2
        for h in range(H):
            ins = V.max(m8[:, r, h, :], src[:, s, h, :])
        ins.then_inc(tk.sem, 1)
        if r == 0 and more(t, 3):
            V.bn_stats(k.stat[:, 0, 1 - s, :], k.x[:, t + 3, :]).then_inc(lnA[0].sem, 1)
        e.wait_ge(tk.sem, tk.at(8 * t + 2 * r + 1))
        e.nop(nofuse=True)
        if r == 0:
            V.tensor_scalar(nm[:, s, :], m8[:, 0, :, 0], -SCALE, None, ALU.mult).then_inc(nm_done.sem, 1)
        for h in range(H):
            ins = V.match_replace(W2[:, s, h, :], m8[:, r, h, :], src[:, s, h, :], TAKEN)
        ins.then_inc(tk.sem, 1)

    def norm_a(e, t, s):
        e.wait_ge(lnA[3].sem, lnA[3].at(t + 1))
        e.nop(nofuse=True)
        nc.vector.tensor_scalar(k.xn[:, s, 0, :], k.x[:, t, :], k.mv[:, 0, s, 0:1], k.rstd[:, 0, s:s + 1],
                                ALU.subtract, ALU.mult).then_inc(lnA[4].sem, 1)

    def norm_b(e, t, s):
        e.wait_ge(lnB[3].sem, lnB[3].at(t + 1))
        e.nop(nofuse=True)
        nc.vector.tensor_scalar(XS[:, t, :], k.xn[:, s, 0, :], k.mv[:, 1, s, 0:1], k.rstd[:, 1, s:s + 1],
                                ALU.subtract, ALU.mult).then_inc(lnB[4].sem, 1)

    nm_done = sem("max_laid")

    def dve_step(e, t, s):
        V = nc.vector
        n, o = more(t, 3), 1 - s
        e.wait_ge(s_masked.sem, s_masked.at(t + 1))
        e.nop(nofuse=True)
        topk_round(e, t, s, 0)
        if n:
            e.wait_ge(lnA[0].sem, lnA[0].at(t + 4))
            e.nop(nofuse=True)
            V.bn_aggr(k.mv[:, 0, o, :], k.stat[:, 0, o, :]).then_inc(lnA[1].sem, 1)
        e.wait_ge(tk.sem, tk.at(8 * t + 2))
        e.nop(nofuse=True)
        topk_round(e, t, s, 1)
        if n:
            e.wait_ge(u_kept.sem, u_kept.at(t + 2))
            e.nop(nofuse=True)
            norm_a(e, t + 3, o)
        e.wait_ge(tk.sem, tk.at(8 * t + 4))
        e.nop(nofuse=True)
        topk_round(e, t, s, 2)
        if n:
            e.wait_ge(lnA[4].sem, lnA[4].at(t + 4))
            e.nop(nofuse=True)
            V.bn_stats(k.stat[:, 1, o, :], k.xn[:, o, 0, :]).then_inc(lnB[0].sem, 1)
        e.wait_ge(tk.sem, tk.at(8 * t + 6))
        e.nop(nofuse=True)
        topk_round(e, t, s, 3)
        if n:
            e.wait_ge(lnB[0].sem, lnB[0].at(t + 4))
            e.nop(nofuse=True)
            V.bn_aggr(k.mv[:, 1, o, :], k.stat[:, 1, o, :]).then_inc(lnB[1].sem, 1)
        e.wait_ge(e_done.sem, e_done.at(t + 1))
        e.wait_ge(tk.sem, tk.at(8 * t + 8))
        V.scalar_tensor_tensor(flat(EX[:, s, :, :]), flat(W2[:, s, :, :]), TAKEN, flat(EX[:, s, :, :]), ALU.is_equal, ALU.mult).then_inc(sel_done.sem, 1)
        e.wait_ge(sel_done.sem, sel_done.at(t + 1))
        V.tensor_reduce(sums[:, s, :], EX[:, s, :, :], AX.X, ALU.add).then_inc(n_step.sem, 1)
        e.wait_ge(n_step.sem, n_step.at(3 * t + 1))
        V.reciprocal(rec[:, s, :], sums[:, s, :]).then_inc(n_step.sem, 1)
        if n:
            norm_b(e, t + 3, o)
        e.wait_ge(n_step.sem, n_step.at(3 * t + 2))
        V.tensor_scalar(rec[:, s, :], rec[:, s, :], tmask[:, t:t + 1] if isinstance(t, int) else tmask[:, bass.ts(t, 1)], None, ALU.mult).then_inc(n_step.sem, 1)
        e.wait_ge(n_step.sem, n_step.at(3 * t + 3))
        V.tensor_tensor(EX[:, s, :, :], EX[:, s, :, :], rec[:, s, :].unsqueeze(2).to_broadcast([P, H, CTX]), ALU.mult).then_inc(a_done.sem, 1)

    def dve(e):
        V = nc.vector
        dve_prep(e)
        for t in range(3):
            s = t % 2
            V.bn_stats(k.stat[:, 0, s, :], k.x[:, t, :]).then_inc(lnA[0].sem, 1)
            e.wait_ge(lnA[0].sem, lnA[0].at(t + 1))
            V.bn_aggr(k.mv[:, 0, s, :], k.stat[:, 0, s, :]).then_inc(lnA[1].sem, 1)
            if t == 2:
                e.wait_ge(u_kept.sem, u_kept.at(1))
                e.wait_ge(xt_full.sem, xt_full.at(1))
            norm_a(e, t, s)
            e.wait_ge(lnA[4].sem, lnA[4].at(t + 1))
            V.bn_stats(k.stat[:, 1, s, :], k.xn[:, s, 0, :]).then_inc(lnB[0].sem, 1)
            e.wait_ge(lnB[0].sem, lnB[0].at(t + 1))
            V.bn_aggr(k.mv[:, 1, s, :], k.stat[:, 1, s, :]).then_inc(lnB[1].sem, 1)
            norm_b(e, t, s)
        pipelined_tiles(e, lambda t, s: dve_step(e, t, s), tail=4)
        for q in range(8):
            e.wait_ge(b_full.sem, b_full.at(q // 2 * 2 + 2))
            V.tensor_copy(XS[:, :, 16 * q:16 * q + 16], ps[:, q, :].rearrange("p (d t) -> p t d", t=TILES)).then_inc(b_laid.sem, 1)
        e.wait_ge(y_done.sem, y_done.at(1))
        lnC.dve_stats(0)
        lnC.dve_aggregate(e, 0, False)
        lnC.dve_apply(e, 0, 0)

        def body(g, more_):
            if more_:
                e.wait_ge(y_done.sem, y_done.at(g + 2))
                e.nop(nofuse=True)
                lnC.dve_stats(g + 1)
                e.wait_ge(lnC.stats.sem, lnC.stats.at(g + 2))
                e.nop(nofuse=True)
                lnC.dve_aggregate(e, g + 1, True)
                e.wait_ge(ht_full.sem, ht_full.at(g + 1))
                lnC.dve_apply(e, g + 1, g + 1)
            e.wait_ge(o_full.sem, o_full.at(g + 1))
            yg = XS[:, bass.ts(g, GT), :]
            V.tensor_tensor(yg, ps[:, 3, :].rearrange("p (j d) -> p j d", j=GT), yg, ALU.add).then_inc(o_added.sem, 1)
            e.wait_ge(o_added.sem, o_added.at(g + 1))
            e.nop(nofuse=True)
            lnD.dve_stats(g)
            e.wait_ge(lnD.stats.sem, lnD.stats.at(g + 1))
            e.nop(nofuse=True)
            lnD.dve_aggregate(e, g, True)
            lnD.dve_apply(e, g, g)

        pipelined_groups(e, body)

    def act_keys(e, t, s):
        e.wait_ge(k_full.sem, k_full.at(t + 1))
        for h in range(H):
            last = nc.scalar.activation(kbd[:, s, :, h, :], ps[:, 2, 0:P].rearrange("p (b j) -> p b j", b=2), ACT.Copy,
                                        scale=head_of[:, h:h + 1])
        last.then_inc(k_laid.sem, 1)
        e.wait_ge(q_full.sem, q_full.at(t + 1))
        nc.scalar.copy(qT[:, s, :], ps[:, 1, 0:P]).then_inc(q_laid.sem, 1)

    def act_scores(e, t, s):
        e.wait_ge(s_full.sem, s_full.at(t + 1))
        if not (isinstance(t, int) and t < 2):
            e.wait_ge(tk.sem, tk.at(8 * t - 14))
        nc.scalar.copy(flat(W[:, s, :, :]), ps[:, 3, 0:H * CTX]).then_inc(s_laid.sem, 1)

    def act_step(e, t, s):
        o = 1 - s
        film = not (isinstance(t, int) and t == 0)
        if more(t, 1):
            act_scores(e, t + 1, o)
        e.wait_ge(v_full.sem, v_full.at(t + 1))
        nc.scalar.copy(vs[0:CTX, s, :, :].rearrange("p b d -> p (b d)"), ps[0:CTX, 4, 0:2 * D]).then_inc(v_laid.sem, 1)
        if film:
            e.wait_ge(a_full.sem, a_full.at(t))
            nc.scalar.copy(aT[0:CTX, o, :], ps[0:CTX, 5, 0:P]).then_inc(a_laid.sem, 1)
        if more(t, 2):
            e.wait_ge(xt_full.sem, xt_full.at(t + 3))
            nc.scalar.copy(k.xnT[:, s, 0:P], ps[:, 0, 0:P]).then_inc(xt_laid.sem, 1)
        e.wait_ge(nm_done.sem, nm_done.at(t + 1))
        for h in range(H):
            last = nc.scalar.activation(EX[:, s, h, :], W[:, s, h, :], ACT.Exp, bias=nm[:, s, h:h + 1], scale=SCALE)
        last.then_inc(e_done.sem, 1)
        if film:
            e.wait_ge(c_full.sem, c_full.at(t))
            nc.scalar.copy(cT[:, o, :], ps[:, 6, 0:P]).then_inc(cT_laid.sem, 1)
        if more(t, 2):
            act_keys(e, t + 2, s)
        if film:
            act_film(e, t - 1, o)

    def act_film(e, t, s):
        e.wait_ge(xs_done.sem, xs_done.at(t))
        e.wait_ge(f_full.sem, f_full.at(t + 1))
        e.nop(nofuse=True)
        nc.scalar.copy(F[:, s, :], ps[:, 7, 0:2 * D])
        nc.scalar.copy(FO[:, t, :], ps[:, 7, 2 * D:4 * D]).then_inc(f_laid.sem, 1)

    def act_last_film(e, t, s):
        e.wait_ge(a_full.sem, a_full.at(t + 1))
        nc.scalar.copy(aT[0:CTX, s, :], ps[0:CTX, 5, 0:P]).then_inc(a_laid.sem, 1)
        e.wait_ge(c_full.sem, c_full.at(t + 1))
        nc.scalar.copy(cT[:, s, :], ps[:, 6, 0:P]).then_inc(cT_laid.sem, 1)
        act_film(e, t, s)

    def act(e):
        e.wait_ge(before.sem, before.end)
        e.wait_ge(w_in.sem, w_in.at(READY))
        e.wait_ge(prep_p.sem, prep_p.at(1))
        e.wait_ge(prep_tt.sem, prep_tt.at(1))
        for t in range(2):
            e.wait_ge(xt_full.sem, xt_full.at(t + 1))
            nc.scalar.copy(k.xnT[:, t, 0:P], ps[:, 0, 0:P]).then_inc(xt_laid.sem, 1)
            act_keys(e, t, t)
        act_scores(e, 0, 0)
        pipelined_tiles(e, lambda t, s: act_step(e, t, s), tail=4)
        act_last_film(e, TILES - 1, 1)
        e.wait_ge(b_laid.sem, b_laid.at(8))

        def turn_copy(n):
            e.wait_ge(ht_full.sem, ht_full.at(n + 1))
            nc.scalar.activation(hin, ps[:, 0, :], ACT.Identity, bias=cols[:, 1:2], scale=cols[:, 0:1]).then_inc(ht_laid.sem, 1)

        turn_copy(0)

        def body(g, more_):
            for c in range(HID):
                e.wait_ge(hid_full.sem, hid_full.at(HID * g + c + 1))
                nc.scalar.activation(hT[:, c % 2, :], ps[:, 1 + c % 2, :], ACT.Gelu, bias=cols[:, 2 + c:3 + c]).then_inc(hid_laid.sem, 1)
            if more_:
                turn_copy(g + 1)

        pipelined_groups(e, body)

    T = nc.tensor

    def pe_turn(e, t, s):
        e.wait_ge(lnA[4].sem, lnA[4].at(t + 1))
        e.wait_ge(xt_laid.sem, xt_laid.at(t))
        T.transpose(ps[:, 0, 0:P], k.xn[:, s, 0, :], k.ident[:]).then_inc(xt_full.sem, 1)

    def pe_keys(e, t, s):
        e.wait_ge(k_laid.sem, k_laid.at(t))
        e.nop(nofuse=True)
        T.matmul(ps[:, 2, 0:P], wk, k.ctxT[:, bass.ts(t, P)], start=True, stop=True).then_inc(k_full.sem, 1)

    def pe_query(e, t, s):
        e.wait_ge(xt_laid.sem, xt_laid.at(t + 1))
        e.wait_ge(q_laid.sem, q_laid.at(t))
        T.matmul(ps[:, 1, 0:P], wq, k.xnT[:, s, 0:P], start=True, stop=True).then_inc(q_full.sem, 1)

    def pe_scores(e, t, s):
        e.wait_ge(q_laid.sem, q_laid.at(t + 1))
        e.wait_ge(k_laid.sem, k_laid.at(t + 1))
        e.wait_ge(s_laid.sem, s_laid.at(t))
        e.nop(nofuse=True)
        for b in range(2):
            last = T.matmul(ps[64 * b:64 * b + 64, 3, 0:H * CTX], qT[:, s, 64 * b:64 * b + 64], flat(kbd[:, s, b, :, :]), start=True, stop=True)
        last.then_inc(s_full.sem, 1)

    def pe_attn(e, t, s):
        e.wait_ge(a_done.sem, a_done.at(t + 1))
        e.wait_ge(a_laid.sem, a_laid.at(t))
        for h in range(H):
            last = T.matmul(ps[0:CTX, 5, 0:P], EX[:, s, h, :], k.ident[:], start=(h == 0), stop=(h == H - 1))
        last.then_inc(a_full.sem, 1)

    def pe_context(e, t, s):
        e.wait_ge(cT_laid.sem, cT_laid.at(t))
        e.wait_ge(a_laid.sem, a_laid.at(t + 1))
        e.nop(nofuse=True)
        for b in range(2):
            last = T.matmul(ps[:, 6, b * SEQ:(b + 1) * SEQ], vs[0:CTX, s, b, :], aT[0:CTX, s, b * SEQ:(b + 1) * SEQ], start=True, stop=True)
        last.then_inc(c_full.sem, 1)

    def pe_film(e, t, s):
        e.wait_ge(f_laid.sem, f_laid.at(t))
        T.matmul(ps[:, 7, :], k.ones, bf[0:1, :], start=True, stop=False)
        e.wait_ge(cT_laid.sem, cT_laid.at(t + 1))
        T.matmul(ps[:, 7, :], cT[:, s, :], wf, start=False, stop=True).then_inc(f_full.sem, 1)

    def pe_step(e, t, s):
        o = 1 - s
        film = not (isinstance(t, int) and t == 0)
        if more(t, 1):
            pe_scores(e, t + 1, o)
        e.wait_ge(c_laid.sem, c_laid.at(t + 1))
        e.wait_ge(v_laid.sem, v_laid.at(t))
        e.nop(nofuse=True)
        for b in range(2):
            last = T.matmul(ps[0:CTX, 4, b * D:(b + 1) * D], cg[:, s, b * CTX:(b + 1) * CTX], wv, start=True, stop=True)
        last.then_inc(v_full.sem, 1)
        if film:
            pe_attn(e, t - 1, o)
        if more(t, 2):
            pe_turn(e, t + 2, s)
            pe_keys(e, t + 2, s)
        if film:
            pe_context(e, t - 1, o)
        if more(t, 2):
            pe_query(e, t + 2, s)
        if film:
            pe_film(e, t - 1, o)

    def pe(e):
        e.wait_ge(w2_in.sem, w2_in.at(48))
        e.wait_ge(prep.sem, prep.at(5))
        T.transpose(ps[:, 0, 0:TILES], tmf[0:TILES, :], k.ident[0:TILES, 0:TILES]).then_inc(prep_t.sem, 1)
        e.wait_ge(prep.sem, prep.at(6))
        e.wait_ge(prep_p.sem, prep_p.at(1))
        e.wait_ge(prep_tt.sem, prep_tt.at(1))
        e.wait_ge(w_in.sem, w_in.at(READY))
        for t in range(2):
            pe_turn(e, t, t)
            pe_keys(e, t, t)
            pe_query(e, t, t)
        pe_scores(e, 0, 0)
        pipelined_tiles(e, lambda t, s: pe_step(e, t, s), tail=4)
        pe_attn(e, TILES - 1, 1)
        pe_context(e, TILES - 1, 1)
        pe_film(e, TILES - 1, 1)
        e.wait_ge(f_laid.sem, f_laid.at(TILES))
        e.wait_ge(xs_done.sem, xs_done.at(TILES))
        e.wait_ge(k.ssm.toep_in.sem, 32)
        for q in range(0, 8, 2):
            for flip in range(2):
                for i in range(16):
                    for b in range(2):
                        bank = q + (b ^ flip)
                        d = 16 * bank + i
                        half = slice(b * SEQ, (b + 1) * SEQ)
                        last = T.matmul(ps[half, bank, i * TILES:(i + 1) * TILES], k.toep[half, d, :], XS[half, :, d], start=True, stop=True)
            last.then_inc(b_full.sem, 2)
        e.wait_ge(b_laid.sem, b_laid.at(8))

        def turn(n):
            e.wait_ge(lnC.out.sem, lnC.out.at(n + 1))
            for j in range(GT):
                last = T.transpose(ps[:, 0, j * P:(j + 1) * P], k.xn[:, 0, j, :], k.ident[:])
            last.then_inc(ht_full.sem, 1)

        turn(0)

        def hidden(g, c):
            if c == 0:
                e.wait_ge(ht_laid.sem, ht_laid.at(g + 1))
            T.matmul(ps[:, 1 + c % 2, :], w1[:, c * P:(c + 1) * P], hin, start=True, stop=True).then_inc(hid_full.sem, 1)

        def outputs(g, c):
            e.wait_ge(hid_laid.sem, hid_laid.at(HID * g + c + 1))
            if c == 0:
                e.wait_ge(o_added.sem, o_added.at(g))
            for j in range(GT):
                T.matmul(ps[:, 3, j * P:(j + 1) * P], hT[:, c % 2, j * P:(j + 1) * P], w2[:, c, :],
                         start=(c == 0 and j == 0), stop=False, skip_group_check=True)

        def body(g, more_):
            hidden(g, 0)
            hidden(g, 1)
            outputs(g, 0)
            hidden(g, 2)
            outputs(g, 1)
            hidden(g, 3)
            if more_:
                turn(g + 1)
            outputs(g, 2)
            outputs(g, 3)
            for j in range(GT):
                last = T.matmul(ps[:, 3, j * P:(j + 1) * P], k.ones, rows[0:1, 4, :], start=False, stop=(j == GT - 1), skip_group_check=True)
            last.then_inc(o_full.sem, 1)

        pipelined_groups(e, body)

    return dict(sp=sp, pe=pe, act=act, dve=dve, pool=pool)


class Thresholds:

    BITS = 31

    def __init__(self, k, io):
        self.k, self.io = k, io
        sem = lambda n: k.sem("thr_" + n)
        self.w_in, self.ready, self.counted, self.total, self.read, self.step = (sem(n) for n in ("loaded", "ready", "counted", "totals", "totals_read", "step"))
        self.abs = k.sb("thr_abs", [P, 1024 + 8])
        self.hits = k.sb("thr_hits", [P, 2, 1024 + 8], BF16)
        self.need = k.sb("thr_need", [P, 8])
        self.count = k.sb("thr_count", [P, 8])
        self.cur = k.sb("thr_found", [P, 8], I32)
        self.cand = k.sb("thr_candidate", [P, 8], I32)
        self.bit = k.sb("thr_bit", [P, 8], I32)
        self.enough = k.sb("thr_enough", [P, 8], I32)
        self.sets = [(0, 512, P * 512), (512, 512, P * 512), (1024, 4, P * 4), (1028, 1, P)]

    def sp(self, e):
        io, a = self.io, self.abs
        with self.k.nc.allow_non_contiguous_dma(reason="biases are small"):
            e.dma_start(a[:, 0:512], io["L1_ffn_W1"]).then_inc(self.w_in.sem, 16)
            e.dma_start(a[:, 512:1024].rearrange("p (c d) -> p c d", c=4), io["L1_ffn_W2"].rearrange("(c p) d -> p c d", p=P)).then_inc(self.w_in.sem, 16)
            e.dma_start(a[:, 1024:1028], io["L1_ffn_b1"].rearrange("(c p) -> p c", p=P)).then_inc(self.w_in.sem, 16)
            e.dma_start(a[:, 1028:1029], io["L1_ffn_b2"].rearrange("(p a) -> p a", a=1)).then_inc(self.w_in.sem, 16)

    def dve_start(self, e):
        V = self.k.nc.vector
        V.memset(self.cur[:], 0)
        V.memset(self.cand[:], 1 << (self.BITS - 1))
        V.memset(self.bit[:], 1 << (self.BITS - 1))
        for i, (_, _, n) in enumerate(self.sets):
            kth = max(1, int(n * 0.1 / 2))
            V.memset(self.need[:, 2 * i:2 * i + 1], float(kth))
            V.memset(self.need[:, 2 * i + 1:2 * i + 2], float(n - kth + 1))
        e.wait_ge(self.w_in.sem, self.w_in.at(64))
        bits = self.abs[:, 0:1029].bitcast(I32)
        V.tensor_scalar(bits, bits, 0x7FFFFFFF, None, ALU.bitwise_and).then_inc(self.ready.sem, 1)
        e.wait_ge(self.ready.sem, self.ready.at(1))

    def dve_round(self, e, t):
        V = self.k.nc.vector
        first, last = isinstance(t, int) and t == 0, isinstance(t, int) and t == self.BITS
        if not first:
            e.wait_ge(self.total.sem, self.total.at(t))
            V.tensor_tensor(self.enough[:], self.k.ps[:, 2, D:D + 8], self.need[:], ALU.is_ge).then_inc(self.read.sem, 1)
            e.wait_ge(self.read.sem, self.read.at(t))
            e.nop(nofuse=True)
            V.copy_predicated(self.cur[:], self.enough[:], self.cand[:])
            V.tensor_scalar(self.bit[:], self.bit[:], 1, None, ALU.logical_shift_right).then_inc(self.step.sem, 1)
            if last:
                return
            e.wait_ge(self.step.sem, self.step.at(2 * t - 1))
            e.nop(nofuse=True)
            V.tensor_tensor(self.cand[:], self.cur[:], self.bit[:], ALU.bitwise_or).then_inc(self.step.sem, 1)
            e.wait_ge(self.step.sem, self.step.at(2 * t))
            e.nop(nofuse=True)
        for i, (at, n, _) in enumerate(self.sets):
            for j in range(2):
                c = 2 * i + j
                ins = V.tensor_scalar(self.hits[:, j, at:at + n], self.abs[:, at:at + n], self.cand[:, c:c + 1].bitcast(F32), 0.0,
                                      ALU.is_ge, ALU.add, accum_out=self.count[:, c:c + 1])
        ins.then_inc(self.counted.sem, 1)

    def pe_total(self, e, t):
        e.wait_ge(self.counted.sem, self.counted.at(t + 1))
        self.k.nc.tensor.matmul(self.k.ps[:, 2, D:D + 8], self.k.onesq[:], self.count[:], start=True, stop=True).then_inc(self.total.sem, 1)

    @property
    def value(self):
        return self.cur[:].bitcast(F32)


def ffn1(k, io):
    th = k.thresholds

    def loads(k, io, v):
        row = lambda n: io[n].rearrange("(a n) -> a n", a=1)
        col = lambda n: io[n].rearrange("(p a) -> p a", a=1)
        return [
            (v.w1[:, 0, :], io["L1_ffn_W1"]),
            (v.w2[:, 0, :, :], io["L1_ffn_W2"].rearrange("(c p) d -> p c d", p=P)),
            (v.b1[:, 0, :], io["L1_ffn_b1"].rearrange("(c p) -> p c", p=P)),
            (v.b2[0:2, :], row("L1_ffn_b2").partition_broadcast(2)),
            (v.wr, io["L1_ffn_Wr"]),
            (v.br[0:8, :], col("L1_ffn_br")),
            (v.gam, col("L1_ffn_ln_gamma")),
            (v.bet, col("L1_ffn_ln_beta")),
        ]

    def prepare(k, io, v):
        V = k.nc.vector
        step, ready = k.sem("f1_perturb_step"), k.sem("f1_perturbed")
        m1, m2, q, a2 = (v.cv.f32(512) for _ in range(4))

        def dve(e):
            e.wait_ge(v.before.sem, v.before.end)
            e.wait_ge(v.w_in.sem, v.w_in.at(16 * len(v.loads)))
            n = 0

            def go(ins):
                nonlocal n
                n += 1
                ins.then_inc(step.sem, 1)
                e.wait_ge(step.sem, step.at(n))

            def perturb(dst, w, a, i, rows=slice(0, P), only=None):
                width = w.shape[-1]
                x1, x2, xq = m1[rows, 0:width], m2[rows, 0:width], q[rows, 0:width]
                top, bot = th.value[rows, 2 * i:2 * i + 1], th.value[rows, 2 * i + 1:2 * i + 2]
                go(V.tensor_scalar(x1, a, top, None, ALU.is_ge))
                go(V.tensor_scalar(x2, a, bot, None, ALU.is_le))
                go(V.tensor_tensor(xq, x1, x2, ALU.mult))
                go(V.tensor_tensor(x2, x2, xq, ALU.subtract))
                go(V.tensor_tensor(x2, x2, x1, ALU.subtract))
                go(V.scalar_tensor_tensor(xq, w, 0.8, x2, ALU.mult, ALU.mult))
                if only is not None:
                    go(V.tensor_scalar(xq, xq, only, None, ALU.mult))
                go(V.tensor_tensor(dst, w, xq, ALU.add))

            perturb(v.w1[:, 1, :], v.w1[:, 0, :], th.abs[:, 0:512], 0)
            w2 = v.w2.rearrange("p x c d -> p x (c d)")
            perturb(w2[:, 1, :], w2[:, 0, :], th.abs[:, 512:1024], 1)
            perturb(v.b1[:, 1, :], v.b1[:, 0, :], th.abs[:, 1024:1028], 2)
            go(V.tensor_scalar(a2[0:2, 0:D].bitcast(I32), v.b2[0:2, :].bitcast(I32), 0x7FFFFFFF, None, ALU.bitwise_and))
            perturb(v.b2[0:2, :], v.b2[0:2, :], a2[0:2, 0:D], 3, slice(0, 2), k.ident[0:2, 1:2])
            V.drain().then_inc(ready.sem, 1)

        def pe(e):
            e.wait_ge(ready.sem, ready.at(1))

        return dict(dve=dve, pe=pe, act=pe)

    toep = k.toep[:].rearrange("p a b -> p (a b)")
    return experts(k, io, "f1", False, 5, loads, k.conv_done, toep, 0, prepare)


def ffn2(k, io, freed, start):
    nc, ps = k.nc, k.ps
    GATE, IC = 6, 4
    HID = IC * P
    sem = lambda n, total=TILES: k.sem("f2_" + n, total)
    w_in, w_sum, w_tot, w_tern = sem("w_loaded", None), sem("w_sums", 1), sem("w_totals", 1), sem("w_ternary", 1)
    w_step, w_turned, w_laid = sem("w_step", 7), sem("w_turned", 3), sem("w_laid", 3)
    q_step, q_done, qt_full, qt_laid = sem("q_step", 5 * GROUPS), sem("q_done", GROUPS), sem("qT_full", GROUPS), sem("qT_laid", GROUPS)
    s_done = sem("h_scale", 3 * TILES)
    g_full, r_done, r2_done, h_done, a_done, hr_done, hq_done = (sem(n) for n in ("gate_up", "relu", "relu_squared", "h", "h_max", "h_rounded", "h_quantized"))
    ht_full, ht_laid, y_full, x_step, x_done = sem("hT_full"), sem("hT_laid"), sem("y_full"), sem("x_added"), sem("x_done", GROUPS)
    before = k.x_ready
    k.x_ready = x_done
    ln = GroupNorm(k, "f2_ln", 0, lambda g, j: k.x[:, 4 * g + j, :], lambda g, j: k.xn[:, 0, j, :])

    cv = Carve(k.arena, start)
    wraw = cv.f32(3, HID)
    wt = cv.f32(3, HID)
    wb = cv.bf16(3, HID)
    wT = cv.bf16(3, HID)
    identb = cv.bf16(P)
    sums, mean, inv = cv.f32(4), cv.f32(4), cv.f32(4)
    am, sc, cgt, cut = cv.f32(GT), cv.f32(GT), cv.f32(2, GT), cv.f32(2, GT)
    qf = cv.f32(GT, D)
    qb = cv.bf16(GT, D)
    qT = cv.bf16(GT * P)
    r, r2, h, hq = (cv.f32(2, HID) for _ in range(4))
    hb = cv.bf16(2, HID)
    hT = cv.bf16(2, HID)
    ah, sh, yc = cv.f32(2), cv.f32(2), cv.f32(2)
    junk = cv.f32(HID)
    onesq = k.onesq
    bank16 = lambda b: ps[:, b, :].bitcast(BF16)

    def sp(e):
        e.wait_ge(freed.sem, freed.end)
        e.dma_start(wraw[:, 0, :].rearrange("p (c d) -> p c d", c=IC), io["L2_ffn_w_gate"].rearrange("(c p) d -> p c d", p=P)).then_inc(w_in.sem, 16)
        e.dma_start(wraw[:, 1, :].rearrange("p (c d) -> p c d", c=IC), io["L2_ffn_w_up"].rearrange("(c p) d -> p c d", p=P)).then_inc(w_in.sem, 16)
        e.dma_start(wraw[:, 2, :], io["L2_ffn_w_down"]).then_inc(w_in.sem, 16)

    T, V, S = nc.tensor, nc.vector, nc.scalar

    def quantize(e, g):
        n = 5 * g
        e.wait_ge(ln.out.sem, ln.out.at(g + 1))
        V.tensor_reduce(am[:], k.xn[:, 0, :, :], AX.X, ALU.max, apply_absolute_value=True).then_inc(q_step.sem, 1)
        e.wait_ge(q_step.sem, q_step.at(n + 1))
        V.tensor_scalar(am[:], am[:], EPSQ, 1.0 / 127.0, ALU.max, ALU.mult).then_inc(q_step.sem, 1)
        e.wait_ge(q_step.sem, q_step.at(n + 2))
        V.reciprocal(sc[:], am[:]).then_inc(q_step.sem, 1)
        e.wait_ge(q_step.sem, q_step.at(n + 3))
        for j in range(GT):
            last = V.tensor_scalar(qf[:, j, :], k.xn[:, 0, j, :], sc[:, j:j + 1], ROUND, ALU.mult, ALU.add)
        last.then_inc(q_step.sem, 1)
        e.wait_ge(q_step.sem, q_step.at(n + 4))
        V.tensor_scalar(qb[:], qf[:], -ROUND, 127.0, ALU.add, ALU.min).then_inc(q_done.sem, 1)

    def scales(e, g):
        V.tensor_scalar(cgt[:, 0, :], am[:], mean[:, 0:1], None, ALU.mult)
        V.tensor_scalar(cut[:, 0, :], am[:], mean[:, 1:2], None, ALU.mult).then_inc(q_step.sem, 1)

    def dve(e):
        e.wait_ge(before.sem, before.end)
        e.wait_ge(w_in.sem, w_in.at(48))
        for i in range(3):
            ins = V.tensor_reduce(sums[:, i:i + 1], wraw[:, i, :], AX.X, ALU.add, apply_absolute_value=True)
        V.tensor_copy(identb[:], k.ident[:]).then_inc(w_sum.sem, 1)
        ln.dve_stats(0)
        e.wait_ge(w_tot.sem, w_tot.at(1))
        V.tensor_scalar(mean[:, 0:3], ps[:, 0, 0:3], 1.0 / (P * HID), EPSQ, ALU.mult, ALU.max).then_inc(w_step.sem, 1)
        e.wait_ge(w_step.sem, w_step.at(1))
        ln.dve_aggregate(e, 0, True)
        V.reciprocal(inv[:, 0:3], mean[:, 0:3]).then_inc(w_step.sem, 1)
        e.wait_ge(w_step.sem, w_step.at(2))
        for i in range(3):
            V.tensor_scalar(wt[:, i, :], wraw[:, i, :], inv[:, i:i + 1], ROUND, ALU.mult, ALU.add).then_inc(w_step.sem, 1)
        V.tensor_scalar(mean[:, 2:3], mean[:, 2:3], k.gates[:, GATE:GATE + 1], None, ALU.mult).then_inc(w_step.sem, 1)
        e.wait_ge(w_step.sem, w_step.at(6))
        V.tensor_scalar(wt[:], wt[:], -ROUND, 1.0, ALU.add, ALU.min).then_inc(w_step.sem, 1)
        e.wait_ge(w_step.sem, w_step.at(7))
        V.tensor_scalar(wb[:], wt[:], -1.0, None, ALU.max).then_inc(w_tern.sem, 1)
        ln.dve_apply(e, 0, 0)
        quantize(e, 0)

        def body(g, more):
            scales(e, g)
            if more:
                ln.dve_stats(g + 1)
            for j in range(GT):
                t, s = GT * g + j, j % 2
                if j == 0:
                    e.wait_ge(q_step.sem, q_step.at(5 * g + 5))
                e.wait_ge(r2_done.sem, r2_done.at(t + 1))
                V.scalar_tensor_tensor(h[:, s, :], ps[:, 2 + s, :], cut[:, 0, j:j + 1], r2[:, s, :], ALU.mult, ALU.mult).then_inc(h_done.sem, 1)
                e.wait_ge(h_done.sem, h_done.at(t + 1))
                V.tensor_reduce(ah[:, s:s + 1], h[:, s, :], AX.X, ALU.max, apply_absolute_value=True).then_inc(a_done.sem, 1)
                if j == 0 and more:
                    e.wait_ge(a_done.sem, a_done.at(t + 1))
                    e.nop(nofuse=True)
                    ln.dve_aggregate(e, g + 1, True)
                e.wait_ge(a_done.sem, a_done.at(t + 1))
                V.tensor_scalar(ah[:, s:s + 1], ah[:, s:s + 1], EPSQ, 1.0 / 127.0, ALU.max, ALU.mult).then_inc(s_done.sem, 1)
                e.wait_ge(s_done.sem, s_done.at(3 * t + 1))
                V.reciprocal(sh[:, s:s + 1], ah[:, s:s + 1]).then_inc(s_done.sem, 1)
                e.wait_ge(s_done.sem, s_done.at(3 * t + 2))
                V.tensor_scalar(hq[:, s, :], h[:, s, :], sh[:, s:s + 1], ROUND, ALU.mult, ALU.add).then_inc(hr_done.sem, 1)
                V.tensor_scalar(yc[:, s:s + 1], ah[:, s:s + 1], mean[:, 2:3], None, ALU.mult).then_inc(s_done.sem, 1)
                e.wait_ge(hr_done.sem, hr_done.at(t + 1))
                V.tensor_scalar(hb[:, s, :], hq[:, s, :], -ROUND, 127.0, ALU.add, ALU.min).then_inc(hq_done.sem, 1)
                if j == 1 and more:
                    ln.dve_apply(e, g + 1, g + 1)
                if j == 2 and more:
                    quantize(e, g + 1)
                if j > 0:
                    add(g, j - 1)
            add(g, GT - 1, True)

        def add(g, j, end=False):
            t, s = GT * g + j, j % 2
            e.wait_ge(s_done.sem, s_done.at(3 * t + 3))
            e.wait_ge(y_full.sem, y_full.at(t + 1))
            V.scalar_tensor_tensor(k.x[:, t, :], ps[:, 7, 0:D], yc[:, s:s + 1], k.x[:, t, :], ALU.mult, ALU.add).then_inc(x_step.sem, 1)
            if end:
                e.wait_ge(x_step.sem, x_step.at(t + 1))
                e.nop(nofuse=True)
                e.sem_inc(x_done.sem, 1)

        pipelined_groups(e, body)

    def pe(e):
        e.wait_ge(w_sum.sem, w_sum.at(1))
        T.matmul(ps[:, 0, 0:3], onesq[:], sums[:, 0:3], start=True, stop=True).then_inc(w_tot.sem, 1)
        e.wait_ge(w_tern.sem, w_tern.at(1))
        for i in range(3):
            for c in range(IC):
                last = T.transpose(bank16(4 + i)[:, c * P:(c + 1) * P], wb[:, i, c * P:(c + 1) * P], identb[:])
            last.then_inc(w_turned.sem, 1)
        e.wait_ge(w_laid.sem, w_laid.at(3))

        def turn(n):
            e.wait_ge(q_done.sem, q_done.at(n + 1))
            for j in range(GT):
                last = T.transpose(bank16(4)[:, j * P:(j + 1) * P], qb[:, j, :], identb[:])
            last.then_inc(qt_full.sem, 1)

        def gate_up(g, j):
            t, s = GT * g + j, j % 2
            if j == 0:
                e.wait_ge(qt_laid.sem, qt_laid.at(g + 1))
            e.wait_ge(h_done.sem, h_done.at(t - 1))
            T.matmul(ps[:, s, :], qT[:, j * P:(j + 1) * P], wT[:, 0, :], start=True, stop=True)
            T.matmul(ps[:, 2 + s, :], qT[:, j * P:(j + 1) * P], wT[:, 1, :], start=True, stop=True).then_inc(g_full.sem, 1)

        def turn_h(g, j):
            t, s = GT * g + j, j % 2
            e.wait_ge(hq_done.sem, hq_done.at(t + 1))
            for c in range(IC):
                last = T.transpose(bank16(5 + s)[:, c * P:(c + 1) * P], hb[:, s, c * P:(c + 1) * P], identb[:])
            last.then_inc(ht_full.sem, 1)

        def down(g, j):
            t, s = GT * g + j, j % 2
            e.wait_ge(ht_laid.sem, ht_laid.at(t + 1))
            e.wait_ge(x_step.sem, x_step.at(t))
            for c in range(IC):
                last = T.matmul(ps[:, 7, 0:D], hT[:, s, c * P:(c + 1) * P], wT[:, 2, c * P:(c + 1) * P], start=(c == 0), stop=(c == IC - 1))
            last.then_inc(y_full.sem, 1)

        turn(0)

        def body(g, more):
            gate_up(g, 0)
            for j in range(GT):
                if j + 1 < GT:
                    gate_up(g, j + 1)
                turn_h(g, j)
                if j == GT - 1 and more:
                    turn(g + 1)
                down(g, j)

        pipelined_groups(e, body)

    def act(e):
        for i in range(3):
            e.wait_ge(w_turned.sem, w_turned.at(i + 1))
            S.copy(wT[:, i, :], bank16(4 + i)[:, 0:HID]).then_inc(w_laid.sem, 1)

        def turn_copy(n):
            e.wait_ge(qt_full.sem, qt_full.at(n + 1))
            S.copy(qT[:], bank16(4)[:, 0:GT * P]).then_inc(qt_laid.sem, 1)

        turn_copy(0)

        def relu(g, j):
            t, s = GT * g + j, j % 2
            e.wait_ge(g_full.sem, g_full.at(t + 1))
            if j == 0:
                e.wait_ge(q_step.sem, q_step.at(5 * g + 5))
            S.activation(r[:, s, :], ps[:, s, :], ACT.Relu, scale=cgt[:, 0, j:j + 1]).then_inc(r_done.sem, 1)

        def body(g, more):
            relu(g, 0)
            for j in range(GT):
                if j + 1 < GT:
                    relu(g, j + 1)
                t, s = GT * g + j, j % 2
                e.wait_ge(ht_full.sem, ht_full.at(t + 1))
                S.copy(hT[:, s, :], bank16(5 + s)[:, 0:HID]).then_inc(ht_laid.sem, 1)
            if more:
                turn_copy(g + 1)

        pipelined_groups(e, body)

    def pool(e):
        e.wait_ge(before.sem, before.end)
        ln.pool_rstd(e, 0)

        def body(g, more):
            for j in range(GT):
                t, s = GT * g + j, j % 2
                e.wait_ge(r_done.sem, r_done.at(t + 1))
                nc.gpsimd.tensor_tensor(r2[:, s, :], r[:, s, :], r[:, s, :], ALU.mult).then_inc(r2_done.sem, 1)
                if j == 0 and more:
                    ln.pool_rstd(e, g + 1)

        pipelined_groups(e, body)

    return dict(sp=sp, pe=pe, act=act, dve=dve, pool=pool)


def ffn3(k, io, freed, start):
    nc, ps = k.nc, k.ps
    GATE, IC, R = 7, 4, 16
    HID = IC * P
    sem = lambda n, total=GROUPS: k.sem("f3_" + n, total)
    w_in, w_step, w_low, w_ready = sem("w_loaded", None), sem("w_step", 6), sem("low_rank", 1), sem("w_ready", 1)
    w_turned, w_laid = sem("w_turned", 2), sem("w_laid", 2)
    u_full, u_laid, t_full, t_laid = (sem(n, 1) for n in ("uT_full", "uT_laid", "fv_full", "fv_laid"))
    xt_full, xt_laid, o_full, x_done = (sem(n) for n in ("xT_full", "xT_laid", "o_full", "x_done"))
    h_full, r_done, h_laid = (sem(n, IC * GROUPS) for n in ("h_full", "relu", "squared"))
    before = k.x_ready
    k.x_ready = x_done
    ln = GroupNorm(k, "f3_ln", 0, lambda g, j: k.x[:, 4 * g + j, :], lambda g, j: k.xn[:, 0, j, :])
    cv = Carve(k.arena, start)
    wf, wp = cv.f32(IC, D), cv.f32(HID)
    tf, tp = cv.f32(IC, D), cv.f32(HID)
    wfT, wpT = cv.f32(HID), cv.f32(IC, D)
    un, uT = cv.f32(IC, R), cv.f32(IC, P)
    fbT, vn, fv = cv.f32(R), cv.f32(D), cv.f32(D)
    gate = cv.f32(1)
    s5, i5 = cv.f32(IC + 1), cv.f32(IC + 1)
    r, hT = cv.f32(2, GT * P), cv.f32(2, GT * P)
    xnT = k.xnT[:, 0, :]
    T, V, S = nc.tensor, nc.vector, nc.scalar

    def sp(e):
        e.wait_ge(freed.sem, freed.end)
        with nc.allow_non_contiguous_dma(reason="a 16 by 16 matrix, transposed"):
            for dst, src in (
                (wf, io["L3_ffn_w_fc"].rearrange("(c p) d -> p c d", p=P)), (wp, io["L3_ffn_w_proj"]),
                (un, io["L3_ffn_u"].rearrange("(c p) r -> p c r", p=P)), (fbT[0:R, :], io["L3_ffn_fast_b"].rearrange("i j -> j i")),
                (vn[0:R, :], io["L3_ffn_v"]), (gate, io["L3_ffn_gate"].rearrange("(a n) -> a n", a=1).partition_broadcast(P)),
            ):
                e.dma_start(dst, src).then_inc(w_in.sem, 16)

    def dve(e):
        e.wait_ge(before.sem, before.end)
        e.wait_ge(w_in.sem, w_in.at(96))
        n = 0

        def go(ins):
            nonlocal n
            n += 1
            ins.then_inc(w_step.sem, 1)
            e.wait_ge(w_step.sem, w_step.at(n))

        ln.dve_stats(0)
        V.tensor_reduce(s5[:, 0:IC], wf[:], AX.X, ALU.add, apply_absolute_value=True)
        go(V.tensor_reduce(s5[:, IC:IC + 1], wp[:], AX.X, ALU.add, apply_absolute_value=True))
        ln.dve_aggregate(e, 0, True)
        V.tensor_scalar(s5[:, 0:IC], s5[:, 0:IC], 1.0 / D, EPSQ, ALU.mult, ALU.max)
        go(V.tensor_scalar(s5[:, IC:IC + 1], s5[:, IC:IC + 1], 1.0 / HID, EPSQ, ALU.mult, ALU.max))
        go(V.reciprocal(i5[:], s5[:]))
        for c in range(IC):
            V.tensor_scalar(tf[:, c, :], wf[:, c, :], i5[:, c:c + 1], ROUND, ALU.mult, ALU.add)
        go(V.tensor_scalar(tp[:], wp[:], i5[:, IC:IC + 1], ROUND, ALU.mult, ALU.add))
        V.tensor_scalar(tf[:], tf[:], -ROUND, 1.0, ALU.add, ALU.min)
        go(V.tensor_scalar(tp[:], tp[:], -ROUND, 1.0, ALU.add, ALU.min))
        for c in range(IC):
            V.tensor_scalar(tf[:, c, :], tf[:, c, :], -1.0, s5[:, c:c + 1], ALU.max, ALU.mult)
        go(V.tensor_scalar(tp[:], tp[:], -1.0, s5[:, IC:IC + 1], ALU.max, ALU.mult))
        e.wait_ge(u_full.sem, u_full.at(1))
        V.tensor_copy(uT[0:R, :, :], ps[0:R, 0, :].rearrange("p (c f) -> p c f", c=IC)).then_inc(u_laid.sem, 1)
        e.wait_ge(t_full.sem, t_full.at(1))
        V.tensor_copy(fv[0:R, :], ps[0:R, 1, 0:D]).then_inc(t_laid.sem, 1)
        e.wait_ge(w_low.sem, w_low.at(1))
        V.scalar_tensor_tensor(tf[:], ps[:, 2, :].rearrange("p (c d) -> p c d", c=IC), gate[:], tf[:], ALU.mult, ALU.add).then_inc(w_ready.sem, 1)
        for i, dst in enumerate((wfT[:], wpT.rearrange("p c d -> p (c d)"))):
            e.wait_ge(w_turned.sem, w_turned.at(i + 1))
            V.tensor_scalar(dst, ps[:, 3 + i, :], 1.0 if i == 0 else k.gates[:, GATE:GATE + 1], None, ALU.mult).then_inc(w_laid.sem, 1)
        ln.dve_apply(e, 0, 0)

        def body(g, more):
            if more:
                ln.dve_stats(g + 1)
                e.wait_ge(ln.stats.sem, ln.stats.at(g + 2))
                e.nop(nofuse=True)
                ln.dve_aggregate(e, g + 1, True)
                e.wait_ge(xt_full.sem, xt_full.at(g + 1))
                e.nop(nofuse=True)
                ln.dve_apply(e, g + 1, g + 1)
            e.wait_ge(o_full.sem, o_full.at(g + 1))
            e.nop(nofuse=True)
            xg = k.x[:, bass.ts(g, GT), :]
            V.tensor_tensor(xg, ps[:, 3, :].rearrange("p (j d) -> p j d", j=GT), xg, ALU.add).then_inc(x_done.sem, 1)

        pipelined_groups(e, body)

    def pe(e):
        e.wait_ge(w_in.sem, w_in.at(96))
        e.wait_ge(before.sem, before.end)
        for c in range(IC):
            last = T.transpose(ps[0:R, 0, c * P:(c + 1) * P], un[:, c, :], k.ident[:])
        last.then_inc(u_full.sem, 1)
        T.matmul(ps[0:R, 1, 0:D], fbT[0:R, :], vn[0:R, :], start=True, stop=True).then_inc(t_full.sem, 1)
        e.wait_ge(u_laid.sem, u_laid.at(1))
        e.wait_ge(t_laid.sem, t_laid.at(1))
        for c in range(IC):
            last = T.matmul(ps[:, 2, c * P:(c + 1) * P], uT[0:R, c, :], fv[0:R, :], start=True, stop=True)
        last.then_inc(w_low.sem, 1)
        e.wait_ge(w_ready.sem, w_ready.at(1))
        for i in range(2):
            for c in range(IC):
                last = T.transpose(ps[:, 3 + i, c * P:(c + 1) * P], tf[:, c, :] if i == 0 else tp[:, c * P:(c + 1) * P], k.ident[:])
            last.then_inc(w_turned.sem, 1)
        e.wait_ge(w_laid.sem, w_laid.at(2))

        def turn(n):
            e.wait_ge(ln.out.sem, ln.out.at(n + 1))
            for j in range(GT):
                last = T.transpose(ps[:, 0, j * P:(j + 1) * P], k.xn[:, 0, j, :], k.ident[:])
            last.then_inc(xt_full.sem, 1)

        def hidden(g, c):
            if c == 0:
                e.wait_ge(xt_laid.sem, xt_laid.at(g + 1))
            T.matmul(ps[:, 1 + c % 2, :], wfT[:, c * P:(c + 1) * P], xnT, start=True, stop=True).then_inc(h_full.sem, 1)

        def outputs(g, c):
            e.wait_ge(h_laid.sem, h_laid.at(IC * g + c + 1))
            if c == 0:
                e.wait_ge(x_done.sem, x_done.at(g))
            for j in range(GT):
                last = T.matmul(ps[:, 3, j * P:(j + 1) * P], hT[:, c % 2, j * P:(j + 1) * P], wpT[:, c, :],
                                start=(c == 0 and j == 0), stop=(c == IC - 1 and j == GT - 1), skip_group_check=True)
            if c == IC - 1:
                last.then_inc(o_full.sem, 1)

        turn(0)

        def body(g, more):
            hidden(g, 0)
            hidden(g, 1)
            outputs(g, 0)
            hidden(g, 2)
            outputs(g, 1)
            hidden(g, 3)
            if more:
                turn(g + 1)
            outputs(g, 2)
            outputs(g, 3)

        pipelined_groups(e, body)

    def act(e):
        def turn_copy(n):
            e.wait_ge(xt_full.sem, xt_full.at(n + 1))
            S.copy(xnT, ps[:, 0, :]).then_inc(xt_laid.sem, 1)

        turn_copy(0)

        def body(g, more):
            for c in range(IC):
                e.wait_ge(h_full.sem, h_full.at(IC * g + c + 1))
                S.activation(r[:, c % 2, :], ps[:, 1 + c % 2, :], ACT.Relu).then_inc(r_done.sem, 1)
            if more:
                turn_copy(g + 1)

        pipelined_groups(e, body)

    def pool(e):
        e.wait_ge(before.sem, before.end)
        ln.pool_rstd(e, 0)

        def body(g, more):
            for c in range(IC):
                e.wait_ge(r_done.sem, r_done.at(IC * g + c + 1))
                nc.gpsimd.tensor_tensor(hT[:, c % 2, :], r[:, c % 2, :], r[:, c % 2, :], ALU.mult).then_inc(h_laid.sem, 1)
                if c == 0 and more:
                    ln.pool_rstd(e, g + 1)

        pipelined_groups(e, body)

    return dict(sp=sp, pe=pe, act=act, dve=dve, pool=pool)


def store(k, io):
    nc = k.nc
    out_done = k.sem("out_stored")
    before = k.x_ready

    def sp(e):
        e.wait_ge(before.sem, before.end)
        e.dma_start(io["out"].rearrange("b s c -> (b s) c").rearrange("(t p) c -> p t c", p=P), k.x[:]).then_inc(out_done.sem, 16)
        e.wait_ge(out_done.sem, out_done.at(16))

    return dict(sp=sp)


def build_program(nc, io, upto=99):
    with ExitStack() as ctx:
        k = allocate(nc, ctx)
        k.thresholds = Thresholds(k, io)
        k.ssm = StateSpaceKernel(k, io)
        new = k.semaphores.next_sublayer
        first, first_ready = setup(k, io)
        loaded = k.x_ready
        new()
        attn0, fold0 = attention(k, io, "a0", 16, "L0_xattn_Wq", "L0_xattn_Wk", "L0_xattn_Wv", "L0_xattn_Wo", "L0_xattn_bo", 0,
                                 None, 0, k.thresholds, k.ssm)
        attn0_done = k.x_ready
        new()
        ff0 = ffn0(k, io, loaded)
        new()
        attn1 = attention_ssm(k, io, attn0_done)
        attn1_done = k.x_ready
        new()
        ff1 = ffn1(k, io)
        new()
        attn2, fold2 = attention(k, io, "a2", 8, "L2_xattn_Wq", "L2_xattn_Wk", "L2_xattn_Wv", "L2_xattn_Wout", "L2_xattn_bout", 2,
                                 attn1_done, 0)
        attn2_done = k.x_ready
        new()
        ff2 = ffn2(k, io, attn1_done, 12300)
        new()
        attn3, fold3 = attention(k, io, "a3", 8, "L3_xattn_Wq", "L3_xattn_Wk", "L3_xattn_Wv", "L3_xattn_Wo", "L3_xattn_bo", 3,
                                 attn2_done, 0)
        new()
        ff3 = ffn3(k, io, attn1_done, 23700)
        queue = [first, dict(sp=k.thresholds.sp), first_ready, fold0, attn0, dict(sp=ff0.pop("sp")),
                 dict(dve=k.ssm.dve_sum, sp=k.ssm.sp_matrices), ff0, attn1, fold2, ff1, attn2, fold3, ff2, attn3, ff3,
                 store(k, io)]
        parts = queue[:upto]
        block = ctx.enter_context(nc.Block())

        @block.sync
        def _(e):
            for part in parts:
                if "sp" in part:
                    part["sp"](e)

        @block.tensor
        def _(e):
            for part in parts:
                if "pe" in part:
                    part["pe"](e)

        @block.scalar
        def _(e):
            for part in parts:
                if "act" in part:
                    part["act"](e)

        @block.vector
        def _(e):
            for part in parts:
                if "dve" in part:
                    part["dve"](e)

        @block.gpsimd
        def _(e):
            for part in parts:
                if "pool" in part:
                    part["pool"](e)


def kernel(**inputs):
    import numpy as np
    import concourse.bacc as bacc
    from concourse.bass_utils import run_bass_kernel_spmd

    nc = bacc.Bacc("TRN2", target_bir_lowering=False, num_devices=1)
    arrays, io = {}, {}
    for name, value in inputs.items():
        a = np.ascontiguousarray(value)
        if a.dtype == np.bool_:
            a = a.view(np.uint8)
        if a.ndim == 0:
            a = a.reshape(1)
        arrays[name] = a
        io[name] = nc.dram_tensor(name, a.shape, mybir.dt.from_np(a.dtype), kind="ExternalInput").ap()
    io["out"] = nc.dram_tensor("out", inputs["x"].shape, F32, kind="ExternalOutput").ap()
    build_program(nc, io)
    return run_bass_kernel_spmd(nc, [arrays], core_ids=[0]).results[0]["out"]
```

```python
from contextlib import ExitStack

import concourse.bass as bass
from concourse import mybir

ALU = mybir.AluOpType
ACT = mybir.ActivationFunctionType
AX = mybir.AxisListType
F32 = mybir.dt.float32
BF16 = mybir.dt.bfloat16
I32 = mybir.dt.int32
U8 = mybir.dt.uint8

P = 128
B, SEQ, D = 64, 64, 128
CTX, DC = 64, 96
TOK = B * SEQ
TILES = TOK // P
GT = 4
GROUPS = TILES // GT
BANK = 512
EPS = 1e-5
EPSQ = 1e-5
ROUND = 12582912.0


class Signal:

    def __init__(self, sem, base, total):
        self.sem, self.base, self.end = sem, base, base + (total or 1)

    def at(self, count):
        return self.base + (max(count, 0) if isinstance(count, int) else count)


class Semaphores:

    def __init__(self, new):
        self.new, self.spare, self.used = new, [], [[]]

    def next_sublayer(self):
        if len(self.used) > 1:
            self.spare += self.used[-2]
        self.used.append([])

    def take(self, name, total=None):
        sem, base = self.spare.pop(0) if total and self.spare else (self.new(name), 0)
        if total:
            self.used[-1].append((sem, base + total))
        return Signal(sem, base, total)


def pipelined_tiles(eng, step, tail=2):
    for t in (0, 1):
        step(t, t % 2)
    with eng.Fori(1, (TILES - tail) // 2) as it:
        step(2 * it, 0)
        step(2 * it + 1, 1)
    for t in range(TILES - tail, TILES):
        step(t, t % 2)


def pipelined_groups(eng, body, tail=1):
    body(0, True)
    with eng.Fori(1, GROUPS - tail) as g:
        body(g, True)
    for g in range(GROUPS - tail, GROUPS):
        body(g, g + 1 < GROUPS)


def group_ahead(g, n):
    return not isinstance(g, int) or g + n < GROUPS


def allocate(nc, ctx):
    k = Parts()
    k.nc = nc
    k.sb = lambda name, shape, dt=F32: ctx.enter_context(nc.sbuf_tensor(name, shape, dt))
    k.semaphores = Semaphores(lambda name: ctx.enter_context(nc.semaphore(name)))
    k.sem = k.semaphores.take
    k.ps = ctx.enter_context(nc.psum_tensor("ps", [P, 8, BANK], F32))
    k.x = k.sb("x_res", [P, TILES, D])
    k.ctxT = k.sb("ctxT", [P, TOK])
    k.ident = k.sb("ident", [P, P])
    k.onesq = k.sb("ones_square", [P, P])
    k.ones = k.onesq[0:1, :]
    k.gates = k.sb("gates", [P, 8])
    k.toep = k.sb("toeplitz", [P, D, SEQ])
    k.arena = k.sb("arena", [P, 30720])
    k.stat = k.sb("ln_stat", [P, 2, GT, 6])
    k.mv = k.sb("ln_mv", [P, 2, GT, 2])
    k.rstd = k.sb("ln_rstd", [P, 2, GT])
    k.veps = k.sb("ln_veps", [P, 2, GT])
    k.half = k.sb("minus_half", [P, GT])
    k.preload = k.sb("table_preload", [P, 1])
    k.eps = k.sb("eps", [P, GT])
    k.xn = k.sb("xn", [P, 2, GT, D])
    k.xnT = k.sb("xnT", [P, 2, GT * P])
    return k


class Parts:
    pass


class Carve:

    def __init__(self, space, start=0):
        self.space, self.at, self.size = space, start, space.shape[1]

    def cut(self, shape, dtype, per_word):
        n = 1
        for s in shape:
            n *= s
        v = self.space[:, self.at:self.at + n // per_word]
        self.at += n // per_word
        assert self.at <= self.size, self.at
        if dtype != F32:
            v = v.bitcast(dtype)
        if len(shape) == 1:
            return v
        names = " ".join(f"a{i}" for i in range(len(shape)))
        return v.rearrange(f"p ({names}) -> p {names}", **{f"a{i}": s for i, s in enumerate(shape[:-1])})

    def f32(self, *shape):
        return self.cut(shape, F32, 1)

    def bf16(self, *shape):
        return self.cut(shape, BF16, 2)


def setup(k, io):
    nc = k.nc
    c_in, g_in, zero, made, turned, laid, tanh = (k.sem("setup_" + n) for n in (
        "ctx_loaded", "gates_loaded", "zeroed", "constants", "ctx_turned", "ctx_laid", "gates_ready"))
    x_in, ready = k.sem("setup_x_loaded"), k.sem("setup_done", 1)
    carve = Carve(k.arena, 24032)
    ctx_tok = carve.f32(TILES, DC)
    graw = carve.f32(8)

    def sp(e):
        e.dma_start(ctx_tok[:], io["ctx_768"].rearrange("b s c -> (b s) c").rearrange("(t p) c -> p t c", p=P)).then_inc(c_in.sem, 16)

    def sp_rest(e):
        e.dma_start(graw[:, 0:4], io["g_xattn"].rearrange("(a n) -> a n", a=1).partition_broadcast(P)).then_inc(g_in.sem, 16)
        e.dma_start(graw[:, 4:8], io["g_ffn"].rearrange("(a n) -> a n", a=1).partition_broadcast(P)).then_inc(g_in.sem, 16)
        k.ssm.sp_load(e)
        e.dma_start(k.x[:], io["x"].rearrange("b s c -> (b s) c").rearrange("(t p) c -> p t c", p=P)).then_inc(x_in.sem, 16)

    def pool(e):
        nc.gpsimd.memset(k.ident[:], 0.0).then_inc(zero.sem, 1)
        e.wait_ge(zero.sem, zero.at(1))
        nc.gpsimd.affine_select(out=k.ident[:], in_=k.ident[:], compare_op=ALU.not_equal, fill=1.0, base=0,
                                pattern=[[-1, P]], channel_multiplier=1).then_inc(made.sem, 1)
        nc.gpsimd.memset(k.onesq[:], 1.0).then_inc(zero.sem, 1)
        e.wait_ge(zero.sem, zero.at(2))
        nc.gpsimd.memset(k.half[:], -0.5).then_inc(zero.sem, 1)
        e.wait_ge(zero.sem, zero.at(3))
        nc.gpsimd.memset(k.eps[:], EPS).then_inc(zero.sem, 1)
        e.wait_ge(zero.sem, zero.at(4))
        nc.gpsimd.memset(k.ctxT[DC:P, :], 0.0).then_inc(zero.sem, 1)
        e.wait_ge(zero.sem, zero.at(5))
        nc.gpsimd.memset(k.ctxT[DC:DC + 1, :], 1.0).then_inc(zero.sem, 1)
        e.wait_ge(zero.sem, zero.at(6))

    def pool_ready(e):
        e.wait_ge(x_in.sem, x_in.at(16))
        e.wait_ge(laid.sem, laid.at(TILES // 4))
        e.wait_ge(made.sem, made.at(1))
        e.wait_ge(tanh.sem, tanh.at(1))
        e.sem_inc(ready.sem, 1)

    def pe(e):
        e.wait_ge(made.sem, made.at(1))
        e.wait_ge(c_in.sem, c_in.at(16))
        for n in range(TILES // 4):
            e.wait_ge(laid.sem, laid.at(n - 7))
            for j in range(4):
                last = nc.tensor.transpose(k.ps[0:DC, n % 8, j * P:(j + 1) * P], ctx_tok[:, 4 * n + j, :], k.ident[:])
            last.then_inc(turned.sem, 1)

    def dve(e):
        k.ssm.dve_start(e)

    def act(e):
        for n in range(TILES // 4):
            e.wait_ge(turned.sem, turned.at(n + 1))
            nc.scalar.copy(k.ctxT[0:DC, n * BANK:(n + 1) * BANK], k.ps[0:DC, n % 8, :]).then_inc(laid.sem, 1)
        k.ssm.act_magnitude(e)
        k.ssm.act_angle(e)
        e.wait_ge(g_in.sem, g_in.at(32))
        nc.scalar.activation(k.gates[:], graw[:], ACT.Tanh).then_inc(tanh.sem, 1)

    k.gates_ready = tanh
    k.x_ready = ready
    k.context_laid, k.context_tiles = laid, TILES // 4
    return dict(sp=sp, pool=pool, pe=pe, dve=dve, act=act), dict(pool=pool_ready), dict(sp=sp_rest)


def attention(k, io, name, heads, wq, wk, wv, wo, bo, gate, freed, start, inputs=None, inputs_freed=None, aside=None, rounds=None, ssm=None):
    nc, gates_ready = k.nc, k.gates_ready
    DH = 64
    SCALE = DH ** -0.5
    C = heads // 2
    INNER = heads * DH
    NG = heads // 4
    SB = heads * CTX // BANK
    ROOM = SB == 1
    YBANK = 5 if ROOM else 2
    sem = lambda n, total=TILES: k.sem(f"{name}_{n}", total)
    w_in, w_turned, w_laid = sem("w_loaded", None), sem("w_turned", 3 * C // 4), sem("w_laid", 3 * C // 4)
    w_made, w_copied, rows_zeroed = sem("w_folded", 2 * (heads // 4) + 1), sem("w_fold_copied", heads // 4), sem("rows_zeroed", 2)
    st_done, mv_done, ve_done, rs_done, xn_done = (sem("ln_" + n) for n in ("stats", "mv", "veps", "rstd", "xn"))
    xt_full, xt_laid = sem("xnT_full"), sem("xnT_laid")
    g_full, g_laid = sem("g_full", NG * TILES), sem("g_laid", NG * TILES)
    s_full, s_max, s_sub, s_exp = sem("scores"), sem("max"), sem("shifted"), sem("exp")
    s_sum, s_rec, s_prob = sem("sum"), sem("recip"), sem("probs")
    p_full, p_laid = sem("probsT_full"), sem("probsT_laid")
    v_full, v0_laid, v1_laid = sem("v_full", 2 * TILES), sem("v0_laid"), sem("v1_laid")
    y_full, x_done = sem("y_full"), sem("x_done")
    c_laid = sem("ctx_tile")

    cv = Carve(k.arena, start)
    inputs = inputs or cv
    w_qk = inputs.f32(2, INNER)
    w_v = inputs.f32(INNER)
    w_o = inputs.f32(C, D)
    bo_row = inputs.f32(D)
    w_T = cv.f32(3, C, P)
    mT = cv.f32(heads, D)
    mT_pair = mT.rearrange("p (c m) d -> p c m d", m=2)
    wvo = cv.f32(2, C, D)
    G = cv.f32(2, heads, P)
    VW = cv.f32(2, 2, C, D)
    PR = cv.f32(2, heads, CTX)
    PT = cv.f32(2, C, P)
    cg = cv.f32(2, P)
    mx = cv.f32(2, heads)
    sm = cv.f32(2, heads)
    rc = cv.f32(2, heads)
    ps = k.ps
    before = k.x_ready
    k.x_ready = x_done
    pairs = 3 * C

    def sp(e):
        if inputs_freed:
            e.wait_ge(inputs_freed.sem, inputs_freed.end)
        e.dma_start(w_qk[:, 0, :], io[wq]).then_inc(w_in.sem, 16)
        e.dma_start(w_qk[0:DC, 1, :], io[wk]).then_inc(w_in.sem, 16)
        e.dma_start(w_v[0:DC, :], io[wv]).then_inc(w_in.sem, 16)
        e.dma_start(w_o[:], io[wo].rearrange("(c p) d -> p c d", p=P)).then_inc(w_in.sem, 16)
        e.dma_start(bo_row[DC:DC + 1, :], io[bo].rearrange("(a d) -> a d", a=1)).then_inc(w_in.sem, 16)

    def fold_pe(e):
        e.wait_ge(k.context_laid.sem, k.context_laid.at(k.context_tiles))
        if freed:
            e.wait_ge(freed.sem, freed.end)
        e.wait_ge(w_in.sem, w_in.at(80))
        for n in range(pairs):
            which, c = divmod(n, C)
            if n % 4 == 0:
                e.wait_ge(w_laid.sem, w_laid.at(n // 4 - 3))
            if which == 0:
                last = nc.tensor.transpose(ps[:, n // 4 % 4, (n % 4) * P:(n % 4 + 1) * P], w_qk[:, 0, c * P:(c + 1) * P], k.ident[:])
            else:
                src = w_qk[0:DC, 1, c * P:(c + 1) * P] if which == 1 else w_v[0:DC, c * P:(c + 1) * P]
                last = nc.tensor.transpose(ps[:, n // 4 % 4, (n % 4) * P:(n % 4) * P + DC], src, k.ident[0:DC, 0:DC])
            if n % 4 == 3:
                last.then_inc(w_turned.sem, 1)
        e.wait_ge(w_laid.sem, w_laid.at(pairs // 4))
        for q in range(heads // 4):
            fold_v, q0 = divmod(q, C // 4)
            e.wait_ge(w_made.sem, w_made.at(2 * q - 2))
            for j in range(4):
                for m in range(2):
                    c, rows = 4 * q0 + j, slice(64 * m, 64 * m + 64)
                    last = nc.tensor.matmul(ps[0:DC, 4 + (2 * q + m) % 4, j * P:(j + 1) * P],
                                            w_T[rows, 2 if fold_v else 1, c, 0:DC],
                                            w_o[rows, c, :] if fold_v else w_T[rows, 0, c, :], start=True, stop=True)
            last.then_inc(w_copied.sem, 1)
        e.wait_ge(w_made.sem, w_made.at(2 * (heads // 4)))

    def fold_pool(e):
        if freed:
            e.wait_ge(freed.sem, freed.end)
        nc.gpsimd.memset(mT[DC:P, :, :], 0.0).then_inc(rows_zeroed.sem, 1)
        e.wait_ge(rows_zeroed.sem, rows_zeroed.at(1))
        nc.gpsimd.memset(wvo[DC:P, :, :, :], 0.0).then_inc(rows_zeroed.sem, 1)
        e.wait_ge(rows_zeroed.sem, rows_zeroed.at(2))

    def fold_act(e):
        for n in range(pairs // 4):
            e.wait_ge(w_turned.sem, w_turned.at(n + 1))
            c0 = 4 * n % C
            src = ps[:, n % 4, :].rearrange("p (c d) -> p c d", c=4)
            if 4 * n < C:
                nc.scalar.copy(w_T[:, 0, c0:c0 + 4, :], src).then_inc(w_laid.sem, 1)
            else:
                nc.scalar.copy(w_T[:, 4 * n // C, c0:c0 + 4, 0:DC], src[:, :, 0:DC]).then_inc(w_laid.sem, 1)
        e.wait_ge(gates_ready.sem, gates_ready.end)
        for q in range(heads // 4):
            fold_v, q0 = divmod(q, C // 4)
            e.wait_ge(w_copied.sem, w_copied.at(q + 1))
            for m in range(2):
                src = ps[0:DC, 4 + (2 * q + m) % 4, :].rearrange("p (c d) -> p c d", c=4)
                if fold_v:
                    nc.scalar.activation(wvo[0:DC, m, 4 * q0:4 * q0 + 4, :], src, ACT.Copy,
                                         scale=k.gates[0:DC, gate:gate + 1]).then_inc(w_made.sem, 1)
                else:
                    nc.scalar.copy(mT_pair[0:DC, 4 * q0:4 * q0 + 4, m, :], src).then_inc(w_made.sem, 1)
        e.wait_ge(rows_zeroed.sem, rows_zeroed.at(2))
        nc.scalar.activation(wvo[DC:DC + 1, 0, 0, :], bo_row[DC:DC + 1, :], ACT.Copy,
                             scale=k.gates[DC:DC + 1, gate:gate + 1]).then_inc(w_made.sem, 1)

    FOLDED = 2 * (heads // 4) + 1

    def ln_stats(e, t, s):
        nc.vector.bn_stats(k.stat[:, s, 0, :], k.x[:, t, :]).then_inc(st_done.sem, 1)

    def ln_aggr(e, t, s):
        nc.vector.bn_aggr(k.mv[:, s, 0, :], k.stat[:, s, 0, :]).then_inc(mv_done.sem, 1)

    def ln_apply(e, t, s):
        e.wait_ge(rs_done.sem, rs_done.at(t + 1))
        nc.vector.tensor_scalar(k.xn[:, s, 0, :], k.x[:, t, :], k.mv[:, s, 0, 0:1], k.rstd[:, s, 0:1],
                                ALU.subtract, ALU.mult).then_inc(xn_done.sem, 1)

    def ln_pool(e, t, s):
        e.wait_ge(mv_done.sem, mv_done.at(t + 1))
        nc.gpsimd.tensor_tensor(k.veps[:, s, 0:1], k.mv[:, s, 0, 1:2], k.eps[:, 0:1], ALU.add).then_inc(ve_done.sem, 1)
        e.wait_ge(ve_done.sem, ve_done.at(t + 1))
        nc.gpsimd.tensor_tensor(k.rstd[:, s, 0:1], k.veps[:, s, 0:1], k.half[:, 0:1], ALU.pow).then_inc(rs_done.sem, 1)

    def more(t, ahead):
        return not isinstance(t, int) or t + ahead < TILES

    def g_product(e, t, s, n):
        if n == 0:
            e.wait_ge(c_laid.sem, c_laid.at(t + 1))
        e.wait_ge(g_laid.sem, g_laid.at(NG * t + n - 1))
        for j in range(4):
            last = nc.tensor.matmul(ps[:, n % 2, j * P:(j + 1) * P], mT[:, 4 * n + j, :], cg[:, s, :], start=True, stop=True)
        last.then_inc(g_full.sem, 1)

    def xn_turn(e, t, s):
        e.wait_ge(xn_done.sem, xn_done.at(t + 1))
        nc.tensor.transpose(ps[:, 3, 0:P], k.xn[:, s, 0, :], k.ident[:]).then_inc(xt_full.sem, 1)

    def v_product(e, t, s, b):
        if SB == 2:
            laid, count = (v1_laid, t) if b == 0 else (v0_laid, t + 1)
        else:
            laid, count = (v0_laid, t) if b == 0 else (v1_laid, t)
        e.wait_ge(laid.sem, laid.at(count))
        for n in range(C * D // BANK):
            for m in range(2):
                bank = 6 + n if SB == 2 else 6 + b
                last = nc.tensor.matmul(ps[64 * m:64 * m + 64, bank, :], cg[:, s, b * CTX:(b + 1) * CTX],
                                        wvo[:, m, 4 * n:4 * n + 4, :], start=True, stop=True)
        last.then_inc(v_full.sem, 1)

    def pe_y(e, t, s):
        e.wait_ge(p_laid.sem, p_laid.at(t + 1))
        e.wait_ge(v0_laid.sem, v0_laid.at(t + 1))
        e.wait_ge(v1_laid.sem, v1_laid.at(t + 1))
        if ROOM:
            e.wait_ge(x_done.sem, x_done.at(t))
        if rounds and more(t, 1):
            rounds.pe_total(e, t)
        for c in range(C):
            for b in range(2):
                last = nc.tensor.matmul(ps[64 * b:64 * b + 64, YBANK, 0:D], PT[:, s, c, 64 * b:64 * b + 64], VW[:, s, b, c, :],
                                        start=(c == 0), stop=(c == C - 1))
        last.then_inc(y_full.sem, 1)

    def pe_step(e, t, s):
        o = 1 - s
        e.wait_ge(g_laid.sem, g_laid.at(NG * (t + 1)))
        e.wait_ge(xt_laid.sem, xt_laid.at(t + 1))
        e.wait_ge(s_sub.sem, s_sub.at(t))
        for n in range(SB):
            for b in range(2):
                last = nc.tensor.matmul(ps[64 * b:64 * b + 64, 4 + n, :], k.xnT[:, s, 64 * b:64 * b + 64],
                                        G[:, s, 8 * n:8 * n + 8, b * CTX:(b + 1) * CTX], start=True, stop=True)
        last.then_inc(s_full.sem, 1)
        v_product(e, t, s, 0)
        if more(t, 1):
            for n in range(NG // 2):
                g_product(e, t + 1, o, n)
        v_product(e, t, s, 1)
        if ROOM and more(t, 1):
            for n in range(NG // 2, NG):
                g_product(e, t + 1, o, n)
        if not (isinstance(t, int) and t == 0):
            pe_y(e, t - 1, o)
        if more(t, 1):
            xn_turn(e, t + 1, o)
        if not ROOM and more(t, 1):
            for n in range(NG // 2, NG):
                g_product(e, t + 1, o, n)
        e.wait_ge(s_prob.sem, s_prob.at(t + 1))
        if not ROOM:
            e.wait_ge(x_done.sem, x_done.at(t))
        if rounds:
            e.wait_ge(rounds.read.sem, rounds.read.at(t))
        if not ROOM and more(t, 1):
            e.wait_ge(xt_laid.sem, xt_laid.at(t + 2))
        for c in range(C):
            last = nc.tensor.transpose(ps[:, 2 + c // 4, c % 4 * P:(c % 4 + 1) * P], PR[:, s, 2 * c:2 * c + 2, :], k.ident[:])
        last.then_inc(p_full.sem, 1)

    def pe(e):
        e.wait_ge(before.sem, before.end)
        e.wait_ge(w_made.sem, w_made.at(FOLDED))
        for n in range(NG):
            g_product(e, 0, 0, n)
        xn_turn(e, 0, 0)
        pipelined_tiles(e, lambda t, s: pe_step(e, t, s))
        pe_y(e, TILES - 1, 1)

    def g_copy(e, t, s, n):
        e.wait_ge(g_full.sem, g_full.at(NG * t + n + 1))
        nc.scalar.copy(G[:, s, 4 * n:4 * n + 4, :], ps[:, n % 2, :].rearrange("p (h j) -> p h j", h=4)).then_inc(g_laid.sem, 1)

    def xn_copy(e, t, s):
        e.wait_ge(xt_full.sem, xt_full.at(t + 1))
        nc.scalar.copy(k.xnT[:, s, 0:P], ps[:, 3, 0:P]).then_inc(xt_laid.sem, 1)

    def act_step(e, t, s):
        o = 1 - s
        e.wait_ge(s_sub.sem, s_sub.at(t + 1))
        nc.scalar.activation(PR[:, s, :, :], PR[:, s, :, :], ACT.Exp, scale=SCALE).then_inc(s_exp.sem, 1)
        if more(t, 1):
            for n in range(NG // 2):
                g_copy(e, t + 1, o, n)
        e.wait_ge(v_full.sem, v_full.at(2 * t + 2))
        src = ps[:, 6:8, :] if SB == 2 else ps[:, 7, :]
        dst = VW[:, s, 1, :, :].rearrange("p c d -> p (c d)")
        if SB == 2:
            dst = dst.rearrange("p (n w) -> p n w", n=2)
        nc.scalar.copy(dst, src).then_inc(v1_laid.sem, 1)
        if more(t, 1):
            if not ROOM:
                xn_copy(e, t + 1, o)
            for n in range(NG // 2, NG):
                g_copy(e, t + 1, o, n)
            if ROOM:
                xn_copy(e, t + 1, o)
        e.wait_ge(p_full.sem, p_full.at(t + 1))
        dst = PT[:, s, :, :].rearrange("p c q -> p (c q)")
        if SB == 2:
            nc.scalar.copy(dst.rearrange("p (n w) -> p n w", n=2), ps[:, 2:4, :]).then_inc(p_laid.sem, 1)
        else:
            nc.scalar.copy(dst, ps[:, 2, :]).then_inc(p_laid.sem, 1)

    def act(e):
        e.wait_ge(before.sem, before.end)
        for n in range(NG):
            g_copy(e, 0, 0, n)
        xn_copy(e, 0, 0)
        pipelined_tiles(e, lambda t, s: act_step(e, t, s))

    def dve_add(e, t):
        e.wait_ge(y_full.sem, y_full.at(t + 1))
        nc.vector.tensor_tensor(k.x[:, t, :], ps[:, YBANK, 0:D], k.x[:, t, :], ALU.add).then_inc(x_done.sem, 1)

    def dve_step(e, t, s):
        S = ps[:, 4:4 + SB, :].rearrange("p n (h j) -> p (n h) j", j=CTX)
        if more(t, 2):
            ln_stats(e, t + 2, s)
        e.wait_ge(s_full.sem, s_full.at(t + 1))
        nc.vector.tensor_reduce(mx[:, s, :], S, AX.X, ALU.max).then_inc(s_max.sem, 1)
        e.wait_ge(s_max.sem, s_max.at(t + 1))
        nc.vector.tensor_tensor(PR[:, s, :, :], S, mx[:, s, :].unsqueeze(2).to_broadcast([P, heads, CTX]), ALU.subtract).then_inc(s_sub.sem, 1)
        if more(t, 2):
            ln_aggr(e, t + 2, s)
        e.wait_ge(v_full.sem, v_full.at(2 * t + 1))
        src = ps[:, 6:8, :] if SB == 2 else ps[:, 6, :]
        dst = VW[:, s, 0, :, :].rearrange("p c d -> p (c d)")
        if SB == 2:
            dst = dst.rearrange("p (n w) -> p n w", n=2)
        nc.vector.tensor_copy(dst, src).then_inc(v0_laid.sem, 1)
        e.wait_ge(s_exp.sem, s_exp.at(t + 1))
        nc.vector.tensor_reduce(sm[:, s, :], PR[:, s, :, :], AX.X, ALU.add).then_inc(s_sum.sem, 1)
        if more(t, 2):
            ln_apply(e, t + 2, s)
        e.wait_ge(s_sum.sem, s_sum.at(t + 1))
        nc.vector.reciprocal(rc[:, s, :], sm[:, s, :]).then_inc(s_rec.sem, 1)
        if not (isinstance(t, int) and t == 0):
            dve_add(e, t - 1)
        if rounds:
            rounds.dve_round(e, t)

    def dve(e):
        if rounds:
            rounds.dve_start(e)
        e.wait_ge(before.sem, before.end)
        for t in range(2):
            ln_stats(e, t, t)
        e.wait_ge(st_done.sem, st_done.at(2))
        for t in range(2):
            ln_aggr(e, t, t)
        for t in range(2):
            ln_apply(e, t, t)

        def step(t, s):
            dve_step(e, t, s)
            if aside and isinstance(t, int) and t == 1:
                aside(e)

        pipelined_tiles(e, step)
        dve_add(e, TILES - 1)

    def ctx_copy(e, t, s):
        nc.gpsimd.tensor_copy(cg[:, s, :], k.ctxT[:, bass.ts(t, P)]).then_inc(c_laid.sem, 1)

    def pool_step(e, t, s):
        if more(t, 2):
            ln_pool(e, t + 2, s)
        e.wait_ge(s_rec.sem, s_rec.at(t + 1))
        nc.gpsimd.tensor_tensor(PR[:, s, :, :], PR[:, s, :, :], rc[:, s, :].unsqueeze(2).to_broadcast([P, heads, CTX]),
                                ALU.mult).then_inc(s_prob.sem, 1)
        if more(t, 2):
            e.wait_ge(v_full.sem, v_full.at(2 * t + 2))
            ctx_copy(e, t + 2, s)
        if ssm:
            ssm.pool_pair(e, t)

    def pool(e):
        e.wait_ge(before.sem, before.end)
        for t in range(2):
            ctx_copy(e, t, t)
        for t in range(2):
            ln_pool(e, t, t)
        pipelined_tiles(e, lambda t, s: pool_step(e, t, s))

    return dict(pe=pe, act=act, dve=dve, pool=pool), dict(sp=sp, pe=fold_pe, act=fold_act, pool=fold_pool)


class GroupNorm:

    def __init__(self, k, name, slot, src, dst):
        self.k, self.s, self.src, self.dst = k, slot, src, dst
        self.stats, self.mv, self.ve, self.rs, self.out = (k.sem(f"{name}_{n}", GROUPS) for n in ("stats", "mv", "veps", "rstd", "normed"))

    def dve_stats(self, g):
        k = self.k
        for j in range(GT):
            last = k.nc.vector.bn_stats(k.stat[:, self.s, j, :], self.src(g, j))
        last.then_inc(self.stats.sem, 1)

    def dve_aggregate(self, e, n, covered):
        k = self.k
        if not covered:
            e.wait_ge(self.stats.sem, self.stats.at(n + 1))
        for j in range(GT):
            last = k.nc.vector.bn_aggr(k.mv[:, self.s, j, :], k.stat[:, self.s, j, :])
        last.then_inc(self.mv.sem, 1)

    def pool_rstd(self, e, n):
        k = self.k
        e.wait_ge(self.mv.sem, self.mv.at(n + 1))
        k.nc.gpsimd.tensor_tensor(k.veps[:, self.s, :], k.mv[:, self.s, :, 1], k.eps[:], ALU.add).then_inc(self.ve.sem, 1)
        e.wait_ge(self.ve.sem, self.ve.at(n + 1))
        k.nc.gpsimd.tensor_tensor(k.rstd[:, self.s, :], k.veps[:, self.s, :], k.half[:], ALU.pow).then_inc(self.rs.sem, 1)

    def dve_apply(self, e, g, n):
        k = self.k
        e.wait_ge(self.rs.sem, self.rs.at(n + 1))
        for j in range(GT):
            last = k.nc.vector.tensor_scalar(self.dst(g, j), self.src(g, j), k.mv[:, self.s, j, 0:1], k.rstd[:, self.s, j:j + 1],
                                             ALU.subtract, ALU.mult)
        last.then_inc(self.out.sem, 1)


def experts(k, io, name, top1, gate, loads, freed, weights, work, prepare=None, aside=None):
    nc = k.nc
    E, C = (8, 1) if top1 else (2, 4)
    U = E * C
    NR = 8
    GELU = ACT.Gelu if top1 else ACT.Gelu_apprx_tanh
    sem = lambda n, total=GROUPS: k.sem(f"{name}_{n}", total)
    w_in, made, xt_full, xt_laid = sem("w_loaded", None), sem("constants", 1), sem("xT_full"), sem("xT_laid")
    h_full, h_laid = sem("h_full", U * GROUPS), sem("h_laid", U * GROUPS)
    o_full, o_used = sem("o_full", E * GROUPS), sem("o_used", E * GROUPS)
    l_full, l_laid, lt_full = sem("logits"), sem("logits_laid"), sem("logitsT")
    r_max, r_shift, r_exp, r_sum, r_w = (sem(n) for n in ("r_max", "r_shift", "r_exp", "r_sum", "r_weights"))
    r_step = sem("r_step", (5 if top1 else 3) * GROUPS)
    wt_full, wt_laid, b_full, x_done = sem("weightsT"), sem("weightsT_laid"), sem("bias_full"), sem("x_done")
    if not top1:
        r2_full, r2_laid = sem("router_in_full"), sem("router_in_laid")

    cv, wk = weights, work
    w1 = cv.f32(E, C * P)
    w2 = cv.f32(E, C, D)
    b1 = cv.f32(E, C)
    b2 = cv.f32(D)
    wr = cv.f32(NR)
    br = cv.f32(1)
    hT = wk.f32(3, GT * P)
    lT = wk.f32(GT * P)
    wT = wk.f32(GT * P)
    rank = wk.f32(NR)
    m4, s4, r4 = wk.f32(GT), wk.f32(GT), wk.f32(GT)
    ex, eq, rk, oh = (wk.f32(GT, NR) for _ in range(4))
    rm = wk.f32(GT)
    wgt = wk.f32(GT, E)
    gam, bet = cv.f32(1), cv.f32(1)
    ln2T = wk.f32(GT * P)
    xnT = k.xnT[:, 0, :]
    ps = k.ps
    before = k.x_ready
    k.x_ready = x_done
    ln = GroupNorm(k, name + "_ln", 0, lambda g, j: k.x[:, 4 * g + j, :], lambda g, j: k.xn[:, 0, j, :])
    ln2 = None if top1 else GroupNorm(k, name + "_ln2", 1, lambda g, j: k.xn[:, 0, j, :], lambda g, j: k.xn[:, 1, j, :])
    v = Parts()
    v.w1, v.w2, v.b1, v.b2, v.wr, v.br, v.gam, v.bet, v.cv, v.w_in = w1, w2, b1, b2, wr, br, gam, bet, cv, w_in
    n_loads = v.loads = loads(k, io, v)
    prep = prepare(k, io, v) if prepare else {}

    def sp(e):
        e.wait_ge(freed.sem, freed.end)
        for dst, src in n_loads:
            with nc.allow_non_contiguous_dma(reason="biases are small"):
                e.dma_start(dst, src).then_inc(w_in.sem, 16)

    READY = 16 * len(n_loads)

    def turn_x(e, n):
        e.wait_ge(ln.out.sem, ln.out.at(n + 1))
        e.wait_ge(xt_laid.sem, xt_laid.at(n))
        if not top1:
            e.wait_ge(r2_laid.sem, r2_laid.at(n))
        for j in range(GT):
            last = nc.tensor.transpose(ps[:, 5, j * P:(j + 1) * P], k.xn[:, 0, j, :], k.ident[:])
        last.then_inc(xt_full.sem, 1)

    def turn_router_in(e, n):
        e.wait_ge(ln2.out.sem, ln2.out.at(n + 1))
        e.wait_ge(xt_laid.sem, xt_laid.at(n + 1))
        for j in range(GT):
            last = nc.tensor.transpose(ps[:, 5, j * P:(j + 1) * P], k.xn[:, 1, j, :], k.ident[:])
        last.then_inc(r2_full.sem, 1)

    def logits(e, n):
        if top1:
            e.wait_ge(xt_laid.sem, xt_laid.at(n + 1))
        else:
            e.wait_ge(r2_laid.sem, r2_laid.at(n + 1))
        e.wait_ge(r_sum.sem, r_sum.at(n))
        nc.tensor.matmul(ps[0:NR, 6, :], wr[:], xnT if top1 else ln2T[:], start=True, stop=True).then_inc(l_full.sem, 1)

    def turn_logits(e, n):
        for j in range(GT):
            last = nc.tensor.transpose(ps[:, 6, j * NR:(j + 1) * NR], lT[0:NR, j * P:(j + 1) * P], k.ident[0:NR, 0:NR])
        last.then_inc(lt_full.sem, 1)

    def hidden(e, g, u):
        if u == 0:
            e.wait_ge(xt_laid.sem, xt_laid.at(g + 1))
        x, c = divmod(u, C)
        nc.tensor.matmul(ps[:, u % 3, :], w1[:, x, c * P:(c + 1) * P], xnT, start=True, stop=True).then_inc(h_full.sem, 1)

    def outputs(e, g, u):
        x, c = divmod(u, C)
        e.wait_ge(h_laid.sem, h_laid.at(U * g + u + 1))
        if c == 0:
            e.wait_ge(o_used.sem, o_used.at(E * g + max(x - 1, 0)))
        for j in range(GT):
            last = nc.tensor.matmul(ps[:, 3 + x % 2, j * P:(j + 1) * P], hT[:, u % 3, j * P:(j + 1) * P], w2[:, x, c, :],
                                    start=(c == 0 and j == 0), stop=(c == C - 1 and j == GT - 1), skip_group_check=True)
        if c == C - 1:
            last.then_inc(o_full.sem, 1)

    def bias_term(e, g):
        e.wait_ge(r_w.sem, r_w.at(g + 1))
        e.wait_ge(x_done.sem, x_done.at(g))
        for j in range(GT):
            last = nc.tensor.transpose(ps[0:E, 7, j * P:(j + 1) * P], wgt[:, j, :], k.ident[:])
        last.then_inc(wt_full.sem, 1)

    def bias_term2(e, g):
        e.wait_ge(wt_laid.sem, wt_laid.at(g + 1))
        for j in range(GT):
            last = nc.tensor.matmul(ps[:, 7, j * P:(j + 1) * P], wT[0:E, j * P:(j + 1) * P], b2[0:E, :], start=True, stop=True)
        last.then_inc(b_full.sem, 1)

    def pe(e):
        if "pe" in prep:
            prep["pe"](e)
        e.wait_ge(w_in.sem, w_in.at(READY))
        turn_x(e, 0)
        if not top1:
            turn_router_in(e, 0)
        logits(e, 0)

        def body(g, more):
            hidden(e, g, 0)
            e.wait_ge(l_laid.sem, l_laid.at(g + 1))
            hidden(e, g, 1)
            turn_logits(e, g)
            for u in range(2, U):
                hidden(e, g, u)
                if u == U - 1 and more:
                    turn_x(e, g + 1)
                if u == 5:
                    bias_term(e, g)
                outputs(e, g, u - 2)
                if u == 6:
                    bias_term2(e, g)
            outputs(e, g, U - 2)
            if more and top1:
                logits(e, g + 1)
            outputs(e, g, U - 1)
            if more and not top1:
                turn_router_in(e, g + 1)
                logits(e, g + 1)

        pipelined_groups(e, body)

    def act(e):
        if "act" in prep:
            prep["act"](e)
        e.wait_ge(w_in.sem, w_in.at(READY))

        def copy_x(n):
            e.wait_ge(xt_full.sem, xt_full.at(n + 1))
            nc.scalar.copy(xnT, ps[:, 5, :]).then_inc(xt_laid.sem, 1)

        def copy_router_in(n):
            e.wait_ge(r2_full.sem, r2_full.at(n + 1))
            nc.scalar.activation(ln2T[:], ps[:, 5, :], ACT.Identity, bias=bet[:], scale=gam[:]).then_inc(r2_laid.sem, 1)

        def copy_logits(n):
            e.wait_ge(l_full.sem, l_full.at(n + 1))
            nc.scalar.activation(lT[0:NR, :], ps[0:NR, 6, :], ACT.Identity, bias=br[0:NR, :]).then_inc(l_laid.sem, 1)

        copy_x(0)
        if not top1:
            copy_router_in(0)
        copy_logits(0)

        def body(g, more):
            for u in range(U):
                if u == 2:
                    e.wait_ge(r_shift.sem, r_shift.at(g + 1))
                    nc.scalar.activation(ex[:], ex[:], ACT.Exp).then_inc(r_exp.sem, 1)
                if u == 5:
                    e.wait_ge(wt_full.sem, wt_full.at(g + 1))
                    nc.scalar.copy(wT[0:E, :], ps[0:E, 7, :]).then_inc(wt_laid.sem, 1)
                x, c = divmod(u, C)
                e.wait_ge(h_full.sem, h_full.at(U * g + u + 1))
                nc.scalar.activation(hT[:, u % 3, :], ps[:, u % 3, :], GELU, bias=b1[:, x, c:c + 1]).then_inc(h_laid.sem, 1)
            if more:
                copy_x(g + 1)
                if not top1:
                    copy_router_in(g + 1)
                copy_logits(g + 1)

        pipelined_groups(e, body)

    def dve(e):
        e.wait_ge(before.sem, before.end)
        e.wait_ge(w_in.sem, w_in.at(READY))
        steps = 5 if top1 else 3
        scaled = steps - 1 if top1 else 1

        def spread(v):
            return v.unsqueeze(2).to_broadcast([P, GT, NR])

        def router(g):
            L = ps[:, 6, 0:GT * NR].rearrange("p (j r) -> p j r", r=NR)
            e.wait_ge(lt_full.sem, lt_full.at(g + 1))
            nc.vector.tensor_reduce(m4[:], L, AX.X, ALU.max).then_inc(r_max.sem, 1)
            e.wait_ge(r_max.sem, r_max.at(g + 1))
            nc.vector.tensor_tensor(ex[:], L, spread(m4), ALU.subtract).then_inc(r_shift.sem, 1)
            if top1:
                nc.vector.tensor_tensor(eq[:], L, spread(m4), ALU.is_equal).then_inc(r_step.sem, 1)
                e.wait_ge(r_step.sem, r_step.at(steps * g + 1))
                nc.vector.tensor_tensor(rk[:], eq[:], rank.unsqueeze(1).to_broadcast([P, GT, NR]), ALU.mult).then_inc(r_step.sem, 1)
                e.wait_ge(r_step.sem, r_step.at(steps * g + 2))
                nc.vector.tensor_reduce(rm[:], rk[:], AX.X, ALU.max).then_inc(r_step.sem, 1)
                e.wait_ge(r_step.sem, r_step.at(steps * g + 3))
                nc.vector.tensor_tensor(oh[:], rk[:], spread(rm), ALU.is_equal)
            e.wait_ge(r_exp.sem, r_exp.at(g + 1))
            nc.vector.tensor_reduce(s4[:], ex[:], AX.X, ALU.add).then_inc(r_sum.sem, 1)
            if not top1:
                nc.vector.tensor_reduce(m4[:], ex[:, :, 1:NR], AX.X, ALU.add)
            e.wait_ge(r_sum.sem, r_sum.at(g + 1))
            nc.vector.reciprocal(r4[:], s4[:]).then_inc(r_step.sem, 1)
            e.wait_ge(r_step.sem, r_step.at(steps * g + scaled))
            nc.vector.tensor_scalar(s4[:], r4[:], k.gates[:, gate:gate + 1], None, ALU.mult).then_inc(r_step.sem, 1)
            e.wait_ge(r_step.sem, r_step.at(steps * g + scaled + 1))
            if top1:
                nc.vector.tensor_tensor(wgt[:], oh[:], spread(s4), ALU.mult).then_inc(r_w.sem, 1)
            else:
                nc.vector.tensor_tensor(wgt[:, :, 0], ex[:, :, 0], s4[:], ALU.mult).then_inc(r_step.sem, 1)
                nc.vector.tensor_tensor(wgt[:, :, 1], m4[:], s4[:], ALU.mult).then_inc(r_w.sem, 1)

        def add_expert(g, x):
            e.wait_ge(o_full.sem, o_full.at(E * g + x + 1))
            if x:
                e.wait_ge(o_used.sem, o_used.at(E * g + x))
            else:
                e.wait_ge(r_w.sem, r_w.at(g + 1))
            for j in range(GT):
                last = nc.vector.scalar_tensor_tensor(k.x[:, 4 * g + j, :], ps[:, 3 + x % 2, j * P:(j + 1) * P], wgt[:, j, x:x + 1],
                                                      k.x[:, 4 * g + j, :], ALU.mult, ALU.add)
            last.then_inc(o_used.sem, 1)

        ln.dve_stats(0)
        ln.dve_aggregate(e, 0, False)
        ln.dve_apply(e, 0, 0)
        if not top1:
            e.wait_ge(ln.out.sem, ln.out.at(1))
            ln2.dve_stats(0)
            ln2.dve_aggregate(e, 0, False)
            ln2.dve_apply(e, 0, 0)
        if aside:
            aside(e)
        e.wait_ge(made.sem, made.at(1))

        def body(g, more):
            if more:
                ln.dve_stats(g + 1)
            router(g)
            if more:
                ln.dve_aggregate(e, g + 1, True)
                if not top1:
                    ln.dve_apply(e, g + 1, g + 1)
                    e.wait_ge(ln.out.sem, ln.out.at(g + 2))
                    ln2.dve_stats(g + 1)
                    e.wait_ge(ln2.stats.sem, ln2.stats.at(g + 2))
            for x in range(E):
                add_expert(g, x)
                if more and x == 0:
                    if top1:
                        ln.dve_apply(e, g + 1, g + 1)
                    else:
                        ln2.dve_aggregate(e, g + 1, True)
                        ln2.dve_apply(e, g + 1, g + 1)
            e.wait_ge(b_full.sem, b_full.at(g + 1))
            e.wait_ge(o_used.sem, o_used.at(E * (g + 1)))
            nc.vector.tensor_tensor(k.x[:, bass.ts(g, GT), :], ps[:, 7, :].rearrange("p (j d) -> p j d", j=GT),
                                    k.x[:, bass.ts(g, GT), :], ALU.add).then_inc(x_done.sem, 1)

        pipelined_groups(e, body)

    def pool(e):
        e.wait_ge(before.sem, before.end)
        for r in range(NR):
            ins = nc.gpsimd.memset(rank[:, r:r + 1], float(NR - r))
        ins.then_inc(made.sem, 1)
        e.wait_ge(made.sem, made.at(1))
        ln.pool_rstd(e, 0)
        if not top1:
            ln2.pool_rstd(e, 0)

        def body(g, more):
            if more:
                ln.pool_rstd(e, g + 1)
                if not top1:
                    ln2.pool_rstd(e, g + 1)

        pipelined_groups(e, body)

    return dict(sp=sp, pe=pe, act=act, dve=dve, pool=pool)


def ffn0(k, io, freed):
    def loads(k, io, v):
        return [
            (v.w1, io["L0_ffn_W1"].rearrange("e d f -> d e f")),
            (v.w2[:, :, 0, :], io["L0_ffn_W2"].rearrange("e f d -> f e d")),
            (v.b1[:, :, 0], io["L0_ffn_b1"].rearrange("e f -> f e")),
            (v.b2[0:8, :], io["L0_ffn_b2"]),
            (v.wr, io["L0_ffn_Wg"]),
            (v.br[0:8, :], io["L0_ffn_bg"].rearrange("(n a) -> n a", a=1)),
        ]
    space = Carve(k.arena, 25000)
    return experts(k, io, "f0", True, 4, loads, freed, space, space, aside=k.ssm.dve_sum)


class StateSpaceKernel:

    N, L = 64, SEQ
    PAIRS = L // 2

    def __init__(self, k, io):
        self.k, self.io = k, io
        sem = lambda n: k.sem("ssm_" + n)
        self.w_in, self.scalar_step, self.step, self.started, self.paired, self.summed = (
            sem(n) for n in ("loaded", "scalar_step", "vector_step", "started", "pairs", "kernel_made"))
        self.stored, self.toep_in = sem("stored"), sem("toeplitz_in")
        self.Z = k.toep[:].rearrange("p a b -> p (a b)").rearrange("p (l c n) -> p l c n", l=self.L, c=2)
        self.padded = k.sb("ssm_padded_kernel", [P, 2 * self.L])
        self.z2 = k.sb("ssm_z_squared", [P, 3, self.N])
        self.t1 = k.sb("ssm_product", [P, 2, 2, self.N])
        self.t2 = k.sb("ssm_cross_product", [P, 2, 2, self.N])
        self.scratch = k.nc.dram_tensor("ssm_toeplitz_scratch", (SEQ, D, SEQ), F32).ap()
        cv = Carve(k.arena, 27200)
        self.a_re, self.a_im, self.c_re, self.c_im = (cv.f32(self.N) for _ in range(4))
        self.ldt, self.dt, self.skip = cv.f32(1), cv.f32(1), cv.f32(1)
        self.ang, self.turns, self.red, self.half, self.er, self.sn, self.sh = (cv.f32(self.N) for _ in range(7))
        self.u, self.v, self.p, self.q, self.den, self.zr, self.zi = (cv.f32(self.N) for _ in range(7))

    def sp_load(self, e):
        io = self.io
        for dst, name in ((self.a_re, "A_re"), (self.a_im, "A_im"), (self.c_re, "C_re"), (self.c_im, "C_im")):
            e.dma_start(dst, io["L1_xattn_" + name]).then_inc(self.w_in.sem, 16)
        for dst, name in ((self.ldt, "log_dt"), (self.skip, "D_skip")):
            e.dma_start(dst, io["L1_xattn_" + name].rearrange("(p a) -> p a", a=1)).then_inc(self.w_in.sem, 16)

    def act_magnitude(self, e):
        S = self.k.nc.scalar
        e.wait_ge(self.w_in.sem, 96)
        S.activation(self.dt, self.ldt, ACT.Exp).then_inc(self.scalar_step.sem, 1)
        e.wait_ge(self.scalar_step.sem, 1)
        S.activation(self.er, self.a_re, ACT.Exp, scale=self.dt).then_inc(self.scalar_step.sem, 1)

    def act_angle(self, e):
        S = self.k.nc.scalar
        e.wait_ge(self.step.sem, 7)
        S.activation(self.sn, self.red, ACT.Sin)
        S.activation(self.sh, self.red, ACT.Sin, scale=0.5).then_inc(self.scalar_step.sem, 1)

    def dve_start(self, e):
        V = self.k.nc.vector
        TWO_PI = 6.283185307179586
        C1 = 6.28125
        C2 = 0.0019350051879882812
        C3 = TWO_PI - C1 - C2
        PI_IN = 3.1415925
        n = 0

        def then(ins):
            nonlocal n
            n += 1
            ins.then_inc(self.step.sem, 1)
            e.wait_ge(self.step.sem, n)

        a_re, a_im, c_re, c_im, zr, zi = self.a_re, self.a_im, self.c_re, self.c_im, self.zr, self.zi
        u, v, p, q, den, Z, z2 = self.u, self.v, self.p, self.q, self.den, self.Z, self.z2
        e.wait_ge(self.scalar_step.sem, 2)
        then(V.tensor_scalar(self.ang, a_im, self.dt, None, ALU.mult))
        then(V.tensor_scalar(self.turns, self.ang, 1.0 / TWO_PI, ROUND, ALU.mult, ALU.add))
        then(V.tensor_scalar(self.turns, self.turns, -ROUND, None, ALU.add))
        then(V.scalar_tensor_tensor(self.red, self.turns, -C1, self.ang, ALU.mult, ALU.add))
        then(V.scalar_tensor_tensor(self.ang, self.turns, -C2, self.red, ALU.mult, ALU.add))
        then(V.scalar_tensor_tensor(self.half, self.turns, -C3, self.ang, ALU.mult, ALU.add))
        then(V.tensor_scalar(self.red, self.half, PI_IN, -PI_IN, ALU.min, ALU.max))
        V.tensor_tensor(den, a_re, a_re, ALU.mult)
        then(V.tensor_tensor(u, a_im, a_im, ALU.mult))
        then(V.tensor_tensor(den, den, u, ALU.add))
        then(V.reciprocal(u, den))
        then(V.tensor_scalar(den, u, 2.0, None, ALU.mult))
        e.wait_ge(self.scalar_step.sem, 3)
        V.tensor_tensor(zi, self.er, self.sn, ALU.mult)
        then(V.tensor_tensor(u, self.sh, self.sh, ALU.mult))
        then(V.tensor_scalar(u, u, -2.0, 1.0, ALU.mult, ALU.add))
        then(V.tensor_tensor(zr, self.er, u, ALU.mult))
        then(V.tensor_scalar(v, zr, -1.0, None, ALU.add))
        V.tensor_tensor(p, c_re, v, ALU.mult)
        V.tensor_tensor(u, c_im, zi, ALU.mult)
        V.tensor_tensor(q, c_re, zi, ALU.mult)
        then(V.tensor_tensor(self.half, c_im, v, ALU.mult))
        V.tensor_tensor(p, p, u, ALU.subtract)
        then(V.tensor_tensor(q, q, self.half, ALU.add))
        then(V.tensor_tensor(u, p, a_re, ALU.mult))
        then(V.tensor_tensor(v, q, a_im, ALU.mult))
        then(V.tensor_tensor(u, u, v, ALU.add))
        then(V.tensor_tensor(Z[:, 0, 0, :], u, den, ALU.mult))
        then(V.tensor_tensor(u, q, a_re, ALU.mult))
        then(V.tensor_tensor(v, p, a_im, ALU.mult))
        then(V.tensor_tensor(u, u, v, ALU.subtract))
        then(V.tensor_tensor(Z[:, 0, 1, :], u, den, ALU.mult))
        then(V.tensor_tensor(u, Z[:, 0, 0, :], zr, ALU.mult))
        then(V.tensor_tensor(v, Z[:, 0, 1, :], zi, ALU.mult))
        then(V.tensor_tensor(Z[:, 1, 0, :], u, v, ALU.subtract))
        then(V.tensor_tensor(u, Z[:, 0, 0, :], zi, ALU.mult))
        then(V.tensor_tensor(v, Z[:, 0, 1, :], zr, ALU.mult))
        then(V.tensor_tensor(Z[:, 1, 1, :], u, v, ALU.add))
        then(V.tensor_tensor(u, zr, zr, ALU.mult))
        then(V.tensor_tensor(v, zi, zi, ALU.mult))
        then(V.tensor_tensor(z2[:, 0, :], u, v, ALU.subtract))
        then(V.tensor_tensor(u, zr, zi, ALU.mult))
        V.tensor_scalar(z2[:, 1, :], u, 2.0, None, ALU.mult)
        V.tensor_scalar(z2[:, 2, :], u, -2.0, None, ALU.mult)
        V.memset(self.padded[:, 0:self.L - 1], 0.0)
        V.memset(self.padded[:, 2 * self.L - 1:2 * self.L], 0.0)
        V.tensor_copy(self.padded[:, self.L - 1:self.L], self.skip).then_inc(self.started.sem, 1)

    def pool_pair(self, e, t):
        if isinstance(t, int) and t == 0:
            return
        G, before, z2 = self.k.nc.gpsimd, self.Z[:, bass.ts(t - 1, 2), :, :], self.z2
        four = lambda v: v.unsqueeze(1).to_broadcast([P, 4, self.N])
        two = lambda v: v.unsqueeze(1).to_broadcast([P, 2, self.N])
        e.wait_ge(self.started.sem, 1)
        if not isinstance(t, int) or t > 1:
            e.wait_ge(self.paired.sem, 2 * (t - 1))
            e.nop(nofuse=True)
        G.tensor_tensor(self.t1[:].rearrange("p a c n -> p (a c) n"), before.rearrange("p a c n -> p (a c) n"), four(z2[:, 0, :]), ALU.mult)
        G.tensor_tensor(self.t2[:, :, 0, :], before[:, :, 1, :], two(z2[:, 2, :]), ALU.mult)
        G.tensor_tensor(self.t2[:, :, 1, :], before[:, :, 0, :], two(z2[:, 1, :]), ALU.mult).then_inc(self.paired.sem, 1)
        e.wait_ge(self.paired.sem, 2 * t - 1)
        e.nop(nofuse=True)
        G.tensor_tensor(self.Z[:, bass.ts(t, 2), :, :], self.t1[:], self.t2[:], ALU.add).then_inc(self.paired.sem, 1)

    def dve_sum(self, e):
        V = self.k.nc.vector
        e.wait_ge(self.paired.sem, 2 * (self.PAIRS - 1))
        V.tensor_copy(self.t1[:, 0, 0, 0:1], self.padded[:, self.L - 1:self.L]).then_inc(self.summed.sem, 1)
        e.wait_ge(self.summed.sem, 1)
        V.tensor_reduce(self.padded[:, self.L - 1:2 * self.L - 1], self.Z[:, :, 0, :], AX.X, ALU.add).then_inc(self.summed.sem, 1)
        e.wait_ge(self.summed.sem, 2)
        V.tensor_tensor(self.padded[:, self.L - 1:self.L], self.padded[:, self.L - 1:self.L], self.t1[:, 0, 0, 0:1], ALU.add).then_inc(self.summed.sem, 1)

    def sp_matrices(self, e):
        e.wait_ge(self.summed.sem, 3)
        windows = self.padded[:, self.L - 1:2 * self.L - 1]
        windows = bass.AP(windows.tensor, windows.offset, [windows.ap[0], [-1, SEQ], [1, SEQ]])
        e.dma_start(self.scratch.rearrange("r d t -> d r t"), windows).then_inc(self.stored.sem, 16)
        e.wait_ge(self.stored.sem, 16)
        for b in range(2):
            e.dma_start(self.k.toep[b * SEQ:(b + 1) * SEQ, :, :], self.scratch).then_inc(self.toep_in.sem, 16)


def attention_ssm(k, io, freed):
    nc = k.nc
    H, DH, GATE, HID = 4, 32, 1, 4
    SCALE = float(DH) ** -0.5
    MASKED, TAKEN = -1e38, -3e38
    sem = lambda n, total=TILES: k.sem("a1_" + n, total)
    io1 = {n[len("L1_xattn_"):]: v for n, v in io.items() if n.startswith("L1_xattn_")}
    before = k.x_ready
    ps = k.ps

    cv = Carve(k.arena)
    U = cv.f32(TILES, D)
    XS = cv.f32(TILES, D)
    FO = cv.f32(TILES, 2 * D)
    wq, wk, wv = cv.f32(P), cv.f32(P), cv.f32(P)
    wf = cv.f32(4 * D)
    wfraw = cv.f32(4 * D)
    bf = cv.f32(4 * D)
    w1 = cv.f32(HID * P)
    w2 = cv.f32(HID, D)
    rows = cv.f32(5, D)
    cols = cv.f32(2 + HID)
    mg = cv.f32(1)
    head_of = cv.f32(H)
    mb = cv.f32(TILES, CTX)
    tmask = cv.f32(TILES)
    start_rings = cv.at
    mask8 = cv.f32(TILES * CTX // 4).bitcast(U8)
    tm8 = cv.f32(P // 4).bitcast(U8)
    tmf = cv.f32(P)
    cv.at = start_rings
    qT = cv.f32(2, P)
    kbd = cv.f32(2, 2, H, CTX)
    W = cv.f32(2, H, CTX)
    W2 = cv.f32(2, H, CTX)
    EX = cv.f32(2, H, CTX)
    m8 = cv.f32(4, H, 8)
    nm, sums, rec = cv.f32(2, H), cv.f32(2, H), cv.f32(2, H)
    vs = cv.f32(2, 2, D)
    aT = cv.f32(2, P)
    cT = cv.f32(2, P)
    F = cv.f32(2, 2 * D)
    cg = cv.f32(2, P)
    cv2 = Carve(k.arena, start_rings)
    hin = cv2.f32(GT * P)
    hT = cv2.f32(2, GT * P)

    w_in, w2_in, prep = sem("w_loaded", None), sem("masks_loaded", None), sem("prepared", 6)
    prep_p, prep_t, prep_tt = sem("prepared_pool", 1), sem("text_mask_turned", 1), sem("text_mask_laid", 1)
    ln_sems = [sem("ln_" + n) for n in ("stats", "mv", "veps", "rstd", "out")]
    ln_stats_done, ln_mv_done, _, ln_rstd_done, ln_out_done = ln_sems
    b_step, b_rstd, b_out = sem("ln2_step", 3 * TILES), sem("ln2_rstd"), sem("ln2_out")
    u_kept, c_laid = sem("u_kept"), sem("ctx_tile")
    xt_full, xt_laid, q_full, q_laid, k_full, k_laid = (sem(n) for n in ("xT_full", "xT_laid", "q_full", "q_laid", "k_full", "k_laid"))
    s_full, s_laid, s_masked, v_full, v_laid = (sem(n) for n in ("scores", "scores_laid", "masked", "v_full", "v_laid"))
    tk = sem("top", 16 * TILES)
    e_done, sel_done, n_step, a_done = sem("exp"), sem("selected"), sem("norm_step", 3 * TILES), sem("attn")
    a_full, a_laid, c_full, cT_laid, f_full, f_laid = (sem(n) for n in ("attnT_full", "attnT_laid", "cT_full", "cT_laid", "film_full", "film_laid"))
    xs_step, xs_done = sem("xs_step"), sem("xs_done")

    b_full, b_laid = sem("conv_full", 8), sem("conv_laid", 8)
    k.conv_done = b_full
    y_step, y_done = sem("y_step", 2 * GROUPS - 2), sem("y_done", GROUPS - 1)
    y0_step, y0_done = sem("y0_step", 2), sem("y0_done", 1)
    hid_full, hid_laid = sem("hid_full", HID * GROUPS), sem("hid_laid", HID * GROUPS)
    ht_full, ht_laid, o_full, o_added = (sem(n, GROUPS) for n in ("hinT_full", "hinT_laid", "ffn_full", "ffn_added"))
    z_step, x_done = sem("z_step", 2 * GROUPS), sem("x_done", GROUPS)
    k.x_ready = x_done
    lnC = GroupNorm(k, "a1_lnC", 0, lambda g, j: XS[:, 4 * g + j, :], lambda g, j: k.xn[:, 0, j, :])
    lnD = GroupNorm(k, "a1_lnD", 1, lambda g, j: XS[:, 4 * g + j, :], lambda g, j: XS[:, 4 * g + j, :])

    def flat(v):
        return v.rearrange("p h j -> p (h j)")

    def more(t, ahead):
        return not isinstance(t, int) or t + ahead < TILES

    loads = [
        (wq, io1["Wq"]), (wk[0:DC, :], io1["Wk"]), (wv[0:DC, :], io1["Wv"]),
        (wfraw[:, 0:2 * D], io1["W_film_in"]), (wfraw[:, 2 * D:], io1["W_film_out"]),
        (bf[0:1, 0:2 * D], io1["b_film_in"].rearrange("(a n) -> a n", a=1)),
        (bf[0:1, 2 * D:], io1["b_film_out"].rearrange("(a n) -> a n", a=1)),
        (w1, io1["W1"]), (w2, io1["W2"].rearrange("(c p) d -> p c d", p=P)),
        (rows[:, 0, :], io1["g_norm_in"].rearrange("(a n) -> a n", a=1).partition_broadcast(P)),
        (rows[:, 1, :], io1["b_norm_in"].rearrange("(a n) -> a n", a=1).partition_broadcast(P)),
        (rows[:, 2, :], io1["g_norm_out"].rearrange("(a n) -> a n", a=1).partition_broadcast(P)),
        (rows[:, 3, :], io1["b_norm_out"].rearrange("(a n) -> a n", a=1).partition_broadcast(P)),
        (rows[0:1, 4, :], io1["b2"].rearrange("(a n) -> a n", a=1)),
        (cols[:, 0:1], io1["g_ffn"].rearrange("(p a) -> p a", a=1)),
        (cols[:, 1:2], io1["b_ffn"].rearrange("(p a) -> p a", a=1)),
        (cols[:, 2:2 + HID], io1["b1"].rearrange("(c p) -> p c", p=P)),
        (mg, io1["mod_gate"].rearrange("(a n) -> a n", a=1).partition_broadcast(P)),
    ]
    READY = 16 * len(loads)
    ctx_mask = io["mask_BxS2_bf1"].rearrange("(t b) j -> b t j", b=2)
    masks = [(mask8[b * SEQ:(b + 1) * SEQ, :].rearrange("p (t j) -> p t j", j=CTX), ctx_mask[b:b + 1].partition_broadcast(SEQ)) for b in range(2)]
    masks.append((tm8[0:TILES, :], io["mask_BxS_bf1"].rearrange("b s -> (b s)").rearrange("(t p) -> t p", p=P)))

    def sp(e):
        e.wait_ge(freed.sem, freed.end)
        with nc.allow_non_contiguous_dma(reason="per-channel columns are small"):
            for dst, src in loads:
                e.dma_start(dst, src).then_inc(w_in.sem, 16)
            for dst, src in masks:
                if len(src.shape) == 4:
                    src = src.rearrange("p a t j -> p (a t) j")
                e.dma_start(dst, src).then_inc(w2_in.sem, 16)

    def ctx_copy(t, s):
        nc.gpsimd.tensor_copy(cg[:, s, :], k.ctxT[:, bass.ts(t, P)]).then_inc(c_laid.sem, 1)

    def rstd(e, ln, t, s, slot):
        e.wait_ge(ln[1].sem, ln[1].at(t + 1))
        nc.gpsimd.tensor_tensor(k.veps[:, slot, s:s + 1], k.mv[:, slot, s, 1:2], k.eps[:, 0:1], ALU.add).then_inc(ln[2].sem, 1)
        e.wait_ge(ln[2].sem, ln[2].at(t + 1))
        nc.gpsimd.tensor_tensor(k.rstd[:, slot, s:s + 1], k.veps[:, slot, s:s + 1], k.half[:, 0:1], ALU.pow).then_inc(ln[3].sem, 1)

    def modulate(e, t, s):
        e.wait_ge(f_laid.sem, f_laid.at(t + 1))
        e.nop(nofuse=True)
        nc.gpsimd.tensor_tensor(XS[:, t, :], XS[:, t, :], F[:, s, 0:D], ALU.mult).then_inc(xs_step.sem, 1)
        e.wait_ge(xs_step.sem, xs_step.at(t + 1))
        e.nop(nofuse=True)
        nc.gpsimd.tensor_tensor(XS[:, t, :], XS[:, t, :], F[:, s, D:2 * D], ALU.add).then_inc(xs_done.sem, 1)

    def keep_u(e, t, s):
        e.wait_ge(ln_out_done.sem, ln_out_done.at(t + 1))
        e.nop(nofuse=True)
        nc.gpsimd.tensor_copy(U[:, t, :], k.xn[:, s, 0, :]).then_inc(u_kept.sem, 1)

    def rstd_u(e, t, s):
        r, v = k.rstd[:, 0, s:s + 1], k.veps[:, 1, s:s + 1]
        e.wait_ge(ln_rstd_done.sem, ln_rstd_done.at(t + 1))
        nc.gpsimd.tensor_tensor(v, k.mv[:, 0, s, 1:2], r, ALU.mult).then_inc(b_step.sem, 1)
        e.wait_ge(b_step.sem, b_step.at(3 * t + 1))
        nc.gpsimd.tensor_tensor(v, v, r, ALU.mult).then_inc(b_step.sem, 1)
        e.wait_ge(b_step.sem, b_step.at(3 * t + 2))
        nc.gpsimd.tensor_tensor(v, v, k.eps[:, 0:1], ALU.add).then_inc(b_step.sem, 1)
        e.wait_ge(b_step.sem, b_step.at(3 * t + 3))
        nc.gpsimd.tensor_tensor(k.rstd[:, 1, s:s + 1], v, k.half[:, 0:1], ALU.pow).then_inc(b_rstd.sem, 1)

    def norm_in(e, t):
        e.wait_ge(b_out.sem, b_out.at(t + 1))
        e.nop(nofuse=True)
        nc.gpsimd.tensor_tensor(XS[:, t, :], XS[:, t, :], rows[:, 0, :], ALU.mult).then_inc(l2_step.sem, 1)
        e.wait_ge(l2_step.sem, l2_step.at(2 * t + 1))
        e.nop(nofuse=True)
        nc.gpsimd.tensor_tensor(XS[:, t, :], XS[:, t, :], rows[:, 1, :], ALU.add).then_inc(l2_step.sem, 1)

    l2_step = sem("l2_step", 2 * TILES)

    def mask_scores(e, t, s):
        e.wait_ge(s_laid.sem, s_laid.at(t + 1))
        e.nop(nofuse=True)
        nc.gpsimd.tensor_tensor(W[:, s, :, :], W[:, s, :, :], mb[:, t, :].unsqueeze(1).to_broadcast([P, H, CTX]), ALU.add).then_inc(s_masked.sem, 1)

    def pool_step(e, t, s):
        o = 1 - s
        if more(t, 1):
            mask_scores(e, t + 1, o)
        if more(t, 2):
            keep_u(e, t + 2, s)
        if more(t, 2):
            norm_in(e, t + 2)
        if more(t, 2):
            e.wait_ge(v_full.sem, v_full.at(t + 1))
            e.nop(nofuse=True)
            ctx_copy(t + 2, s)
        if more(t, 4):
            rstd(e, ln_sems, t + 4, s, 0)
            e.wait_ge(b_out.sem, b_out.at(t + 3))
            rstd_u(e, t + 4, s)
        if not (isinstance(t, int) and t == 0):
            modulate(e, t - 1, o)

    def tail_sum(e, engine, g, step, done, n):
        yg = XS[:, bass.ts(g, GT), :]
        fo = FO[:, bass.ts(g, GT), :]
        engine.tensor_tensor(yg, yg, fo[:, :, 0:D], ALU.mult).then_inc(step.sem, 1)
        e.wait_ge(step.sem, step.at(2 * n + 1))
        e.nop(nofuse=True)
        engine.tensor_tensor(yg, yg, fo[:, :, D:2 * D], ALU.add).then_inc(step.sem, 1)
        e.wait_ge(step.sem, step.at(2 * n + 2))
        e.nop(nofuse=True)
        engine.tensor_tensor(yg, yg, U[:, bass.ts(g, GT), :], ALU.add).then_inc(done.sem, 1)

    def pool(e):
        e.wait_ge(before.sem, before.end)
        e.wait_ge(prep_p.sem, prep_p.at(1))
        e.wait_ge(prep_tt.sem, prep_tt.at(1))
        e.wait_ge(w_in.sem, w_in.at(READY))
        for t in range(2):
            ctx_copy(t, t)
        for t in range(2):
            rstd(e, ln_sems, t, t, 0)
            rstd_u(e, t, t)
        for t in range(2):
            keep_u(e, t, t)
        for t in (2, 3):
            rstd(e, ln_sems, t, t % 2, 0)
            e.wait_ge(b_out.sem, b_out.at(t - 1))
            rstd_u(e, t, t % 2)
        norm_in(e, 0)
        norm_in(e, 1)
        mask_scores(e, 0, 0)
        pipelined_tiles(e, lambda t, s: pool_step(e, t, s), tail=4)
        modulate(e, TILES - 1, 1)
        def pool_sum(g):
            tail_sum(e, nc.gpsimd, g, y_step, y_done, g - 1)

        e.wait_ge(b_laid.sem, b_laid.at(8))
        e.wait_ge(f_laid.sem, f_laid.at(TILES))
        e.wait_ge(u_kept.sem, u_kept.at(TILES))
        pool_sum(1)
        lnC.pool_rstd(e, 0)
        lnC.pool_rstd(e, 1)
        pool_sum(2)

        def body(g, _):
            if group_ahead(g, 2):
                lnC.pool_rstd(e, g + 2)
            if group_ahead(g, 3):
                pool_sum(g + 3)
            lnD.pool_rstd(e, g)

        pipelined_groups(e, body, tail=3)


    def dve_prep(e):
        e.wait_ge(before.sem, before.end)
        e.wait_ge(w_in.sem, w_in.at(READY))
        e.wait_ge(w2_in.sem, w2_in.at(48))
        V = nc.vector
        V.tensor_scalar(mb.rearrange("p t j -> p (t j)"), mask8, -1.0, -MASKED, ALU.add, ALU.mult).then_inc(prep_p.sem, 1)
        V.memset(wk[DC:P, :], 0.0)
        V.memset(wv[DC:P, :], 0.0)
        V.memset(head_of[:], 0.0).then_inc(prep.sem, 1)
        e.wait_ge(prep.sem, prep.at(1))
        for h in range(H):
            V.memset(head_of[h * DH:(h + 1) * DH, h:h + 1], 1.0)
        V.tensor_scalar(wf, wfraw, mg, None, ALU.mult).then_inc(prep.sem, 1)
        V.tensor_scalar(bf[0:1, :], bf[0:1, :], mg[0:1, :], None, ALU.mult).then_inc(prep.sem, 1)
        V.tensor_scalar(rows[:, 2:4, :], rows[:, 2:4, :], k.gates[:, GATE:GATE + 1], None, ALU.mult).then_inc(prep.sem, 1)
        V.tensor_scalar(tmf[0:TILES, :], tm8[0:TILES, :], 1.0 / H, None, ALU.mult).then_inc(prep.sem, 1)
        e.wait_ge(prep.sem, prep.at(5))
        bfv = bf[0:1, :].rearrange("p (a b d) -> p a b d", a=2, b=2)
        V.tensor_scalar(bfv[:, :, 0, :], bfv[:, :, 0, :], 1.0, None, ALU.add).then_inc(prep.sem, 1)
        e.wait_ge(prep_t.sem, prep_t.at(1))
        V.tensor_copy(tmask, ps[:, 0, 0:TILES]).then_inc(prep_tt.sem, 1)
        e.wait_ge(prep.sem, prep.at(6))
        e.wait_ge(prep_p.sem, prep_p.at(1))

    def topk_round(e, t, s, r):
        V = nc.vector
        src = W if r == 0 else W2
        before_round = 16 * t + 4 * r
        for half in range(2):
            if r > 0:
                e.wait_ge(tk.sem, tk.at(before_round - 1 + half))
                e.nop(nofuse=True)
            for h in (2 * half, 2 * half + 1):
                ins = V.max(m8[:, r, h, :], src[:, s, h, :])
            ins.then_inc(tk.sem, 1)
        for half in range(2):
            e.wait_ge(tk.sem, tk.at(before_round + 1 + half))
            e.nop(nofuse=True)
            for h in (2 * half, 2 * half + 1):
                ins = V.match_replace(W2[:, s, h, :], m8[:, r, h, :], src[:, s, h, :], TAKEN)
            ins.then_inc(tk.sem, 1)
        if r == 0:
            V.tensor_scalar(nm[:, s, :], m8[:, 0, :, 0], -SCALE, None, ALU.mult).then_inc(nm_done.sem, 1)

    def norm_a(e, t, s):
        e.wait_ge(ln_rstd_done.sem, ln_rstd_done.at(t + 1))
        e.nop(nofuse=True)
        nc.vector.tensor_scalar(k.xn[:, s, 0, :], k.x[:, t, :], k.mv[:, 0, s, 0:1], k.rstd[:, 0, s:s + 1],
                                ALU.subtract, ALU.mult).then_inc(ln_out_done.sem, 1)

    nm_done = sem("max_laid")

    def stats_a(e, t, s):
        nc.vector.bn_stats(k.stat[:, 0, s, :], k.x[:, t, :]).then_inc(ln_stats_done.sem, 1)

    def aggregate_a(e, t, s):
        e.wait_ge(ln_stats_done.sem, ln_stats_done.at(t + 1))
        e.nop(nofuse=True)
        nc.vector.bn_aggr(k.mv[:, 0, s, :], k.stat[:, 0, s, :]).then_inc(ln_mv_done.sem, 1)

    def dve_step(e, t, s):
        V = nc.vector
        o = 1 - s
        e.wait_ge(s_masked.sem, s_masked.at(t + 1))
        e.nop(nofuse=True)
        topk_round(e, t, s, 0)
        if more(t, 4):
            stats_a(e, t + 4, s)
        topk_round(e, t, s, 1)
        if more(t, 3):
            e.wait_ge(u_kept.sem, u_kept.at(t + 2))
            e.nop(nofuse=True)
            e.wait_ge(xt_full.sem, xt_full.at(t + 2))
            e.wait_ge(b_out.sem, b_out.at(t + 2))
            norm_a(e, t + 3, o)
        topk_round(e, t, s, 2)
        if more(t, 4):
            aggregate_a(e, t + 4, s)
        topk_round(e, t, s, 3)
        e.wait_ge(e_done.sem, e_done.at(t + 1))
        e.wait_ge(tk.sem, tk.at(16 * t + 16))
        V.scalar_tensor_tensor(flat(EX[:, s, :, :]), flat(W2[:, s, :, :]), TAKEN, flat(EX[:, s, :, :]), ALU.is_equal, ALU.mult).then_inc(sel_done.sem, 1)
        e.wait_ge(sel_done.sem, sel_done.at(t + 1))
        V.tensor_reduce(sums[:, s, :], EX[:, s, :, :], AX.X, ALU.add).then_inc(n_step.sem, 1)
        e.wait_ge(n_step.sem, n_step.at(3 * t + 1))
        V.reciprocal(rec[:, s, :], sums[:, s, :]).then_inc(n_step.sem, 1)
        e.wait_ge(n_step.sem, n_step.at(3 * t + 2))
        V.tensor_scalar(rec[:, s, :], rec[:, s, :], tmask[:, t:t + 1] if isinstance(t, int) else tmask[:, bass.ts(t, 1)], None, ALU.mult).then_inc(n_step.sem, 1)
        e.wait_ge(n_step.sem, n_step.at(3 * t + 3))
        V.tensor_tensor(EX[:, s, :, :], EX[:, s, :, :], rec[:, s, :].unsqueeze(2).to_broadcast([P, H, CTX]), ALU.mult).then_inc(a_done.sem, 1)

    def dve(e):
        V = nc.vector
        dve_prep(e)
        for t in range(4):
            s = t % 2
            stats_a(e, t, s)
            if t > 1:
                e.wait_ge(b_rstd.sem, b_rstd.at(t - 1))
            aggregate_a(e, t, s)
            if t == 2:
                e.wait_ge(b_out.sem, b_out.at(1))
                e.wait_ge(u_kept.sem, u_kept.at(1))
                e.wait_ge(xt_full.sem, xt_full.at(1))
            if t < 3:
                norm_a(e, t, s)
                e.wait_ge(ln_out_done.sem, ln_out_done.at(t + 1))
        pipelined_tiles(e, lambda t, s: dve_step(e, t, s), tail=4)
        k.perturb(e)
        for q in range(7):
            e.wait_ge(b_full.sem, b_full.at(q // 2 * 2 + 2))
            V.tensor_copy(XS[:, :, 16 * q:16 * q + 16], ps[:, q, :].rearrange("p (d t) -> p t d", t=TILES)).then_inc(b_laid.sem, 1)
        e.wait_ge(b_laid.sem, b_laid.at(8))
        e.wait_ge(f_laid.sem, f_laid.at(TILES))
        e.wait_ge(u_kept.sem, u_kept.at(TILES))
        tail_sum(e, V, 0, y0_step, y0_done, 0)
        for g in range(2):
            if g == 0:
                e.wait_ge(y0_done.sem, y0_done.at(1))
            else:
                e.wait_ge(y_done.sem, y_done.at(1))
            lnC.dve_stats(g)
            lnC.dve_aggregate(e, g, False)
            e.wait_ge(ht_full.sem, ht_full.at(g))
            lnC.dve_apply(e, g, g)

        def add_to_x(g):
            yg, xg = XS[:, bass.ts(g, GT), :], k.x[:, bass.ts(g, GT), :]
            e.wait_ge(lnD.out.sem, lnD.out.at(g + 1))
            e.nop(nofuse=True)
            V.tensor_tensor(yg, yg, rows[:, 2, :].unsqueeze(1).to_broadcast([P, GT, D]), ALU.mult).then_inc(z_step.sem, 1)
            e.wait_ge(z_step.sem, z_step.at(2 * g + 1))
            e.nop(nofuse=True)
            V.tensor_tensor(yg, yg, rows[:, 3, :].unsqueeze(1).to_broadcast([P, GT, D]), ALU.add).then_inc(z_step.sem, 1)
            e.wait_ge(z_step.sem, z_step.at(2 * g + 2))
            e.nop(nofuse=True)
            V.tensor_tensor(xg, xg, yg, ALU.add).then_inc(x_done.sem, 1)

        def body(g, _):
            ahead = group_ahead(g, 2)
            if ahead:
                e.wait_ge(y_done.sem, y_done.at(g + 2))
                e.nop(nofuse=True)
                lnC.dve_stats(g + 2)
                e.wait_ge(lnC.stats.sem, lnC.stats.at(g + 3))
                e.nop(nofuse=True)
                lnC.dve_aggregate(e, g + 2, True)
            e.wait_ge(o_full.sem, o_full.at(g + 1))
            yg = XS[:, bass.ts(g, GT), :]
            V.tensor_tensor(yg, ps[:, 3, :].rearrange("p (j d) -> p j d", j=GT), yg, ALU.add).then_inc(o_added.sem, 1)
            if ahead:
                e.wait_ge(ht_full.sem, ht_full.at(g + 2))
                lnC.dve_apply(e, g + 2, g + 2)
            e.wait_ge(o_added.sem, o_added.at(g + 1))
            e.nop(nofuse=True)
            lnD.dve_stats(g)
            e.wait_ge(lnD.stats.sem, lnD.stats.at(g + 1))
            e.nop(nofuse=True)
            lnD.dve_aggregate(e, g, True)
            if not (isinstance(g, int) and g == 0):
                add_to_x(g - 1)
            lnD.dve_apply(e, g, g)

        pipelined_groups(e, body, tail=3)
        add_to_x(GROUPS - 1)

    def act_keys(e, t, s):
        e.wait_ge(k_full.sem, k_full.at(t + 1))
        for h in range(H):
            last = nc.scalar.activation(kbd[:, s, :, h, :], ps[:, 2, 0:P].rearrange("p (b j) -> p b j", b=2), ACT.Copy,
                                        scale=head_of[:, h:h + 1])
        last.then_inc(k_laid.sem, 1)
        e.wait_ge(q_full.sem, q_full.at(t + 1))
        nc.scalar.copy(qT[:, s, :], ps[:, 1, 0:P]).then_inc(q_laid.sem, 1)

    def act_norm_u(e, t, s):
        e.wait_ge(ln_out_done.sem, ln_out_done.at(t + 1))
        e.wait_ge(b_rstd.sem, b_rstd.at(t + 1))
        e.nop(nofuse=True)
        nc.scalar.activation(XS[:, t, :], k.xn[:, s, 0, :], ACT.Copy, scale=k.rstd[:, 1, s:s + 1]).then_inc(b_out.sem, 1)

    def act_scores(e, t, s):
        e.wait_ge(s_full.sem, s_full.at(t + 1))
        if not (isinstance(t, int) and t < 2):
            e.wait_ge(tk.sem, tk.at(16 * t - 28))
        nc.scalar.copy(flat(W[:, s, :, :]), ps[:, 3, 0:H * CTX]).then_inc(s_laid.sem, 1)

    def act_step(e, t, s):
        o = 1 - s
        film = not (isinstance(t, int) and t == 0)
        if more(t, 1):
            act_scores(e, t + 1, o)
        e.wait_ge(v_full.sem, v_full.at(t + 1))
        nc.scalar.copy(vs[0:CTX, s, :, :].rearrange("p b d -> p (b d)"), ps[0:CTX, 4, 0:2 * D]).then_inc(v_laid.sem, 1)
        if film:
            e.wait_ge(a_full.sem, a_full.at(t))
            nc.scalar.copy(aT[0:CTX, o, :], ps[0:CTX, 5, 0:P]).then_inc(a_laid.sem, 1)
        if more(t, 2):
            e.wait_ge(xt_full.sem, xt_full.at(t + 3))
            nc.scalar.copy(k.xnT[:, s, 0:P], ps[:, 0, 0:P]).then_inc(xt_laid.sem, 1)
        e.wait_ge(nm_done.sem, nm_done.at(t + 1))
        for h in range(H):
            last = nc.scalar.activation(EX[:, s, h, :], W[:, s, h, :], ACT.Exp, bias=nm[:, s, h:h + 1], scale=SCALE)
        last.then_inc(e_done.sem, 1)
        if film:
            e.wait_ge(c_full.sem, c_full.at(t))
            nc.scalar.copy(cT[:, o, :], ps[:, 6, 0:P]).then_inc(cT_laid.sem, 1)
        if more(t, 2):
            act_keys(e, t + 2, s)
        if more(t, 3):
            act_norm_u(e, t + 3, o)
        if film:
            act_film(e, t - 1, o)

    def act_film(e, t, s):
        e.wait_ge(xs_done.sem, xs_done.at(t))
        e.wait_ge(f_full.sem, f_full.at(t + 1))
        e.nop(nofuse=True)
        nc.scalar.copy(F[:, s, :], ps[:, 7, 0:2 * D])
        nc.scalar.copy(FO[:, t, :], ps[:, 7, 2 * D:4 * D]).then_inc(f_laid.sem, 1)

    def act_last_film(e, t, s):
        e.wait_ge(a_full.sem, a_full.at(t + 1))
        nc.scalar.copy(aT[0:CTX, s, :], ps[0:CTX, 5, 0:P]).then_inc(a_laid.sem, 1)
        e.wait_ge(c_full.sem, c_full.at(t + 1))
        nc.scalar.copy(cT[:, s, :], ps[:, 6, 0:P]).then_inc(cT_laid.sem, 1)
        act_film(e, t, s)

    def act(e):
        e.wait_ge(before.sem, before.end)
        e.wait_ge(w_in.sem, w_in.at(READY))
        e.wait_ge(prep_p.sem, prep_p.at(1))
        e.wait_ge(prep_tt.sem, prep_tt.at(1))
        for t in range(2):
            act_norm_u(e, t, t)
            e.wait_ge(xt_full.sem, xt_full.at(t + 1))
            nc.scalar.copy(k.xnT[:, t, 0:P], ps[:, 0, 0:P]).then_inc(xt_laid.sem, 1)
            act_keys(e, t, t)
        act_norm_u(e, 2, 0)
        act_scores(e, 0, 0)
        pipelined_tiles(e, lambda t, s: act_step(e, t, s), tail=4)
        act_last_film(e, TILES - 1, 1)
        nc.scalar.activation(k.preload[:], k.half[:, 0:1], ACT.Gelu)
        e.wait_ge(b_full.sem, b_full.at(8))
        nc.scalar.copy(XS[:, :, 112:128], ps[:, 7, :].rearrange("p (d t) -> p t d", t=TILES)).then_inc(b_laid.sem, 1)
        e.wait_ge(b_laid.sem, b_laid.at(8))

        def turn_copy(n):
            e.wait_ge(ht_full.sem, ht_full.at(n + 1))
            nc.scalar.activation(hin, ps[:, 0, :], ACT.Identity, bias=cols[:, 1:2], scale=cols[:, 0:1]).then_inc(ht_laid.sem, 1)

        turn_copy(0)

        def body(g, more_):
            for c in range(HID):
                e.wait_ge(hid_full.sem, hid_full.at(HID * g + c + 1))
                nc.scalar.activation(hT[:, c % 2, :], ps[:, 1 + c % 2, :], ACT.Gelu, bias=cols[:, 2 + c:3 + c]).then_inc(hid_laid.sem, 1)
            if more_:
                turn_copy(g + 1)

        pipelined_groups(e, body)

    T = nc.tensor

    def pe_turn(e, t, s):
        e.wait_ge(ln_out_done.sem, ln_out_done.at(t + 1))
        e.wait_ge(xt_laid.sem, xt_laid.at(t))
        T.transpose(ps[:, 0, 0:P], k.xn[:, s, 0, :], k.ident[:]).then_inc(xt_full.sem, 1)

    def pe_keys(e, t, s):
        e.wait_ge(k_laid.sem, k_laid.at(t))
        e.nop(nofuse=True)
        T.matmul(ps[:, 2, 0:P], wk, k.ctxT[:, bass.ts(t, P)], start=True, stop=True).then_inc(k_full.sem, 1)

    def pe_query(e, t, s):
        e.wait_ge(xt_laid.sem, xt_laid.at(t + 1))
        e.wait_ge(q_laid.sem, q_laid.at(t))
        T.matmul(ps[:, 1, 0:P], wq, k.xnT[:, s, 0:P], start=True, stop=True).then_inc(q_full.sem, 1)

    def pe_scores(e, t, s):
        e.wait_ge(q_laid.sem, q_laid.at(t + 1))
        e.wait_ge(k_laid.sem, k_laid.at(t + 1))
        e.wait_ge(s_laid.sem, s_laid.at(t))
        e.nop(nofuse=True)
        for b in range(2):
            last = T.matmul(ps[64 * b:64 * b + 64, 3, 0:H * CTX], qT[:, s, 64 * b:64 * b + 64], flat(kbd[:, s, b, :, :]), start=True, stop=True)
        last.then_inc(s_full.sem, 1)

    def pe_attn(e, t, s):
        e.wait_ge(a_done.sem, a_done.at(t + 1))
        e.wait_ge(a_laid.sem, a_laid.at(t))
        for h in range(H):
            last = T.matmul(ps[0:CTX, 5, 0:P], EX[:, s, h, :], k.ident[:], start=(h == 0), stop=(h == H - 1))
        last.then_inc(a_full.sem, 1)

    def pe_context(e, t, s):
        e.wait_ge(cT_laid.sem, cT_laid.at(t))
        e.wait_ge(a_laid.sem, a_laid.at(t + 1))
        e.nop(nofuse=True)
        for b in range(2):
            last = T.matmul(ps[:, 6, b * SEQ:(b + 1) * SEQ], vs[0:CTX, s, b, :], aT[0:CTX, s, b * SEQ:(b + 1) * SEQ], start=True, stop=True)
        last.then_inc(c_full.sem, 1)

    def pe_film(e, t, s):
        e.wait_ge(f_laid.sem, f_laid.at(t))
        T.matmul(ps[:, 7, :], k.ones, bf[0:1, :], start=True, stop=False)
        e.wait_ge(cT_laid.sem, cT_laid.at(t + 1))
        T.matmul(ps[:, 7, :], cT[:, s, :], wf, start=False, stop=True).then_inc(f_full.sem, 1)

    def pe_step(e, t, s):
        o = 1 - s
        film = not (isinstance(t, int) and t == 0)
        if more(t, 1):
            pe_scores(e, t + 1, o)
        e.wait_ge(c_laid.sem, c_laid.at(t + 1))
        e.wait_ge(v_laid.sem, v_laid.at(t))
        e.nop(nofuse=True)
        for b in range(2):
            last = T.matmul(ps[0:CTX, 4, b * D:(b + 1) * D], cg[:, s, b * CTX:(b + 1) * CTX], wv, start=True, stop=True)
        last.then_inc(v_full.sem, 1)
        if film:
            pe_attn(e, t - 1, o)
        if more(t, 2):
            pe_turn(e, t + 2, s)
            pe_keys(e, t + 2, s)
        if film:
            pe_context(e, t - 1, o)
        if more(t, 2):
            pe_query(e, t + 2, s)
        if film:
            pe_film(e, t - 1, o)

    def pe(e):
        e.wait_ge(w2_in.sem, w2_in.at(48))
        e.wait_ge(prep.sem, prep.at(5))
        T.transpose(ps[:, 0, 0:TILES], tmf[0:TILES, :], k.ident[0:TILES, 0:TILES]).then_inc(prep_t.sem, 1)
        e.wait_ge(prep.sem, prep.at(6))
        e.wait_ge(prep_p.sem, prep_p.at(1))
        e.wait_ge(prep_tt.sem, prep_tt.at(1))
        e.wait_ge(w_in.sem, w_in.at(READY))
        for t in range(2):
            pe_turn(e, t, t)
            pe_keys(e, t, t)
            pe_query(e, t, t)
        pe_scores(e, 0, 0)
        pipelined_tiles(e, lambda t, s: pe_step(e, t, s), tail=4)
        pe_attn(e, TILES - 1, 1)
        pe_context(e, TILES - 1, 1)
        pe_film(e, TILES - 1, 1)
        e.wait_ge(f_laid.sem, f_laid.at(TILES))
        e.wait_ge(xs_done.sem, xs_done.at(TILES))
        e.wait_ge(k.ssm.toep_in.sem, 32)
        for q in range(0, 8, 2):
            for flip in range(2):
                for i in range(16):
                    for b in range(2):
                        bank = q + (b ^ flip)
                        d = 16 * bank + i
                        half = slice(b * SEQ, (b + 1) * SEQ)
                        last = T.matmul(ps[half, bank, i * TILES:(i + 1) * TILES], k.toep[half, d, :], XS[half, :, d], start=True, stop=True)
            last.then_inc(b_full.sem, 2)
        e.wait_ge(b_laid.sem, b_laid.at(8))

        def turn(n):
            e.wait_ge(lnC.out.sem, lnC.out.at(n + 1))
            for j in range(GT):
                last = T.transpose(ps[:, 0, j * P:(j + 1) * P], k.xn[:, 0, j, :], k.ident[:])
            last.then_inc(ht_full.sem, 1)

        turn(0)

        def hidden(g, c):
            if c == 0:
                e.wait_ge(ht_laid.sem, ht_laid.at(g + 1))
            T.matmul(ps[:, 1 + c % 2, :], w1[:, c * P:(c + 1) * P], hin, start=True, stop=True).then_inc(hid_full.sem, 1)

        def outputs(g, c):
            e.wait_ge(hid_laid.sem, hid_laid.at(HID * g + c + 1))
            if c == 0:
                e.wait_ge(o_added.sem, o_added.at(g))
            for j in range(GT):
                T.matmul(ps[:, 3, j * P:(j + 1) * P], hT[:, c % 2, j * P:(j + 1) * P], w2[:, c, :],
                         start=(c == 0 and j == 0), stop=False, skip_group_check=True)

        def body(g, more_):
            hidden(g, 0)
            hidden(g, 1)
            outputs(g, 0)
            hidden(g, 2)
            outputs(g, 1)
            hidden(g, 3)
            if more_:
                turn(g + 1)
            outputs(g, 2)
            outputs(g, 3)
            for j in range(GT):
                last = T.matmul(ps[:, 3, j * P:(j + 1) * P], k.ones, rows[0:1, 4, :], start=False, stop=(j == GT - 1), skip_group_check=True)
            last.then_inc(o_full.sem, 1)

        pipelined_groups(e, body)

    return dict(sp=sp, pe=pe, act=act, dve=dve, pool=pool)


class Thresholds:

    BITS = 31

    def __init__(self, k, io):
        self.k, self.io = k, io
        sem = lambda n: k.sem("thr_" + n)
        self.w_in, self.ready, self.counted, self.total, self.read, self.step = (sem(n) for n in ("loaded", "ready", "counted", "totals", "totals_read", "step"))
        self.abs = k.sb("thr_abs", [P, 1024 + 8])
        self.hits = k.sb("thr_hits", [P, 2, 1024 + 8], BF16)
        self.need = k.sb("thr_need", [P, 8])
        self.count = k.sb("thr_count", [P, 8])
        self.cur = k.sb("thr_found", [P, 8], I32)
        self.cand = k.sb("thr_candidate", [P, 8], I32)
        self.bit = k.sb("thr_bit", [P, 8], I32)
        self.enough = k.sb("thr_enough", [P, 8], I32)
        self.sets = [(0, 512, P * 512), (512, 512, P * 512), (1024, 4, P * 4), (1028, 1, P)]

    def sp(self, e):
        io, a = self.io, self.abs
        with self.k.nc.allow_non_contiguous_dma(reason="biases are small"):
            e.dma_start(a[:, 0:512], io["L1_ffn_W1"]).then_inc(self.w_in.sem, 16)
            e.dma_start(a[:, 512:1024].rearrange("p (c d) -> p c d", c=4), io["L1_ffn_W2"].rearrange("(c p) d -> p c d", p=P)).then_inc(self.w_in.sem, 16)
            e.dma_start(a[:, 1024:1028], io["L1_ffn_b1"].rearrange("(c p) -> p c", p=P)).then_inc(self.w_in.sem, 16)
            e.dma_start(a[:, 1028:1029], io["L1_ffn_b2"].rearrange("(p a) -> p a", a=1)).then_inc(self.w_in.sem, 16)

    def dve_start(self, e):
        V = self.k.nc.vector
        V.memset(self.cur[:], 0)
        V.memset(self.cand[:], 1 << (self.BITS - 1))
        V.memset(self.bit[:], 1 << (self.BITS - 1))
        for i, (_, _, n) in enumerate(self.sets):
            kth = max(1, int(n * 0.1 / 2))
            V.memset(self.need[:, 2 * i:2 * i + 1], float(kth))
            V.memset(self.need[:, 2 * i + 1:2 * i + 2], float(n - kth + 1))
        e.wait_ge(self.w_in.sem, self.w_in.at(64))
        bits = self.abs[:, 0:1029].bitcast(I32)
        V.tensor_scalar(bits, bits, 0x7FFFFFFF, None, ALU.bitwise_and).then_inc(self.ready.sem, 1)
        e.wait_ge(self.ready.sem, self.ready.at(1))

    def dve_round(self, e, t):
        V = self.k.nc.vector
        first, last = isinstance(t, int) and t == 0, isinstance(t, int) and t == self.BITS
        if not first:
            e.wait_ge(self.total.sem, self.total.at(t))
            V.tensor_tensor(self.enough[:], self.k.ps[:, 2, D:D + 8], self.need[:], ALU.is_ge).then_inc(self.read.sem, 1)
            e.wait_ge(self.read.sem, self.read.at(t))
            e.nop(nofuse=True)
            V.copy_predicated(self.cur[:], self.enough[:], self.cand[:])
            V.tensor_scalar(self.bit[:], self.bit[:], 1, None, ALU.logical_shift_right).then_inc(self.step.sem, 1)
            if last:
                return
            e.wait_ge(self.step.sem, self.step.at(2 * t - 1))
            e.nop(nofuse=True)
            V.tensor_tensor(self.cand[:], self.cur[:], self.bit[:], ALU.bitwise_or).then_inc(self.step.sem, 1)
            e.wait_ge(self.step.sem, self.step.at(2 * t))
            e.nop(nofuse=True)
        for i, (at, n, _) in enumerate(self.sets):
            for j in range(2):
                c = 2 * i + j
                ins = V.tensor_scalar(self.hits[:, j, at:at + n], self.abs[:, at:at + n], self.cand[:, c:c + 1].bitcast(F32), 0.0,
                                      ALU.is_ge, ALU.add, accum_out=self.count[:, c:c + 1])
        ins.then_inc(self.counted.sem, 1)

    def pe_total(self, e, t):
        e.wait_ge(self.counted.sem, self.counted.at(t + 1))
        self.k.nc.tensor.matmul(self.k.ps[:, 2, D:D + 8], self.k.onesq[:], self.count[:], start=True, stop=True).then_inc(self.total.sem, 1)

    @property
    def value(self):
        return self.cur[:].bitcast(F32)


def ffn1(k, io, freed):
    th = k.thresholds

    def loads(k, io, v):
        row = lambda n: io[n].rearrange("(a n) -> a n", a=1)
        col = lambda n: io[n].rearrange("(p a) -> p a", a=1)
        return [
            (v.w1[:, 0, :], io["L1_ffn_W1"]),
            (v.w2[:, 0, :, :], io["L1_ffn_W2"].rearrange("(c p) d -> p c d", p=P)),
            (v.b1[:, 0, :], io["L1_ffn_b1"].rearrange("(c p) -> p c", p=P)),
            (v.b2[0:2, :], row("L1_ffn_b2").partition_broadcast(2)),
            (v.wr, io["L1_ffn_Wr"]),
            (v.br[0:8, :], col("L1_ffn_br")),
            (v.gam, col("L1_ffn_ln_gamma")),
            (v.bet, col("L1_ffn_ln_beta")),
        ]

    def prepare(k, io, v):
        V = k.nc.vector
        step, ready = k.sem("f1_perturb_step"), k.sem("f1_perturbed")
        m1, m2, q, a2 = v.cv.f32(512), v.cv.f32(512), v.cv.f32(512), v.cv.f32(D)

        def dve(e):
            e.wait_ge(v.w_in.sem, v.w_in.at(16 * len(v.loads)))
            n = 0

            def go(ins):
                nonlocal n
                n += 1
                ins.then_inc(step.sem, 1)
                e.wait_ge(step.sem, step.at(n))

            def perturb(dst, w, a, i, rows=slice(0, P), only=None):
                width = w.shape[-1]
                x1, x2, xq = m1[rows, 0:width], m2[rows, 0:width], q[rows, 0:width]
                top, bot = th.value[rows, 2 * i:2 * i + 1], th.value[rows, 2 * i + 1:2 * i + 2]
                go(V.tensor_scalar(x1, a, top, None, ALU.is_ge))
                go(V.tensor_scalar(x2, a, bot, None, ALU.is_le))
                go(V.tensor_tensor(xq, x1, x2, ALU.mult))
                go(V.tensor_tensor(x2, x2, xq, ALU.subtract))
                go(V.tensor_tensor(x2, x2, x1, ALU.subtract))
                go(V.scalar_tensor_tensor(xq, w, 0.8, x2, ALU.mult, ALU.mult))
                if only is not None:
                    go(V.tensor_scalar(xq, xq, only, None, ALU.mult))
                go(V.tensor_tensor(dst, w, xq, ALU.add))

            perturb(v.w1[:, 1, :], v.w1[:, 0, :], th.abs[:, 0:512], 0)
            w2 = v.w2.rearrange("p x c d -> p x (c d)")
            perturb(w2[:, 1, :], w2[:, 0, :], th.abs[:, 512:1024], 1)
            perturb(v.b1[:, 1, :], v.b1[:, 0, :], th.abs[:, 1024:1028], 2)
            go(V.tensor_scalar(a2[0:2, 0:D].bitcast(I32), v.b2[0:2, :].bitcast(I32), 0x7FFFFFFF, None, ALU.bitwise_and))
            perturb(v.b2[0:2, :], v.b2[0:2, :], a2[0:2, 0:D], 3, slice(0, 2), k.ident[0:2, 1:2])
            V.drain().then_inc(ready.sem, 1)

        def pe(e):
            e.wait_ge(ready.sem, ready.at(1))

        k.perturb = dve
        return dict(pe=pe, act=pe)

    weights = Carve(k.arena, 26819)
    work = Carve(k.toep[:].rearrange("p a b -> p (a b)"))
    return experts(k, io, "f1", False, 5, loads, freed, weights, work, prepare)


def ffn2(k, io, freed, start):
    nc, ps = k.nc, k.ps
    GATE, IC = 6, 4
    HID = IC * P
    PAIRS = TILES // 2
    sem = lambda n, total=PAIRS: k.sem("f2_" + n, total)
    w_in, w_sum, w_tot, w_tern = sem("w_loaded", None), sem("w_sums", 1), sem("w_totals", 1), sem("w_ternary", 1)
    w_step, w_turned, w_laid = sem("w_step", 7), sem("w_turned", 3), sem("w_laid", 3)
    q_step, q_done, qt_full, qt_laid = sem("q_step", 5 * GROUPS), sem("q_done", GROUPS), sem("qT_full", GROUPS), sem("qT_laid", GROUPS)
    g_full, u_full, r_done, r2_done, h_done, a_done, hr_done, hq_done = (sem(n) for n in ("gate_full", "up_full", "relu", "relu_squared", "h", "h_max", "h_rounded", "h_quantized"))
    s_done, ht_full, ht_laid, y_full, x_step = sem("h_scale", 2 * PAIRS), sem("hT_full"), sem("hT_laid"), sem("y_full"), sem("x_added")
    x_done = sem("x_done", GROUPS)
    before = k.x_ready
    k.x_ready = x_done
    ln = GroupNorm(k, "f2_ln", 0, lambda g, j: k.x[:, 4 * g + j, :], lambda g, j: k.xn[:, 0, j, :])

    cv = Carve(k.arena, start)
    wraw = cv.f32(3, HID)
    wt = cv.f32(3, HID)
    wb = cv.bf16(3, HID)
    wT = cv.bf16(3, HID)
    identb = cv.bf16(P)
    sums, mean, inv = cv.f32(4), cv.f32(4), cv.f32(4)
    am, sc, cgt, cut = (cv.f32(GT) for _ in range(4))
    qf = cv.f32(GT, D)
    qb = cv.bf16(GT, D)
    qT = cv.bf16(GT * P)
    r, r2, h, hq = (cv.f32(2, HID) for _ in range(4))
    hb = cv.bf16(2, HID)
    hT = cv.bf16(2, HID)
    ah, sh, yc = cv.f32(2), cv.f32(2), cv.f32(2, 2)
    onesq = k.onesq
    bank16 = lambda b: ps[:, b, :].bitcast(BF16)

    def sp(e):
        e.wait_ge(freed.sem, freed.end)
        e.dma_start(wraw[:, 0, :].rearrange("p (c d) -> p c d", c=IC), io["L2_ffn_w_gate"].rearrange("(c p) d -> p c d", p=P)).then_inc(w_in.sem, 16)
        e.dma_start(wraw[:, 1, :].rearrange("p (c d) -> p c d", c=IC), io["L2_ffn_w_up"].rearrange("(c p) d -> p c d", p=P)).then_inc(w_in.sem, 16)
        e.dma_start(wraw[:, 2, :], io["L2_ffn_w_down"]).then_inc(w_in.sem, 16)

    T, V, S = nc.tensor, nc.vector, nc.scalar

    def quantize(e, g):
        n = 5 * g
        e.wait_ge(ln.out.sem, ln.out.at(g + 1))
        V.tensor_reduce(am[:], k.xn[:, 0, :, :], AX.X, ALU.max, apply_absolute_value=True).then_inc(q_step.sem, 1)
        e.wait_ge(q_step.sem, q_step.at(n + 1))
        V.tensor_scalar(am[:], am[:], EPSQ, 1.0 / 127.0, ALU.max, ALU.mult).then_inc(q_step.sem, 1)
        e.wait_ge(q_step.sem, q_step.at(n + 2))
        V.reciprocal(sc[:], am[:]).then_inc(q_step.sem, 1)
        e.wait_ge(q_step.sem, q_step.at(n + 3))
        for j in range(GT):
            last = V.tensor_scalar(qf[:, j, :], k.xn[:, 0, j, :], sc[:, j:j + 1], ROUND, ALU.mult, ALU.add)
        last.then_inc(q_step.sem, 1)
        e.wait_ge(q_step.sem, q_step.at(n + 4))
        V.tensor_scalar(qb[:], qf[:], -ROUND, 127.0, ALU.add, ALU.min).then_inc(q_done.sem, 1)

    def scales(e, g):
        V.tensor_scalar(cgt[:], am[:], mean[:, 0:1], None, ALU.mult)
        V.tensor_scalar(cut[:], am[:], mean[:, 1:2], None, ALU.mult).then_inc(q_step.sem, 1)

    def dve(e):
        e.wait_ge(before.sem, before.end)
        e.wait_ge(w_in.sem, w_in.at(48))
        for i in range(3):
            ins = V.tensor_reduce(sums[:, i:i + 1], wraw[:, i, :], AX.X, ALU.add, apply_absolute_value=True)
        V.tensor_copy(identb[:], k.ident[:]).then_inc(w_sum.sem, 1)
        ln.dve_stats(0)
        e.wait_ge(w_tot.sem, w_tot.at(1))
        V.tensor_scalar(mean[:, 0:3], ps[:, 0, 0:3], 1.0 / (P * HID), EPSQ, ALU.mult, ALU.max).then_inc(w_step.sem, 1)
        e.wait_ge(w_step.sem, w_step.at(1))
        ln.dve_aggregate(e, 0, True)
        V.reciprocal(inv[:, 0:3], mean[:, 0:3]).then_inc(w_step.sem, 1)
        e.wait_ge(w_step.sem, w_step.at(2))
        for i in range(3):
            V.tensor_scalar(wt[:, i, :], wraw[:, i, :], inv[:, i:i + 1], ROUND, ALU.mult, ALU.add).then_inc(w_step.sem, 1)
        V.tensor_scalar(mean[:, 2:3], mean[:, 2:3], k.gates[:, GATE:GATE + 1], None, ALU.mult).then_inc(w_step.sem, 1)
        e.wait_ge(w_step.sem, w_step.at(6))
        V.tensor_scalar(wt[:], wt[:], -ROUND, 1.0, ALU.add, ALU.min).then_inc(w_step.sem, 1)
        e.wait_ge(w_step.sem, w_step.at(7))
        V.tensor_scalar(wb[:], wt[:], -1.0, None, ALU.max).then_inc(w_tern.sem, 1)
        ln.dve_apply(e, 0, 0)
        quantize(e, 0)

        scales(e, 0)

        def pair(g, i, more):
            p, js = 2 * g + i, (2 * i, 2 * i + 1)
            if i == 0 and more:
                ln.dve_stats(g + 1)
            e.wait_ge(u_full.sem, u_full.at(p + 1))
            e.wait_ge(r2_done.sem, r2_done.at(p + 1))
            for s, j in enumerate(js):
                last = V.scalar_tensor_tensor(h[:, s, :], ps[:, 2 + s, :], cut[:, j:j + 1], r2[:, s, :], ALU.mult, ALU.mult)
            last.then_inc(h_done.sem, 1)
            e.wait_ge(h_done.sem, h_done.at(p + 1))
            V.tensor_reduce(ah[:], h[:], AX.X, ALU.max, apply_absolute_value=True).then_inc(a_done.sem, 1)
            if i == 0 and more:
                ln.dve_aggregate(e, g + 1, True)
            if i == 1 and more:
                scales(e, g + 1)
            e.wait_ge(a_done.sem, a_done.at(p + 1))
            V.tensor_scalar(ah[:], ah[:], EPSQ, 1.0 / 127.0, ALU.max, ALU.mult).then_inc(s_done.sem, 1)
            if i == 1:
                add(g, 0)
            elif not (isinstance(g, int) and g == 0):
                add(g - 1, 1)
            e.wait_ge(s_done.sem, s_done.at(2 * p + 1))
            V.reciprocal(sh[:], ah[:]).then_inc(s_done.sem, 1)
            V.tensor_scalar(yc[:, i, :], ah[:], mean[:, 2:3], None, ALU.mult)
            if i == 0 and more:
                ln.dve_apply(e, g + 1, g + 1)
            e.wait_ge(s_done.sem, s_done.at(2 * p + 2))
            for s in range(2):
                last = V.tensor_scalar(hq[:, s, :], h[:, s, :], sh[:, s:s + 1], ROUND, ALU.mult, ALU.add)
            last.then_inc(hr_done.sem, 1)
            e.wait_ge(hr_done.sem, hr_done.at(p + 1))
            V.tensor_scalar(hb[:], hq[:], -ROUND, 127.0, ALU.add, ALU.min).then_inc(hq_done.sem, 1)
            if i == 0 and more:
                quantize(e, g + 1)

        def add(g, i):
            p = 2 * g + i
            e.wait_ge(y_full.sem, y_full.at(p + 1))
            for s in range(2):
                t = GT * g + 2 * i + s
                last = V.scalar_tensor_tensor(k.x[:, t, :], ps[:, 7, s * D:(s + 1) * D], yc[:, i, s:s + 1], k.x[:, t, :], ALU.mult, ALU.add)
            last.then_inc(x_step.sem, 1)
            if i == 1:
                e.wait_ge(x_step.sem, x_step.at(p + 1))
                e.sem_inc(x_done.sem, 1)

        def body(g, more):
            pair(g, 0, more)
            pair(g, 1, more)

        pipelined_groups(e, body)
        add(GROUPS - 1, 1)

    def pe_sums(e):
        e.wait_ge(w_sum.sem, w_sum.at(1))
        T.matmul(ps[:, 0, 0:3], onesq[:], sums[:, 0:3], start=True, stop=True).then_inc(w_tot.sem, 1)
        e.wait_ge(w_step.sem, w_step.at(1))

    def pe(e):
        e.wait_ge(w_tern.sem, w_tern.at(1))
        for i in range(3):
            for c in range(IC):
                last = T.transpose(bank16(4 + i)[:, c * P:(c + 1) * P], wb[:, i, c * P:(c + 1) * P], identb[:])
            last.then_inc(w_turned.sem, 1)
        e.wait_ge(w_laid.sem, w_laid.at(3))

        def turn(n):
            e.wait_ge(q_done.sem, q_done.at(n + 1))
            for j in range(GT):
                last = T.transpose(bank16(4)[:, j * P:(j + 1) * P], qb[:, j, :], identb[:])
            last.then_inc(qt_full.sem, 1)

        def gate_up(g, i):
            p = 2 * g + i
            if i == 0:
                e.wait_ge(qt_laid.sem, qt_laid.at(g + 1))
            e.wait_ge(r_done.sem, r_done.at(p))
            for s in range(2):
                j = 2 * i + s
                last = T.matmul(ps[:, s, :], qT[:, j * P:(j + 1) * P], wT[:, 0, :], start=True, stop=True)
            last.then_inc(g_full.sem, 1)
            e.wait_ge(h_done.sem, h_done.at(p))
            for s in range(2):
                j = 2 * i + s
                last = T.matmul(ps[:, 2 + s, :], qT[:, j * P:(j + 1) * P], wT[:, 1, :], start=True, stop=True)
            last.then_inc(u_full.sem, 1)

        def turn_h(g, i):
            p = 2 * g + i
            e.wait_ge(hq_done.sem, hq_done.at(p + 1))
            for s in range(2):
                for c in range(IC):
                    last = T.transpose(bank16(5 + s)[:, c * P:(c + 1) * P], hb[:, s, c * P:(c + 1) * P], identb[:])
            last.then_inc(ht_full.sem, 1)

        def down(g, i):
            p = 2 * g + i
            e.wait_ge(ht_laid.sem, ht_laid.at(p + 1))
            e.wait_ge(x_step.sem, x_step.at(p))
            for s in range(2):
                for c in range(IC):
                    last = T.matmul(ps[:, 7, s * D:(s + 1) * D], hT[:, s, c * P:(c + 1) * P], wT[:, 2, c * P:(c + 1) * P], start=(c == 0), stop=(c == IC - 1))
            last.then_inc(y_full.sem, 1)

        turn(0)
        gate_up(0, 0)

        def body(g, more):
            gate_up(g, 1)
            turn_h(g, 0)
            down(g, 0)
            if more:
                turn(g + 1)
                gate_up(g + 1, 0)
            turn_h(g, 1)
            down(g, 1)

        pipelined_groups(e, body)

    def act(e):
        for i in range(3):
            e.wait_ge(w_turned.sem, w_turned.at(i + 1))
            S.copy(wT[:, i, :], bank16(4 + i)[:, 0:HID]).then_inc(w_laid.sem, 1)

        def turn_copy(n):
            e.wait_ge(qt_full.sem, qt_full.at(n + 1))
            S.copy(qT[:], bank16(4)[:, 0:GT * P]).then_inc(qt_laid.sem, 1)

        turn_copy(0)

        def relu_squared(g, i):
            p = 2 * g + i
            e.wait_ge(r2_done.sem, r2_done.at(p))
            e.wait_ge(g_full.sem, g_full.at(p + 1))
            if i == 0:
                e.wait_ge(q_step.sem, q_step.at(5 * g + 5))
            for s in range(2):
                j = 2 * i + s
                last = S.activation(r[:, s, :], ps[:, s, :], ACT.Relu, scale=cgt[:, j:j + 1])
            last.then_inc(r_done.sem, 1)
            e.wait_ge(r_done.sem, r_done.at(p + 1))
            e.wait_ge(h_done.sem, h_done.at(p))
            S.activation(r2[:], r[:], ACT.Square).then_inc(r2_done.sem, 1)

        def copy_h(g, i):
            p = 2 * g + i
            e.wait_ge(ht_full.sem, ht_full.at(p + 1))
            for s in range(2):
                last = S.copy(hT[:, s, :], bank16(5 + s)[:, 0:HID])
            last.then_inc(ht_laid.sem, 1)

        relu_squared(0, 0)

        def body(g, more):
            relu_squared(g, 1)
            copy_h(g, 0)
            if more:
                turn_copy(g + 1)
                relu_squared(g + 1, 0)
            copy_h(g, 1)

        pipelined_groups(e, body)

    def pool(e):
        e.wait_ge(before.sem, before.end)
        ln.pool_rstd(e, 0)

        def body(g, more):
            if more:
                ln.pool_rstd(e, g + 1)

        pipelined_groups(e, body)

    return dict(sp=sp, pe_sums=pe_sums, pe=pe, act=act, dve=dve, pool=pool)


def ffn3(k, io, freed, start):
    nc, ps = k.nc, k.ps
    GATE, IC, R = 7, 4, 16
    HID = IC * P
    sem = lambda n, total=GROUPS: k.sem("f3_" + n, total)
    w_in, w_step, w_low, w_ready = sem("w_loaded", None), sem("w_step", 6), sem("low_rank", 1), sem("w_ready", 1)
    w_turned, w_laid = sem("w_turned", 2), sem("w_laid", 2)
    u_full, u_laid, t_full, t_laid = (sem(n, 1) for n in ("uT_full", "uT_laid", "fv_full", "fv_laid"))
    xt_full, xt_laid, o_full, x_done = (sem(n) for n in ("xT_full", "xT_laid", "o_full", "x_done"))
    h_full, r_done, h_laid = (sem(n, IC * GROUPS) for n in ("h_full", "relu", "squared"))
    before = k.x_ready
    k.x_ready = x_done
    ln = GroupNorm(k, "f3_ln", 0, lambda g, j: k.x[:, 4 * g + j, :], lambda g, j: k.xn[:, 0, j, :])
    cv = Carve(k.arena, start)
    wf, wp = cv.f32(IC, D), cv.f32(HID)
    tf, tp = cv.f32(IC, D), cv.f32(HID)
    wfT, wpT = cv.f32(HID), cv.f32(IC, D)
    un, uT = cv.f32(IC, R), cv.f32(IC, P)
    fbT, vn, fv = cv.f32(R), cv.f32(D), cv.f32(D)
    gate = cv.f32(1)
    s5, i5 = cv.f32(IC + 1), cv.f32(IC + 1)
    r, hT = cv.f32(2, GT * P), cv.f32(IC, GT * P)
    HBANK = (1, 2, 5, 6)
    xnT = k.xnT[:, 0, :]
    T, V, S = nc.tensor, nc.vector, nc.scalar

    def sp(e):
        e.wait_ge(freed.sem, freed.end)
        with nc.allow_non_contiguous_dma(reason="a 16 by 16 matrix, transposed"):
            for dst, src in (
                (wf, io["L3_ffn_w_fc"].rearrange("(c p) d -> p c d", p=P)), (wp, io["L3_ffn_w_proj"]),
                (un, io["L3_ffn_u"].rearrange("(c p) r -> p c r", p=P)), (fbT[0:R, :], io["L3_ffn_fast_b"].rearrange("i j -> j i")),
                (vn[0:R, :], io["L3_ffn_v"]), (gate, io["L3_ffn_gate"].rearrange("(a n) -> a n", a=1).partition_broadcast(P)),
            ):
                e.dma_start(dst, src).then_inc(w_in.sem, 16)

    def dve_round(e):
        e.wait_ge(w_in.sem, w_in.at(96))
        n = 0

        def go(ins):
            nonlocal n
            n += 1
            ins.then_inc(w_step.sem, 1)
            e.wait_ge(w_step.sem, w_step.at(n))

        V.tensor_reduce(s5[:, 0:IC], wf[:], AX.X, ALU.add, apply_absolute_value=True)
        go(V.tensor_reduce(s5[:, IC:IC + 1], wp[:], AX.X, ALU.add, apply_absolute_value=True))
        V.tensor_scalar(s5[:, 0:IC], s5[:, 0:IC], 1.0 / D, EPSQ, ALU.mult, ALU.max)
        go(V.tensor_scalar(s5[:, IC:IC + 1], s5[:, IC:IC + 1], 1.0 / HID, EPSQ, ALU.mult, ALU.max))
        go(V.reciprocal(i5[:], s5[:]))
        for c in range(IC):
            V.tensor_scalar(tf[:, c, :], wf[:, c, :], i5[:, c:c + 1], ROUND, ALU.mult, ALU.add)
        go(V.tensor_scalar(tp[:], wp[:], i5[:, IC:IC + 1], ROUND, ALU.mult, ALU.add))
        V.tensor_scalar(tf[:], tf[:], -ROUND, 1.0, ALU.add, ALU.min)
        go(V.tensor_scalar(tp[:], tp[:], -ROUND, 1.0, ALU.add, ALU.min))
        for c in range(IC):
            V.tensor_scalar(tf[:, c, :], tf[:, c, :], -1.0, s5[:, c:c + 1], ALU.max, ALU.mult)
        go(V.tensor_scalar(tp[:], tp[:], -1.0, s5[:, IC:IC + 1], ALU.max, ALU.mult))

    k.round_next = dve_round

    def dve(e):
        e.wait_ge(before.sem, before.end)
        ln.dve_stats(0)
        e.wait_ge(u_full.sem, u_full.at(1))
        V.tensor_copy(uT[0:R, :, :], ps[0:R, 0, :].rearrange("p (c f) -> p c f", c=IC)).then_inc(u_laid.sem, 1)
        ln.dve_aggregate(e, 0, False)
        e.wait_ge(t_full.sem, t_full.at(1))
        V.tensor_copy(fv[0:R, :], ps[0:R, 1, 0:D]).then_inc(t_laid.sem, 1)
        ln.dve_apply(e, 0, 0)
        e.wait_ge(w_low.sem, w_low.at(1))
        V.scalar_tensor_tensor(tf[:], ps[:, 2, :].rearrange("p (c d) -> p c d", c=IC), gate[:], tf[:], ALU.mult, ALU.add).then_inc(w_ready.sem, 1)
        for i, dst in enumerate((wfT[:], wpT.rearrange("p c d -> p (c d)"))):
            e.wait_ge(w_turned.sem, w_turned.at(i + 1))
            V.tensor_scalar(dst, ps[:, 3 + i, :], 1.0 if i == 0 else k.gates[:, GATE:GATE + 1], None, ALU.mult).then_inc(w_laid.sem, 1)

        def square(g, c):
            e.wait_ge(r_done.sem, r_done.at(IC * g + c + 1))
            V.tensor_tensor(hT[:, c, :], ps[:, HBANK[c], :], r[:, c % 2, :], ALU.mult).then_inc(h_laid.sem, 1)

        def body(g, more):
            square(g, 0)
            if more:
                ln.dve_stats(g + 1)
            square(g, 1)
            if more:
                e.wait_ge(ln.stats.sem, ln.stats.at(g + 2))
                e.nop(nofuse=True)
                ln.dve_aggregate(e, g + 1, True)
            square(g, 2)
            if more:
                ln.dve_apply(e, g + 1, g + 1)
            square(g, 3)
            e.wait_ge(o_full.sem, o_full.at(g + 1))
            e.nop(nofuse=True)
            xg = k.x[:, bass.ts(g, GT), :]
            V.tensor_tensor(xg, ps[:, 3, :].rearrange("p (j d) -> p j d", j=GT), xg, ALU.add).then_inc(x_done.sem, 1)

        pipelined_groups(e, body)

    def pe(e):
        e.wait_ge(w_in.sem, w_in.at(96))
        e.wait_ge(before.sem, before.end)
        for c in range(IC):
            last = T.transpose(ps[0:R, 0, c * P:(c + 1) * P], un[:, c, :], k.ident[:])
        last.then_inc(u_full.sem, 1)
        T.matmul(ps[0:R, 1, 0:D], fbT[0:R, :], vn[0:R, :], start=True, stop=True).then_inc(t_full.sem, 1)
        e.wait_ge(u_laid.sem, u_laid.at(1))
        e.wait_ge(t_laid.sem, t_laid.at(1))
        for c in range(IC):
            last = T.matmul(ps[:, 2, c * P:(c + 1) * P], uT[0:R, c, :], fv[0:R, :], start=True, stop=True)
        last.then_inc(w_low.sem, 1)
        e.wait_ge(w_ready.sem, w_ready.at(1))
        for i in range(2):
            for c in range(IC):
                last = T.transpose(ps[:, 3 + i, c * P:(c + 1) * P], tf[:, c, :] if i == 0 else tp[:, c * P:(c + 1) * P], k.ident[:])
            last.then_inc(w_turned.sem, 1)
        e.wait_ge(w_laid.sem, w_laid.at(2))

        def turn(n):
            e.wait_ge(ln.out.sem, ln.out.at(n + 1))
            for j in range(GT):
                last = T.transpose(ps[:, 0, j * P:(j + 1) * P], k.xn[:, 0, j, :], k.ident[:])
            last.then_inc(xt_full.sem, 1)

        def hidden(g, c):
            if c == 0:
                e.wait_ge(xt_laid.sem, xt_laid.at(g + 1))
            T.matmul(ps[:, HBANK[c], :], wfT[:, c * P:(c + 1) * P], xnT, start=True, stop=True).then_inc(h_full.sem, 1)

        def outputs(g, c):
            e.wait_ge(h_laid.sem, h_laid.at(IC * g + c + 1))
            if c == 0:
                e.wait_ge(x_done.sem, x_done.at(g))
            for j in range(GT):
                last = T.matmul(ps[:, 3, j * P:(j + 1) * P], hT[:, c, j * P:(j + 1) * P], wpT[:, c, :],
                                start=(c == 0 and j == 0), stop=(c == IC - 1 and j == GT - 1), skip_group_check=True)
            if c == IC - 1:
                last.then_inc(o_full.sem, 1)

        turn(0)

        def body(g, more):
            hidden(g, 0)
            hidden(g, 1)
            outputs(g, 0)
            hidden(g, 2)
            outputs(g, 1)
            hidden(g, 3)
            if more:
                turn(g + 1)
            outputs(g, 2)
            outputs(g, 3)

        pipelined_groups(e, body)

    def act(e):
        def turn_copy(n):
            e.wait_ge(xt_full.sem, xt_full.at(n + 1))
            S.copy(xnT, ps[:, 0, :]).then_inc(xt_laid.sem, 1)

        turn_copy(0)

        def body(g, more):
            for c in range(IC):
                e.wait_ge(h_full.sem, h_full.at(IC * g + c + 1))
                S.activation(r[:, c % 2, :], ps[:, HBANK[c], :], ACT.Relu).then_inc(r_done.sem, 1)
            if more:
                turn_copy(g + 1)

        pipelined_groups(e, body)

    def pool(e):
        e.wait_ge(before.sem, before.end)
        ln.pool_rstd(e, 0)

        def body(g, more):
            if more:
                ln.pool_rstd(e, g + 1)

        pipelined_groups(e, body)

    return dict(sp=sp, pe=pe, act=act, dve=dve, pool=pool)


def store(k, io):
    nc = k.nc
    out_done = k.sem("out_stored")
    before = k.x_ready

    def sp(e):
        e.wait_ge(before.sem, before.end)
        e.dma_start(io["out"].rearrange("b s c -> (b s) c").rearrange("(t p) c -> p t c", p=P), k.x[:]).then_inc(out_done.sem, 16)
        e.wait_ge(out_done.sem, out_done.at(16))

    return dict(sp=sp)


def build_program(nc, io, upto=99):
    with ExitStack() as ctx:
        k = allocate(nc, ctx)
        k.thresholds = Thresholds(k, io)
        k.ssm = StateSpaceKernel(k, io)
        new = k.semaphores.next_sublayer
        first, first_ready, first_rest = setup(k, io)
        loaded = k.x_ready
        new()
        attn0, fold0 = attention(k, io, "a0", 16, "L0_xattn_Wq", "L0_xattn_Wk", "L0_xattn_Wv", "L0_xattn_Wo", "L0_xattn_bo", 0,
                                 None, 0, rounds=k.thresholds, ssm=k.ssm)
        attn0_done = k.x_ready
        new()
        ff0 = ffn0(k, io, loaded)
        ff0_done = k.x_ready
        new()
        attn1 = attention_ssm(k, io, attn0_done)
        attn1_done = k.x_ready
        toep = k.toep[:].rearrange("p a b -> p (a b)")
        new()
        ff1 = ffn1(k, io, ff0_done)
        ff1_done = k.x_ready
        new()
        attn2, fold2 = attention(k, io, "a2", 8, "L2_xattn_Wq", "L2_xattn_Wk", "L2_xattn_Wv", "L2_xattn_Wout", "L2_xattn_bout", 2,
                                 attn1_done, 0, Carve(toep, 6016), k.conv_done)
        attn2_done = k.x_ready
        new()
        ff2 = ffn2(k, io, attn1_done, 12300)
        new()
        attn3, fold3 = attention(k, io, "a3", 8, "L3_xattn_Wq", "L3_xattn_Wk", "L3_xattn_Wv", "L3_xattn_Wo", "L3_xattn_bo", 3,
                                 attn2_done, 0, Carve(toep), ff1_done, lambda e: k.round_next(e))
        new()
        ff3 = ffn3(k, io, attn2_done, 23700)
        queue = [first, dict(sp=fold0.pop("sp")), first_rest, dict(sp=k.thresholds.sp), first_ready, fold0, attn0, dict(sp=ff0.pop("sp")),
                 dict(sp=k.ssm.sp_matrices), ff0, attn1, dict(sp=ff1.pop("sp")), fold2,
                 dict(sp=ff2.pop("sp")), ff1, attn2, dict(pe=ff2.pop("pe_sums")), fold3, ff2,
                 dict(sp=ff3.pop("sp")), attn3, ff3,
                 store(k, io)]
        parts = queue[:upto]
        block = ctx.enter_context(nc.Block())

        @block.sync
        def _(e):
            for part in parts:
                if "sp" in part:
                    part["sp"](e)

        @block.tensor
        def _(e):
            for part in parts:
                if "pe" in part:
                    part["pe"](e)

        @block.scalar
        def _(e):
            for part in parts:
                if "act" in part:
                    part["act"](e)

        @block.vector
        def _(e):
            for part in parts:
                if "dve" in part:
                    part["dve"](e)

        @block.gpsimd
        def _(e):
            for part in parts:
                if "pool" in part:
                    part["pool"](e)


def kernel(**inputs):
    import numpy as np
    import concourse.bacc as bacc
    from concourse.bass_utils import run_bass_kernel_spmd

    nc = bacc.Bacc("TRN2", target_bir_lowering=False, num_devices=1)
    arrays, io = {}, {}
    for name, value in inputs.items():
        a = np.ascontiguousarray(value)
        if a.dtype == np.bool_:
            a = a.view(np.uint8)
        if a.ndim == 0:
            a = a.reshape(1)
        arrays[name] = a
        io[name] = nc.dram_tensor(name, a.shape, mybir.dt.from_np(a.dtype), kind="ExternalInput").ap()
    io["out"] = nc.dram_tensor("out", inputs["x"].shape, F32, kind="ExternalOutput").ap()
    build_program(nc, io)
    return run_bass_kernel_spmd(nc, [arrays], core_ids=[0]).results[0]["out"]
```
